# Optimizing a Trainium2 kernel written in Bass

```python
import numpy as np
import jax
import jax.numpy as jnp

def _softmax(x, axis=-1):
    return jax.nn.softmax(x, axis=axis)

def _gelu(x):
    return jax.nn.gelu(x, approximate=True)

def _silu(x):
    return jax.nn.silu(x)

def _sigmoid(x):
    return jax.nn.sigmoid(x)

def _layernorm(x, axis=-1, eps=1e-05):
    m = jnp.mean(x, axis=axis, keepdims=True)
    v = jnp.var(x, axis=axis, keepdims=True)
    return (x - m) / jnp.sqrt(v + eps)

def _scatter_add(tgt, idx, src, axis=0):
    return tgt.at[idx].add(src)

def _segment_sum(src, seg, n):
    return jax.ops.segment_sum(src, seg, n)
kernel_name = 'mk_perceiver_d2_seqx_r4_2ea988'

def setup_inputs(seed: int=0):
    np.random.seed(seed)
    _w = jnp.asarray

    def _rec_inputs():
        import jax
        import jax.numpy as jnp
        _rk = jax.random.key(seed)
        x = -0.0005207 + 1.001 * jax.random.normal(jax.random.fold_in(_rk, 1), (1, 256, 256), jnp.float32)
        _lenS = 256 - jax.random.randint(jax.random.fold_in(_rk, 7), (1,), 0, max(1, 256 // 4) + 1, jnp.int32)
        _lenS2 = 4096 - jax.random.randint(jax.random.fold_in(_rk, 8), (1,), 0, max(1, 4096 // 4) + 1, jnp.int32)
        _ctx_1024P = jax.random.normal(jax.random.fold_in(_rk, 11), (1, 16, 256), jnp.float32)
        _ctx_1024c = jax.random.dirichlet(jax.random.fold_in(_rk, 511), 0.3 * jnp.ones((16,), jnp.float32), (1, 4096))
        _ctx_1024t = jnp.einsum('bsk,bkd->bsd', _ctx_1024c, _ctx_1024P)
        _ctx_1024t = _ctx_1024t * jax.lax.rsqrt(jnp.mean(jnp.square(_ctx_1024t)) + 1e-12) * 0.953939
        ctx_1024 = -0.000514642 + 1.00011 * (_ctx_1024t + 0.3 * jax.random.normal(jax.random.fold_in(_rk, 611), (1, 4096, 256), jnp.float32))
        _validS = jnp.arange(256)[None, :] < _lenS[:, None]
        _validS2 = jnp.arange(4096)[None, :] < _lenS2[:, None]
        _causal = jnp.tril(jnp.ones((256, 256), dtype=bool))
        mask_Bx1xSxS2_ff1 = jnp.where(jnp.ones((1, 1, 256, 4096), dtype=bool), 1.0, 0.0).astype(jnp.float32)
        return (x, ctx_1024, mask_Bx1xSxS2_ff1)
    x, ctx_1024, mask_Bx1xSxS2_ff1 = _rec_inputs()

    def _L0_xattn_setup():
        import jax, jax.numpy as jnp
        import numpy as np
        import math
        B, S, D, H = (1, 512, 256, 16)
        DK = D // H
        DH = 64
        LOG_T_MIN = math.log(0.1)
        LOG_T_MAX = math.log(10.0)

        def _linear(x, W, b):
            return x @ W.T + b
        key = jax.random.key(seed)
        ks = jax.random.split(key, 20)
        p = 0.02
        return {'query': jax.random.normal(ks[0], (B, S, D), jnp.float32), 'key': jax.random.normal(ks[1], (B, S, D), jnp.float32), 'value': jax.random.normal(ks[2], (B, S, D), jnp.float32), 'Wq': jax.random.normal(ks[3], (D, D), jnp.float32) * p, 'bq': jax.random.normal(ks[4], (D,), jnp.float32) * p, 'Wk': jax.random.normal(ks[5], (D, D), jnp.float32) * p, 'bk': jax.random.normal(ks[6], (D,), jnp.float32) * p, 'Wv': jax.random.normal(ks[7], (D, D), jnp.float32) * p, 'bv': jax.random.normal(ks[8], (D,), jnp.float32) * p, 'Wo': jax.random.normal(ks[9], (D, D), jnp.float32) * p, 'bo': jax.random.normal(ks[10], (D,), jnp.float32) * p, 'w1': jax.random.normal(ks[11], (DH, 3), jnp.float32) * 0.3, 'b1': jax.random.normal(ks[12], (DH,), jnp.float32) * 0.1, 'w2': jax.random.normal(ks[13], (DH, DH), jnp.float32) * 0.1, 'b2': jax.random.normal(ks[14], (DH,), jnp.float32) * 0.1, 'w3': jax.random.normal(ks[15], (1, DH), jnp.float32) * 0.1, 'b3': jnp.full((1,), (LOG_T_MIN + LOG_T_MAX) / 2, jnp.float32)}
    _L0_xattn_all = _L0_xattn_setup()
    _L0_xattn_in = {k: v for k, v in _L0_xattn_all.items() if k in ('Wq', 'bq', 'Wk', 'bk', 'Wv', 'bv', 'Wo', 'bo', 'w1', 'b1', 'w2', 'b2', 'w3', 'b3')}
    del _L0_xattn_all

    def _L0_attn_setup():
        import jax, jax.numpy as jnp
        import numpy as np
        HEADS = 16
        THETA = 10000.0

        def _rope(x):
            b, n, d = x.shape
            half = d // 2
            inv_freq = 1.0 / THETA ** (jnp.arange(0, d, 2, dtype=jnp.float32) / d)
            ang = jnp.arange(n, dtype=jnp.float32)[:, None] * inv_freq
            cos, sin = (jnp.cos(ang), jnp.sin(ang))
            xp = x.reshape(b, n, half, 2)
            x1, x2 = (xp[..., 0], xp[..., 1])
            out = jnp.stack([x1 * cos - x2 * sin, x2 * cos + x1 * sin], axis=-1)
            return out.reshape(b, n, d)
        key = jax.random.key(seed)
        ks = jax.random.split(key, 8)
        B, N, C = (8, 512, 256)
        s = C ** (-0.5)
        return {'x': jax.random.normal(ks[0], (B, N, C), jnp.float32), 'Wq': jax.random.normal(ks[1], (C, C), jnp.float32) * s, 'bq': jax.random.normal(ks[2], (C,), jnp.float32) * 0.01, 'Wk': jax.random.normal(ks[3], (C, C), jnp.float32) * s, 'bk': jax.random.normal(ks[4], (C,), jnp.float32) * 0.01, 'Wv': jax.random.normal(ks[5], (C, C), jnp.float32) * s, 'bv': jax.random.normal(ks[6], (C,), jnp.float32) * 0.01, 'gamma': jnp.ones((C,), jnp.float32), 'beta': jnp.zeros((C,), jnp.float32)}
    _L0_attn_all = _L0_attn_setup()
    _L0_attn_in = {k: v for k, v in _L0_attn_all.items() if k in ('Wq', 'bq', 'Wk', 'bk', 'Wv', 'bv', 'gamma', 'beta')}
    del _L0_attn_all

    def _L0_ffn_setup():
        import jax, jax.numpy as jnp
        import numpy as np
        B, S, D = (2, 256, 256)
        H, HD = (16, 64)
        E_R = 31
        K_ACT = 3
        INTER = 256
        EPS = 1e-05
        BASE = 10000.0

        def _rmsnorm(x, gamma):
            rms = jnp.sqrt(jnp.mean(x * x, axis=-1, keepdims=True) + EPS)
            return x / rms * gamma

        def _rope(x, theta):
            seq = x.shape[2]
            angles = jnp.arange(seq, dtype=theta.dtype)[:, None] * theta
            cos = jnp.cos(angles)[None, None]
            sin = jnp.sin(angles)[None, None]
            x1, x2 = (x[..., 0::2], x[..., 1::2])
            return jnp.concatenate([x1 * cos - x2 * sin, x1 * sin + x2 * cos], axis=-1)

        def _forward(x, theta, gamma1, gamma2, q_w, q_b, k_w, k_b, v_w, v_b, o_w, o_b, router_w, router_b, sh_w1, sh_b1, sh_w2, sh_b2, re_w1, re_b1, re_w2, re_b2):
            b, s, d = x.shape
            xn = _rmsnorm(x, gamma1)
            q = (xn @ q_w + q_b).reshape(b, s, H, HD).transpose(0, 2, 1, 3)
            k = (xn @ k_w + k_b).reshape(b, s, H, HD).transpose(0, 2, 1, 3)
            v = (xn @ v_w + v_b).reshape(b, s, H, HD).transpose(0, 2, 1, 3)
            q = _rope(q, theta)
            k = _rope(k, theta)
            scale = 1.0 / np.sqrt(HD)
            scores = jnp.einsum('bhqd,bhkd->bhqk', q, k) * scale
            causal = jnp.tril(jnp.ones((s, s), dtype=bool))
            scores = jnp.where(causal, scores, -jnp.inf)
            attn = jax.nn.softmax(scores, axis=-1)
            ctx = jnp.einsum('bhqk,bhkd->bhqd', attn, v)
            ctx = ctx.transpose(0, 2, 1, 3).reshape(b, s, H * HD)
            attn_out = ctx @ o_w + o_b + xn
            an = _rmsnorm(attn_out, gamma2)
            shared = jax.nn.gelu(an @ sh_w1 + sh_b1, approximate=False) @ sh_w2 + sh_b2
            logits = an @ router_w + router_b
            aff = jax.nn.softmax(logits, axis=-1)
            topv, topi = jax.lax.top_k(aff, K_ACT)
            gates = jnp.sum(jax.nn.one_hot(topi, E_R, dtype=aff.dtype) * topv[..., None], axis=-2)
            h = jax.nn.gelu(jnp.einsum('bsd,edh->besh', an, re_w1) + re_b1[None, :, None, :], approximate=False)
            routed = jnp.einsum('bse,besh,ehd->bsd', gates, h, re_w2) + jnp.einsum('bse,ed->bsd', gates, re_b2)
            return shared + routed + an + attn_out
        key = jax.random.key(seed)
        ks = jax.random.split(key, 24)
        s = 0.02
        theta = BASE ** (-jnp.arange(HD // 2, dtype=jnp.float32) * 2.0 / HD)
        inp = {'x': jax.random.normal(ks[0], (B, S, D), jnp.float32), 'positions': jnp.arange(S, dtype=jnp.int32), 'theta': theta, 'gamma1': jnp.ones((D,), jnp.float32), 'gamma2': jnp.ones((D,), jnp.float32), 'q_w': jax.random.normal(ks[1], (D, H * HD), jnp.float32) * s, 'q_b': jnp.zeros((H * HD,), jnp.float32), 'k_w': jax.random.normal(ks[2], (D, H * HD), jnp.float32) * s, 'k_b': jnp.zeros((H * HD,), jnp.float32), 'v_w': jax.random.normal(ks[3], (D, H * HD), jnp.float32) * s, 'v_b': jnp.zeros((H * HD,), jnp.float32), 'o_w': jax.random.normal(ks[4], (H * HD, D), jnp.float32) * s, 'o_b': jnp.zeros((D,), jnp.float32), 'router_w': jax.random.normal(ks[5], (D, E_R), jnp.float32) * s, 'router_b': jnp.zeros((E_R,), jnp.float32), 'sh_w1': jax.random.normal(ks[6], (D, INTER), jnp.float32) * s, 'sh_b1': jnp.zeros((INTER,), jnp.float32), 'sh_w2': jax.random.normal(ks[7], (INTER, D), jnp.float32) * s, 'sh_b2': jnp.zeros((D,), jnp.float32), 're_w1': jax.random.normal(ks[8], (E_R, D, INTER), jnp.float32) * s, 're_b1': jnp.zeros((E_R, INTER), jnp.float32), 're_w2': jax.random.normal(ks[9], (E_R, INTER, D), jnp.float32) * s, 're_b2': jnp.zeros((E_R, D), jnp.float32)}
        return inp
    _L0_ffn_all = _L0_ffn_setup()
    _L0_ffn_in = {k: v for k, v in _L0_ffn_all.items() if k in ('positions', 'theta', 'gamma1', 'gamma2', 'q_w', 'q_b', 'k_w', 'k_b', 'v_w', 'v_b', 'o_w', 'o_b', 'router_w', 'router_b', 'sh_w1', 'sh_b1', 'sh_w2', 'sh_b2', 're_w1', 're_b1', 're_w2', 're_b2')}
    del _L0_ffn_all

    def _L1_xattn_setup():
        import math
        import jax, jax.numpy as jnp
        import numpy as np
        B, T, DMODEL, NUM_HEADS = (2, 512, 256, 16)
        HEAD_DIM = DMODEL // NUM_HEADS
        MAX_TIMESCALE = 10000.0

        def _sinusoid_reversed(batch, length, dim):
            pos = jnp.arange(length - 1, -1, -1, dtype=jnp.float32)
            n = dim // 2
            inv = jnp.exp(jnp.arange(n, dtype=jnp.float32) * (-math.log(MAX_TIMESCALE) / (n - 1)))
            st = pos[:, None] * inv[None, :]
            emb = jnp.concatenate([jnp.sin(st), jnp.cos(st)], axis=-1)
            return jnp.broadcast_to(emb[None], (batch, length, dim))

        def _relative_shift(x):
            b, h, t, TT = x.shape
            x = jnp.pad(x, ((0, 0), (0, 0), (0, 0), (1, 0)))
            x = jnp.reshape(x, (b, h, TT + 1, t))[:, :, 1:, :]
            return jnp.reshape(x, (b, h, t, TT))
        key = jax.random.key(seed)
        ks = jax.random.split(key, 16)
        s = 1.0 / math.sqrt(DMODEL)
        d = {'x': jax.random.normal(ks[0], (B, T, DMODEL), jnp.float32), 'y': jax.random.normal(ks[1], (B, T, DMODEL), jnp.float32), 'mask': jnp.ones((B, 1, T, T), jnp.float32), 'Wq': jax.random.normal(ks[2], (DMODEL, DMODEL), jnp.float32) * s, 'bq': jnp.zeros((DMODEL,), jnp.float32), 'Wk': jax.random.normal(ks[3], (DMODEL, DMODEL), jnp.float32) * s, 'bk': jnp.zeros((DMODEL,), jnp.float32), 'Wv': jax.random.normal(ks[4], (DMODEL, DMODEL), jnp.float32) * s, 'bv': jnp.zeros((DMODEL,), jnp.float32), 'Wp': jax.random.normal(ks[5], (DMODEL, DMODEL), jnp.float32) * s, 'bp': jnp.zeros((DMODEL,), jnp.float32), 'r_w_bias': jax.random.normal(ks[6], (1, 1, NUM_HEADS, HEAD_DIM), jnp.float32) * 0.02, 'r_r_bias': jax.random.normal(ks[7], (1, 1, NUM_HEADS, HEAD_DIM), jnp.float32) * 0.02, 'Wo': jax.random.normal(ks[8], (DMODEL, DMODEL), jnp.float32) * s, 'bo': jnp.zeros((DMODEL,), jnp.float32)}
        return d
    _L1_xattn_all = _L1_xattn_setup()
    _L1_xattn_in = {k: v for k, v in _L1_xattn_all.items() if k in ('Wq', 'bq', 'Wk', 'bk', 'Wv', 'bv', 'Wp', 'bp', 'r_w_bias', 'r_r_bias', 'Wo', 'bo')}
    del _L1_xattn_all

    def _L1_attn_setup():
        import jax, jax.numpy as jnp
        import numpy as np
        import math
        EPS_LN = 1e-05
        SCALE = 16.0

        def layer_norm(x, g):
            mean = jnp.mean(x, axis=-1, keepdims=True)
            var = jnp.var(x, axis=-1, keepdims=True)
            return (x - mean) * jax.lax.rsqrt(var + EPS_LN) * g

        def l2norm(t):
            n = jnp.linalg.norm(t, axis=-1, keepdims=True)
            return t / jnp.maximum(n, 1e-12)
        key = jax.random.key(seed)
        ks = jax.random.split(key, 4)
        b, n, dim, h, dh = (4, 512, 256, 8, 64)
        inner = h * dh
        x = jax.random.normal(ks[0], (b, n, dim), dtype=jnp.float32)
        Wq = jax.random.normal(ks[1], (dim, inner), dtype=jnp.float32) * dim ** (-0.5)
        Wkv = jax.random.normal(ks[2], (dim, 2 * dh), dtype=jnp.float32) * dim ** (-0.5)
        Wout = jax.random.normal(ks[3], (inner, dim), dtype=jnp.float32) * inner ** (-0.5)
        norm_g = jnp.ones((dim,), dtype=jnp.float32)
        out_norm_g = jnp.ones((dim,), dtype=jnp.float32)
        return {'x': x, 'norm_g': norm_g, 'Wq': Wq, 'Wkv': Wkv, 'Wout': Wout, 'out_norm_g': out_norm_g}
    _L1_attn_all = _L1_attn_setup()
    _L1_attn_in = {k: v for k, v in _L1_attn_all.items() if k in ('norm_g', 'Wq', 'Wkv', 'Wout', 'out_norm_g')}
    del _L1_attn_all

    def _L1_ffn_setup():
        import jax, jax.numpy as jnp
        import numpy as np
        B, S, D = (4, 512, 256)
        E, H, TOP_K = (8, 512, 2)
        key = jax.random.key(seed)
        k_x, k_g, k_w1, k_w2, k_w3 = jax.random.split(key, 5)
        s_d = 1.0 / np.sqrt(D)
        s_h = 1.0 / np.sqrt(H)
        return {'x': jax.random.normal(k_x, (B, S, D), dtype=jnp.float32), 'w_gate': jax.random.normal(k_g, (D, E), dtype=jnp.float32) * s_d, 'w1': jax.random.normal(k_w1, (E, D, H), dtype=jnp.float32) * s_d, 'w3': jax.random.normal(k_w3, (E, D, H), dtype=jnp.float32) * s_d, 'w2': jax.random.normal(k_w2, (E, H, D), dtype=jnp.float32) * s_h}
    _L1_ffn_all = _L1_ffn_setup()
    _L1_ffn_in = {k: v for k, v in _L1_ffn_all.items() if k in ('w_gate', 'w1', 'w3', 'w2')}
    del _L1_ffn_all
    return {'x': x, 'ctx_1024': ctx_1024, 'mask_Bx1xSxS2_ff1': mask_Bx1xSxS2_ff1, 'L0_xattn_Wq': _L0_xattn_in['Wq'], 'L0_xattn_bq': _L0_xattn_in['bq'], 'L0_xattn_Wk': _L0_xattn_in['Wk'], 'L0_xattn_bk': _L0_xattn_in['bk'], 'L0_xattn_Wv': _L0_xattn_in['Wv'], 'L0_xattn_bv': _L0_xattn_in['bv'], 'L0_xattn_Wo': _L0_xattn_in['Wo'], 'L0_xattn_bo': _L0_xattn_in['bo'], 'L0_xattn_w1': _L0_xattn_in['w1'], 'L0_xattn_b1': _L0_xattn_in['b1'], 'L0_xattn_w2': _L0_xattn_in['w2'], 'L0_xattn_b2': _L0_xattn_in['b2'], 'L0_xattn_w3': _L0_xattn_in['w3'], 'L0_xattn_b3': _L0_xattn_in['b3'], 'L0_attn_Wq': _L0_attn_in['Wq'], 'L0_attn_bq': _L0_attn_in['bq'], 'L0_attn_Wk': _L0_attn_in['Wk'], 'L0_attn_bk': _L0_attn_in['bk'], 'L0_attn_Wv': _L0_attn_in['Wv'], 'L0_attn_bv': _L0_attn_in['bv'], 'L0_attn_gamma': _L0_attn_in['gamma'], 'L0_attn_beta': _L0_attn_in['beta'], 'L0_ffn_positions': _L0_ffn_in['positions'], 'L0_ffn_theta': _L0_ffn_in['theta'], 'L0_ffn_gamma1': _L0_ffn_in['gamma1'], 'L0_ffn_gamma2': _L0_ffn_in['gamma2'], 'L0_ffn_q_w': _L0_ffn_in['q_w'], 'L0_ffn_q_b': _L0_ffn_in['q_b'], 'L0_ffn_k_w': _L0_ffn_in['k_w'], 'L0_ffn_k_b': _L0_ffn_in['k_b'], 'L0_ffn_v_w': _L0_ffn_in['v_w'], 'L0_ffn_v_b': _L0_ffn_in['v_b'], 'L0_ffn_o_w': _L0_ffn_in['o_w'], 'L0_ffn_o_b': _L0_ffn_in['o_b'], 'L0_ffn_router_w': _L0_ffn_in['router_w'], 'L0_ffn_router_b': _L0_ffn_in['router_b'], 'L0_ffn_sh_w1': _L0_ffn_in['sh_w1'], 'L0_ffn_sh_b1': _L0_ffn_in['sh_b1'], 'L0_ffn_sh_w2': _L0_ffn_in['sh_w2'], 'L0_ffn_sh_b2': _L0_ffn_in['sh_b2'], 'L0_ffn_re_w1': _L0_ffn_in['re_w1'], 'L0_ffn_re_b1': _L0_ffn_in['re_b1'], 'L0_ffn_re_w2': _L0_ffn_in['re_w2'], 'L0_ffn_re_b2': _L0_ffn_in['re_b2'], 'L1_xattn_Wq': _L1_xattn_in['Wq'], 'L1_xattn_bq': _L1_xattn_in['bq'], 'L1_xattn_Wk': _L1_xattn_in['Wk'], 'L1_xattn_bk': _L1_xattn_in['bk'], 'L1_xattn_Wv': _L1_xattn_in['Wv'], 'L1_xattn_bv': _L1_xattn_in['bv'], 'L1_xattn_Wp': _L1_xattn_in['Wp'], 'L1_xattn_bp': _L1_xattn_in['bp'], 'L1_xattn_r_w_bias': _L1_xattn_in['r_w_bias'], 'L1_xattn_r_r_bias': _L1_xattn_in['r_r_bias'], 'L1_xattn_Wo': _L1_xattn_in['Wo'], 'L1_xattn_bo': _L1_xattn_in['bo'], 'L1_attn_norm_g': _L1_attn_in['norm_g'], 'L1_attn_Wq': _L1_attn_in['Wq'], 'L1_attn_Wkv': _L1_attn_in['Wkv'], 'L1_attn_Wout': _L1_attn_in['Wout'], 'L1_attn_out_norm_g': _L1_attn_in['out_norm_g'], 'L1_ffn_w_gate': _L1_ffn_in['w_gate'], 'L1_ffn_w1': _L1_ffn_in['w1'], 'L1_ffn_w3': _L1_ffn_in['w3'], 'L1_ffn_w2': _L1_ffn_in['w2']}

def reference(x, ctx_1024, mask_Bx1xSxS2_ff1, L0_xattn_Wq, L0_xattn_bq, L0_xattn_Wk, L0_xattn_bk, L0_xattn_Wv, L0_xattn_bv, L0_xattn_Wo, L0_xattn_bo, L0_xattn_w1, L0_xattn_b1, L0_xattn_w2, L0_xattn_b2, L0_xattn_w3, L0_xattn_b3, L0_attn_Wq, L0_attn_bq, L0_attn_Wk, L0_attn_bk, L0_attn_Wv, L0_attn_bv, L0_attn_gamma, L0_attn_beta, L0_ffn_positions, L0_ffn_theta, L0_ffn_gamma1, L0_ffn_gamma2, L0_ffn_q_w, L0_ffn_q_b, L0_ffn_k_w, L0_ffn_k_b, L0_ffn_v_w, L0_ffn_v_b, L0_ffn_o_w, L0_ffn_o_b, L0_ffn_router_w, L0_ffn_router_b, L0_ffn_sh_w1, L0_ffn_sh_b1, L0_ffn_sh_w2, L0_ffn_sh_b2, L0_ffn_re_w1, L0_ffn_re_b1, L0_ffn_re_w2, L0_ffn_re_b2, L1_xattn_Wq, L1_xattn_bq, L1_xattn_Wk, L1_xattn_bk, L1_xattn_Wv, L1_xattn_bv, L1_xattn_Wp, L1_xattn_bp, L1_xattn_r_w_bias, L1_xattn_r_r_bias, L1_xattn_Wo, L1_xattn_bo, L1_attn_norm_g, L1_attn_Wq, L1_attn_Wkv, L1_attn_Wout, L1_attn_out_norm_g, L1_ffn_w_gate, L1_ffn_w1, L1_ffn_w3, L1_ffn_w2):
    import jax
    import jax.numpy as jnp

    def _L0_xattn_ref(query, key, value, Wq, bq, Wk, bk, Wv, bv, Wo, bo, w1, b1, w2, b2, w3, b3):
        import jax, jax.numpy as jnp
        import numpy as np
        import math
        B, S, D, H = (1, 512, 256, 16)
        DK = D // H
        DH = 64
        LOG_T_MIN = math.log(0.1)
        LOG_T_MAX = math.log(10.0)

        def _linear(x, W, b):
            return x @ W.T + b
        b, sq, d = query.shape
        sk = key.shape[1]
        h, dk = (H, DK)
        Q = _linear(query, Wq, bq).reshape(b, sq, h, dk).transpose(0, 2, 1, 3)
        K = _linear(key, Wk, bk).reshape(b, sk, h, dk).transpose(0, 2, 1, 3)
        V = _linear(value, Wv, bv).reshape(b, sk, h, dk).transpose(0, 2, 1, 3)
        qk = jnp.einsum('bhqd,bhkd->bhqk', Q, K)
        scores = qk / math.sqrt(dk)
        mean_sim = scores.mean(axis=(-2, -1))
        max_sim = scores.max(axis=-1).mean(axis=-1)
        probs = jax.nn.softmax(scores, axis=-1)
        entropy_proxy = jnp.var(probs, axis=-1, ddof=1).mean(axis=-1)
        feats = jnp.stack([mean_sim, max_sim, entropy_proxy], axis=-1)
        hidden = jax.nn.gelu(_linear(feats, w1, b1), approximate=False)
        hidden = jax.nn.gelu(_linear(hidden, w2, b2), approximate=False)
        log_t = jnp.clip(_linear(hidden, w3, b3), LOG_T_MIN, LOG_T_MAX)
        t = jnp.exp(log_t)[..., None]
        attn_scores = qk / (2.0 * t)
        attn = jax.nn.softmax(attn_scores, axis=-1)
        attn = jnp.nan_to_num(attn, nan=0.0)
        out = jnp.einsum('bhqk,bhkd->bhqd', attn, V)
        out = out.transpose(0, 2, 1, 3).reshape(b, sq, d)
        return _linear(out, Wo, bo)

    def _L0_attn_ref(x, Wq, bq, Wk, bk, Wv, bv, gamma, beta):
        import jax, jax.numpy as jnp
        import numpy as np
        HEADS = 16
        THETA = 10000.0

        def _rope(x):
            b, n, d = x.shape
            half = d // 2
            inv_freq = 1.0 / THETA ** (jnp.arange(0, d, 2, dtype=jnp.float32) / d)
            ang = jnp.arange(n, dtype=jnp.float32)[:, None] * inv_freq
            cos, sin = (jnp.cos(ang), jnp.sin(ang))
            xp = x.reshape(b, n, half, 2)
            x1, x2 = (xp[..., 0], xp[..., 1])
            out = jnp.stack([x1 * cos - x2 * sin, x2 * cos + x1 * sin], axis=-1)
            return out.reshape(b, n, d)
        b, n, c = x.shape
        h = HEADS
        d = c // h
        gelu = lambda t: jax.nn.gelu(t, approximate=False)
        q = gelu(x @ Wq.T + bq) + 0.21
        k = gelu(x @ Wk.T + bk) + 0.21
        v = x @ Wv.T + bv
        q_r = _rope(q)
        k_r = _rope(k)
        split = lambda t: t.reshape(b, n, h, d).transpose(0, 2, 1, 3)
        qh, kh, vh, qrh, krh = (split(q), split(k), split(v), split(q_r), split(k_r))
        z = 1.0 / (jnp.einsum('bhnd,bhd->bhn', qh, kh.mean(axis=2)) + 1e-06)
        scale = n ** (-0.5)
        kv = jnp.einsum('bhnd,bhne->bhde', krh * scale, vh * scale)
        out = jnp.einsum('bhnd,bhde->bhne', qrh, kv) * z[..., None]
        out = out.transpose(0, 2, 1, 3).reshape(b, n, c)
        res = out + x
        mu = res.mean(-1, keepdims=True)
        var = res.var(-1, keepdims=True)
        return (res - mu) / jnp.sqrt(var + 1e-12) * gamma + beta

    def _L0_ffn_ref(x, positions, theta, gamma1, gamma2, q_w, q_b, k_w, k_b, v_w, v_b, o_w, o_b, router_w, router_b, sh_w1, sh_b1, sh_w2, sh_b2, re_w1, re_b1, re_w2, re_b2):
        import jax, jax.numpy as jnp
        import numpy as np
        B, S, D = (2, 256, 256)
        H, HD = (16, 64)
        E_R = 31
        K_ACT = 3
        INTER = 256
        EPS = 1e-05
        BASE = 10000.0

        def _rmsnorm(x, gamma):
            rms = jnp.sqrt(jnp.mean(x * x, axis=-1, keepdims=True) + EPS)
            return x / rms * gamma

        def _rope(x, theta):
            seq = x.shape[2]
            angles = jnp.arange(seq, dtype=theta.dtype)[:, None] * theta
            cos = jnp.cos(angles)[None, None]
            sin = jnp.sin(angles)[None, None]
            x1, x2 = (x[..., 0::2], x[..., 1::2])
            return jnp.concatenate([x1 * cos - x2 * sin, x1 * sin + x2 * cos], axis=-1)

        def _forward(x, theta, gamma1, gamma2, q_w, q_b, k_w, k_b, v_w, v_b, o_w, o_b, router_w, router_b, sh_w1, sh_b1, sh_w2, sh_b2, re_w1, re_b1, re_w2, re_b2):
            b, s, d = x.shape
            xn = _rmsnorm(x, gamma1)
            q = (xn @ q_w + q_b).reshape(b, s, H, HD).transpose(0, 2, 1, 3)
            k = (xn @ k_w + k_b).reshape(b, s, H, HD).transpose(0, 2, 1, 3)
            v = (xn @ v_w + v_b).reshape(b, s, H, HD).transpose(0, 2, 1, 3)
            q = _rope(q, theta)
            k = _rope(k, theta)
            scale = 1.0 / np.sqrt(HD)
            scores = jnp.einsum('bhqd,bhkd->bhqk', q, k) * scale
            causal = jnp.tril(jnp.ones((s, s), dtype=bool))
            scores = jnp.where(causal, scores, -jnp.inf)
            attn = jax.nn.softmax(scores, axis=-1)
            ctx = jnp.einsum('bhqk,bhkd->bhqd', attn, v)
            ctx = ctx.transpose(0, 2, 1, 3).reshape(b, s, H * HD)
            attn_out = ctx @ o_w + o_b + xn
            an = _rmsnorm(attn_out, gamma2)
            shared = jax.nn.gelu(an @ sh_w1 + sh_b1, approximate=False) @ sh_w2 + sh_b2
            logits = an @ router_w + router_b
            aff = jax.nn.softmax(logits, axis=-1)
            topv, topi = jax.lax.top_k(aff, K_ACT)
            gates = jnp.sum(jax.nn.one_hot(topi, E_R, dtype=aff.dtype) * topv[..., None], axis=-2)
            h = jax.nn.gelu(jnp.einsum('bsd,edh->besh', an, re_w1) + re_b1[None, :, None, :], approximate=False)
            routed = jnp.einsum('bse,besh,ehd->bsd', gates, h, re_w2) + jnp.einsum('bse,ed->bsd', gates, re_b2)
            return shared + routed + an + attn_out
        del positions
        return _forward(x, theta, gamma1, gamma2, q_w, q_b, k_w, k_b, v_w, v_b, o_w, o_b, router_w, router_b, sh_w1, sh_b1, sh_w2, sh_b2, re_w1, re_b1, re_w2, re_b2)

    def _L1_xattn_ref(x, y, mask, Wq, bq, Wk, bk, Wv, bv, Wp, bp, r_w_bias, r_r_bias, Wo, bo):
        import math
        import jax, jax.numpy as jnp
        import numpy as np
        B, T, DMODEL, NUM_HEADS = (2, 512, 256, 16)
        HEAD_DIM = DMODEL // NUM_HEADS
        MAX_TIMESCALE = 10000.0

        def _sinusoid_reversed(batch, length, dim):
            pos = jnp.arange(length - 1, -1, -1, dtype=jnp.float32)
            n = dim // 2
            inv = jnp.exp(jnp.arange(n, dtype=jnp.float32) * (-math.log(MAX_TIMESCALE) / (n - 1)))
            st = pos[:, None] * inv[None, :]
            emb = jnp.concatenate([jnp.sin(st), jnp.cos(st)], axis=-1)
            return jnp.broadcast_to(emb[None], (batch, length, dim))

        def _relative_shift(x):
            b, h, t, TT = x.shape
            x = jnp.pad(x, ((0, 0), (0, 0), (0, 0), (1, 0)))
            x = jnp.reshape(x, (b, h, TT + 1, t))[:, :, 1:, :]
            return jnp.reshape(x, (b, h, t, TT))
        b, t, _ = x.shape
        kv_t = y.shape[1]
        q = (x @ Wq + bq).reshape(b, t, NUM_HEADS, HEAD_DIM)
        k = (y @ Wk + bk).reshape(b, kv_t, NUM_HEADS, HEAD_DIM)
        v = (y @ Wv + bv).reshape(b, kv_t, NUM_HEADS, HEAD_DIM)
        content = jnp.einsum('bthd,bThd->bhtT', q + r_w_bias, k)
        pe = _sinusoid_reversed(b, kv_t, DMODEL) @ Wp + bp
        pe = pe.reshape(b, kv_t, NUM_HEADS, HEAD_DIM)
        rel = jnp.einsum('bthd,bThd->bhtT', q + r_r_bias, pe)
        rel = _relative_shift(rel)
        attn = (content + rel) * (1.0 / math.sqrt(HEAD_DIM))
        attn = attn * mask - 10000000000.0 * (1.0 - mask)
        p = jax.nn.softmax(attn, axis=-1)
        out = jnp.einsum('bhtT,bThd->bthd', p, v).reshape(b, t, DMODEL)
        return out @ Wo + bo

    def _L1_attn_ref(x, norm_g, Wq, Wkv, Wout, out_norm_g):
        import jax, jax.numpy as jnp
        import numpy as np
        import math
        EPS_LN = 1e-05
        SCALE = 16.0

        def layer_norm(x, g):
            mean = jnp.mean(x, axis=-1, keepdims=True)
            var = jnp.var(x, axis=-1, keepdims=True)
            return (x - mean) * jax.lax.rsqrt(var + EPS_LN) * g

        def l2norm(t):
            n = jnp.linalg.norm(t, axis=-1, keepdims=True)
            return t / jnp.maximum(n, 1e-12)
        b, n, dim = x.shape
        h = 8
        dh = Wkv.shape[-1] // 2
        xn = layer_norm(x, norm_g)
        q = xn @ Wq
        kv = xn @ Wkv
        k, v = (kv[..., :dh], kv[..., dh:])
        q = q.reshape(b, n, h, dh).transpose(0, 2, 1, 3)
        q = q * SCALE
        q = l2norm(q)
        k = l2norm(k)
        rs = math.sqrt(SCALE)
        q = q * rs
        k = k * rs
        sim = jnp.einsum('bhid,bjd->bhij', q, k)
        attn = jax.nn.softmax(sim.astype(jnp.float32), axis=-1).astype(sim.dtype)
        out = jnp.einsum('bhij,bjd->bhid', attn, v)
        out = out.transpose(0, 2, 1, 3).reshape(b, n, h * dh)
        out = out @ Wout
        return layer_norm(out, out_norm_g)

    def _L1_ffn_ref(x, w_gate, w1, w3, w2):
        import jax, jax.numpy as jnp
        import numpy as np
        B, S, D = (4, 512, 256)
        E, H, TOP_K = (8, 512, 2)
        bsz, seq_len, embed_dim = x.shape
        xt = x.reshape(-1, embed_dim)
        T = xt.shape[0]
        logits = xt @ w_gate
        top_logits, sel = jax.lax.top_k(logits, TOP_K)
        probs = jax.nn.softmax(top_logits, axis=-1).astype(x.dtype)
        h = jax.nn.silu(jnp.einsum('td,edh->eth', xt, w1)) * jnp.einsum('td,edh->eth', xt, w3)
        y = jnp.einsum('eth,ehd->etd', h, w2)
        t_idx = jnp.arange(T)
        yk = y[sel.T, t_idx[None, :], :]
        out = jnp.einsum('ktd,tk->td', yk, probs)
        return out.reshape(bsz, seq_len, embed_dim)
    x = x + _L0_xattn_ref(_layernorm(x, axis=-1), ctx_1024, ctx_1024, L0_xattn_Wq, L0_xattn_bq, L0_xattn_Wk, L0_xattn_bk, L0_xattn_Wv, L0_xattn_bv, L0_xattn_Wo, L0_xattn_bo, L0_xattn_w1, L0_xattn_b1, L0_xattn_w2, L0_xattn_b2, L0_xattn_w3, L0_xattn_b3)
    x = x + _L0_attn_ref(_layernorm(x, axis=-1), L0_attn_Wq, L0_attn_bq, L0_attn_Wk, L0_attn_bk, L0_attn_Wv, L0_attn_bv, L0_attn_gamma, L0_attn_beta)
    x = x + _L0_ffn_ref(_layernorm(x, axis=-1), L0_ffn_positions, L0_ffn_theta, L0_ffn_gamma1, L0_ffn_gamma2, L0_ffn_q_w, L0_ffn_q_b, L0_ffn_k_w, L0_ffn_k_b, L0_ffn_v_w, L0_ffn_v_b, L0_ffn_o_w, L0_ffn_o_b, L0_ffn_router_w, L0_ffn_router_b, L0_ffn_sh_w1, L0_ffn_sh_b1, L0_ffn_sh_w2, L0_ffn_sh_b2, L0_ffn_re_w1, L0_ffn_re_b1, L0_ffn_re_w2, L0_ffn_re_b2)
    x = x + _L1_xattn_ref(_layernorm(x, axis=-1), ctx_1024, mask_Bx1xSxS2_ff1, L1_xattn_Wq, L1_xattn_bq, L1_xattn_Wk, L1_xattn_bk, L1_xattn_Wv, L1_xattn_bv, L1_xattn_Wp, L1_xattn_bp, L1_xattn_r_w_bias, L1_xattn_r_r_bias, L1_xattn_Wo, L1_xattn_bo)
    x = x + _L1_attn_ref(_layernorm(x, axis=-1), L1_attn_norm_g, L1_attn_Wq, L1_attn_Wkv, L1_attn_Wout, L1_attn_out_norm_g)
    x = x + _L1_ffn_ref(_layernorm(x, axis=-1), L1_ffn_w_gate, L1_ffn_w1, L1_ffn_w3, L1_ffn_w2)
    return x

_drawn_inputs = setup_inputs


def setup_inputs(seed=0):
    import zlib

    import numpy as np

    out = dict(_drawn_inputs(seed))
    spreads = {'L0_attn_gamma': (1.0, 0.2),
     'L0_attn_beta': (0.0, 0.1),
     'L0_ffn_gamma1': (1.0, 0.2),
     'L0_ffn_gamma2': (1.0, 0.2),
     'L0_ffn_q_b': (0.0, 0.8),
     'L0_ffn_k_b': (0.0, 0.8),
     'L0_ffn_v_b': (0.0, 0.1),
     'L0_ffn_o_b': (0.0, 0.1),
     'L0_ffn_router_b': (0.0, 0.8),
     'L0_ffn_sh_b1': (0.0, 0.8),
     'L0_ffn_sh_b2': (0.0, 0.302),
     'L0_ffn_re_b1': (0.0, 0.8),
     'L0_ffn_re_b2': (0.0, 0.8),
     'L1_xattn_bq': (0.0, 0.1),
     'L1_xattn_bk': (0.0, 0.1),
     'L1_xattn_bv': (0.0, 0.307),
     'L1_xattn_bp': (0.0, 0.1),
     'L1_xattn_bo': (0.0, 0.335),
     'L1_attn_norm_g': (1.0, 0.2),
     'L1_attn_out_norm_g': (1.0, 0.2)}
    factors = {'L0_xattn_Wq': 8.0,
     'L0_xattn_bq': 8.0,
     'L0_xattn_Wk': 8.0,
     'L0_xattn_bk': 200.0,
     'L0_xattn_bv': 5.936,
     'L0_xattn_w1': 8.0,
     'L0_xattn_b1': 8.0,
     'L0_xattn_w2': 8.0,
     'L0_xattn_b2': 8.0,
     'L0_xattn_w3': 8.0,
     'L0_attn_Wq': 3.072,
     'L0_attn_bq': 200.0,
     'L0_attn_bk': 149.12,
     'L0_attn_bv': 7.487,
     'L0_ffn_theta': 8.0,
     'L0_ffn_q_w': 8.0,
     'L0_ffn_k_w': 8.0,
     'L0_ffn_router_w': 8.0,
     'L0_ffn_sh_w1': 3.545,
     'L0_ffn_sh_w2': 3.121,
     'L0_ffn_re_w1': 8.0,
     'L0_ffn_re_w2': 8.0}
    for name, (base, spread) in spreads.items():
        noise = np.random.default_rng([zlib.crc32(name.encode()), seed]).standard_normal(out[name].shape)
        drawn = base * np.exp(spread * noise) if base else spread * noise
        out[name] = jnp.asarray(drawn.astype(out[name].dtype))
    for name, factor in factors.items():
        out[name] = (out[name] * factor).astype(out[name].dtype)
    return out
```

```python
from contextlib import ExitStack

import numpy as np

import concourse.bass as bass
from concourse import mybir

F32 = mybir.dt.float32
BF16 = mybir.dt.bfloat16
ALU = mybir.AluOpType
ACT = mybir.ActivationFunctionType
AX = mybir.AxisListType.X

P = 128
S = 256
D = 256
NT = S // P
KC = D // P
S2 = 4096
NCH = S2 // P
NHALF = 2
HALF = S2 // NHALF
H = 16
DK = D // H
DV = DK + 1
QUAD = 32
NQ4 = P // QUAD
ROWS = 6 * DK
MAXROWS = ROWS + 3
BANK = 512
LOG_T_MIN, LOG_T_MAX = float(np.log(0.1)), float(np.log(10.0))
Q_PARTS = (0, 1, 2, 0, 1, 0)
K_PARTS = (0, 0, 0, 1, 1, 2)


class Chain:

    def __init__(self, eng, sem, base=0):
        self.eng, self.sem, self.n, self.base = eng, sem, 0, base

    def __call__(self, ins):
        self.n += 1
        ins.then_inc(self.sem, 1)
        self.eng.wait_ge(self.sem, self.base + self.n)


class Frame:

    def __init__(self, nc, ctx, ins, out):
        self.nc, self.ctx, self.ins, self.out = nc, ctx, ins, out
        self.layer, self.sems = "", []

    def sb(self, ctx, name, shape, dt=F32):
        return ctx.enter_context(self.nc.sbuf_tensor(f"{self.layer}_{name}", shape, dt))

    def ps(self, ctx, name, shape, dt=F32):
        return ctx.enter_context(self.nc.psum_tensor(f"{self.layer}_{name}", shape, dt))

    def sem(self, name):
        self.sems.append(self.nc.alloc_semaphore(name=f"{self.layer}_{name}"))
        return self.sems[-1]


def rows_of(dram):
    return dram.rearrange("(c p) n -> p c n", p=P)


def layer_norm(f, dve, step, y, x, eps, var_ready, root_ready, n=0):
    nc = f.nc
    for t in range(NT):
        step(nc.vector.bn_stats(f.stats[:, t, :], x[:, t, :]))
        step(nc.vector.bn_aggr(f.mv[:, t, :], f.stats[:, t, :]))
    nc.vector.tensor_scalar(f.rstd[:], f.mv[:, :, 1], eps, None, ALU.add).then_inc(var_ready, 1)
    dve.wait_ge(root_ready, n + 1)
    step(nc.vector.reciprocal(f.rstd[:], f.rstd[:]))
    for t in range(NT):
        step(nc.vector.tensor_scalar(y[:, t, :], x[:, t, :], f.mv[:, t, 0:1], f.rstd[:, t:t + 1],
                                     ALU.subtract, ALU.mult))


def take_root(f, act, var_ready, root_ready, n=0):
    act.wait_ge(var_ready, n + 1)
    f.nc.scalar.sqrt(f.rstd[:], f.rstd[:]).then_inc(root_ready, 1)


def transpose_tokens(nc, out_ps, y, ident):
    for c in range(y.shape[2] // P):
        for t in range(NT):
            last = nc.tensor.transpose(out_ps[:, c, t * P:(t + 1) * P], y[:, t, c * P:(c + 1) * P], ident)
    return last


def prologue(f):
    nc, i = f.nc, f.ins
    f.layer = "pro"
    loaded_x, loaded_ctx, loaded_sin, loaded_w = (f.sem(n) for n in ("loaded_x", "loaded_ctx", "loaded_sin", "loaded_w"))
    ones_set, proj_done, evacuated = f.sem("ones_set"), f.sem("proj_done"), f.sem("evacuated")
    rest_done, split_done = f.sem("rest_done"), f.sem("split_done")
    stored = [f.sem(f"stored{b}") for b in range(2)]
    v_stored = [f.sem(f"v_stored{b}") for b in range(2)]
    second_done = f.sem("second_done")
    with ExitStack() as ctx:
        ctxT = f.sb(ctx, "ctxT", [P, KC, S2])
        sinT = f.sb(ctx, "sinT", [P, KC, S2])
        w = f.sb(ctx, "w", [P, 5, KC, D])
        bcol = f.sb(ctx, "bcol", [P, 3, KC])
        brow = f.sb(ctx, "brow", [1, 2, D])
        whole = f.sb(ctx, "whole", [P, 2, HALF])
        rest = f.sb(ctx, "rest", [P, HALF])
        parts = f.sb(ctx, "parts", [P, 2, 3, HALF], BF16)
        values = f.sb(ctx, "values", [P, 2, H, HALF // D, DV])
        ps = f.ps(ctx, "ps", [P, 2, HALF])
        key_groups = [(m, t, h) for m in range(3) for t in range(KC) for h in range(NHALF)]
        CPG = HALF // D
        value_groups = [(m, g) for m in range(2) for g in range(NCH // CPG)]
        NK = len(key_groups)
        block = ctx.enter_context(nc.Block())

        @block.sync
        def _(sp):
            sp.dma_start(f.x[:], i["x"].rearrange("b (t p) d -> p (b t) d", p=P)).then_inc(loaded_x, 16)
            sp.dma_start(f.ident[:], i["c_ident"]).then_inc(loaded_x, 16)
            for n, name in enumerate(("L0_xattn_Wk", "L1_xattn_Wk", "L1_xattn_Wp", "L0_xattn_Wv", "L1_xattn_Wv")):
                sp.dma_start(w[:, n], rows_of(i[name])).then_inc(loaded_w, 16)
            for n, name in enumerate(("L0_xattn_bk", "L1_xattn_bk", "L1_xattn_bp")):
                sp.dma_start(bcol[:, n], i[name]).then_inc(loaded_w, 16)
            for n, name in enumerate(("L0_xattn_bv", "L1_xattn_bv")):
                sp.dma_start(brow[:, n], i[name]).then_inc(loaded_w, 16)
            for h in range(NHALF):
                sp.dma_start(ctxT[:, :, h * HALF:(h + 1) * HALF],
                             rows_of(i["ctx_1024"])[:, :, h * HALF:(h + 1) * HALF]).then_inc(loaded_ctx, 16)
            sp.dma_start(sinT[:], rows_of(i["c_sinusoids"])).then_inc(loaded_sin, 16)
            for g, (m, t, h) in enumerate(key_groups):
                sp.wait_ge(split_done, 2 * (g + 1))
                dst = f.key_parts[m, :, t * P:(t + 1) * P, h * HALF:(h + 1) * HALF]
                sp.dma_start(dst.rearrange("s p n -> p s n"), parts[:, g % 2]).then_inc(stored[g % 2], 16)
            for g, (m, q) in enumerate(value_groups):
                sp.wait_ge(evacuated, NK + g + 1)
                sp.dma_start(f.value_rows[m, :, :, q * CPG:(q + 1) * CPG].rearrange("h p k d -> p h (k d)"),
                             values[:, g % 2].rearrange("p h k d -> p h (k d)")).then_inc(v_stored[g % 2], 16)
            for b in range(2):
                sp.wait_ge(stored[b], 16 * NK // 2)
                sp.wait_ge(v_stored[b], 16 * len(value_groups) // 2)

        @block.tensor
        def _(pe):
            pe.wait_ge(loaded_w, 160)
            pe.wait_ge(loaded_ctx, 32)
            for g, (m, t, h) in enumerate(key_groups):
                if g >= 2:
                    pe.wait_ge(evacuated, g - 1)
                if m == 2:
                    pe.wait_ge(loaded_sin, 16)
                src = sinT if m == 2 else ctxT
                for n in range(HALF // BANK):
                    for c in range(KC):
                        at = h * HALF + n * BANK
                        mm = nc.tensor.matmul(ps[:, g % 2, n * BANK:(n + 1) * BANK], w[:, m, c, t * P:(t + 1) * P],
                                              src[:, c, at:at + BANK], start=(c == 0), stop=(c == KC - 1))
                mm.then_inc(proj_done, 1)
            pe.wait_ge(ones_set, 1)
            for g, (m, q) in enumerate(value_groups):
                pe.wait_ge(evacuated, NK + g - 1)
                for k in range(CPG):
                    at = (q * CPG + k) * P
                    out = ps[:, g % 2, k * D:(k + 1) * D]
                    for c in range(KC):
                        nc.tensor.matmul(out, ctxT[:, c, at:at + P], w[:, 3 + m, c, :], start=(c == 0), stop=False)
                    mm = nc.tensor.matmul(out, f.ones[0:1, :], brow[:, m, :], start=False, stop=True)
                mm.then_inc(proj_done, 1)

        @block.scalar
        def _(act):
            act.wait_ge(loaded_w, 160)
            for g, (m, t, h) in enumerate(key_groups):
                act.wait_ge(proj_done, g + 1)
                if g >= 2:
                    act.wait_ge(split_done, 2 * (g - 1))
                    act.wait_ge(stored[g % 2], 16 * (g // 2))
                if m == 0:
                    acc = dict(accum_out=f.key_sums[:, t, h:h + 1])
                else:
                    acc = {}
                nc.scalar.activation(whole[:, g % 2], ps[:, g % 2], ACT.Identity, bias=bcol[:, m, t:t + 1], **acc)
                nc.scalar.activation(parts[:, g % 2, 0], ps[:, g % 2], ACT.Identity,
                                     bias=bcol[:, m, t:t + 1]).then_inc(evacuated, 1)
            for g, (m, q) in enumerate(value_groups):
                act.wait_ge(proj_done, NK + g + 1)
                if g == 0:
                    act.wait_ge(ones_set, 2)
                if g >= 2:
                    act.wait_ge(v_stored[g % 2], 16 * (g // 2))
                src = ps[:, g % 2].rearrange("p (k h d) -> p h k d", k=CPG, h=H)
                nc.scalar.copy(values[:, g % 2, :, :, 0:DK], src).then_inc(evacuated, 1)

        @block.vector
        def _(dve):
            nc.vector.memset(f.ones[:], 1.0).then_inc(ones_set, 1)
            nc.vector.memset(values[:, :, :, :, DK:DV], 1.0).then_inc(ones_set, 1)
            for g in range(NK):
                dve.wait_ge(evacuated, g + 1)
                if g >= 1:
                    dve.wait_ge(split_done, 2 * g)
                nc.vector.tensor_tensor(rest[:], whole[:, g % 2], parts[:, g % 2, 0], ALU.subtract).then_inc(rest_done, 1)
                dve.wait_ge(rest_done, g + 1)
                nc.vector.tensor_copy(parts[:, g % 2, 1], rest[:]).then_inc(second_done, 1)
                dve.wait_ge(second_done, g + 1)
                nc.vector.tensor_tensor(parts[:, g % 2, 2], rest[:], parts[:, g % 2, 1], ALU.subtract).then_inc(split_done, 2)


def cross0(f):
    nc, i = f.nc, f.ins
    f.layer = "xa"
    loaded = f.sem("loaded")
    pe_small, act_small, dve_small = f.sem("pe_small"), f.sem("act_small"), f.sem("dve_small")
    dve_steps, act_steps = f.sem("dve_steps"), f.sem("act_steps")
    parts_stored, q_loaded, k_free, kb_free = (f.sem(n) for n in ("parts_stored", "q_loaded", "k_free", "kb_free"))
    k_loaded = [f.sem(f"k_loaded{b}") for b in range(2)]
    kb_loaded = [f.sem(f"kb_loaded{b}") for b in range(2)]
    scored, max_ready, stats_done = f.sem("scored"), f.sem("max_ready"), f.sem("stats_done")
    max_raw, max_kept, raw_free = f.sem("max_raw"), f.sem("max_kept"), f.sem("raw_free")
    scoredT, probs_ready, probs_used, pv_done, pv_read = (
        f.sem(n) for n in ("scoredT", "probs_ready", "probs_used", "pv_done", "pv_read"))
    recip_done, sums_free = f.sem("recip_done"), f.sem("sums_free")
    with ExitStack() as ctx:
        wq = f.sb(ctx, "wq", [P, KC, D])
        wo = f.sb(ctx, "wo", [P, KC, D])
        bq = f.sb(ctx, "bq", [P, KC])
        bo = f.sb(ctx, "bo", [1, D])
        w1b = f.sb(ctx, "w1b", [P, 3, 64])
        w2 = f.sb(ctx, "w2", [64, 64])
        w3 = f.sb(ctx, "w3", [64, 1])
        w3b = f.sb(ctx, "w3b", [64, P])
        b1 = f.sb(ctx, "b1", [64, 1])
        b2 = f.sb(ctx, "b2", [64, 1])
        b3 = f.sb(ctx, "b3", [P, 1])
        head_of = f.sb(ctx, "head_of", [P, KC, H])
        xn = f.sb(ctx, "xn", [P, NT, D])
        xnT = f.sb(ctx, "xnT", [P, KC, S])
        q = f.sb(ctx, "q", [P, KC, S])
        qrest = f.sb(ctx, "qrest", [P, KC, S])
        qparts = f.sb(ctx, "qparts", [P, 3, KC, S], BF16)
        q_sums = f.sb(ctx, "q_sums", [P, KC])
        k_sums = f.sb(ctx, "k_sums", [P, KC])
        qk_sum = f.sb(ctx, "qk_sum", [P, KC, H])
        q96 = f.sb(ctx, "q96", [P, H, S], BF16)
        k96 = f.sb(ctx, "k96", [P, 2, S2], BF16)
        NU = NT * NHALF
        maxima = f.sb(ctx, "maxima", [P, H, NU])
        nbias = f.sb(ctx, "nbias", [P, 2])
        nbias2 = f.sb(ctx, "nbias2", [P, 2])
        zs = f.sb(ctx, "zs", [P, H, NU])
        es = f.sb(ctx, "es", [P, H, NU])
        exps = f.sb(ctx, "exps", [P, 2, HALF])
        m_all = f.sb(ctx, "m_all", [P, H, NT])
        wgt = f.sb(ctx, "wgt", [P, H, NU])
        z_all = f.sb(ctx, "z_all", [P, H, NT])
        e_all = f.sb(ctx, "e_all", [P, H, NT])
        max_now = f.sb(ctx, "max_now", [P, 2])
        mneg = f.sb(ctx, "mneg", [P, H * NT])
        mrow = f.sb(ctx, "mrow", [H * NT, P])
        mrest = f.sb(ctx, "mrest", [H * NT, P])
        mparts = f.sb(ctx, "mparts", [H * NT, 3, P], BF16)
        hid1 = f.sb(ctx, "hid1", [64, H])
        hid2 = f.sb(ctx, "hid2", [64, H])
        logt = f.sb(ctx, "logt", [P, H])
        tscale = f.sb(ctx, "tscale", [P, H + 2])
        t_now = f.sb(ctx, "t_now", [P, 2])
        GC = 4
        NG = NCH // GC
        UNITS = H * NG
        probs = f.sb(ctx, "probs", [P, 2, GC, S])
        rz = f.sb(ctx, "rz", [P, 2, NT])
        vhead = f.sb(ctx, "vhead", [P, 2, NCH, DV])
        gather = f.sb(ctx, "gather", [P, DV])
        sumsT = f.sb(ctx, "sumsT", [P, 2, S])
        attn = f.sb(ctx, "attn", [P, NT, H, DK])
        attnT = f.sb(ctx, "attnT", [P, KC, S])

        with ExitStack() as inner:
            block = inner.enter_context(nc.Block())
            ps = f.ps(inner, "ps", [P, 2, HALF])
            var_ready, root_ready = f.sem("var_ready"), f.sem("root_ready")

            @block.sync
            def _(sp):
                loads = [(wq[:], rows_of(i["L0_xattn_Wq"])), (wo[:], rows_of(i["L0_xattn_Wo"])),
                         (bq[:], i["L0_xattn_bq"]), (bo[:], i["L0_xattn_bo"]),
                         (w2[:], i["L0_xattn_w2"]), (w3[:], i["L0_xattn_w3"]),
                         (b1[:], i["L0_xattn_b1"]), (b2[:], i["L0_xattn_b2"]),
                         (b3[:], i["L0_xattn_b3"].partition_broadcast(P)), (head_of[:], i["c_head_of"]),
                         (w1b[:], i["L0_xattn_w1"].partition_broadcast(P))]
                for dst, src in loads:
                    sp.dma_start(dst, src).then_inc(loaded, 16)
                sp.wait_ge(dve_small, 4)
                for s in range(3):
                    sp.dma_start(f.query_parts[0, s].rearrange("(c p) n -> p c n", p=P),
                                 qparts[:, s]).then_inc(parts_stored, 16)
                sp.wait_ge(parts_stored, 48)
                for r, s in enumerate(Q_PARTS):
                    sp.dma_start(q96[r * DK:(r + 1) * DK], f.query_parts[0, s].rearrange("(h d) n -> d h n", d=DK)
                                 ).then_inc(q_loaded, 16)
                with sp.Fori(0, H // 2) as pair:
                    for b in range(2):
                        sp.wait_ge(k_free, 2 * pair + b + 1)
                        for r, s in enumerate(K_PARTS):
                            src = f.key_heads[0, s, bass.ds(2 * pair + b, 1)]
                            sp.dma_start(k96[r * DK:(r + 1) * DK, b:b + 1, :], src.rearrange("h d n -> d h n")
                                         ).then_inc(k_loaded[b], 16)

            @block.tensor
            def _(pe):
                pe.sem_inc(k_free, 2)
                pe.wait_ge(loaded, 16 * 11)
                pe.wait_ge(dve_small, 1)
                flat = ps[:, 0, 0:KC * S].rearrange("p (c n) -> p c n", c=KC)
                transpose_tokens(nc, flat, xn, f.ident[:]).then_inc(pe_small, 1)
                pe.wait_ge(act_small, 1)
                for m in range(KC):
                    for c in range(KC):
                        mm = nc.tensor.matmul(ps[:, 1, m * S:(m + 1) * S], wq[:, c, m * P:(m + 1) * P], xnT[:, c, :],
                                              start=(c == 0), stop=(c == KC - 1))
                mm.then_inc(pe_small, 1)
                pe.wait_ge(q_loaded, 96)
                pe.wait_ge(act_small, 2)
                with pe.Fori(0, H // 2) as pair:
                    for b in range(2):
                        pe.wait_ge(k_loaded[b], 96 * (pair + 1))
                        for u in range(NU):
                            t, h = u // NHALF, u % NHALF
                            pe.wait_ge(stats_done, (2 * pair + b) * NU + u + 1)
                            for n in range(HALF // BANK):
                                at = h * HALF + n * BANK
                                mm = nc.tensor.matmul(ps[:, u % 2, n * BANK:(n + 1) * BANK],
                                                      q96[0:ROWS, bass.ds(2 * pair + b, 1), t * P:(t + 1) * P],
                                                      k96[0:ROWS, b, at:at + BANK], start=True, stop=True)
                            mm.then_inc(scored, 1)
                        pe.wait_ge(scored, (2 * pair + b + 1) * NU)
                        pe.sem_inc(k_free, 1)

            @block.scalar
            def _(act):
                act.sem_inc(stats_done, 2)
                act.sem_inc(act_steps, 1)
                take_root(f, act, var_ready, root_ready)
                act.wait_ge(pe_small, 1)
                nc.scalar.copy(xnT[:], ps[:, 0, 0:KC * S].rearrange("p (c n) -> p c n", c=KC)).then_inc(act_small, 1)
                act.wait_ge(loaded, 16 * 11)
                act.wait_ge(pe_small, 2)
                for m in range(KC):
                    ins = nc.scalar.activation(q[:, m], ps[:, 1, m * S:(m + 1) * S], ACT.Identity,
                                               bias=bq[:, m:m + 1], accum_out=q_sums[:, m:m + 1])
                ins.then_inc(act_small, 1)
                with act.Fori(0, H // 2) as pair:
                    for b in range(2):
                        for u in range(NU):
                            n = (2 * pair + b) * NU + u
                            at = u % 2
                            act.wait_ge(max_ready, n + 1)
                            act.wait_ge(act_steps, n + 1)
                            act.nop()
                            nc.scalar.activation(exps[:, 0], ps[:, at], ACT.Exp, scale=DK ** -0.5,
                                                 bias=nbias[:, at:at + 1],
                                                 accum_out=zs[:, bass.ds(2 * pair + b, 1), u:u + 1]).then_inc(act_steps, 1)
                            act.wait_ge(stats_done, n + 2)
                            act.nop()
                            nc.scalar.activation(exps[:, 1], ps[:, at], ACT.Exp, scale=2 * DK ** -0.5,
                                                 bias=nbias2[:, at:at + 1],
                                                 accum_out=es[:, bass.ds(2 * pair + b, 1), u:u + 1]).then_inc(stats_done, 1)
                act.wait_ge(act_steps, H * NU + 1)

            @block.vector
            def _(dve):
                step = Chain(dve, dve_steps)
                layer_norm(f, dve, step, xn, f.x, 1e-5, var_ready, root_ready)
                dve.sem_inc(dve_small, 1)
                dve.wait_ge(act_small, 2)
                step(nc.vector.tensor_copy(qparts[:, 0], q[:]))
                step(nc.vector.tensor_tensor(qrest[:], q[:], qparts[:, 0], ALU.subtract))
                dve.sem_inc(dve_small, 1)
                step(nc.vector.tensor_copy(qparts[:, 1], qrest[:]))
                dve.sem_inc(dve_small, 1)
                step(nc.vector.tensor_tensor(qparts[:, 2], qrest[:], qparts[:, 1], ALU.subtract))
                dve.sem_inc(dve_small, 1)
                with dve.Fori(0, H // 2) as pair:
                    for b in range(2):
                        for u in range(NU):
                            n = (2 * pair + b) * NU + u
                            at = u % 2
                            dve.wait_ge(scored, n + 1)
                            dve.wait_ge(stats_done, n + 1)
                            nc.vector.tensor_reduce(max_now[:, at:at + 1], ps[:, at], AX, ALU.max).then_inc(max_raw, 1)
                            dve.wait_ge(max_raw, n + 1)
                            nc.vector.tensor_scalar(nbias[:, at:at + 1], max_now[:, at:at + 1], -DK ** -0.5, None, ALU.mult)
                            nc.vector.tensor_scalar(nbias2[:, at:at + 1], max_now[:, at:at + 1], -2 * DK ** -0.5, None,
                                                    ALU.mult).then_inc(max_ready, 1)
                            nc.vector.tensor_copy(maxima[:, bass.ds(2 * pair + b, 1), u:u + 1],
                                                  max_now[:, at:at + 1]).then_inc(max_kept, 1)
                            dve.wait_ge(max_kept, n + 1)

        with ExitStack() as inner:
            block = inner.enter_context(nc.Block())
            small = f.ps(inner, "small", [P, 4, BANK])
            featured, hid_mm, hid_act, t_mm, t_ready = (f.sem(n) for n in ("featured", "hid_mm", "hid_act", "t_mm", "t_ready"))
            m_T, m_split, m_stored, m_loaded, w_in, w_out, w3_set = (
                f.sem(n) for n in ("m_T", "m_split", "m_stored", "m_loaded", "w_in", "w_out", "w3_set"))
            dve_steps2 = f.sem("dve_steps2")

            @block.sync
            def _(sp):
                sp.wait_ge(m_split, 1)
                sp.dma_start(f.max_parts.rearrange("s (r p) -> r s p", p=P), mparts[:]).then_inc(m_stored, 16)
                sp.wait_ge(m_stored, 16)
                sp.dma_start(q96[ROWS:MAXROWS], f.max_parts.rearrange("s (h n) -> s h n", h=H)).then_inc(m_loaded, 16)
                sp.wait_ge(m_loaded, 16)

            @block.vector
            def _(dve):
                step = Chain(dve, dve_steps2)
                nc.vector.memset(k96[ROWS:MAXROWS], 1.0)
                step(nc.vector.tensor_scalar(w3b[:], f.ident[0:64, :], 0.0, w3[:, 0:1], ALU.mult, ALU.add))
                dve.sem_inc(w3_set, 1)
                mx = maxima[:].rearrange("p h (t a) -> p h t a", a=NHALF)
                wv = wgt[:].rearrange("p h (t a) -> p h t a", a=NHALF)
                step(nc.vector.tensor_reduce(m_all[:], mx, AX, ALU.max))
                step(nc.vector.tensor_scalar(mneg[:], m_all[:].rearrange("p h t -> p (h t)"), -1.0, None, ALU.mult))
                dve.sem_inc(m_T, 1)
                for a in range(NHALF):
                    step(nc.vector.tensor_tensor(wv[:, :, :, a], mx[:, :, :, a], m_all[:], ALU.subtract))
                dve.sem_inc(w_in, 1)
                dve.wait_ge(w_out, 1)
                step(nc.vector.tensor_tensor(zs[:], zs[:], wgt[:], ALU.mult))
                step(nc.vector.tensor_tensor(es[:], es[:], wgt[:], ALU.mult))
                step(nc.vector.tensor_tensor(es[:], es[:], wgt[:], ALU.mult))
                zv = zs[:].rearrange("p h (t a) -> p h t a", a=NHALF)
                ev = es[:].rearrange("p h (t a) -> p h t a", a=NHALF)
                step(nc.vector.tensor_tensor(z_all[:], zv[:, :, :, 0], zv[:, :, :, 1], ALU.add))
                step(nc.vector.tensor_tensor(e_all[:], ev[:, :, :, 0], ev[:, :, :, 1], ALU.add))
                step(nc.vector.reciprocal(z_all[:], z_all[:]))
                step(nc.vector.tensor_tensor(e_all[:], e_all[:], z_all[:], ALU.mult))
                step(nc.vector.tensor_tensor(e_all[:], e_all[:], z_all[:], ALU.mult))
                step(nc.vector.tensor_scalar(e_all[:], e_all[:], 1.0 / S2, 1.0 / ((S2 - 1) * S), ALU.subtract, ALU.mult))
                step(nc.vector.tensor_scalar(m_all[:], m_all[:], DK ** -0.5 / S, None, ALU.mult))
                step(nc.vector.tensor_tensor(k_sums[:], f.key_sums[:, :, 0], f.key_sums[:, :, 1], ALU.add))
                step(nc.vector.tensor_tensor(k_sums[:], k_sums[:], q_sums[:], ALU.mult))
                step(nc.vector.tensor_scalar(k_sums[:], k_sums[:], DK ** -0.5 / S / S2, None, ALU.mult))
                for c in range(KC):
                    step(nc.vector.tensor_scalar(qk_sum[:, c], head_of[:, c], k_sums[:, c:c + 1], None, ALU.mult))
                dve.sem_inc(featured, 1)
                dve.wait_ge(m_T, 2)
                step(nc.vector.tensor_copy(mrow[:], small[0:H * NT, 3, 0:P]))
                step(nc.vector.tensor_copy(mparts[:, 0], mrow[:]))
                step(nc.vector.tensor_tensor(mrest[:], mrow[:], mparts[:, 0], ALU.subtract))
                step(nc.vector.tensor_copy(mparts[:, 1], mrest[:]))
                step(nc.vector.tensor_tensor(mparts[:, 2], mrest[:], mparts[:, 1], ALU.subtract))
                dve.sem_inc(m_split, 1)
                dve.wait_ge(t_mm, 1)
                step(nc.vector.tensor_scalar(logt[:], small[:, 2, 0:H], b3[:, 0:1], LOG_T_MIN, ALU.add, ALU.max))
                step(nc.vector.tensor_scalar(logt[:], logt[:], LOG_T_MAX, None, ALU.min))
                dve.sem_inc(t_ready, 1)
                dve.wait_ge(t_ready, 2)
                step(nc.vector.tensor_scalar(tscale[:, 0:H], tscale[:, 0:H], 0.5, None, ALU.mult))
                step(nc.vector.memset(tscale[:, H:H + 2], 1.0))

            @block.scalar
            def _(act):
                act.wait_ge(w_in, 1)
                nc.scalar.activation(wgt[:], wgt[:], ACT.Exp, scale=DK ** -0.5).then_inc(w_out, 1)
                act.wait_ge(hid_mm, 1)
                nc.scalar.activation(hid1[:], small[0:64, 0, 0:H], ACT.Gelu, bias=b1[:, 0:1]).then_inc(hid_act, 1)
                act.wait_ge(hid_mm, 2)
                nc.scalar.activation(hid2[:], small[0:64, 1, 0:H], ACT.Gelu, bias=b2[:, 0:1]).then_inc(hid_act, 1)
                act.wait_ge(t_ready, 1)
                nc.scalar.activation(tscale[:, 0:H], logt[:], ACT.Exp, scale=-1.0).then_inc(t_ready, 1)

            @block.tensor
            def _(pe):
                pe.wait_ge(m_T, 1)
                nc.tensor.transpose(small[0:H * NT, 3, 0:P], mneg[:], f.ident[:]).then_inc(m_T, 1)
                pe.wait_ge(featured, 1)
                pairs = [(w1b[:, 0], qk_sum[:, c]) for c in range(KC)]
                pairs += [(w1b[:, 1], m_all[:, :, t]) for t in range(NT)]
                pairs += [(w1b[:, 2], e_all[:, :, t]) for t in range(NT)]
                for n, (a, b) in enumerate(pairs):
                    mm = nc.tensor.matmul(small[0:64, 0, 0:H], a, b, start=(n == 0), stop=(n == len(pairs) - 1))
                mm.then_inc(hid_mm, 1)
                pe.wait_ge(hid_act, 1)
                nc.tensor.matmul(small[0:64, 1, 0:H], w2[:], hid1[:], start=True, stop=True).then_inc(hid_mm, 1)
                pe.wait_ge(hid_act, 2)
                pe.wait_ge(w3_set, 1)
                nc.tensor.matmul(small[:, 2, 0:H], w3b[:], hid2[:], start=True, stop=True).then_inc(t_mm, 1)

        with ExitStack() as inner:
            block = inner.enter_context(nc.Block())
            ps = f.ps(inner, "psT", [P, 2, GC * S])
            sums = f.ps(inner, "sums", [P, 2, BANK])
            both = f.ps(inner, "both", [P, 2 * NT, QUAD])
            out_T, out_sb, out_mm, out_ready = f.sem("out_T"), f.sem("out_sb"), f.sem("out_mm"), f.sem("out_ready")
            t_now_ready, sums_sb, gathered, zeroed = (f.sem(n) for n in ("t_now_ready", "sums_sb", "gathered", "zeroed"))
            g_loaded = f.sem("g_loaded")

            @block.sync
            def _(sp):
                sp.dma_start(gather[:], i["c_gather"]).then_inc(g_loaded, 16)
                with sp.Fori(0, H // 2) as pair:
                    for b in range(2):
                        sp.wait_ge(kb_free, 2 * pair + b + 1)
                        for r, s in enumerate(K_PARTS):
                            src = f.key_heads[0, s, bass.ds(2 * pair + b, 1)]
                            sp.dma_start(k96[r * DK:(r + 1) * DK, b:b + 1, :], src.rearrange("h d n -> d h n")
                                         ).then_inc(kb_loaded[b], 16)
                        sp.dma_start(vhead[:, b:b + 1], f.value_rows[0, bass.ds(2 * pair + b, 1)].rearrange(
                            "h p k d -> p h k d")).then_inc(kb_loaded[b], 16)

            @block.tensor
            def _(pe):
                pe.sem_inc(kb_free, 2)
                pe.wait_ge(g_loaded, 16)
                pe.wait_ge(zeroed, 1)

                def weigh(head, b, g, n):
                    for c in range(GC):
                        mm = nc.tensor.matmul(sums[c * QUAD:c * QUAD + DV, b, 0:S], vhead[:, b, g * GC + c, :],
                                              probs[:, g % 2, c, :], start=(g == 0), stop=(g == NG - 1))
                    mm.then_inc(probs_used, 1)
                    if g == NG - 1:
                        pe.wait_ge(probs_used, n + 3)
                        pe.sem_inc(pv_done, 1)
                        pe.sem_inc(kb_free, 1)

                def bring_together(head, b):
                    pe.wait_ge(sums_sb, head + 1)
                    pe.wait_ge(pv_read, head + 1)
                    for t in range(NT):
                        mm = nc.tensor.matmul(both[:, NT * b + t, 0:DV], sumsT[:, b, t * P:(t + 1) * P], gather[:],
                                              start=True, stop=True)
                    mm.then_inc(gathered, 1)

                def heads(pair, first):
                    for b in range(2):
                        head = 2 * pair + b
                        pe.wait_ge(kb_loaded[b], 112 * (pair + 1))
                        for g in range(NG):
                            n = head * NG + g
                            pe.wait_ge(probs_ready, n + 1)
                            for c in range(GC):
                                at = (g * GC + c) * P
                                mm = nc.tensor.matmul(ps[:, g % 2, c * S:(c + 1) * S], k96[0:MAXROWS, b, at:at + P],
                                                      q96[0:MAXROWS, bass.ds(head, 1), :], start=True, stop=True)
                            mm.then_inc(scoredT, 1)
                            if g == 0 and b == 0 and first:
                                continue
                            pe.wait_ge(probs_ready, n + 2)
                            if g == 0:
                                weigh(head - 1, 1 - b, NG - 1, n - 1)
                                continue
                            if g == 1:
                                pe.wait_ge(sums_free, head + 1)
                            weigh(head, b, g - 1, n - 1)
                            if g == 2 and not (first and b == 0):
                                bring_together(head - 1, 1 - b)

                heads(0, True)
                with pe.Fori(1, H // 2) as pair:
                    heads(pair, False)
                pe.wait_ge(probs_ready, UNITS + 2)
                weigh(H - 1, 1, NG - 1, UNITS - 1)
                bring_together(H - 1, 1)
                pe.wait_ge(out_T, 1)
                flat = ps[:, 0, 0:KC * S].rearrange("p (c n) -> p c n", c=KC)
                attn_rows = attn[:].rearrange("p t h d -> p t (h d)")
                transpose_tokens(nc, flat, attn_rows, f.ident[:]).then_inc(out_T, 1)
                pe.wait_ge(out_sb, 1)
                for t in range(NT):
                    out = ps[:, 1, t * D:(t + 1) * D]
                    for c in range(KC):
                        nc.tensor.matmul(out, attnT[:, c, t * P:(t + 1) * P], wo[:, c, :], start=(c == 0), stop=False)
                    mm = nc.tensor.matmul(out, f.ones[0:1, :], bo[:], start=False, stop=True)
                mm.then_inc(out_mm, 1)

            @block.scalar
            def _(act):
                act.sem_inc(probs_ready, 2)
                with act.Fori(0, H // 2) as pair:
                    for b in range(2):
                        act.wait_ge(t_now_ready, 2 * pair + b + 1)
                        for g in range(NG):
                            n = (2 * pair + b) * NG + g
                            act.wait_ge(scoredT, n + 1)
                            act.wait_ge(probs_used, n + 1)
                            nc.scalar.activation(probs[:, g % 2].rearrange("p c n -> p (c n)"), ps[:, g % 2], ACT.Exp,
                                                 scale=t_now[:, b:b + 1]).then_inc(probs_ready, 1)
                act.wait_ge(out_T, 2)
                nc.scalar.copy(attnT[:], ps[:, 0, 0:KC * S].rearrange("p (c n) -> p c n", c=KC)).then_inc(out_sb, 1)

            @block.vector
            def _(dve):
                nc.vector.memset(sums[:], 0.0).then_inc(zeroed, 1)
                dve.sem_inc(probs_used, 2)
                dve.sem_inc(pv_read, 2)
                dve.sem_inc(sums_free, 2)
                nc.vector.tensor_copy(t_now[:], tscale[:, 0:2]).then_inc(t_now_ready, 2)
                with dve.Fori(0, H // 2) as pair:
                    for b in range(2):
                        head = 2 * pair + b
                        dve.wait_ge(pv_done, head + 1)
                        nc.vector.tensor_scalar(t_now[:, b:b + 1], tscale[:, bass.ds(head + 2, 1)], 1.0, None, ALU.mult
                                                ).then_inc(t_now_ready, 1)
                        nc.vector.tensor_copy(sumsT[:, b], sums[:, b, 0:S]).then_inc(sums_sb, 1)
                        dve.wait_ge(sums_sb, head + 1)
                        dve.sem_inc(sums_free, 1)
                        dve.wait_ge(gathered, head + 1)
                        nc.vector.reciprocal(rz[:, b], both[:, NT * b:NT * (b + 1), DK]).then_inc(recip_done, 1)
                        dve.wait_ge(recip_done, head + 1)
                        for t in range(NT):
                            ins = nc.vector.tensor_scalar(attn[:, t, bass.ds(head, 1), :], both[:, NT * b + t, 0:DK],
                                                          rz[:, b, t:t + 1], None, ALU.mult)
                        ins.then_inc(pv_read, 1)
                dve.wait_ge(pv_read, H + 2)
                dve.sem_inc(out_T, 1)
                dve.wait_ge(out_mm, 1)
                nc.vector.tensor_tensor(f.x[:], f.x[:], ps[:, 1, 0:NT * D].rearrange("p (t n) -> p t n", t=NT),
                                        ALU.add).then_inc(out_ready, 1)
                dve.wait_ge(out_ready, 1)


def linear_attn(f):
    nc, i = f.nc, f.ins
    f.layer = "la"
    s = {n: f.sem(n) for n in ("loaded", "var_ready", "root_ready", "dve_steps", "pool_steps", "z_ready", "zT_mm",
                               "zT_sb", "q_mm", "k_mm", "v_mm", "q_gelu", "k_gelu", "v_sb", "k_ready", "mean_mm",
                               "krot_ready", "kv_mm", "kv_masked", "qrot_ready", "qT_mm", "qT_sb", "out_mm")}
    with ExitStack() as ctx:
        w = f.sb(ctx, "w", [P, 3, KC, D])
        b = f.sb(ctx, "b", [1, 3, D])
        gain = f.sb(ctx, "gain", [P, 2, D])
        rope = f.sb(ctx, "rope", [P, 2, NT, D // 2])
        same_head = f.sb(ctx, "same_head", [P, KC, D])
        z = f.sb(ctx, "z", [P, NT, D])
        zT = f.sb(ctx, "zT", [P, KC, S])
        q, k, v = (f.sb(ctx, n, [P, NT, D]) for n in "qkv")
        qr, kr = (f.sb(ctx, n, [P, NT, D]) for n in ("qr", "kr"))
        tq, tk = (f.sb(ctx, n, [P, NT, D // 2]) for n in ("tq", "tk"))
        qrT = f.sb(ctx, "qrT", [P, KC, S])
        kv = f.sb(ctx, "kv", [P, KC, D])
        prod = f.sb(ctx, "prod", [P, NT, D])
        den = f.sb(ctx, "den", [P, NT, H])
        res = f.sb(ctx, "res", [P, NT, D])
        ps = f.ps(ctx, "ps", [P, 8, BANK])
        tiles = lambda n: ps[:, n].rearrange("p (t n) -> p t n", t=NT)
        block = ctx.enter_context(nc.Block())

        @block.sync
        def _(sp):
            loads = [(w[:, n], rows_of(i[f"L0_attn_W{c}"])) for n, c in enumerate("qkv")]
            loads += [(b[:, n], i[f"L0_attn_b{c}"]) for n, c in enumerate("qkv")]
            loads += [(gain[:, n], i[f"L0_attn_{c}"].partition_broadcast(P)) for n, c in enumerate(("gamma", "beta"))]
            loads += [(rope[:], i["c_rope"]), (same_head[:], i["c_same_head"])]
            for dst, src in loads:
                sp.dma_start(dst, src).then_inc(s["loaded"], 16)

        @block.tensor
        def _(pe):
            pe.wait_ge(s["z_ready"], 1)
            transpose_tokens(nc, tiles(0), z, f.ident[:]).then_inc(s["zT_mm"], 1)
            pe.wait_ge(s["loaded"], 160)
            pe.wait_ge(s["zT_sb"], 1)
            for m, done in enumerate(("q_mm", "k_mm", "v_mm")):
                for t in range(NT):
                    out = tiles(1 + m)[:, t]
                    for c in range(KC):
                        nc.tensor.matmul(out, zT[:, c, t * P:(t + 1) * P], w[:, m, c, :], start=(c == 0), stop=False)
                    mm = nc.tensor.matmul(out, f.ones[0:1, :], b[:, m, :], start=False, stop=True)
                mm.then_inc(s[done], 1)
            pe.wait_ge(s["k_ready"], 1)
            for t in range(NT):
                mm = nc.tensor.matmul(ps[:, 4, 0:D], f.ones[:], k[:, t, :], start=(t == 0), stop=(t == NT - 1))
            mm.then_inc(s["mean_mm"], 1)
            pe.wait_ge(s["krot_ready"], 1)
            pe.wait_ge(s["v_sb"], 1)
            for c in range(KC):
                for t in range(NT):
                    mm = nc.tensor.matmul(tiles(5)[:, c], kr[:, t, c * P:(c + 1) * P], v[:, t, :],
                                          start=(t == 0), stop=(t == NT - 1))
            mm.then_inc(s["kv_mm"], 1)
            pe.wait_ge(s["qrot_ready"], 1)
            transpose_tokens(nc, tiles(6), qr, f.ident[:]).then_inc(s["qT_mm"], 1)
            pe.wait_ge(s["qT_sb"], 1)
            pe.wait_ge(s["kv_masked"], 1)
            for t in range(NT):
                for c in range(KC):
                    mm = nc.tensor.matmul(tiles(7)[:, t], qrT[:, c, t * P:(t + 1) * P], kv[:, c, :],
                                          start=(c == 0), stop=(c == KC - 1))
            mm.then_inc(s["out_mm"], 1)

        @block.scalar
        def _(act):
            take_root(f, act, s["var_ready"], s["root_ready"])
            act.wait_ge(s["zT_mm"], 1)
            nc.scalar.copy(zT[:], tiles(0)).then_inc(s["zT_sb"], 1)
            act.wait_ge(s["q_mm"], 1)
            nc.scalar.activation(q[:], tiles(1), ACT.Gelu).then_inc(s["q_gelu"], 1)
            act.wait_ge(s["k_mm"], 1)
            nc.scalar.activation(k[:], tiles(2), ACT.Gelu).then_inc(s["k_gelu"], 1)
            act.wait_ge(s["v_mm"], 1)
            nc.scalar.copy(v[:], tiles(3)).then_inc(s["v_sb"], 1)
            act.wait_ge(s["qT_mm"], 1)
            nc.scalar.copy(qrT[:], tiles(6)).then_inc(s["qT_sb"], 1)
            take_root(f, act, s["var_ready"], s["root_ready"], 1)

        def rotate(eng, step, out, a, tmp):
            o, p = (y[:].rearrange("p t (n two) -> p t n two", two=2) for y in (out, a))
            cos, sin = rope[:, 0], rope[:, 1]
            step(eng.tensor_tensor(o[:, :, :, 0], p[:, :, :, 0], cos, ALU.mult))
            step(eng.tensor_tensor(tmp[:], p[:, :, :, 1], sin, ALU.mult))
            step(eng.tensor_tensor(o[:, :, :, 0], o[:, :, :, 0], tmp[:], ALU.subtract))
            step(eng.tensor_tensor(o[:, :, :, 1], p[:, :, :, 1], cos, ALU.mult))
            step(eng.tensor_tensor(tmp[:], p[:, :, :, 0], sin, ALU.mult))
            step(eng.tensor_tensor(o[:, :, :, 1], o[:, :, :, 1], tmp[:], ALU.add))

        @block.gpsimd
        def _(pool):
            step = Chain(pool, s["pool_steps"])
            pool.wait_ge(s["loaded"], 160)
            pool.wait_ge(s["k_gelu"], 1)
            step(nc.gpsimd.tensor_scalar(k[:], k[:], 0.21, None, ALU.add))
            pool.sem_inc(s["k_ready"], 1)
            rotate(nc.gpsimd, step, kr, k, tk)
            pool.sem_inc(s["krot_ready"], 1)

        @block.vector
        def _(dve):
            step = Chain(dve, s["dve_steps"])
            layer_norm(f, dve, step, z, f.x, 1e-5, s["var_ready"], s["root_ready"])
            dve.sem_inc(s["z_ready"], 1)
            dve.wait_ge(s["loaded"], 160)
            dve.wait_ge(s["q_gelu"], 1)
            step(nc.vector.tensor_scalar(q[:], q[:], 0.21, None, ALU.add))
            rotate(nc.vector, step, qr, q, tq)
            dve.sem_inc(s["qrot_ready"], 1)
            dve.wait_ge(s["mean_mm"], 1)
            for t in range(NT):
                step(nc.vector.tensor_tensor(prod[:, t], q[:, t], ps[:, 4, 0:D], ALU.mult))
            heads = prod[:].rearrange("p t (h d) -> p t h d", h=H)
            step(nc.vector.tensor_reduce(den[:], heads, AX, ALU.add))
            step(nc.vector.tensor_scalar(den[:], den[:], 1.0 / S, 1e-6, ALU.mult, ALU.add))
            step(nc.vector.reciprocal(den[:], den[:]))
            dve.wait_ge(s["kv_mm"], 1)
            step(nc.vector.scalar_tensor_tensor(out=kv[:], in0=tiles(5), scalar=1.0 / S, in1=same_head[:],
                                                op0=ALU.mult, op1=ALU.mult))
            dve.sem_inc(s["kv_masked"], 1)
            dve.wait_ge(s["out_mm"], 1)
            for t in range(NT):
                step(nc.vector.tensor_tensor(res[:, t].rearrange("p (h d) -> p h d", h=H),
                                             tiles(7)[:, t].rearrange("p (h d) -> p h d", h=H),
                                             den[:, t].unsqueeze(2).to_broadcast([P, H, DK]), ALU.mult))
            step(nc.vector.tensor_tensor(res[:], res[:], z[:], ALU.add))
            layer_norm(f, dve, step, prod, res, 1e-12, s["var_ready"], s["root_ready"], 1)
            for t in range(NT):
                step(nc.vector.tensor_tensor(prod[:, t], prod[:, t], gain[:, 0], ALU.mult))
                step(nc.vector.tensor_tensor(prod[:, t], prod[:, t], gain[:, 1], ALU.add))
            step(nc.vector.tensor_tensor(f.x[:], f.x[:], prod[:], ALU.add))


TAU = 2 * np.pi
TAU_PARTS = (6.28125, float(np.float32(TAU - 6.28125) // 2 ** -21 * 2 ** -21), 0.0)
TAU_PARTS = TAU_PARTS[:2] + (float(TAU - TAU_PARTS[0] - TAU_PARTS[1]),)
ROUND = 1.5 * 2 ** 23
PI_BELOW = float(np.nextafter(np.float32(np.pi), np.float32(0)))
HD = 64
NF = BANK // D
E0, TOP0 = 31, 3
EXPERTS0 = E0 + 1
I0 = 256
EW0 = KC * I0 + I0 // P * D + I0 // P
RING = 4


def rms_norm(f, dve, step, y, x, gain, square, eps, var_ready, root_ready, n):
    nc = f.nc
    for t in range(NT):
        step(nc.vector.tensor_tensor_reduce(out=square[:, t], in0=x[:, t], in1=x[:, t], scale=1.0 / D, scalar=0.0,
                                            op0=ALU.mult, op1=ALU.add, accum_out=f.rstd[:, t:t + 1]))
    nc.vector.tensor_scalar(f.rstd[:], f.rstd[:], eps, None, ALU.add).then_inc(var_ready, 1)
    dve.wait_ge(root_ready, n + 1)
    step(nc.vector.reciprocal(f.rstd[:], f.rstd[:]))
    for t in range(NT):
        step(nc.vector.scalar_tensor_tensor(out=y[:, t], in0=x[:, t], scalar=f.rstd[:, t:t + 1], in1=gain,
                                            op0=ALU.mult, op1=ALU.mult))


class ShortAttention:

    def __init__(self, f, ctx, heads, scale, causal):
        self.f, self.heads, self.scale, self.causal = f, heads, scale, causal
        self.s = {n: f.sem(n) for n in ("scored", "masked", "max_raw", "max_ready", "exp_done", "rz_ready",
                                        "normed", "probsT_mm", "probsT_sb", "attn_mm", "attn_sb")}
        self.scores = f.ps(ctx, "scores", [P, 2, NT, S])
        self.probsT_ps = f.ps(ctx, "probsT_ps", [P, 2, NT, S])
        self.attn_ps = f.ps(ctx, "attn_ps", [P, 2, BANK])
        self.masked = f.sb(ctx, "masked", [P, 2, NT, S])
        self.top = f.sb(ctx, "top", [P, 2, NT])
        self.ntop = f.sb(ctx, "ntop", [P, 2, NT])
        self.z = f.sb(ctx, "z", [P, 2, NT])
        self.rz = f.sb(ctx, "rz", [P, 2, NT])
        self.probs = f.sb(ctx, "probs", [P, 2, NT, S])
        self.normed = f.sb(ctx, "normed", [P, 2, NT, S])
        self.probsT = f.sb(ctx, "probsT", [P, 2, NT, S])
        self.attnT = f.sb(ctx, "attnT", [P, heads // 2, S])

    def tensor(self, pe, products, v):
        nc, s = self.f.nc, self.s
        for n in range(self.heads + 2):
            if n < self.heads:
                if n >= 2:
                    pe.wait_ge(s["masked"] if self.causal else s["exp_done"], n - 1)
                for t in range(NT):
                    pairs = products(n, t)
                    for k, (a, b) in enumerate(pairs):
                        mm = nc.tensor.matmul(self.scores[:, n % 2, t], a, b, start=(k == 0), stop=(k == len(pairs) - 1))
                mm.then_inc(s["scored"], 1)
            h = n - 1
            if 0 <= h < self.heads:
                pe.wait_ge(s["normed"], h + 1)
                if h >= 2:
                    pe.wait_ge(s["probsT_sb"], h - 1)
                for k in range(NT):
                    for t in range(NT):
                        mm = nc.tensor.transpose(self.probsT_ps[:, h % 2, k, t * P:(t + 1) * P],
                                                 self.normed[:, h % 2, t, k * P:(k + 1) * P], self.f.ident[:])
                mm.then_inc(s["probsT_mm"], 1)
            h = n - 2
            if h >= 0:
                pair, side = h // 2, h % 2
                pe.wait_ge(s["probsT_sb"], h + 1)
                if pair >= 2 and side == 0:
                    pe.wait_ge(s["attn_sb"], pair - 1)
                for k in range(NT):
                    mm = nc.tensor.matmul(self.attn_ps[side * HD:(side + 1) * HD, pair % 2, 0:S], v(h, k),
                                          self.probsT[:, h % 2, k], start=(k == 0), stop=(k == NT - 1))
                if side:
                    mm.then_inc(s["attn_mm"], 1)

    def scalar(self, act):
        nc, s = self.f.nc, self.s
        for n in range(self.heads + 2):
            h = n
            if h < self.heads:
                b = h % 2
                act.wait_ge(s["max_ready"], h + 1)
                if h >= 2:
                    act.wait_ge(s["normed"], h - 1)
                for t in range(NT):
                    src = self.masked[:, b, t] if self.causal else self.scores[:, b, t]
                    ins = nc.scalar.activation(self.probs[:, b, t], src, ACT.Exp, bias=self.ntop[:, b, t:t + 1],
                                               accum_out=self.z[:, b, t:t + 1])
                ins.then_inc(s["exp_done"], 1)
            h = n - 1
            if 0 <= h < self.heads:
                act.wait_ge(s["probsT_mm"], h + 1)
                if h >= 4:
                    act.wait_ge(s["attn_mm"], (h - 2) // 2)
                elif h >= 2:
                    act.wait_ge(s["attn_mm"], 1)
                nc.scalar.copy(self.probsT[:, h % 2], self.probsT_ps[:, h % 2]).then_inc(s["probsT_sb"], 1)

    def vector(self, dve, mask=None):
        nc, s = self.f.nc, self.s
        for n in range(self.heads + 3):
            h = n
            if h < self.heads:
                b = h % 2
                dve.wait_ge(s["scored"], h + 1)
                if h >= 2:
                    dve.wait_ge(s["exp_done"], h - 1)
                src = self.scores[:, b]
                if self.causal:
                    nc.vector.scalar_tensor_tensor(out=self.masked[:, b], in0=src, scalar=self.scale, in1=mask,
                                                   op0=ALU.mult, op1=ALU.add).then_inc(s["masked"], 1)
                    dve.wait_ge(s["masked"], h + 1)
                    src = self.masked[:, b]
                nc.vector.tensor_reduce(self.top[:, b], src, AX, ALU.max).then_inc(s["max_raw"], 1)
                dve.wait_ge(s["max_raw"], h + 1)
                nc.vector.tensor_scalar(self.ntop[:, b], self.top[:, b], -1.0, None, ALU.mult).then_inc(s["max_ready"], 1)
            h = n - 1
            if 0 <= h < self.heads:
                b = h % 2
                dve.wait_ge(s["exp_done"], h + 1)
                nc.vector.reciprocal(self.rz[:, b], self.z[:, b]).then_inc(s["rz_ready"], 1)
                dve.wait_ge(s["rz_ready"], h + 1)
                if h >= 2:
                    dve.wait_ge(s["probsT_mm"], h - 1)
                for t in range(NT):
                    ins = nc.vector.tensor_scalar(self.normed[:, b, t], self.probs[:, b, t], self.rz[:, b, t:t + 1],
                                                  None, ALU.mult)
                ins.then_inc(s["normed"], 1)
            h = n - 3
            if h >= 0 and h % 2:
                dve.wait_ge(s["attn_mm"], h // 2 + 1)
                nc.vector.tensor_copy(self.attnT[:, h // 2], self.attn_ps[:, h // 2 % 2, 0:S]).then_inc(s["attn_sb"], 1)


def route(nc, step, gates, score, before, over, same, rank, top):
    n = score.shape[1]
    mine = score.unsqueeze(2).to_broadcast([P, n, n])
    other = score.unsqueeze(1).to_broadcast([P, n, n])
    step(nc.vector.tensor_tensor(over, other, mine, ALU.is_gt))
    step(nc.vector.tensor_tensor(same, other, mine, ALU.is_equal))
    step(nc.vector.tensor_tensor(same, same, before, ALU.mult))
    step(nc.vector.tensor_tensor(over, over, same, ALU.add))
    step(nc.vector.tensor_reduce(rank, over, AX, ALU.add))
    step(nc.vector.scalar_tensor_tensor(out=gates, in0=rank, scalar=float(top), in1=score, op0=ALU.is_lt, op1=ALU.mult))


def block0(f):
    nc, i = f.nc, f.ins
    f.layer = "b0"
    with ExitStack() as outer:
        xn = f.sb(outer, "xn", [P, NT, D])
        z = f.sb(outer, "zin", [P, NT, D])
        square = f.sb(outer, "square", [P, NT, D])
        gain1 = f.sb(outer, "gain1", [P, D])
        gain2 = f.sb(outer, "gain2", [P, D])
        G = D * 4 // (2 * P)
        NQ = H * HD
        with ExitStack() as ctx:
            s = {n: f.sem(n) for n in ("loaded", "w_loaded", "var_ready", "root_ready", "dve_steps", "pool_steps",
                                       "angles", "waves", "xn_ready", "xnT_mm", "xnT_sb", "v_mm", "v_sb", "qk_mm",
                                       "qk_sb", "q_rot", "k_rot", "out_mm")}
            wq, wk, wv = (f.sb(ctx, n, [P, KC, NQ]) for n in ("wq", "wk", "wv"))
            wo = f.sb(ctx, "wo", [P, NQ // P, D])
            bqk = f.sb(ctx, "bqk", [P, 2, NQ // P])
            bv = f.sb(ctx, "bv", [1, NQ])
            bo = f.sb(ctx, "bo", [1, D])
            mask = f.sb(ctx, "mask", [P, NT, S])
            theta = f.sb(ctx, "theta", [P, 1])
            pos = f.sb(ctx, "pos", [P, S])
            angle, turn, red = (f.sb(ctx, n, [P, 2, S]) for n in ("angle", "turn", "red"))
            waves = f.sb(ctx, "waves", [P, 2, S])
            xnT = f.sb(ctx, "xnT", [P, KC, S])
            v = f.sb(ctx, "v", [P, NT, NQ])
            raw = f.sb(ctx, "raw", [P, 2, 2, S])
            q = f.sb(ctx, "q", [P, G, 2, S])
            k = f.sb(ctx, "k", [P, G, 2, S])
            tc = f.sb(ctx, "tc", [P, 2, 2, S])
            ts = f.sb(ctx, "ts", [P, 2, 2, S])
            ps = f.ps(ctx, "ps", [P, 2, BANK])
            att = ShortAttention(f, ctx, H, HD ** -0.5, True)
            tiles = lambda n: ps[:, n].rearrange("p (t n) -> p t n", t=NT)
            block = ctx.enter_context(nc.Block())

            @block.sync
            def _(sp):
                for g in range(4):
                    sp.dma_start(theta[32 * g:32 * g + 32], i["L0_ffn_theta"]).then_inc(s["loaded"], 16)
                for dst, src in ((pos, "c_pos"), (mask, "c_causal"), (bqk, "L0_ffn_qk_b"), (bv, "L0_ffn_v_b"),
                                 (bo, "L0_ffn_o_b")):
                    sp.dma_start(dst[:], i[src]).then_inc(s["loaded"], 16)
                for dst, src in ((gain1, "L0_ffn_gamma1"), (gain2, "L0_ffn_gamma2")):
                    sp.dma_start(dst[:], i[src].partition_broadcast(P)).then_inc(s["loaded"], 16)
                for dst, src in ((wv, "L0_ffn_v_w"), (wq, "L0_ffn_q_w"), (wk, "L0_ffn_k_w"), (wo, "L0_ffn_o_w")):
                    sp.dma_start(dst[:], rows_of(i[src])).then_inc(s["w_loaded"], 16)

            @block.tensor
            def _(pe):
                pe.wait_ge(s["xn_ready"], 1)
                transpose_tokens(nc, tiles(0), xn, f.ident[:]).then_inc(s["xnT_mm"], 1)
                pe.wait_ge(s["w_loaded"], 64)
                pe.wait_ge(s["xnT_sb"], 1)
                n = 1
                for g in range(G):
                    for m, w in enumerate((wq, wk)):
                        if n >= 3:
                            pe.wait_ge(s["qk_sb"], n - 2)
                        for part in range(2):
                            for c in range(KC):
                                at = (2 * g + part) * P
                                mm = nc.tensor.matmul(tiles(n % 2)[:, part], w[:, c, at:at + P], xnT[:, c, :],
                                                      start=(c == 0), stop=(c == KC - 1))
                        mm.then_inc(s["qk_mm"], 1)
                        n += 1
                for t in range(NT):
                    for half in range(NQ // BANK):
                        pe.wait_ge(s["qk_sb"], n - 2) if n - 2 <= 2 * G else pe.wait_ge(s["v_sb"], n - 2 - 2 * G)
                        for c in range(KC):
                            nc.tensor.matmul(ps[:, n % 2], xnT[:, c, t * P:(t + 1) * P],
                                             wv[:, c, half * BANK:(half + 1) * BANK], start=(c == 0), stop=False)
                        nc.tensor.matmul(ps[:, n % 2], f.ones[0:1, :], bv[:, half * BANK:(half + 1) * BANK],
                                         start=False, stop=True).then_inc(s["v_mm"], 1)
                        n += 1
                pe.wait_ge(s["q_rot"], G)
                pe.wait_ge(s["k_rot"], G)
                pe.wait_ge(s["v_sb"], 4)

                def products(h, t):
                    g, at = h // 4, 32 * (h % 4)
                    return [(q[at:at + 32, g, part, t * P:(t + 1) * P], k[at:at + 32, g, part, :]) for part in range(2)]

                att.tensor(pe, products, lambda h, kt: v[:, kt, h * HD:(h + 1) * HD])
                pe.wait_ge(att.s["attn_sb"], H // 2)
                for t in range(NT):
                    out = tiles(0)[:, t]
                    for c in range(NQ // P):
                        nc.tensor.matmul(out, att.attnT[:, c, t * P:(t + 1) * P], wo[:, c, :], start=(c == 0), stop=False)
                    mm = nc.tensor.matmul(out, f.ones[0:1, :], bo[:], start=False, stop=True)
                mm.then_inc(s["out_mm"], 1)

            @block.scalar
            def _(act):
                act.wait_ge(s["angles"], 1)
                nc.scalar.activation(waves[:], red[:], ACT.Sin).then_inc(s["waves"], 1)
                take_root(f, act, s["var_ready"], s["root_ready"])
                take_root(f, act, s["var_ready"], s["root_ready"], 1)
                act.wait_ge(s["xnT_mm"], 1)
                nc.scalar.copy(xnT[:], tiles(0)).then_inc(s["xnT_sb"], 1)
                n = 1
                for g in range(G):
                    for m in range(2):
                        act.wait_ge(s["qk_mm"], n)
                        if g:
                            act.wait_ge(s["q_rot"] if m == 0 else s["k_rot"], g)
                        for part in range(2):
                            ins = nc.scalar.activation(raw[:, m, part], tiles(n % 2)[:, part], ACT.Identity,
                                                       bias=bqk[:, m, 2 * g + part:2 * g + part + 1])
                        ins.then_inc(s["qk_sb"], 1)
                        n += 1
                for t in range(NT):
                    for half in range(NQ // BANK):
                        act.wait_ge(s["v_mm"], t * NQ // BANK + half + 1)
                        nc.scalar.copy(v[:, t, half * BANK:(half + 1) * BANK], ps[:, n % 2]).then_inc(s["v_sb"], 1)
                        n += 1
                att.scalar(act)

            def rotate(eng, wait, step, m, dst, done):
                cos, sin = (waves[:, a].unsqueeze(1).to_broadcast([P, 2, S]) for a in range(2))
                for g in range(G):
                    wait(s["qk_sb"], 2 * g + m + 1)
                    step(eng.tensor_tensor(tc[:, m], raw[:, m], cos, ALU.mult))
                    step(eng.tensor_tensor(ts[:, m], raw[:, m], sin, ALU.mult))
                    eng.tensor_tensor(dst[:, g, 0], tc[:, m, 0], ts[:, m, 1], ALU.subtract)
                    step(eng.tensor_tensor(dst[:, g, 1], tc[:, m, 1], ts[:, m, 0], ALU.add))
                    step(eng.tensor_copy(mark[:, m:m + 1], dst[:, g, 1, 0:1]))
                    done(g)

            mark = f.sb(ctx, "mark", [P, 2])

            @block.gpsimd
            def _(pool):
                step = Chain(pool, s["pool_steps"])
                pool.wait_ge(s["waves"], 1)
                rotate(nc.gpsimd, pool.wait_ge, step, 1, k, lambda g: pool.sem_inc(s["k_rot"], 1))

            @block.vector
            def _(dve):
                step = Chain(dve, s["dve_steps"])
                dve.wait_ge(s["loaded"], 16 * 11)
                for a in range(2):
                    step(nc.vector.tensor_scalar(angle[:, a], pos[:], theta[:, 0:1], None, ALU.mult))
                    step(nc.vector.tensor_scalar(turn[:, a], angle[:, a], 1 / TAU, 0.25 * (1 - a), ALU.mult, ALU.add))
                step(nc.vector.tensor_scalar(turn[:], turn[:], ROUND, None, ALU.add))
                step(nc.vector.tensor_scalar(turn[:], turn[:], ROUND, None, ALU.subtract))
                step(nc.vector.scalar_tensor_tensor(out=red[:], in0=turn[:], scalar=-TAU_PARTS[0], in1=angle[:],
                                                    op0=ALU.mult, op1=ALU.add))
                for part in TAU_PARTS[1:]:
                    step(nc.vector.scalar_tensor_tensor(out=red[:], in0=turn[:], scalar=-part, in1=red[:],
                                                        op0=ALU.mult, op1=ALU.add))
                step(nc.vector.tensor_scalar(red[:, 0], red[:, 0], TAU / 4, None, ALU.add))
                step(nc.vector.tensor_scalar(red[:], red[:], PI_BELOW, -PI_BELOW, ALU.min, ALU.max))
                dve.sem_inc(s["angles"], 1)
                layer_norm(f, dve, step, z, f.x, 1e-5, s["var_ready"], s["root_ready"])
                rms_norm(f, dve, step, xn, z, gain1[:], square, 1e-5, s["var_ready"], s["root_ready"], 1)
                dve.sem_inc(s["xn_ready"], 1)
                dve.wait_ge(s["waves"], 1)
                rotate(nc.vector, dve.wait_ge, step, 0, q, lambda g: dve.sem_inc(s["q_rot"], 1))
                att.vector(dve, mask[:])
                dve.wait_ge(s["out_mm"], 1)
                step(nc.vector.tensor_tensor(xn[:], xn[:], tiles(0), ALU.add))

        with ExitStack() as ctx:
            s = {n: f.sem("e_" + n) for n in ("loaded", "w_free", "var_ready", "root_ready", "dve_steps", "an_ready",
                                              "anT_mm", "anT_sb", "logits_mm", "top_ready", "exp_done", "gates_ready",
                                              "gatesT_mm", "gatesT_sb", "b2_mm", "x_ready", "in_mm", "in_sb", "out_mm",
                                              "summed", "inner_used")}
            w_loaded = [f.sem(f"e_w_loaded{n}") for n in range(RING)]
            w = f.sb(ctx, "e_w", [P, RING, EW0])
            router = f.sb(ctx, "router", [P, KC, E0])
            rb = f.sb(ctx, "rb", [1, E0])
            b2 = f.sb(ctx, "e_b2", [EXPERTS0, D])
            before = f.sb(ctx, "before", [P, E0, E0])
            over, same = (f.sb(ctx, n, [P, E0, E0]) for n in ("over", "same"))
            an = f.sb(ctx, "an", [P, NT, D])
            anT = f.sb(ctx, "anT", [P, KC, S])
            top, ntop, zsum = (f.sb(ctx, n, [P, NT]) for n in ("e_top", "e_ntop", "zsum"))
            aff = f.sb(ctx, "aff", [P, NT, E0])
            rank = f.sb(ctx, "rank", [P, NT, E0])
            gates = f.sb(ctx, "gates", [P, NT, EXPERTS0])
            gatesT = f.sb(ctx, "gatesT", [EXPERTS0, S])
            inner = f.sb(ctx, "inner", [P, 2, I0 // P, S])
            ps = f.ps(ctx, "e_ps", [P, 4, BANK])
            in_ps = f.ps(ctx, "in_ps", [P, 2, I0 // P, S])
            out_ps = f.ps(ctx, "out_ps", [P, 2, NT, D])
            tiles = lambda n: ps[:, n].rearrange("p (t n) -> p t n", t=NT)
            block = ctx.enter_context(nc.Block())

            @block.sync
            def _(sp):
                for dst, src in ((router[:], rows_of(i["L0_ffn_router_w"])), (rb[:], i["L0_ffn_router_b"]),
                                 (b2[:], i["L0_ffn_e_b2"]), (before[:], i["c_before31"].partition_broadcast(P))):
                    sp.dma_start(dst, src).then_inc(s["loaded"], 16)
                for n in range(RING):
                    sp.dma_start(w[:, n], i["L0_ffn_e_w"][n]).then_inc(w_loaded[n], 16)
                with sp.Fori(1, EXPERTS0 // RING) as r:
                    for n in range(RING):
                        sp.wait_ge(s["w_free"], (r - 1) * RING + n + 1)
                        src = i["L0_ffn_e_w"][bass.ds(r * RING + n, 1)]
                        sp.dma_start(w[:, n:n + 1], src.rearrange("e p n -> p e n")).then_inc(w_loaded[n], 16)

            @block.tensor
            def _(pe):
                pe.wait_ge(s["an_ready"], 1)
                transpose_tokens(nc, tiles(0), an, f.ident[:]).then_inc(s["anT_mm"], 1)
                pe.wait_ge(s["loaded"], 64)
                pe.wait_ge(s["anT_sb"], 1)
                for t in range(NT):
                    out = ps[:, 1, t * E0:(t + 1) * E0]
                    for c in range(KC):
                        nc.tensor.matmul(out, anT[:, c, t * P:(t + 1) * P], router[:, c, :], start=(c == 0), stop=False)
                    mm = nc.tensor.matmul(out, f.ones[0:1, :], rb[:], start=False, stop=True)
                mm.then_inc(s["logits_mm"], 1)

                def expert_in(r, n):
                    pe.wait_ge(w_loaded[n], 16 * (r + 1))
                    pe.wait_ge(s["in_sb"], RING * r + n + 1)
                    for a in range(I0 // P):
                        for c in range(KC):
                            mm = nc.tensor.matmul(in_ps[:, n % 2, a], w[:, n, c * I0 + a * P:c * I0 + (a + 1) * P],
                                                  anT[:, c, :], start=(c == 0), stop=(c == KC - 1))
                    mm.then_inc(s["in_mm"], 1)

                def expert_out(r, n):
                    pe.wait_ge(s["in_sb"], RING * r + n + 3)
                    pe.wait_ge(s["summed"], 2 * (RING * r + n) + 2)
                    for t in range(NT):
                        for a in range(I0 // P):
                            at = KC * I0 + a * D
                            mm = nc.tensor.matmul(out_ps[:, n % 2, t], inner[:, n % 2, a, t * P:(t + 1) * P],
                                                  w[:, n, at:at + D], start=(a == 0), stop=(a == I0 // P - 1))
                    mm.then_inc(s["out_mm"], 1)
                    pe.wait_ge(s["out_mm"], RING * r + n + 1)
                    pe.sem_inc(s["w_free"], 1)
                    pe.sem_inc(s["inner_used"], 1)

                pe.sem_inc(s["inner_used"], 2)
                expert_in(0, 0)
                pe.wait_ge(s["gates_ready"], 1)
                for t in range(NT):
                    mm = nc.tensor.transpose(ps[0:EXPERTS0, 2, t * P:(t + 1) * P], gates[:, t, :], f.ident[:])
                mm.then_inc(s["gatesT_mm"], 1)
                pe.wait_ge(s["gatesT_sb"], 1)
                for t in range(NT):
                    mm = nc.tensor.matmul(tiles(3)[:, t], gatesT[:, t * P:(t + 1) * P], b2[:], start=True, stop=True)
                mm.then_inc(s["b2_mm"], 1)
                with pe.Fori(0, EXPERTS0 // RING - 1) as r:
                    for n in range(RING):
                        expert_in(r if n < RING - 1 else r + 1, (n + 1) % RING)
                        expert_out(r, n)
                r = EXPERTS0 // RING - 1
                for n in range(RING):
                    if n < RING - 1:
                        expert_in(r, n + 1)
                    expert_out(r, n)

            @block.scalar
            def _(act):
                act.sem_inc(s["in_sb"], 2)
                take_root(f, act, s["var_ready"], s["root_ready"])
                act.wait_ge(s["anT_mm"], 1)
                nc.scalar.copy(anT[:], tiles(0)).then_inc(s["anT_sb"], 1)
                act.wait_ge(s["top_ready"], 1)
                for t in range(NT):
                    ins = nc.scalar.activation(aff[:, t], ps[:, 1, t * E0:(t + 1) * E0], ACT.Exp, bias=ntop[:, t:t + 1],
                                               accum_out=zsum[:, t:t + 1])
                ins.then_inc(s["exp_done"], 1)
                act.wait_ge(s["gatesT_mm"], 1)
                nc.scalar.copy(gatesT[:], ps[0:EXPERTS0, 2, 0:S]).then_inc(s["gatesT_sb"], 1)
                with act.Fori(0, EXPERTS0 // RING) as r:
                    for n in range(RING):
                        act.wait_ge(s["in_mm"], RING * r + n + 1)
                        act.wait_ge(s["inner_used"], RING * r + n + 1)
                        for a in range(I0 // P):
                            at = EW0 - I0 // P + a
                            ins = nc.scalar.activation(inner[:, n % 2, a], in_ps[:, n % 2, a], ACT.Gelu,
                                                       bias=w[:, n, at:at + 1])
                        ins.then_inc(s["in_sb"], 1)

            @block.vector
            def _(dve):
                step = Chain(dve, s["dve_steps"])
                dve.sem_inc(s["summed"], 4)
                rms_norm(f, dve, step, an, xn, gain2[:], square, 1e-5, s["var_ready"], s["root_ready"], 0)
                dve.sem_inc(s["an_ready"], 1)
                step(nc.vector.tensor_tensor(f.x[:], f.x[:], xn[:], ALU.add))
                step(nc.vector.tensor_tensor(f.x[:], f.x[:], an[:], ALU.add))
                dve.wait_ge(s["logits_mm"], 1)
                step(nc.vector.tensor_reduce(top[:], ps[:, 1, 0:NT * E0].rearrange("p (t e) -> p t e", t=NT), AX, ALU.max))
                step(nc.vector.tensor_scalar(ntop[:], top[:], -1.0, None, ALU.mult))
                dve.sem_inc(s["top_ready"], 1)
                dve.wait_ge(s["exp_done"], 1)
                step(nc.vector.reciprocal(zsum[:], zsum[:]))
                step(nc.vector.memset(gates[:], 1.0))
                for t in range(NT):
                    step(nc.vector.tensor_scalar(aff[:, t], aff[:, t], zsum[:, t:t + 1], None, ALU.mult))
                    route(nc, step, gates[:, t, 0:E0], aff[:, t], before[:], over[:], same[:], rank[:, t], TOP0)
                dve.sem_inc(s["gates_ready"], 1)
                dve.wait_ge(s["b2_mm"], 1)
                step(nc.vector.tensor_tensor(f.x[:], f.x[:], tiles(3), ALU.add))
                with dve.Fori(0, EXPERTS0 // RING) as r:
                    for n in range(RING):
                        e = RING * r + n
                        dve.wait_ge(s["out_mm"], e + 1)
                        for t in range(NT):
                            dve.wait_ge(s["summed"], 2 * e + t + 3)
                            nc.vector.scalar_tensor_tensor(out=f.x[:, t], in0=out_ps[:, n % 2, t],
                                                           scalar=gates[:, t, bass.ds(e, 1)], in1=f.x[:, t],
                                                           op0=ALU.mult, op1=ALU.add).then_inc(s["summed"], 1)
                dve.wait_ge(s["summed"], 2 * EXPERTS0 + 4)


U = NT * NHALF
SUB = HALF // 2
CPS = SUB // P
UNITS = H * U
PITCH = S2 + 1


def cross1(f):
    nc, i = f.nc, f.ins
    f.layer = "xb"
    rel_dram = f.rel_dram
    with ExitStack() as ctx:
        bcols = f.sb(ctx, "bcols", [P, 3, KC])
        qc96 = f.sb(ctx, "qc96", [P, H, S], BF16)
        qr96 = f.sb(ctx, "qr96", [P, H, S], BF16)
        mask = f.sb(ctx, "mask", [P, NT, S2])
        minus = f.sb(ctx, "minus", [P, NT, S2])
        top_all = f.sb(ctx, "top_all", [P, H, U])
        o_all = f.sb(ctx, "o_all", [P, H, U, DV])

        with ExitStack() as inner:
            s = {n: f.sem("a_" + n) for n in ("loaded", "mask_loaded", "var_ready", "root_ready", "dve_steps", "xn_ready",
                                              "xnT_mm", "xnT_sb", "q_mm", "split", "stored", "q_loaded", "pool_steps",
                                              "mask_done")}
            wq = f.sb(inner, "wq", [P, KC, D])
            xn = f.sb(inner, "xn", [P, NT, D])
            xnT = f.sb(inner, "xnT", [P, KC, S])
            q = f.sb(inner, "q", [P, KC, S])
            qb = f.sb(inner, "qb", [P, 2, KC, S])
            rest = f.sb(inner, "rest", [P, 2, KC, S])
            parts = f.sb(inner, "parts", [P, 2, 3, KC, S], BF16)
            ps = f.ps(inner, "a_ps", [P, 2, BANK])
            tiles = lambda n: ps[:, n].rearrange("p (t n) -> p t n", t=NT)
            block = inner.enter_context(nc.Block())

            @block.sync
            def _(sp):
                for dst, src in ((wq[:], rows_of(i["L1_xattn_Wq"])), (bcols[:], i["L1_xattn_bcols"])):
                    sp.dma_start(dst, src).then_inc(s["loaded"], 16)
                sp.dma_start(mask[:], i["mask"].rearrange("(t p) n -> p t n", p=P)).then_inc(s["mask_loaded"], 16)
                sp.wait_ge(s["split"], 1)
                for m in range(2):
                    for part in range(3):
                        sp.dma_start(f.query_parts[1 + m, part].rearrange("(c p) n -> p c n", p=P),
                                     parts[:, m, part]).then_inc(s["stored"], 16)
                sp.wait_ge(s["stored"], 96)
                for m, dst in enumerate((qc96, qr96)):
                    for r, part in enumerate(Q_PARTS):
                        src = f.query_parts[1 + m, part].rearrange("(h d) n -> d h n", d=DK)
                        sp.dma_start(dst[r * DK:(r + 1) * DK], src).then_inc(s["q_loaded"], 16)
                sp.wait_ge(s["q_loaded"], 192)

            @block.tensor
            def _(pe):
                pe.wait_ge(s["xn_ready"], 1)
                transpose_tokens(nc, tiles(0), xn, f.ident[:]).then_inc(s["xnT_mm"], 1)
                pe.wait_ge(s["loaded"], 32)
                pe.wait_ge(s["xnT_sb"], 1)
                for m in range(KC):
                    for c in range(KC):
                        mm = nc.tensor.matmul(tiles(1)[:, m], wq[:, c, m * P:(m + 1) * P], xnT[:, c, :],
                                              start=(c == 0), stop=(c == KC - 1))
                mm.then_inc(s["q_mm"], 1)

            @block.scalar
            def _(act):
                take_root(f, act, s["var_ready"], s["root_ready"])
                act.wait_ge(s["xnT_mm"], 1)
                nc.scalar.copy(xnT[:], tiles(0)).then_inc(s["xnT_sb"], 1)

            @block.gpsimd
            def _(pool):
                pool.wait_ge(s["mask_loaded"], 16)
                nc.gpsimd.tensor_scalar(minus[:], mask[:], 1.0, 1e10, ALU.subtract, ALU.mult).then_inc(s["mask_done"], 1)
                pool.wait_ge(s["mask_done"], 1)

            @block.vector
            def _(dve):
                step = Chain(dve, s["dve_steps"])
                layer_norm(f, dve, step, xn, f.x, 1e-5, s["var_ready"], s["root_ready"])
                dve.sem_inc(s["xn_ready"], 1)
                dve.wait_ge(s["q_mm"], 1)
                dve.wait_ge(s["loaded"], 32)
                for c in range(KC):
                    step(nc.vector.tensor_scalar(q[:, c], tiles(1)[:, c], bcols[:, 0, c:c + 1], None, ALU.add))
                    for m in range(2):
                        step(nc.vector.tensor_scalar(qb[:, m, c], q[:, c], bcols[:, 1 + m, c:c + 1], DK ** -0.5,
                                                     ALU.add, ALU.mult))
                step(nc.vector.tensor_copy(parts[:, :, 0], qb[:]))
                step(nc.vector.tensor_tensor(rest[:], qb[:], parts[:, :, 0], ALU.subtract))
                step(nc.vector.tensor_copy(parts[:, :, 1], rest[:]))
                step(nc.vector.tensor_tensor(parts[:, :, 2], rest[:], parts[:, :, 1], ALU.subtract))
                dve.sem_inc(s["split"], 1)

        with ExitStack() as inner:
            names = ("rel_mm", "rel_out", "cont_mm", "cont_out", "masked", "halves_max", "top_raw", "top_ready",
                     "exp_done", "turned", "weighed", "sums_sb", "gathered", "sums_read", "zero_set", "g_loaded", "top_begun", "top_kept")
            s = {n: f.sem("b_" + n) for n in names}
            turned_sb = [f.sem(f"b_turned_sb{n}") for n in range(2)]
            rel_stored = [f.sem(f"b_rel_stored{n}") for n in range(U)]
            rel_back = [f.sem(f"b_rel_back{n}") for n in range(U)]
            kc_loaded = [f.sem(f"b_kc_loaded{n}") for n in range(2)]
            v_loaded = [f.sem(f"b_v_loaded{n}") for n in range(2)]
            kr_loaded = [f.sem(f"b_kr_loaded{n}") for n in range(2)]
            kc96 = f.sb(inner, "kc96", [ROWS, 2, S2], BF16)
            kr96 = f.sb(inner, "kr96", [ROWS, 2, S2], BF16)
            out0 = f.sb(inner, "out0", [P, HALF + 1])
            out1 = f.sb(inner, "out1", [P, HALF])
            row = f.sb(inner, "row", [P, U, HALF])
            top2 = f.sb(inner, "top2", [P, U, 2])
            top = f.sb(inner, "top", [P, U])
            ntop = f.sb(inner, "ntop", [P, U])
            turned = f.sb(inner, "turned", [P, 2, CPS, P])
            vhead = f.sb(inner, "vhead", [P, 2, NCH, DV])
            gather = f.sb(inner, "gather", [P, DV])
            sumsT = f.sb(inner, "sumsT", [P, 2, P])
            rel_ps = f.ps(inner, "rel_ps", [P, SUB])
            cont_ps = f.ps(inner, "cont_ps", [P, SUB])
            turn_ps = f.ps(inner, "turn_ps", [P, SUB])
            sum_ps = f.ps(inner, "sum_ps", [P, BANK])
            both = f.ps(inner, "both", [P, 2, QUAD])
            block = inner.enter_context(nc.Block())
            LOOPS = H // 2 - 1

            def where(p, c):
                return 2 * U * p + c, 2 * p + c // U, c % U, c // U % 2, c % U // NHALF, c % NHALF

            def slots(eng, slot, before=None):
                for n in range(-U, 3):
                    slot(0, n, n)
                with eng.Fori(0, LOOPS) as p:
                    for c in range(3, 3 + 2 * U):
                        slot(p, c, None)
                for n in range(2 * U * LOOPS + 3, UNITS + 3):
                    slot(LOOPS, n - 2 * U * LOOPS, n)

            def runs(n, ahead):
                return n is None or 0 <= n + ahead < UNITS

            @block.sync
            def _(sp):
                def load_keys(p, c, which, dst, loaded):
                    b = c // U % 2
                    for r, part in enumerate(K_PARTS):
                        src = f.key_heads[which, part, bass.ds(2 * p + c // U, 1)]
                        sp.dma_start(dst[r * DK:(r + 1) * DK, b:b + 1, :], src.rearrange("h d n -> d h n")
                                     ).then_inc(loaded[b], 16)

                def read_back(p, c, first=False):
                    n, head, u, b, t, half = where(p, c)
                    if not first:
                        sp.wait_ge(s["turned"], 2 * n - 2 * U + 2)
                    for k in ((0, 1), (0, 1, 2), (2, 3), (2, 3))[u]:
                        sp.wait_ge(rel_stored[k], 16 * (head + 1))
                    src = rel_back_view[half][bass.ds(head, 1), t * P:(t + 1) * P, :]
                    sp.dma_start(row[:, u:u + 1, :], src.rearrange("h p n -> p h n")).then_inc(rel_back[u], 16)

                def store(p, c):
                    n, head, u, b, t, half = where(p, c)
                    sp.wait_ge(s["rel_out"], 2 * n + 3)
                    rows = rel_rows[bass.ds(head, 1), t * P:(t + 1) * P, :]
                    if half == 0:
                        dst, src = rows[:, :, 0:HALF + 1], out0
                    else:
                        dst, src = rows[:, :, HALF + 1:PITCH], out1
                    sp.dma_start(dst.rearrange("h p n -> p (h n)"), src[:]).then_inc(rel_stored[u], 16)

                rel_rows = rel_dram[:, 0:S * PITCH].rearrange("h (r n) -> h r n", n=PITCH)
                shifted = rel_dram[:, S:S + S * S2].rearrange("h (r n) -> h r n", n=S2)
                rel_back_view = [shifted[:, :, h * HALF:(h + 1) * HALF] for h in range(NHALF)]

                def slot(p, c, n):
                    if runs(n, 2):
                        read_back(p, c + 2, first=n is not None and n + 2 < U)
                    if runs(n, U):
                        store(p, c + U)
                    if c % U == 1 and (n is None or 0 < n < UNITS - U):
                        if n is None or n > U:
                            sp.wait_ge(s["cont_mm"], 2 * U * (2 * p + c // U))
                        load_keys(p, c + U, 1, kc96, kc_loaded)
                    if c % U == 2 and (n is None or 0 < n < UNITS - U):
                        if n is None or n > U:
                            sp.wait_ge(s["weighed"], 2 * U * (2 * p + c // U) + 2)
                        load_values(p, c + U)
                    if c % (2 * U) in (U - 1, U + 2) and (n is None or 0 < n < UNITS - 2 * U):
                        sp.wait_ge(s["rel_mm"], 2 * U * (2 * p + c // U + 1))
                        load_keys(p, c + 2 * U, 2, kr96, kr_loaded)

                def load_values(p, c):
                    b = c // U % 2
                    sp.dma_start(vhead[:, b:b + 1], f.value_rows[1, bass.ds(2 * p + c // U, 1)].rearrange(
                        "h p k d -> p h k d")).then_inc(v_loaded[b], 16)

                sp.dma_start(gather[:], i["c_gather"]).then_inc(s["g_loaded"], 16)
                load_keys(0, 0, 2, kr96, kr_loaded)
                load_keys(0, 0, 1, kc96, kc_loaded)
                load_keys(0, U, 2, kr96, kr_loaded)
                load_values(0, 0)
                slots(sp, slot)

            @block.tensor
            def _(pe):
                def scores(p, c, part, q96, k96, out, loaded, free, done):
                    n, head, u, b, t, half = where(p, c)
                    if u == 0 and part == 0:
                        pe.wait_ge(loaded[b], 96 * (p + c // U // 2 + 1))
                    pe.wait_ge(free, 2 * n + part + 1)
                    for k in range(SUB // BANK):
                        at = half * HALF + part * SUB + k * BANK
                        mm = nc.tensor.matmul(out[:, k * BANK:(k + 1) * BANK],
                                              q96[0:ROWS, bass.ds(head, 1), t * P:(t + 1) * P],
                                              k96[:, b, at:at + BANK], start=True, stop=True)
                    mm.then_inc(done, 1)

                def content(p, c, part):
                    scores(p, c, part, qc96, kc96, cont_ps, kc_loaded, s["cont_out"], s["cont_mm"])

                def relative(p, c, part):
                    scores(p, c, part, qr96, kr96, rel_ps, kr_loaded, s["rel_out"], s["rel_mm"])

                def turn(p, c, part):
                    n, head, u, b, t, half = where(p, c)
                    pe.wait_ge(s["exp_done"], n + 1)
                    pe.wait_ge(turned_sb[1 - part], n + 1)
                    for k in range(CPS):
                        at = part * SUB + k * P
                        mm = nc.tensor.transpose(turn_ps[:, k * P:(k + 1) * P], row[:, u, at:at + P], f.ident[:])
                    mm.then_inc(s["turned"], 1)

                def weigh(p, c, part):
                    n, head, u, b, t, half = where(p, c)
                    pe.wait_ge(turned_sb[part], n + 1 + part)
                    if u == 0 and part == 0:
                        pe.wait_ge(v_loaded[b], 16 * (p + c // U // 2 + 1))
                    if part == 0:
                        pe.wait_ge(s["sums_sb"], n + 1)
                    for k in range(CPS):
                        at = k % NQ4 * QUAD
                        mm = nc.tensor.matmul(sum_ps[at:at + DV, 0:P], vhead[:, b, half * NCH // 2 + part * CPS + k, :],
                                              turned[:, part, k, :], start=(part == 0 and k < NQ4),
                                              stop=(part == 1 and k >= CPS - NQ4))
                    mm.then_inc(s["weighed"], 1)

                def bring_together(p, c):
                    n, head, u, b, t, half = where(p, c)
                    pe.wait_ge(s["sums_sb"], n + 2)
                    pe.wait_ge(s["sums_read"], n + 1)
                    nc.tensor.matmul(both[:, u % 2, 0:DV], sumsT[:, u % 2, :], gather[:], start=True, stop=True
                                     ).then_inc(s["gathered"], 1)

                def slot(p, c, n):
                    if runs(n, 0):
                        content(p, c, 0)
                    if runs(n, -3):
                        bring_together(p, c - 3)
                    if runs(n, -2):
                        turn(p, c - 2, 0)
                    if runs(n, U):
                        relative(p, c + U, 0)
                    if runs(n, 0):
                        content(p, c, 1)
                    if runs(n, -2):
                        turn(p, c - 2, 1)
                        weigh(p, c - 2, 0)
                    if runs(n, U):
                        relative(p, c + U, 1)
                    if runs(n, -2):
                        weigh(p, c - 2, 1)

                pe.wait_ge(s["g_loaded"], 16)
                pe.wait_ge(s["zero_set"], 2)
                slots(pe, slot)

            @block.scalar
            def _(act):
                act.sem_inc(s["rel_out"], 1)

                def evacuate(p, c, part):
                    n, head, u, b, t, half = where(p, c)
                    act.wait_ge(s["rel_mm"], 2 * n + part + 1)
                    if part == 0 and u >= NHALF:
                        act.wait_ge(rel_stored[u - NHALF], 16 * (head + 1))
                    elif part == 0 and not (isinstance(n, int) and n < U):
                        act.wait_ge(rel_stored[u + NHALF], 16 * head)
                    elif part == 0 and u == 0:
                        act.wait_ge(s["zero_set"], 1)
                    out = out1 if half else out0[:, 1:HALF + 1]
                    nc.scalar.copy(out[:, part * SUB:(part + 1) * SUB], rel_ps[:]).then_inc(s["rel_out"], 1)

                def exponentials(p, c):
                    n, head, u, b, t, half = where(p, c)
                    act.wait_ge(s["top_ready"], n + 1)
                    nc.scalar.activation(row[:, u], row[:, u], ACT.Exp, bias=ntop[:, u:u + 1]).then_inc(s["exp_done"], 1)

                def copy_turned(p, c):
                    n, head, u, b, t, half = where(p, c)
                    act.wait_ge(s["turned"], 2 * n + 1)
                    act.wait_ge(s["weighed"], 2 * n + 1)
                    nc.scalar.copy(turned[:, 0].rearrange("p k n -> p (k n)"), turn_ps[:]).then_inc(turned_sb[0], 1)

                def slot(p, c, n):
                    if runs(n, -2):
                        copy_turned(p, c - 2)
                    if runs(n, U):
                        evacuate(p, c + U, 0)
                    if runs(n, -1):
                        exponentials(p, c - 1)
                    if runs(n, U):
                        evacuate(p, c + U, 1)

                slots(act, slot)
                act.wait_ge(s["exp_done"], UNITS)

            @block.gpsimd
            def _(pool):
                def slot(p, c, n):
                    if not runs(n, 0):
                        return
                    n, head, u, b, t, half = where(p, c)
                    for part in range(2):
                        at = part * SUB
                        pool.wait_ge(s["cont_out"], 2 * n + part + 2)
                        nc.gpsimd.tensor_tensor(row[:, u, at:at + SUB], row[:, u, at:at + SUB],
                                                mask[:, t, half * HALF + at:half * HALF + at + SUB],
                                                ALU.mult).then_inc(s["masked"], 1)

                slots(pool, slot)

            @block.vector
            def _(dve):
                nc.vector.memset(out0[:, 0:1], 0.0).then_inc(s["zero_set"], 1)
                nc.vector.memset(sum_ps[:], 0.0).then_inc(s["zero_set"], 1)
                dve.sem_inc(s["sums_sb"], 1)
                dve.sem_inc(s["cont_out"], 1)
                dve.sem_inc(turned_sb[1], 1)
                dve.sem_inc(s["weighed"], 2)
                dve.sem_inc(s["sums_read"], 2)

                def add(p, c, part):
                    n, head, u, b, t, half = where(p, c)
                    if part == 0:
                        dve.wait_ge(rel_back[u], 16 * (head + 1))
                    dve.wait_ge(s["cont_mm"], 2 * n + part + 1)
                    at = part * SUB
                    nc.vector.tensor_tensor(row[:, u, at:at + SUB], cont_ps[:], row[:, u, at:at + SUB],
                                            ALU.add).then_inc(s["cont_out"], 1)

                def top_of(p, c, part):
                    n, head, u, b, t, half = where(p, c)
                    dve.wait_ge(s["masked"], 2 * n + part + 1)
                    dve.sem_inc(s["top_begun"], 1)
                    at = part * SUB
                    nc.vector.tensor_tensor_reduce(out=row[:, u, at:at + SUB], in0=row[:, u, at:at + SUB],
                                                   in1=minus[:, t, half * HALF + at:half * HALF + at + SUB], scale=1.0,
                                                   scalar=-3e38, op0=ALU.add, op1=ALU.max,
                                                   accum_out=top2[:, u, part:part + 1]).then_inc(s["halves_max"], 1)
                    if part == 1:
                        dve.wait_ge(s["halves_max"], 2 * n + 2)
                        nc.vector.tensor_tensor(top[:, u:u + 1], top2[:, u, 0:1], top2[:, u, 1:2], ALU.max
                                                ).then_inc(s["top_raw"], 1)
                        dve.wait_ge(s["top_raw"], n + 1)
                        nc.vector.tensor_scalar(ntop[:, u:u + 1], top[:, u:u + 1], -1.0, None, ALU.mult
                                                ).then_inc(s["top_ready"], 1)
                        nc.vector.tensor_copy(top_all[:, bass.ds(head, 1), u:u + 1], top[:, u:u + 1]
                                              ).then_inc(s["top_kept"], 1)

                def copy_turned(p, c):
                    n, head, u, b, t, half = where(p, c)
                    dve.wait_ge(s["turned"], 2 * n + 2)
                    dve.wait_ge(s["weighed"], 2 * n + 2)
                    nc.vector.tensor_copy(turned[:, 1].rearrange("p k n -> p (k n)"), turn_ps[:]
                                          ).then_inc(turned_sb[1], 1)

                def sums_out(p, c):
                    n, head, u, b, t, half = where(p, c)
                    dve.wait_ge(s["weighed"], 2 * n + 4)
                    nc.vector.tensor_copy(sumsT[:, u % 2], sum_ps[:, 0:P]).then_inc(s["sums_sb"], 1)

                def keep_sums(p, c):
                    n, head, u, b, t, half = where(p, c)
                    dve.wait_ge(s["gathered"], n + 1)
                    nc.vector.tensor_scalar(o_all[:, bass.ds(head, 1), u, :], both[:, u % 2, 0:DV], 1.0, None,
                                            ALU.mult).then_inc(s["sums_read"], 1)

                def slot(p, c, n):
                    if runs(n, -1):
                        top_of(p, c - 1, 0)
                    if runs(n, -3):
                        sums_out(p, c - 3)
                    if runs(n, 0):
                        add(p, c, 0)
                    if runs(n, -1):
                        top_of(p, c - 1, 1)
                    if runs(n, 0):
                        add(p, c, 1)
                    if runs(n, -2):
                        copy_turned(p, c - 2)
                    if runs(n, -3):
                        keep_sums(p, c - 3)

                slots(dve, slot)
                dve.wait_ge(s["sums_read"], UNITS + 2)
                dve.wait_ge(s["top_kept"], UNITS)

        with ExitStack() as inner:
            s = {n: f.sem("c_" + n) for n in ("loaded", "dve_steps", "w_in", "w_out", "o_ready", "oT_mm", "oT_sb", "out_mm")}
            wo = f.sb(inner, "wo", [P, KC, D])
            bo = f.sb(inner, "bo", [1, D])
            m = f.sb(inner, "m", [P, H, NT])
            wgt = f.sb(inner, "wgt", [P, H, U])
            total = f.sb(inner, "total", [P, NT, H, DV])
            z = f.sb(inner, "z", [P, NT, H])
            attn = f.sb(inner, "attn", [P, NT, H, DK])
            attnT = f.sb(inner, "attnT", [P, KC, S])
            ps = f.ps(inner, "c_ps", [P, 2, BANK])
            tiles = lambda n: ps[:, n].rearrange("p (t n) -> p t n", t=NT)
            block = inner.enter_context(nc.Block())

            @block.sync
            def _(sp):
                sp.dma_start(wo[:], rows_of(i["L1_xattn_Wo"])).then_inc(s["loaded"], 16)
                sp.dma_start(bo[:], i["L1_xattn_bo"]).then_inc(s["loaded"], 16)

            @block.vector
            def _(dve):
                step = Chain(dve, s["dve_steps"])
                halves = lambda y: y[:].rearrange("p h (t a) -> p h t a", a=NHALF)
                step(nc.vector.tensor_reduce(m[:], halves(top_all), AX, ALU.max))
                for a in range(NHALF):
                    step(nc.vector.tensor_tensor(halves(wgt)[:, :, :, a], halves(top_all)[:, :, :, a], m[:], ALU.subtract))
                dve.sem_inc(s["w_in"], 1)
                dve.wait_ge(s["w_out"], 1)
                step(nc.vector.tensor_tensor(o_all[:], o_all[:], wgt[:].unsqueeze(3).to_broadcast([P, H, U, DV]), ALU.mult))
                for t in range(NT):
                    step(nc.vector.tensor_tensor(total[:, t], o_all[:, :, NHALF * t, :], o_all[:, :, NHALF * t + 1, :],
                                                 ALU.add))
                step(nc.vector.reciprocal(z[:], total[:, :, :, DK]))
                for t in range(NT):
                    step(nc.vector.tensor_tensor(attn[:, t], total[:, t, :, 0:DK],
                                                 z[:, t].unsqueeze(2).to_broadcast([P, H, DK]), ALU.mult))
                dve.sem_inc(s["o_ready"], 1)
                dve.wait_ge(s["out_mm"], 1)
                step(nc.vector.tensor_tensor(f.x[:], f.x[:], tiles(1), ALU.add))

            @block.scalar
            def _(act):
                act.wait_ge(s["w_in"], 1)
                nc.scalar.activation(wgt[:], wgt[:], ACT.Exp).then_inc(s["w_out"], 1)
                act.wait_ge(s["oT_mm"], 1)
                nc.scalar.copy(attnT[:], tiles(0)).then_inc(s["oT_sb"], 1)

            @block.tensor
            def _(pe):
                pe.wait_ge(s["o_ready"], 1)
                transpose_tokens(nc, tiles(0), attn[:].rearrange("p t h d -> p t (h d)"), f.ident[:]
                                 ).then_inc(s["oT_mm"], 1)
                pe.wait_ge(s["loaded"], 32)
                pe.wait_ge(s["oT_sb"], 1)
                for t in range(NT):
                    for c in range(KC):
                        nc.tensor.matmul(tiles(1)[:, t], attnT[:, c, t * P:(t + 1) * P], wo[:, c, :],
                                         start=(c == 0), stop=False)
                    mm = nc.tensor.matmul(tiles(1)[:, t], f.ones[0:1, :], bo[:], start=False, stop=True)
                mm.then_inc(s["out_mm"], 1)


HM = 8
E1, TOP1 = 8, 2
I1 = 512
RING1 = 2


def multi_query(f):
    nc, i = f.nc, f.ins
    f.layer = "mq"
    s = {n: f.sem(n) for n in ("loaded", "var_ready", "root_ready", "dve_steps", "xn_ready", "xnT_mm", "xnT_sb",
                               "q_mm", "kv_mm", "sums_ready", "norms_ready", "scaled", "qT_mm", "qT_sb", "out_mm")}
    NQ = HM * HD
    with ExitStack() as ctx:
        wq = f.sb(ctx, "wq", [P, KC, NQ])
        wkv = f.sb(ctx, "wkv", [P, KC, 2 * HD])
        wo = f.sb(ctx, "wo", [P, NQ // P, D])
        gain = f.sb(ctx, "gain", [P, 2, D])
        z = f.sb(ctx, "zn", [P, NT, D])
        xn = f.sb(ctx, "xn", [P, NT, D])
        xnT = f.sb(ctx, "xnT", [P, KC, S])
        q = f.sb(ctx, "q", [P, NT, NQ])
        kv = f.sb(ctx, "kv", [P, NT, 2 * HD])
        square = f.sb(ctx, "square", [P, NT, NQ + HD])
        norms = f.sb(ctx, "norms", [P, NT, HM + 1])
        kk = f.sb(ctx, "kk", [P, NT, 2 * HD])
        qT = f.sb(ctx, "qT", [P, NQ // P, S])
        kT = f.sb(ctx, "kT", [P, S])
        ps = f.ps(ctx, "ps", [P, 2, BANK])
        att = ShortAttention(f, ctx, HM, 1.0, False)
        tiles = lambda n: ps[:, n].rearrange("p (t n) -> p t n", t=NT)
        block = ctx.enter_context(nc.Block())

        @block.sync
        def _(sp):
            loads = [(wq[:], rows_of(i["L1_attn_Wq"])), (wkv[:], rows_of(i["L1_attn_Wkv"])),
                     (wo[:], rows_of(i["L1_attn_Wout"]))]
            loads += [(gain[:, n], i[f"L1_attn_{m}"].partition_broadcast(P)) for n, m in enumerate(("norm_g", "out_norm_g"))]
            for dst, src in loads:
                sp.dma_start(dst, src).then_inc(s["loaded"], 16)

        @block.tensor
        def _(pe):
            pe.wait_ge(s["xn_ready"], 1)
            transpose_tokens(nc, tiles(0), xn, f.ident[:]).then_inc(s["xnT_mm"], 1)
            pe.wait_ge(s["loaded"], 80)
            pe.wait_ge(s["xnT_sb"], 1)
            for t in range(NT):
                if t == 1:
                    pe.wait_ge(s["xnT_sb"], 1)
                for c in range(KC):
                    mm = nc.tensor.matmul(ps[:, t], xnT[:, c, t * P:(t + 1) * P], wq[:, c, :],
                                          start=(c == 0), stop=(c == KC - 1))
                mm.then_inc(s["q_mm"], 1)
            for t in range(NT):
                for c in range(KC):
                    mm = nc.tensor.matmul(att.attn_ps[:, 0, t * 2 * HD:(t + 1) * 2 * HD], xnT[:, c, t * P:(t + 1) * P],
                                          wkv[:, c, :], start=(c == 0), stop=(c == KC - 1))
            mm.then_inc(s["kv_mm"], 1)
            pe.wait_ge(s["scaled"], 1)
            for n in range(NQ // P):
                for t in range(NT):
                    mm = nc.tensor.transpose(tiles(n // 2)[:, n % 2, t * P:(t + 1) * P], q[:, t, n * P:(n + 1) * P],
                                             f.ident[:])
            mm.then_inc(s["qT_mm"], 1)
            for t in range(NT):
                mm = nc.tensor.transpose(att.attn_ps[:, 1, t * P:(t + 1) * P], kk[:, t, :], f.ident[:])
            mm.then_inc(s["qT_mm"], 1)
            pe.wait_ge(s["qT_sb"], 3)

            def products(h, t):
                at = HD * (h % 2)
                return [(qT[at:at + HD, h // 2, t * P:(t + 1) * P], kT[at:at + HD, :])]

            att.tensor(pe, products, lambda h, kt: kv[:, kt, HD:2 * HD])
            pe.wait_ge(att.s["attn_sb"], HM // 2)
            for t in range(NT):
                for c in range(NQ // P):
                    mm = nc.tensor.matmul(tiles(0)[:, t], att.attnT[:, c, t * P:(t + 1) * P], wo[:, c, :],
                                          start=(c == 0), stop=(c == NQ // P - 1))
            mm.then_inc(s["out_mm"], 1)

        @block.scalar
        def _(act):
            take_root(f, act, s["var_ready"], s["root_ready"])
            take_root(f, act, s["var_ready"], s["root_ready"], 1)
            act.wait_ge(s["xnT_mm"], 1)
            nc.scalar.copy(xnT[:], tiles(0)).then_inc(s["xnT_sb"], 1)
            act.wait_ge(s["sums_ready"], 1)
            nc.scalar.sqrt(norms[:], norms[:]).then_inc(s["norms_ready"], 1)
            act.wait_ge(s["qT_mm"], 2)
            for n in range(2):
                nc.scalar.copy(qT[:, 2 * n:2 * n + 2], tiles(n)).then_inc(s["qT_sb"], 1)
            nc.scalar.copy(kT[:], att.attn_ps[:, 1, 0:S]).then_inc(s["qT_sb"], 1)
            att.scalar(act)
            take_root(f, act, s["var_ready"], s["root_ready"], 2)

        @block.vector
        def _(dve):
            step = Chain(dve, s["dve_steps"])
            layer_norm(f, dve, step, z, f.x, 1e-5, s["var_ready"], s["root_ready"])
            layer_norm(f, dve, step, xn, z, 1e-5, s["var_ready"], s["root_ready"], 1)
            dve.wait_ge(s["loaded"], 80)
            for t in range(NT):
                step(nc.vector.tensor_tensor(xn[:, t], xn[:, t], gain[:, 0], ALU.mult))
            dve.sem_inc(s["xn_ready"], 1)
            dve.wait_ge(s["q_mm"], 2)
            dve.wait_ge(s["kv_mm"], 1)
            step(nc.vector.tensor_copy(q[:], ps[:]))
            step(nc.vector.tensor_copy(kv[:], att.attn_ps[:, 0, 0:NT * 2 * HD].rearrange("p (t n) -> p t n", t=NT)))
            step(nc.vector.scalar_tensor_tensor(out=square[:, :, 0:NQ], in0=q[:], scalar=16.0 ** 2, in1=q[:],
                                                op0=ALU.mult, op1=ALU.mult))
            step(nc.vector.tensor_tensor(square[:, :, NQ:], kv[:, :, 0:HD], kv[:, :, 0:HD], ALU.mult))
            step(nc.vector.tensor_reduce(norms[:], square[:].rearrange("p t (h d) -> p t h d", d=HD), AX, ALU.add))
            dve.sem_inc(s["sums_ready"], 1)
            dve.wait_ge(s["norms_ready"], 1)
            step(nc.vector.tensor_scalar(norms[:], norms[:], 1e-12, None, ALU.max))
            step(nc.vector.reciprocal(norms[:], norms[:]))
            step(nc.vector.tensor_scalar(norms[:, :, 0:HM], norms[:, :, 0:HM], 16.0 * 4.0, None, ALU.mult))
            for t in range(NT):
                step(nc.vector.tensor_tensor(q[:, t].rearrange("p (h d) -> p h d", h=HM),
                                             q[:, t].rearrange("p (h d) -> p h d", h=HM),
                                             norms[:, t, 0:HM].unsqueeze(2).to_broadcast([P, HM, HD]), ALU.mult))
                for n in range(2):
                    step(nc.vector.tensor_scalar(kk[:, t, n * HD:(n + 1) * HD], kv[:, t, 0:HD], norms[:, t, HM:HM + 1],
                                                 4.0, ALU.mult, ALU.mult))
            dve.sem_inc(s["scaled"], 1)
            att.vector(dve)
            dve.wait_ge(s["out_mm"], 1)
            step(nc.vector.tensor_copy(z[:], tiles(0)))
            layer_norm(f, dve, step, xn, z, 1e-5, s["var_ready"], s["root_ready"], 2)
            for t in range(NT):
                step(nc.vector.tensor_tensor(xn[:, t], xn[:, t], gain[:, 1], ALU.mult))
            step(nc.vector.tensor_tensor(f.x[:], f.x[:], xn[:], ALU.add))


def mixture1(f):
    nc, i = f.nc, f.ins
    f.layer = "m1"
    s = {n: f.sem(n) for n in ("loaded", "w_free", "var_ready", "root_ready", "dve_steps", "xn_ready", "xnT_mm",
                               "xnT_sb", "logits_mm", "top_ready", "exp_done", "gated_mm", "silu_done", "silu_used",
                               "inner_done", "inner_used", "out_mm", "summed")}
    w_loaded = [f.sem(f"w_loaded{n}") for n in range(RING1)]
    NI = I1 // P
    with ExitStack() as ctx:
        w13 = f.sb(ctx, "w13", [P, RING1, 2, KC, I1])
        w2 = f.sb(ctx, "w2", [P, RING1, NI, D])
        wg = f.sb(ctx, "wg", [P, KC, E1])
        before = f.sb(ctx, "before", [P, E1, E1])
        over, same = (f.sb(ctx, n, [P, E1, E1]) for n in ("over", "same"))
        xn = f.sb(ctx, "xn", [P, NT, D])
        xnT = f.sb(ctx, "xnT", [P, KC, S])
        logits, exps, rank, gates = (f.sb(ctx, n, [P, NT, E1]) for n in ("logits", "exps", "rank", "gates"))
        ntop, zsum = (f.sb(ctx, n, [P, NT]) for n in ("ntop", "zsum"))
        act_in = f.sb(ctx, "act_in", [P, 2, 2, S])
        inner = f.sb(ctx, "inner", [P, 2, NI, S])
        in_ps = f.ps(ctx, "in_ps", [P, 2, 2, 2, S])
        out_ps = f.ps(ctx, "out_ps", [P, 2, NT, D])
        ps = f.ps(ctx, "ps", [P, 2, BANK])
        tiles = lambda n: ps[:, n].rearrange("p (t n) -> p t n", t=NT)
        block = ctx.enter_context(nc.Block())

        @block.sync
        def _(sp):
            sp.dma_start(wg[:], rows_of(i["L1_ffn_w_gate"])).then_inc(s["loaded"], 16)
            sp.dma_start(before[:], i["c_before8"].partition_broadcast(P)).then_inc(s["loaded"], 16)

            def load(e, n):
                for m, src in enumerate((i["L1_ffn_w1"], i["L1_ffn_w3"])):
                    sp.dma_start(w13[:, n, m], src[bass.ds(e, 1)].rearrange("e (c p) n -> p (e c) n", p=P)
                                 ).then_inc(w_loaded[n], 16)
                sp.dma_start(w2[:, n], i["L1_ffn_w2"][bass.ds(e, 1)].rearrange("e (c p) n -> p (e c) n", p=P)
                             ).then_inc(w_loaded[n], 16)

            for n in range(RING1):
                load(n, n)
            with sp.Fori(1, E1 // RING1) as r:
                for n in range(RING1):
                    sp.wait_ge(s["w_free"], (r - 1) * RING1 + n + 1)
                    load(r * RING1 + n, n)

        @block.tensor
        def _(pe):
            pe.sem_inc(s["inner_used"], 2)
            pe.wait_ge(s["xn_ready"], 1)
            transpose_tokens(nc, tiles(0), xn, f.ident[:]).then_inc(s["xnT_mm"], 1)
            pe.wait_ge(s["loaded"], 32)
            pe.wait_ge(s["xnT_sb"], 1)
            for t in range(NT):
                for c in range(KC):
                    mm = nc.tensor.matmul(ps[:, 1, t * E1:(t + 1) * E1], xnT[:, c, t * P:(t + 1) * P], wg[:, c, :],
                                          start=(c == 0), stop=(c == KC - 1))
            mm.then_inc(s["logits_mm"], 1)

            def expert_in(r, n, half):
                if half == 0:
                    pe.wait_ge(w_loaded[n], 48 * (r + 1))
                pe.wait_ge(s["silu_used"], 2 * (RING1 * r + n) + half + 1)
                for m in range(2):
                    for a in range(2):
                        at = (2 * half + a) * P
                        for c in range(KC):
                            mm = nc.tensor.matmul(in_ps[:, half, m, a], w13[:, n, m, c, at:at + P], xnT[:, c, :],
                                                  start=(c == 0), stop=(c == KC - 1))
                mm.then_inc(s["gated_mm"], 1)

            def expert_out(r, n):
                e = RING1 * r + n
                pe.wait_ge(s["inner_done"], 2 * e + 2)
                pe.wait_ge(s["summed"], 2 * e + 2)
                for t in range(NT):
                    for a in range(NI):
                        mm = nc.tensor.matmul(out_ps[:, n, t], inner[:, n, a, t * P:(t + 1) * P], w2[:, n, a, :],
                                              start=(a == 0), stop=(a == NI - 1))
                mm.then_inc(s["out_mm"], 1)
                pe.wait_ge(s["out_mm"], e + 1)
                pe.sem_inc(s["w_free"], 1)
                pe.sem_inc(s["inner_used"], 1)

            expert_in(0, 0, 0)
            with pe.Fori(0, E1 // RING1 - 1) as r:
                for n in range(RING1):
                    expert_in(r, n, 1)
                    expert_in(r + (n + 1) // RING1, (n + 1) % RING1, 0)
                    expert_out(r, n)
            r = E1 // RING1 - 1
            for n in range(RING1):
                expert_in(r, n, 1)
                if n < RING1 - 1:
                    expert_in(r, n + 1, 0)
                expert_out(r, n)

        @block.scalar
        def _(act):
            take_root(f, act, s["var_ready"], s["root_ready"])
            act.wait_ge(s["xnT_mm"], 1)
            nc.scalar.copy(xnT[:], tiles(0)).then_inc(s["xnT_sb"], 1)
            act.wait_ge(s["top_ready"], 1)
            for t in range(NT):
                ins = nc.scalar.activation(exps[:, t], logits[:, t], ACT.Exp, bias=ntop[:, t:t + 1])
            ins.then_inc(s["exp_done"], 1)
            with act.Fori(0, E1 // RING1) as r:
                for n in range(RING1):
                    for half in range(2):
                        u = 2 * (RING1 * r + n) + half
                        act.wait_ge(s["gated_mm"], u + 1)
                        act.wait_ge(s["silu_used"], u + 1)
                        nc.scalar.activation(act_in[:, half], in_ps[:, half, 0], ACT.Silu).then_inc(s["silu_done"], 1)

        @block.vector
        def _(dve):
            step = Chain(dve, s["dve_steps"])
            dve.sem_inc(s["silu_used"], 2)
            dve.sem_inc(s["summed"], 4)
            layer_norm(f, dve, step, xn, f.x, 1e-5, s["var_ready"], s["root_ready"])
            dve.sem_inc(s["xn_ready"], 1)
            dve.wait_ge(s["logits_mm"], 1)
            step(nc.vector.tensor_copy(logits[:], ps[:, 1, 0:NT * E1].rearrange("p (t e) -> p t e", t=NT)))
            step(nc.vector.tensor_reduce(ntop[:], logits[:], AX, ALU.max))
            step(nc.vector.tensor_scalar(ntop[:], ntop[:], -1.0, None, ALU.mult))
            dve.sem_inc(s["top_ready"], 1)
            dve.wait_ge(s["loaded"], 32)
            for t in range(NT):
                route(nc, step, gates[:, t], logits[:, t], before[:], over[:], same[:], rank[:, t], TOP1)
            dve.wait_ge(s["exp_done"], 1)
            for t in range(NT):
                step(nc.vector.scalar_tensor_tensor(out=gates[:, t], in0=rank[:, t], scalar=float(TOP1), in1=exps[:, t],
                                                    op0=ALU.is_lt, op1=ALU.mult))
            step(nc.vector.tensor_reduce(zsum[:], gates[:], AX, ALU.add))
            step(nc.vector.reciprocal(zsum[:], zsum[:]))
            for t in range(NT):
                step(nc.vector.tensor_scalar(gates[:, t], gates[:, t], zsum[:, t:t + 1], None, ALU.mult))

            def multiply(r, n):
                for half in range(2):
                    u = 2 * (RING1 * r + n) + half
                    dve.wait_ge(s["silu_done"], u + 1)
                    if half == 0:
                        dve.wait_ge(s["inner_used"], RING1 * r + n + 1)
                    ins = nc.vector.tensor_tensor(inner[:, n, 2 * half:2 * half + 2], act_in[:, half], in_ps[:, half, 1],
                                                  ALU.mult).then_inc(s["inner_done"], 1)
                    dve.wait_ge(s["inner_done"], u + 1)
                    dve.sem_inc(s["silu_used"], 1)

            def add(r, n):
                e = RING1 * r + n
                dve.wait_ge(s["out_mm"], e + 1)
                for t in range(NT):
                    dve.wait_ge(s["summed"], 2 * e + t + 3)
                    nc.vector.scalar_tensor_tensor(out=f.x[:, t], in0=out_ps[:, n, t], scalar=gates[:, t, bass.ds(e, 1)],
                                                   in1=f.x[:, t], op0=ALU.mult, op1=ALU.add).then_inc(s["summed"], 1)

            with dve.Fori(0, E1 // RING1) as r:
                for n in range(RING1):
                    multiply(r, n)
                    add(r, n)
            dve.wait_ge(s["summed"], 2 * E1 + 4)


def constants():
    c = {}
    c["c_ident"] = np.eye(P, dtype=np.float32)
    inv = np.exp(np.arange(D // 2, dtype=np.float32) * np.float32(-np.log(10000.0) / (D // 2 - 1)))
    st = np.arange(S2 - 1, -1, -1, dtype=np.float32)[None, :] * inv[:, None]
    c["c_sinusoids"] = np.concatenate([np.sin(st), np.cos(st)], 0).astype(np.float32)
    head = (np.arange(D) // DK)
    c["c_head_of"] = (head[:, None] == np.arange(H)[None, :]).astype(np.float32).reshape(KC, P, H).transpose(1, 0, 2)
    r = np.arange(P)
    c["c_gather"] = (r[:, None] % QUAD == np.arange(DV)[None, :]).astype(np.float32)
    inv = 1.0 / 10000.0 ** (np.arange(0, D, 2, dtype=np.float32) / D)
    ang = np.arange(S, dtype=np.float32)[:, None] * inv.astype(np.float32)
    c["c_rope"] = np.stack([np.cos(ang), np.sin(ang)]).astype(np.float32).reshape(2, NT, P, D // 2).transpose(2, 0, 1, 3)
    c["c_same_head"] = (head[:, None] == head[None, :]).astype(np.float32).reshape(KC, P, D).transpose(1, 0, 2)
    c["c_pos"] = np.broadcast_to(np.arange(S, dtype=np.float32), (P, S))
    q = np.arange(NT)[None, :, None] * P + np.arange(P)[:, None, None]
    c["c_causal"] = np.where(np.arange(S)[None, None, :] <= q, 0.0, -1e30).astype(np.float32)
    e = np.arange(E0)
    c["c_before31"] = (e[None, :] < e[:, None]).astype(np.float32).reshape(1, E0, E0)
    e = np.arange(E1)
    c["c_before8"] = (e[None, :] < e[:, None]).astype(np.float32).reshape(1, E1, E1)
    return {k: np.ascontiguousarray(v) for k, v in c.items()}


def columns(a):
    return np.ascontiguousarray(np.reshape(a, (-1, P)).T)


def lay_out(v):
    t = lambda a: np.ascontiguousarray(np.asarray(a).T)
    row = lambda a: np.ascontiguousarray(np.asarray(a).reshape(1, -1))
    col = lambda a: np.ascontiguousarray(np.asarray(a).reshape(-1, 1))
    a = {"x": np.asarray(v["x"]), "ctx_1024": t(np.asarray(v["ctx_1024"])[0])}
    for n in ("Wq", "Wk", "Wv", "Wo", "w1", "w2", "w3"):
        a[f"L0_xattn_{n}"] = t(v[f"L0_xattn_{n}"])
    for n in ("bq", "bk"):
        a[f"L0_xattn_{n}"] = columns(v[f"L0_xattn_{n}"])
    for n in ("bv", "bo", "b3"):
        a[f"L0_xattn_{n}"] = row(v[f"L0_xattn_{n}"])
    for n in ("b1", "b2"):
        a[f"L0_xattn_{n}"] = col(v[f"L0_xattn_{n}"])
    for n in ("Wq", "Wk", "Wv", "Wp", "Wo"):
        a[f"L1_xattn_{n}"] = np.asarray(v[f"L1_xattn_{n}"])
    for n in ("bk", "bp", "bq"):
        a[f"L1_xattn_{n}"] = columns(v[f"L1_xattn_{n}"])
    for n in ("bv", "bo"):
        a[f"L1_xattn_{n}"] = row(v[f"L1_xattn_{n}"])
    for n in "qkv":
        a[f"L0_attn_W{n}"] = t(v[f"L0_attn_W{n}"])
        a[f"L0_attn_b{n}"] = row(v[f"L0_attn_b{n}"])
    for n in ("gamma", "beta"):
        a[f"L0_attn_{n}"] = row(v[f"L0_attn_{n}"])
    n = "L0_ffn_"
    turned = lambda w: np.ascontiguousarray(np.asarray(w).reshape(-1, H // 4, 4, HD // 2, 2).transpose(0, 1, 4, 2, 3)
                                            ).reshape(-1, H * HD)
    a[n + "q_w"], a[n + "k_w"] = turned(v[n + "q_w"]), turned(v[n + "k_w"])
    a[n + "qk_b"] = np.ascontiguousarray(np.stack([columns(turned(v[n + b])) for b in ("q_b", "k_b")], 1))
    for m in ("v_w", "o_w", "router_w"):
        a[n + m] = np.asarray(v[n + m])
    for m in ("v_b", "o_b", "router_b", "gamma1", "gamma2"):
        a[n + m] = row(v[n + m])
    a[n + "theta"] = col(v[n + "theta"])
    both = lambda x, y: np.concatenate([np.asarray(x), np.asarray(y)[None]])
    w1 = both(v[n + "re_w1"], v[n + "sh_w1"]).reshape(EXPERTS0, KC, P, I0)
    w2 = both(v[n + "re_w2"], v[n + "sh_w2"]).reshape(EXPERTS0, I0 // P, P, D)
    b1 = both(v[n + "re_b1"], v[n + "sh_b1"]).reshape(EXPERTS0, I0 // P, P, 1)
    a[n + "e_w"] = np.ascontiguousarray(np.concatenate(
        [y.transpose(0, 2, 1, 3).reshape(EXPERTS0, P, -1) for y in (w1, w2, b1)], 2))
    a[n + "e_b2"] = both(v[n + "re_b2"], v[n + "sh_b2"])
    a["L1_xattn_bcols"] = np.ascontiguousarray(np.stack(
        [columns(v[f"L1_xattn_{m}"]) for m in ("bq", "r_w_bias", "r_r_bias")], 1))
    a["mask"] = np.asarray(v["mask_Bx1xSxS2_ff1"]).reshape(S, S2)
    for m in ("attn_Wq", "attn_Wkv", "attn_Wout", "ffn_w_gate", "ffn_w1", "ffn_w3", "ffn_w2"):
        a[f"L1_{m}"] = np.asarray(v[f"L1_{m}"])
    for m in ("norm_g", "out_norm_g"):
        a[f"L1_attn_{m}"] = row(v[f"L1_attn_{m}"])
    return a


LAYERS = [prologue, cross0, linear_attn, block0, cross1, multi_query, mixture1]


def run(f, layer):
    f.sems = []
    layer(f)
    f.nc.clear_and_free_semaphores(f.sems)
    f.nc.all_engine_barrier()


def build(nc, ins, out):
    with ExitStack() as ctx:
        f = Frame(nc, ctx, ins, out)
        f.key_parts = nc.dram_tensor("key_parts", (3, 3, D, S2), BF16, kind="Internal").ap()
        f.key_heads = f.key_parts.rearrange("m s (h d) n -> m s h d n", d=DK)
        f.query_parts = nc.dram_tensor("query_parts", (3, 3, D, S), BF16, kind="Internal").ap()
        f.value_rows = nc.dram_tensor("value_rows", (2, H, P, NCH, DV), F32, kind="Internal").ap()
        f.max_parts = nc.dram_tensor("max_parts", (3, H * S), BF16, kind="Internal").ap()
        f.rel_dram = nc.dram_tensor("rel_scores", (H, S * PITCH), F32, kind="Internal").ap()
        f.x = f.sb(ctx, "x", [P, NT, D])
        f.ident = f.sb(ctx, "ident", [P, P])
        f.ones = f.sb(ctx, "ones", [P, P])
        f.stats = f.sb(ctx, "stats", [P, NT, 6])
        f.mv = f.sb(ctx, "mv", [P, NT, 2])
        f.rstd = f.sb(ctx, "rstd", [P, NT])
        f.key_sums = f.sb(ctx, "key_sums", [P, KC, NHALF])
        for layer in LAYERS:
            run(f, layer)
        f.layer, f.sems = "end", []
        stored = f.sem("stored")
        block = ctx.enter_context(nc.Block())

        @block.sync
        def _(sp):
            sp.dma_start(out.rearrange("b (t p) d -> p (b t) d", p=P), f.x[:]).then_inc(stored, 16)
            sp.wait_ge(stored, 16)


def kernel(**inputs):
    import concourse.bacc as bacc
    from concourse.bass_utils import run_bass_kernel_spmd

    nc = bacc.Bacc("TRN2", target_bir_lowering=False, num_devices=1)
    arrays = {**lay_out(inputs), **constants()}
    ins = {n: nc.dram_tensor(f"in_{n}", a.shape, mybir.dt.from_np(a.dtype), kind="ExternalInput").ap()
           for n, a in arrays.items()}
    out = nc.dram_tensor("out_x", (1, S, D), F32, kind="ExternalOutput").ap()
    build(nc, ins, out)
    r = run_bass_kernel_spmd(nc, [{f"in_{n}": a for n, a in arrays.items()}], core_ids=[0])
    return r.results[0]["out_x"]
```

```python
from contextlib import ExitStack

import numpy as np

import concourse.bass as bass
from concourse import mybir

F32 = mybir.dt.float32
BF16 = mybir.dt.bfloat16
ALU = mybir.AluOpType
ACT = mybir.ActivationFunctionType
AX = mybir.AxisListType.X

P = 128
S = 256
D = 256
NT = S // P
KC = D // P
S2 = 4096
NCH = S2 // P
NHALF = 2
HALF = S2 // NHALF
H = 16
DK = D // H
DV = DK + 1
QUAD = 32
NQ4 = P // QUAD
QUARTER = S2 // 4
NQU = S2 // QUARTER
ROWS = 6 * DK
MAXROWS = ROWS + 3
BANK = 512
LOG_T_MIN, LOG_T_MAX = float(np.log(0.1)), float(np.log(10.0))
Q_PARTS = (0, 1, 2, 0, 1, 0)
K_TIMES = ((0, 3), (1, 2), (2, 1))
KEYS_IN = 16 * len(K_TIMES)


class Chain:

    def __init__(self, eng, sem, base=0):
        self.eng, self.sem, self.n, self.base = eng, sem, 0, base

    def __call__(self, ins):
        self.n += 1
        ins.then_inc(self.sem, 1)
        self.eng.wait_ge(self.sem, self.base + self.n)


class Frame:

    def __init__(self, nc, ctx, ins, out):
        self.nc, self.ctx, self.ins, self.out = nc, ctx, ins, out
        self.layer, self.sems = "", []

    def sb(self, ctx, name, shape, dt=F32):
        return ctx.enter_context(self.nc.sbuf_tensor(f"{self.layer}_{name}", shape, dt))

    def ps(self, ctx, name, shape, dt=F32):
        return ctx.enter_context(self.nc.psum_tensor(f"{self.layer}_{name}", shape, dt))

    def sem(self, name):
        self.sems.append(self.nc.alloc_semaphore(name=f"{self.layer}_{name}"))
        return self.sems[-1]


def rows_of(dram):
    return dram.rearrange("(c p) n -> p c n", p=P)


def load_key_parts(f, sp, dst, which, head, loaded):
    at = 0
    for part, times in K_TIMES:
        rows = times * DK
        src = f.key_heads[which, part, bass.ds(head, 1)].to_broadcast([times, DK, S2])
        sp.dma_start(dst[at:at + rows], src).then_inc(loaded, 16)
        at += rows


def layer_norm(f, dve, step, y, x, eps, var_ready, root_ready, n=0):
    nc = f.nc
    for t in range(NT):
        step(nc.vector.bn_stats(f.stats[:, t, :], x[:, t, :]))
        step(nc.vector.bn_aggr(f.mv[:, t, :], f.stats[:, t, :]))
    nc.vector.tensor_scalar(f.rstd[:], f.mv[:, :, 1], eps, None, ALU.add).then_inc(var_ready, 1)
    dve.wait_ge(root_ready, n + 1)
    step(nc.vector.reciprocal(f.rstd[:], f.rstd[:]))
    for t in range(NT):
        step(nc.vector.tensor_scalar(y[:, t, :], x[:, t, :], f.mv[:, t, 0:1], f.rstd[:, t:t + 1],
                                     ALU.subtract, ALU.mult))


def take_root(f, act, var_ready, root_ready, n=0):
    act.wait_ge(var_ready, n + 1)
    f.nc.scalar.sqrt(f.rstd[:], f.rstd[:]).then_inc(root_ready, 1)


def transpose_tokens(nc, out_ps, y, ident):
    for c in range(y.shape[2] // P):
        for t in range(NT):
            last = nc.tensor.transpose(out_ps[:, c, t * P:(t + 1) * P], y[:, t, c * P:(c + 1) * P], ident)
    return last


def cross0(f):
    nc, i = f.nc, f.ins
    f.layer = "xa"
    dve_small, parts_stored, q_loaded, k_free, kb_free = (
        f.sem(n) for n in ("dve_small", "parts_stored", "q_loaded", "k_free", "kb_free"))
    k_loaded = [f.sem(f"k_loaded{b}") for b in range(2)]
    kb_loaded = [f.sem(f"kb_loaded{b}") for b in range(2)]
    scoredT, probs_ready, probs_used, pv_done, pv_read = (
        f.sem(n) for n in ("scoredT", "probs_ready", "probs_used", "pv_done", "pv_read"))
    recip_done, sums_free = f.sem("recip_done"), f.sem("sums_free")
    small_loaded, later_loaded, sin_loaded = (f.sem(n) for n in ("small_loaded", "later_loaded", "sin_loaded"))
    with ExitStack() as ctx:
        wq = f.sb(ctx, "wq", [P, KC, D])
        wo = f.sb(ctx, "wo", [P, KC, D])
        bq = f.sb(ctx, "bq", [P, KC])
        bo = f.sb(ctx, "bo", [1, D])
        w1b = f.sb(ctx, "w1b", [P, 3, 64])
        w2 = f.sb(ctx, "w2", [64, 64])
        w3 = f.sb(ctx, "w3", [64, 1])
        w3b = f.sb(ctx, "w3b", [64, P])
        b1 = f.sb(ctx, "b1", [64, 1])
        b2 = f.sb(ctx, "b2", [64, 1])
        b3 = f.sb(ctx, "b3", [P, 1])
        head_of = f.sb(ctx, "head_of", [P, KC, H])
        xn = f.sb(ctx, "xn", [P, NT, D])
        xnT = f.sb(ctx, "xnT", [P, KC, S])
        q = f.sb(ctx, "q", [P, KC, S])
        qrest = f.sb(ctx, "qrest", [P, KC, S])
        qparts = f.sb(ctx, "qparts", [P, 3, KC, S], BF16)
        q_sums = f.sb(ctx, "q_sums", [P, KC])
        k_sums = f.sb(ctx, "k_sums", [P, KC])
        qk_sum = f.sb(ctx, "qk_sum", [P, KC, H])
        q96 = f.sb(ctx, "q96", [P, H, S], BF16)
        k96 = f.sb(ctx, "k96", [P, 2, S2], BF16)
        NU = NT * NQU
        stats_all = f.sb(ctx, "stats_all", [P, H, 3, NU])
        minima, zs, es = (stats_all[:, :, k] for k in range(3))
        m_all = f.sb(ctx, "m_all", [P, H, NT])
        wgt = f.sb(ctx, "wgt", [P, H, NU])
        z_all = f.sb(ctx, "z_all", [P, H, NT])
        e_all = f.sb(ctx, "e_all", [P, H, NT])
        mneg = f.sb(ctx, "mneg", [P, H * NT])
        mrow = f.sb(ctx, "mrow", [H * NT, P])
        mrest = f.sb(ctx, "mrest", [H * NT, P])
        mparts = f.sb(ctx, "mparts", [H * NT, 3, P], BF16)
        hid1 = f.sb(ctx, "hid1", [64, H])
        hid2 = f.sb(ctx, "hid2", [64, H])
        logt = f.sb(ctx, "logt", [P, H])
        tscale = f.sb(ctx, "tscale", [P, H + 2])
        t_now = f.sb(ctx, "t_now", [P, 2])
        bv = f.sb(ctx, "bv", [P, D])
        GC = 4
        NG = NCH // GC
        UNITS = H * NG
        attn = f.sb(ctx, "attn", [P, NT, H, DK])
        attnT = f.sb(ctx, "attnT", [P, KC, S])
        both_passes = ctx.enter_context(ExitStack())
        ctxT = f.sb(both_passes, "ctxT", [P, KC, S2])
        sinT = f.sb(both_passes, "sinT", [P, KC, S2])
        wk = f.sb(both_passes, "wk", [P, 3, KC, D])
        wv = f.sb(both_passes, "wv", [P, 2 * KC, KC, P])
        bcol = f.sb(both_passes, "bcol", [P, 3, KC])
        whole = f.sb(both_passes, "whole", [P, 2, QUARTER])
        rest = f.sb(both_passes, "rest", [P, QUARTER])
        parts = f.sb(both_passes, "parts", [P, 4, 3, QUARTER], BF16)
        key_groups = [(g, t) for g in range(NQU) for t in range(KC)]

        with ExitStack() as inner:
            s = {n: f.sem("a_" + n) for n in ("x_loaded", "q_w_loaded", "k_w_loaded", "var_ready", "root_ready", "dve_steps",
                                              "xn_ready", "xnT_mm", "xnT_sb", "q_mm", "q_read", "q_split", "projected",
                                              "evacuated", "rest_done", "second_done", "split_done", "ones_set")}
            ctx_loaded = [f.sem(f"a_ctx_loaded{g}") for g in range(NQU)]
            stored = [f.sem(f"a_stored{b}") for b in range(4)]
            block = inner.enter_context(nc.Block())
            ps = f.ps(inner, "a_ps", [P, 4, QUARTER])

            @block.sync
            def _(sp):
                sp.dma_start(f.x[:], i["x"].rearrange("b (t p) d -> p (b t) d", p=P)).then_inc(s["x_loaded"], 16)
                sp.dma_start(f.ident[:], i["c_ident"]).then_inc(s["x_loaded"], 16)
                sp.dma_start(wq[:], rows_of(i["L0_xattn_Wq"])).then_inc(s["q_w_loaded"], 16)
                sp.dma_start(bq[:], i["L0_xattn_bq"]).then_inc(s["q_w_loaded"], 16)
                sp.dma_start(wk[:, 0], rows_of(i["L0_xattn_Wk"])).then_inc(s["k_w_loaded"], 16)
                sp.dma_start(bcol[:, 0], i["L0_xattn_bk"]).then_inc(s["k_w_loaded"], 16)
                for g in range(NQU):
                    sp.dma_start(ctxT[:, :, g * QUARTER:(g + 1) * QUARTER],
                                 rows_of(i["ctx_1024"])[:, :, g * QUARTER:(g + 1) * QUARTER]).then_inc(ctx_loaded[g], 16)
                sp.wait_ge(s["q_split"], 1)
                for part in range(3):
                    sp.dma_start(f.query_parts[0, part].rearrange("(c p) n -> p c n", p=P),
                                 qparts[:, part]).then_inc(parts_stored, 16)
                sp.wait_ge(parts_stored, 48)
                for r, part in enumerate(Q_PARTS):
                    sp.dma_start(q96[r * DK:(r + 1) * DK], f.query_parts[0, part].rearrange("(h d) n -> d h n", d=DK)
                                 ).then_inc(q_loaded, 16)
                for n, name in enumerate(("L1_xattn_Wk", "L1_xattn_Wp")):
                    sp.dma_start(wk[:, 1 + n], rows_of(i[name])).then_inc(later_loaded, 16)
                for n, name in enumerate(("L1_xattn_bk", "L1_xattn_bp")):
                    sp.dma_start(bcol[:, 1 + n], i[name]).then_inc(later_loaded, 16)
                for m in range(2):
                    for t in range(KC):
                        sp.dma_start(wv[:, m * KC + t], rows_of(i[f"L{m}_xattn_Wv"])[:, :, t * P:(t + 1) * P]
                                     ).then_inc(later_loaded, 16)
                for n, (g, t) in enumerate(key_groups):
                    sp.wait_ge(s["split_done"], n + 1)
                    dst = f.key_parts[0, :, t * P:(t + 1) * P, g * QUARTER:(g + 1) * QUARTER]
                    sp.dma_start(dst.rearrange("s p n -> p s n"), parts[:, n % 4]).then_inc(stored[n % 4], 16)
                for b in range(4):
                    sp.wait_ge(stored[b], 16 * len(key_groups) // 4)
                sp.wait_ge(q_loaded, 96)

            @block.tensor
            def _(pe):
                pe.wait_ge(s["x_loaded"], 32)
                pe.wait_ge(s["xn_ready"], 1)
                flat = ps[:, 0, 0:KC * S].rearrange("p (c n) -> p c n", c=KC)
                transpose_tokens(nc, flat, xn, f.ident[:]).then_inc(s["xnT_mm"], 1)
                pe.wait_ge(s["q_w_loaded"], 32)
                pe.wait_ge(s["xnT_sb"], 1)
                for m in range(KC):
                    for c in range(KC):
                        mm = nc.tensor.matmul(ps[:, 1, m * S:(m + 1) * S], wq[:, c, m * P:(m + 1) * P], xnT[:, c, :],
                                              start=(c == 0), stop=(c == KC - 1))
                mm.then_inc(s["q_mm"], 1)
                pe.wait_ge(s["k_w_loaded"], 32)
                for n, (g, t) in enumerate(key_groups):
                    if t == 0:
                        pe.wait_ge(ctx_loaded[g], 16)
                    if n == 2:
                        pe.wait_ge(s["q_read"], 1)
                    if n >= 4:
                        pe.wait_ge(s["evacuated"], n - 3)
                    for k in range(QUARTER // BANK):
                        for c in range(KC):
                            at = g * QUARTER + k * BANK
                            mm = nc.tensor.matmul(ps[:, (n + 2) % 4, k * BANK:(k + 1) * BANK],
                                                  wk[:, 0, c, t * P:(t + 1) * P], ctxT[:, c, at:at + BANK],
                                                  start=(c == 0), stop=(c == KC - 1))
                    mm.then_inc(s["projected"], 1)

            @block.gpsimd
            def _(pool):
                nc.gpsimd.memset(k96[ROWS:MAXROWS], 1.0).then_inc(s["ones_set"], 1)
                pool.wait_ge(s["ones_set"], 1)

            @block.scalar
            def _(act):
                take_root(f, act, s["var_ready"], s["root_ready"])
                act.wait_ge(s["xnT_mm"], 1)
                nc.scalar.copy(xnT[:], ps[:, 0, 0:KC * S].rearrange("p (c n) -> p c n", c=KC)).then_inc(s["xnT_sb"], 1)
                act.wait_ge(s["k_w_loaded"], 32)
                for n, (g, t) in enumerate(key_groups):
                    act.wait_ge(s["projected"], n + 1)
                    if n >= 2:
                        act.wait_ge(s["split_done"], n - 1)
                    if n >= 4:
                        act.wait_ge(stored[n % 4], 16 * (n // 4))
                    nc.scalar.activation(whole[:, n % 2], ps[:, (n + 2) % 4], ACT.Identity, bias=bcol[:, 0, t:t + 1],
                                         accum_out=f.key_sums[:, t, g:g + 1])
                    nc.scalar.activation(parts[:, n % 4, 0], ps[:, (n + 2) % 4], ACT.Identity,
                                         bias=bcol[:, 0, t:t + 1]).then_inc(s["evacuated"], 1)

            @block.vector
            def _(dve):
                step = Chain(dve, s["dve_steps"])
                step(nc.vector.memset(f.ones[:], 1.0))
                dve.wait_ge(s["x_loaded"], 32)
                layer_norm(f, dve, step, xn, f.x, 1e-5, s["var_ready"], s["root_ready"])
                dve.sem_inc(s["xn_ready"], 1)
                dve.wait_ge(s["q_w_loaded"], 32)
                dve.wait_ge(s["q_mm"], 1)
                for m in range(KC):
                    step(nc.vector.tensor_scalar(q[:, m], ps[:, 1, m * S:(m + 1) * S], bq[:, m:m + 1], -DK ** -0.5,
                                                 ALU.add, ALU.mult))
                dve.sem_inc(s["q_read"], 1)
                step(nc.vector.tensor_copy(qparts[:, 0], q[:]))
                step(nc.vector.tensor_tensor(qrest[:], q[:], qparts[:, 0], ALU.subtract))
                step(nc.vector.tensor_copy(qparts[:, 1], qrest[:]))
                step(nc.vector.tensor_tensor(qparts[:, 2], qrest[:], qparts[:, 1], ALU.subtract))
                dve.sem_inc(s["q_split"], 1)
                step(nc.vector.tensor_reduce(q_sums[:], q[:], AX, ALU.add))
                for n in range(len(key_groups)):
                    dve.wait_ge(s["evacuated"], n + 1)
                    if n >= 1:
                        dve.wait_ge(s["split_done"], n)
                    nc.vector.tensor_tensor(rest[:], whole[:, n % 2], parts[:, n % 4, 0], ALU.subtract
                                            ).then_inc(s["rest_done"], 1)
                    dve.wait_ge(s["rest_done"], n + 1)
                    nc.vector.tensor_copy(parts[:, n % 4, 1], rest[:]).then_inc(s["second_done"], 1)
                    dve.wait_ge(s["second_done"], n + 1)
                    nc.vector.tensor_tensor(parts[:, n % 4, 2], rest[:], parts[:, n % 4, 1], ALU.subtract
                                            ).then_inc(s["split_done"], 1)

        with ExitStack() as inner:
            HPB = 2 * KC
            NB = H // HPB
            CPH = NCH // HPB
            SLOTS = NU + NU // 2
            exps = f.sb(inner, "exps", [P, 4, QUARTER])
            squares = f.sb(inner, "squares", [P, 2, QUARTER])
            stats = f.sb(inner, "stats", [P, 2, 3, NU])
            values = f.sb(inner, "values", [P, 2, H // 2, CPH, DV])
            s = {n: f.sem("b_" + n) for n in ("scored", "projected", "product_out", "min_ready", "exp_done", "even_squared",
                                              "odd_squared", "kept", "split_steps", "split_done",
                                              "ones_set", "squares_begun", "split_begun")}
            parts_out = [f.sem(f"b_parts_out{b}") for b in range(2)]
            values_stored = [f.sem(f"b_values_stored{b}") for b in range(2)]
            block = inner.enter_context(nc.Block())
            ps = f.ps(inner, "b_ps", [P, 4, QUARTER])

            def bodies(eng, body):
                body(0, True)
                with eng.Fori(1, NB) as it:
                    body(it, False)

            @block.sync
            def _(sp):
                key_stores = f.key_parts[:, :, :, :].rearrange("m s (t p) (g n) -> m t g p s n", p=P, g=NB)
                value_stores = f.value_rows.rearrange("m (t h) p k d -> (m t) p h k d", t=KC)
                sp.sem_inc(k_free, 2)

                def load_small():
                    small = [(wo[:], rows_of(i["L0_xattn_Wo"])), (bo[:], i["L0_xattn_bo"]),
                             (bv[:], i["L0_xattn_bv"].partition_broadcast(P)),
                             (w2[:], i["L0_xattn_w2"]), (w3[:], i["L0_xattn_w3"]),
                             (b1[:], i["L0_xattn_b1"]), (b2[:], i["L0_xattn_b2"]),
                             (b3[:], i["L0_xattn_b3"].partition_broadcast(P)), (head_of[:], i["c_head_of"]),
                             (w1b[:], i["L0_xattn_w1"].partition_broadcast(P))]
                    for dst, src in small:
                        sp.dma_start(dst, src).then_inc(small_loaded, 16)

                def store(it, c):
                    b = c % 2
                    sp.wait_ge(s["split_done"], HPB * it + c + 3)
                    sp.dma_start(key_stores[1 + c // KC, c % KC][bass.ds(it, 1)].rearrange("g p s n -> p (g s) n"),
                                 parts[:, b]).then_inc(parts_out[b], 16)
                    sp.wait_ge(s["product_out"], NU // 2 * (HPB * it + c + 2))
                    dst = value_stores[bass.ds(it, 1), :, :, c * CPH:(c + 1) * CPH, :]
                    sp.dma_start(dst.rearrange("m p h k d -> p (m h) k d"), values[:, b]).then_inc(values_stored[b], 16)

                def body(it, first):
                    for c in range(HPB):
                        sp.wait_ge(k_free, HPB * it + c + 1)
                        load_key_parts(f, sp, k96[0:ROWS, c % 2], 0, HPB * it + c, k_loaded[c % 2])
                        if first and c == 1:
                            for g in range(NQU):
                                sp.dma_start(sinT[:, :, g * QUARTER:(g + 1) * QUARTER],
                                             rows_of(i["c_sinusoids"])[:, :, g * QUARTER:(g + 1) * QUARTER]
                                             ).then_inc(sin_loaded, 16)
                            load_small()
                        if c >= 2:
                            store(it, c - 2)
                        elif not first:
                            store(it - 1, c - 2 + HPB)

                bodies(sp, body)
                for c in (HPB - 2, HPB - 1):
                    store(NB - 1, c)

            @block.tensor
            def _(pe):
                pe.wait_ge(later_loaded, 16 * (4 + 2 * KC))

                def buffer_free(h, slot):
                    h, slot = (h, slot - 4) if slot >= 4 else (h - 1, slot - 4 + SLOTS)
                    j, u = slot // 3, 2 * (slot // 3) + slot % 3
                    if slot % 3 == 2:
                        pe.wait_ge(s["product_out"], NU // 2 * (h + 1) + j + 1)
                    else:
                        pe.wait_ge(s["exp_done"], NU * (h + 1) + u + 1)

                def scores(it, c, u):
                    h, slot = HPB * it + c, u + u // 2
                    buffer_free(h, slot)
                    t, g = u // NQU, u % NQU
                    for k in range(QUARTER // BANK):
                        at = g * QUARTER + k * BANK
                        mm = nc.tensor.matmul(ps[:, slot % 4, k * BANK:(k + 1) * BANK],
                                              q96[0:ROWS, bass.ds(h, 1), t * P:(t + 1) * P],
                                              k96[0:ROWS, c % 2, at:at + BANK], start=True, stop=True)
                    mm.then_inc(s["scored"], 1)

                def product(it, c, j):
                    h, slot = HPB * it + c, 3 * j + 2
                    buffer_free(h, slot)
                    out = ps[:, slot % 4, 0:BANK]
                    if j < 2:
                        src = (ctxT, sinT)[c // KC]
                        if src is sinT and j == 0:
                            pe.wait_ge(sin_loaded, 16 * NQU)
                        for k in range(KC):
                            mm = nc.tensor.matmul(out, wk[:, 1 + c // KC, k, c % KC * P:(c % KC + 1) * P],
                                                  src[:, k, bass.ds(it * QUARTER + j * BANK, BANK)],
                                                  start=(k == 0), stop=(k == KC - 1))
                    else:
                        for n in range(CPH // 2):
                            at = (c * CPH + (j - 2) * CPH // 2 + n) * P
                            for k in range(KC):
                                mm = nc.tensor.matmul(out[:, n * P:(n + 1) * P], ctxT[:, k, at:at + P],
                                                      wv[:, bass.ds(it, 1), k, :], start=(k == 0), stop=(k == KC - 1))
                    mm.then_inc(s["projected"], 1)

                with pe.Fori(0, NB) as it:
                    for c in range(HPB):
                        pe.wait_ge(k_loaded[c % 2], KEYS_IN * (it * HPB // 2 + c // 2 + 1))
                        for j in range(NU // 2):
                            scores(it, c, 2 * j)
                            scores(it, c, 2 * j + 1)
                            product(it, c, j)
                        pe.wait_ge(s["scored"], (HPB * it + c + 1) * NU)
                        pe.sem_inc(k_free, 1)

            @block.scalar
            def _(act):
                act.sem_inc(s["exp_done"], NU)
                act.sem_inc(s["product_out"], NU // 2)
                act.sem_inc(s["even_squared"], 2)
                act.wait_ge(s["ones_set"], 1)

                def exponential(it, c, u):
                    h, slot = HPB * it + c, u + u // 2
                    act.wait_ge(s["min_ready"], NU * h + u + 1)
                    act.wait_ge(s["odd_squared" if u % 2 else "even_squared"], NU // 2 * h + u // 2 + 1)
                    act.nop()
                    nc.scalar.activation(exps[:, u % 4], ps[:, slot % 4], ACT.Exp, scale=-1.0,
                                         bias=stats[:, c % 2, 0, u:u + 1], accum_out=stats[:, c % 2, 1, u:u + 1]
                                         ).then_inc(s["exp_done"], 1)

                def square(it, c, u):
                    h = HPB * it + c
                    act.wait_ge(s["exp_done"], NU * (h + 1) + u + 1)
                    act.wait_ge(s["even_squared"], NU // 2 * h + u // 2 + 2)
                    act.nop()
                    nc.scalar.activation(squares[:, 0], exps[:, u % 4], ACT.Square,
                                         accum_out=stats[:, c % 2, 2, u:u + 1]).then_inc(s["even_squared"], 1)

                def product_out(it, c, j):
                    h, slot = HPB * it + c, 3 * j + 2
                    act.wait_ge(s["projected"], NU // 2 * h + j + 1)
                    src = ps[:, slot % 4, 0:BANK]
                    if j < 2:
                        if j == 0:
                            act.wait_ge(s["split_done"], h + 1)
                        act.nop()
                        nc.scalar.activation(whole[:, c % 2, j * BANK:(j + 1) * BANK], src, ACT.Identity,
                                             bias=bcol[:, 1 + c // KC, c % KC:c % KC + 1]).then_inc(s["product_out"], 1)
                    else:
                        if j == 2:
                            act.wait_ge(values_stored[c % 2], 16 * (it * HPB // 2 + c // 2 + 1))
                        half = CPH // 2
                        dst = values[:, c % 2, :, (j - 2) * half:(j - 1) * half, 0:DK]
                        act.nop()
                        nc.scalar.copy(dst, src.rearrange("p (k h d) -> p h k d", k=half, h=H // 2)
                                       ).then_inc(s["product_out"], 1)

                with act.Fori(0, NB) as it:
                    for c in range(HPB):
                        act.wait_ge(s["kept"], HPB * it + c + 1)
                        for j in range(NU // 2):
                            exponential(it, c, 2 * j)
                            exponential(it, c, 2 * j + 1)
                            square(it, c, 2 * j)
                            product_out(it, c, j)

            @block.vector
            def _(dve):
                nc.vector.memset(values[:, :, :, :, DK:DV], 1.0).then_inc(s["ones_set"], 1)
                dve.sem_inc(s["odd_squared"], 2)
                dve.sem_inc(s["kept"], 2)

                def minimum(it, c, u):
                    h, slot = HPB * it + c, u + u // 2
                    dve.wait_ge(s["scored"], NU * h + u + 1)
                    nc.vector.tensor_reduce(stats[:, c % 2, 0, u:u + 1], ps[:, slot % 4], AX, ALU.min
                                            ).then_inc(s["min_ready"], 1)

                def square(it, c, u):
                    h = HPB * it + c
                    dve.wait_ge(s["exp_done"], NU * (h + 1) + u + 1)
                    dve.wait_ge(s["odd_squared"], NU // 2 * h + u // 2 + 2)
                    dve.sem_inc(s["squares_begun"], 1)
                    nc.vector.tensor_tensor_reduce(out=squares[:, 1], in0=exps[:, u % 4], in1=exps[:, u % 4], scale=1.0,
                                                   scalar=0.0, op0=ALU.mult, op1=ALU.add,
                                                   accum_out=stats[:, c % 2, 2, u:u + 1]).then_inc(s["odd_squared"], 1)

                def keep(it, c):
                    h = HPB * it + c
                    """Keeps the statistics of a head when all are there."""
                    dve.wait_ge(s["odd_squared"], NU // 2 * (h + 1) + 2)
                    dve.wait_ge(s["even_squared"], NU // 2 * (h + 1) + 2)
                    dve.wait_ge(s["exp_done"], NU * (h + 2))
                    nc.vector.tensor_scalar(stats_all[:, bass.ds(h, 1)].rearrange("p h k u -> p (h k) u"), stats[:, c % 2],
                                            1.0, None, ALU.mult).then_inc(s["kept"], 1)

                def body(it, first):
                    for c in range(HPB):
                        dve.wait_ge(s["kept"], HPB * it + c + 1)
                        for j in range(NU // 2):
                            minimum(it, c, 2 * j)
                            if j > 0:
                                square(it, c, 2 * j - 1)
                            elif c > 0:
                                square(it, c - 1, NU - 1)
                            elif not first:
                                square(it - 1, HPB - 1, NU - 1)
                            minimum(it, c, 2 * j + 1)
                            if j == 1 and c > 0:
                                keep(it, c - 1)
                            elif j == 1 and not first:
                                keep(it - 1, HPB - 1)

                bodies(dve, body)
                square(NB - 1, HPB - 1, NU - 1)
                keep(NB - 1, HPB - 1)
                dve.wait_ge(s["kept"], H + 2)

            @block.gpsimd
            def _(pool):
                pool.sem_inc(s["split_done"], 2)
                for b in range(2):
                    pool.sem_inc(parts_out[b], 16)
                    pool.sem_inc(values_stored[b], 16)

                def split(it, c):
                    h, b = HPB * it + c, c % 2
                    pool.wait_ge(s["product_out"], NU // 2 * (h + 1) + 2)
                    pool.wait_ge(parts_out[b], 16 * (it * HPB // 2 + c // 2 + 1))
                    steps = [lambda: nc.gpsimd.tensor_scalar(parts[:, b, 0], whole[:, b], 1.0, None, ALU.mult),
                             lambda: nc.gpsimd.tensor_tensor(rest[:], whole[:, b], parts[:, b, 0], ALU.subtract),
                             lambda: nc.gpsimd.tensor_scalar(parts[:, b, 1], rest[:], 1.0, None, ALU.mult),
                             lambda: nc.gpsimd.tensor_tensor(parts[:, b, 2], rest[:], parts[:, b, 1], ALU.subtract)]
                    for n, piece in enumerate(steps):
                        pool.sem_inc(s["split_begun"], 1)
                        piece().then_inc(s["split_steps"], 1)
                        pool.wait_ge(s["split_steps"], len(steps) * h + n + 1)
                    pool.sem_inc(s["split_done"], 1)

                with pool.Fori(0, NB) as it:
                    for c in range(HPB):
                        split(it, c)

        both_passes.close()

        with ExitStack() as inner:
            block = inner.enter_context(nc.Block())
            small = f.ps(inner, "small", [P, 4, BANK])
            featured, hid_mm, hid_act, t_mm, t_ready = (f.sem(n) for n in ("featured", "hid_mm", "hid_act", "t_mm", "t_ready"))
            m_T, m_split, m_stored, m_loaded, w_in, w_out, w3_set = (
                f.sem(n) for n in ("m_T", "m_split", "m_stored", "m_loaded", "w_in", "w_out", "w3_set"))
            dve_steps2 = f.sem("dve_steps2")

            @block.sync
            def _(sp):
                sp.wait_ge(m_split, 1)
                sp.dma_start(f.max_parts.rearrange("s (r p) -> r s p", p=P), mparts[:]).then_inc(m_stored, 16)
                sp.wait_ge(m_stored, 16)
                sp.dma_start(q96[ROWS:MAXROWS], f.max_parts.rearrange("s (h n) -> s h n", h=H)).then_inc(m_loaded, 16)
                sp.wait_ge(m_loaded, 16)
                for b in range(2):
                    sp.wait_ge(parts_out[b], 16 * H // 2 + 16)
                    sp.wait_ge(values_stored[b], 16 * H // 2 + 16)

            @block.vector
            def _(dve):
                step = Chain(dve, dve_steps2)
                dve.wait_ge(small_loaded, 160)
                step(nc.vector.tensor_scalar(w3b[:], f.ident[0:64, :], 0.0, w3[:, 0:1], ALU.mult, ALU.add))
                dve.sem_inc(w3_set, 1)
                quarters = lambda y: y.rearrange("p h (t a) -> p h t a", a=NQU)
                step(nc.vector.tensor_reduce(m_all[:], quarters(minima), AX, ALU.min))
                step(nc.vector.tensor_scalar(mneg[:], m_all[:].rearrange("p h t -> p (h t)"), -1.0, None, ALU.mult))
                dve.sem_inc(m_T, 1)
                for a in range(NQU):
                    step(nc.vector.tensor_tensor(quarters(wgt[:])[:, :, :, a], m_all[:], quarters(minima)[:, :, :, a],
                                                 ALU.subtract))
                dve.sem_inc(w_in, 1)
                dve.wait_ge(w_out, 1)
                step(nc.vector.tensor_tensor(zs, zs, wgt[:], ALU.mult))
                step(nc.vector.tensor_tensor(es, es, wgt[:], ALU.mult))
                step(nc.vector.tensor_tensor(es, es, wgt[:], ALU.mult))
                step(nc.vector.tensor_reduce(z_all[:], quarters(zs), AX, ALU.add))
                step(nc.vector.tensor_reduce(e_all[:], quarters(es), AX, ALU.add))
                step(nc.vector.reciprocal(z_all[:], z_all[:]))
                step(nc.vector.tensor_tensor(e_all[:], e_all[:], z_all[:], ALU.mult))
                step(nc.vector.tensor_tensor(e_all[:], e_all[:], z_all[:], ALU.mult))
                step(nc.vector.tensor_scalar(e_all[:], e_all[:], 1.0 / S2, 1.0 / ((S2 - 1) * S), ALU.subtract, ALU.mult))
                step(nc.vector.tensor_scalar(m_all[:], m_all[:], -1.0 / S, None, ALU.mult))
                step(nc.vector.tensor_reduce(k_sums[:], f.key_sums[:], AX, ALU.add))
                step(nc.vector.tensor_tensor(k_sums[:], k_sums[:], q_sums[:], ALU.mult))
                step(nc.vector.tensor_scalar(k_sums[:], k_sums[:], -1.0 / S / S2, None, ALU.mult))
                for c in range(KC):
                    step(nc.vector.tensor_scalar(qk_sum[:, c], head_of[:, c], k_sums[:, c:c + 1], None, ALU.mult))
                dve.sem_inc(featured, 1)
                dve.wait_ge(m_T, 2)
                step(nc.vector.tensor_copy(mrow[:], small[0:H * NT, 3, 0:P]))
                step(nc.vector.tensor_copy(mparts[:, 0], mrow[:]))
                step(nc.vector.tensor_tensor(mrest[:], mrow[:], mparts[:, 0], ALU.subtract))
                step(nc.vector.tensor_copy(mparts[:, 1], mrest[:]))
                step(nc.vector.tensor_tensor(mparts[:, 2], mrest[:], mparts[:, 1], ALU.subtract))
                dve.sem_inc(m_split, 1)
                dve.wait_ge(t_mm, 1)
                step(nc.vector.tensor_scalar(logt[:], small[:, 2, 0:H], b3[:, 0:1], LOG_T_MIN, ALU.add, ALU.max))
                step(nc.vector.tensor_scalar(logt[:], logt[:], LOG_T_MAX, None, ALU.min))
                dve.sem_inc(t_ready, 1)
                dve.wait_ge(t_ready, 2)
                step(nc.vector.tensor_scalar(tscale[:, 0:H], tscale[:, 0:H], -2.0, None, ALU.mult))
                step(nc.vector.memset(tscale[:, H:H + 2], 1.0))

            @block.scalar
            def _(act):
                act.wait_ge(small_loaded, 160)
                act.wait_ge(w_in, 1)
                nc.scalar.activation(wgt[:], wgt[:], ACT.Exp).then_inc(w_out, 1)
                act.wait_ge(hid_mm, 1)
                nc.scalar.activation(hid1[:], small[0:64, 0, 0:H], ACT.Gelu, bias=b1[:, 0:1]).then_inc(hid_act, 1)
                act.wait_ge(hid_mm, 2)
                nc.scalar.activation(hid2[:], small[0:64, 1, 0:H], ACT.Gelu, bias=b2[:, 0:1]).then_inc(hid_act, 1)
                act.wait_ge(t_ready, 1)
                nc.scalar.activation(tscale[:, 0:H], logt[:], ACT.Exp, scale=-1.0).then_inc(t_ready, 1)

            @block.tensor
            def _(pe):
                pe.wait_ge(small_loaded, 160)
                pe.wait_ge(m_T, 1)
                nc.tensor.transpose(small[0:H * NT, 3, 0:P], mneg[:], f.ident[:]).then_inc(m_T, 1)
                pe.wait_ge(featured, 1)
                pairs = [(w1b[:, 0], qk_sum[:, c]) for c in range(KC)]
                pairs += [(w1b[:, 1], m_all[:, :, t]) for t in range(NT)]
                pairs += [(w1b[:, 2], e_all[:, :, t]) for t in range(NT)]
                for n, (a, b) in enumerate(pairs):
                    mm = nc.tensor.matmul(small[0:64, 0, 0:H], a, b, start=(n == 0), stop=(n == len(pairs) - 1))
                mm.then_inc(hid_mm, 1)
                pe.wait_ge(hid_act, 1)
                nc.tensor.matmul(small[0:64, 1, 0:H], w2[:], hid1[:], start=True, stop=True).then_inc(hid_mm, 1)
                pe.wait_ge(hid_act, 2)
                pe.wait_ge(w3_set, 1)
                nc.tensor.matmul(small[:, 2, 0:H], w3b[:], hid2[:], start=True, stop=True).then_inc(t_mm, 1)

        with ExitStack() as inner:
            block = inner.enter_context(nc.Block())
            probs = f.sb(inner, "probs", [P, 4, GC, S])
            rz = f.sb(inner, "rz", [P, 2, NT])
            vhead = f.sb(inner, "vhead", [P, 2, NCH, DV])
            gather = f.sb(inner, "gather", [P, DV])
            sumsT = f.sb(inner, "sumsT", [P, 2, S])
            ps = f.ps(inner, "psT", [P, 2, GC * S])
            sums = f.ps(inner, "sums", [P, 2, BANK])
            both = f.ps(inner, "both", [P, 2 * NT, QUAD])
            out_T, out_sb, out_mm, out_ready = f.sem("out_T"), f.sem("out_sb"), f.sem("out_mm"), f.sem("out_ready")
            t_now_ready, sums_sb, gathered, zeroed = (f.sem(n) for n in ("t_now_ready", "sums_sb", "gathered", "zeroed"))
            g_loaded = f.sem("g_loaded")

            @block.sync
            def _(sp):
                sp.dma_start(gather[:], i["c_gather"]).then_inc(g_loaded, 16)
                with sp.Fori(0, H // 2) as pair:
                    for b in range(2):
                        sp.wait_ge(kb_free, 2 * pair + b + 1)
                        load_key_parts(f, sp, k96[0:ROWS, b], 0, 2 * pair + b, kb_loaded[b])
                        sp.dma_start(vhead[:, b:b + 1], f.value_rows[0, bass.ds(2 * pair + b, 1)].rearrange(
                            "h p k d -> p h k d")).then_inc(kb_loaded[b], 16)

            @block.tensor
            def _(pe):
                pe.sem_inc(kb_free, 2)
                pe.wait_ge(g_loaded, 16)
                pe.wait_ge(zeroed, 1)

                def weigh(head, b, g, n):
                    for c in range(GC):
                        mm = nc.tensor.matmul(sums[c * QUAD:c * QUAD + DV, b, 0:S], vhead[:, b, g * GC + c, :],
                                              probs[:, g % 4, c, :], start=(g == 0), stop=(g == NG - 1))
                    mm.then_inc(probs_used, 1)
                    if g == NG - 1:
                        pe.wait_ge(probs_used, n + 5)
                        pe.sem_inc(pv_done, 1)
                        pe.sem_inc(kb_free, 1)

                def bring_together(head, b):
                    pe.wait_ge(sums_sb, head + 1)
                    pe.wait_ge(pv_read, head + 1)
                    for t in range(NT):
                        mm = nc.tensor.matmul(both[:, NT * b + t, 0:DV], sumsT[:, b, t * P:(t + 1) * P], gather[:],
                                              start=True, stop=True)
                    mm.then_inc(gathered, 1)

                def heads(pair, first):
                    for b in range(2):
                        head = 2 * pair + b
                        pe.wait_ge(kb_loaded[b], (KEYS_IN + 16) * (pair + 1))
                        for g in range(NG):
                            n = head * NG + g
                            pe.wait_ge(probs_ready, n + 1)
                            for c in range(GC):
                                at = (g * GC + c) * P
                                mm = nc.tensor.matmul(ps[:, g % 2, c * S:(c + 1) * S], k96[0:MAXROWS, b, at:at + P],
                                                      q96[0:MAXROWS, bass.ds(head, 1), :], start=True, stop=True)
                            mm.then_inc(scoredT, 1)
                            if g >= 2:
                                if g == 2:
                                    pe.wait_ge(sums_free, head + 1)
                                weigh(head, b, g - 2, n - 2)
                            elif not (first and b == 0):
                                weigh(head - 1, 1 - b, NG + g - 2, n - 2)
                            if g == 3 and not (first and b == 0):
                                bring_together(head - 1, 1 - b)

                heads(0, True)
                with pe.Fori(1, H // 2) as pair:
                    heads(pair, False)
                for g in (NG - 2, NG - 1):
                    pe.wait_ge(probs_ready, UNITS - NG + g + 3)
                    weigh(H - 1, 1, g, UNITS - NG + g)
                bring_together(H - 1, 1)
                pe.wait_ge(out_T, 1)
                flat = ps[:, 0, 0:KC * S].rearrange("p (c n) -> p c n", c=KC)
                attn_rows = attn[:].rearrange("p t h d -> p t (h d)")
                transpose_tokens(nc, flat, attn_rows, f.ident[:]).then_inc(out_T, 1)
                pe.wait_ge(out_sb, 1)
                for t in range(NT):
                    out = ps[:, 1, t * D:(t + 1) * D]
                    for c in range(KC):
                        nc.tensor.matmul(out, attnT[:, c, t * P:(t + 1) * P], wo[:, c, :], start=(c == 0), stop=False)
                    mm = nc.tensor.matmul(out, f.ones[0:1, :], bo[:], start=False, stop=True)
                mm.then_inc(out_mm, 1)

            @block.scalar
            def _(act):
                act.sem_inc(probs_ready, 2)
                with act.Fori(0, H // 2) as pair:
                    for b in range(2):
                        act.wait_ge(t_now_ready, 2 * pair + b + 1)
                        for g in range(NG):
                            n = (2 * pair + b) * NG + g
                            act.wait_ge(scoredT, n + 1)
                            act.wait_ge(probs_used, n + 1)
                            nc.scalar.activation(probs[:, g % 4].rearrange("p c n -> p (c n)"), ps[:, g % 2], ACT.Exp,
                                                 scale=t_now[:, b:b + 1]).then_inc(probs_ready, 1)
                act.wait_ge(out_T, 2)
                nc.scalar.copy(attnT[:], ps[:, 0, 0:KC * S].rearrange("p (c n) -> p c n", c=KC)).then_inc(out_sb, 1)

            @block.vector
            def _(dve):
                nc.vector.memset(sums[:], 0.0).then_inc(zeroed, 1)
                dve.sem_inc(probs_used, 4)
                dve.sem_inc(pv_read, 2)
                dve.sem_inc(sums_free, 2)
                nc.vector.tensor_copy(t_now[:], tscale[:, 0:2]).then_inc(t_now_ready, 2)
                with dve.Fori(0, H // 2) as pair:
                    for b in range(2):
                        head = 2 * pair + b
                        dve.wait_ge(pv_done, head + 1)
                        nc.vector.tensor_scalar(t_now[:, b:b + 1], tscale[:, bass.ds(head + 2, 1)], 1.0, None, ALU.mult
                                                ).then_inc(t_now_ready, 1)
                        nc.vector.tensor_copy(sumsT[:, b], sums[:, b, 0:S]).then_inc(sums_sb, 1)
                        dve.wait_ge(sums_sb, head + 1)
                        dve.sem_inc(sums_free, 1)
                        dve.wait_ge(gathered, head + 1)
                        nc.vector.reciprocal(rz[:, b], both[:, NT * b:NT * (b + 1), DK]).then_inc(recip_done, 1)
                        dve.wait_ge(recip_done, head + 1)
                        for t in range(NT):
                            ins = nc.vector.tensor_scalar(attn[:, t, bass.ds(head, 1), :], both[:, NT * b + t, 0:DK],
                                                          rz[:, b, t:t + 1], None, ALU.mult)
                        ins.then_inc(pv_read, 1)
                dve.wait_ge(pv_read, H + 2)
                nc.vector.tensor_tensor(attn[:], attn[:], bv[:].rearrange("p (h d) -> p h d", h=H).unsqueeze(1)
                                        .to_broadcast([P, NT, H, DK]), ALU.add).then_inc(pv_read, 1)
                dve.wait_ge(pv_read, H + 3)
                dve.sem_inc(out_T, 1)
                dve.wait_ge(out_mm, 1)
                nc.vector.tensor_tensor(f.x[:], f.x[:], ps[:, 1, 0:NT * D].rearrange("p (t n) -> p t n", t=NT),
                                        ALU.add).then_inc(out_ready, 1)
                dve.wait_ge(out_ready, 1)


def linear_attn(f):
    nc, i = f.nc, f.ins
    f.layer = "la"
    s = {n: f.sem(n) for n in ("loaded", "var_ready", "root_ready", "dve_steps", "pool_steps", "z_ready", "zT_mm",
                               "zT_sb", "q_mm", "k_mm", "v_mm", "q_gelu", "k_gelu", "v_sb", "k_ready", "mean_mm",
                               "krot_ready", "kv_mm", "kv_masked", "qrot_ready", "qT_mm", "qT_sb", "out_mm")}
    with ExitStack() as ctx:
        w = f.sb(ctx, "w", [P, 3, KC, D])
        b = f.sb(ctx, "b", [1, 3, D])
        gain = f.sb(ctx, "gain", [P, 2, D])
        rope = f.sb(ctx, "rope", [P, 2, NT, D // 2])
        same_head = f.sb(ctx, "same_head", [P, KC, D])
        z = f.sb(ctx, "z", [P, NT, D])
        zT = f.sb(ctx, "zT", [P, KC, S])
        q, k, v = (f.sb(ctx, n, [P, NT, D]) for n in "qkv")
        qr, kr = (f.sb(ctx, n, [P, NT, D]) for n in ("qr", "kr"))
        tq, tk = (f.sb(ctx, n, [P, NT, D // 2]) for n in ("tq", "tk"))
        qrT = f.sb(ctx, "qrT", [P, KC, S])
        kv = f.sb(ctx, "kv", [P, KC, D])
        prod = f.sb(ctx, "prod", [P, NT, D])
        den = f.sb(ctx, "den", [P, NT, H])
        res = f.sb(ctx, "res", [P, NT, D])
        ps = f.ps(ctx, "ps", [P, 8, BANK])
        tiles = lambda n: ps[:, n].rearrange("p (t n) -> p t n", t=NT)
        block = ctx.enter_context(nc.Block())

        @block.sync
        def _(sp):
            loads = [(w[:, n], rows_of(i[f"L0_attn_W{c}"])) for n, c in enumerate("qkv")]
            loads += [(b[:, n], i[f"L0_attn_b{c}"]) for n, c in enumerate("qkv")]
            loads += [(gain[:, n], i[f"L0_attn_{c}"].partition_broadcast(P)) for n, c in enumerate(("gamma", "beta"))]
            loads += [(rope[:], i["c_rope"]), (same_head[:], i["c_same_head"])]
            for dst, src in loads:
                sp.dma_start(dst, src).then_inc(s["loaded"], 16)

        @block.tensor
        def _(pe):
            pe.wait_ge(s["z_ready"], 1)
            transpose_tokens(nc, tiles(0), z, f.ident[:]).then_inc(s["zT_mm"], 1)
            pe.wait_ge(s["loaded"], 160)
            pe.wait_ge(s["zT_sb"], 1)
            for m, done in enumerate(("q_mm", "k_mm", "v_mm")):
                for t in range(NT):
                    out = tiles(1 + m)[:, t]
                    for c in range(KC):
                        nc.tensor.matmul(out, zT[:, c, t * P:(t + 1) * P], w[:, m, c, :], start=(c == 0), stop=False)
                    mm = nc.tensor.matmul(out, f.ones[0:1, :], b[:, m, :], start=False, stop=True)
                mm.then_inc(s[done], 1)
            pe.wait_ge(s["k_ready"], 1)
            for t in range(NT):
                mm = nc.tensor.matmul(ps[:, 4, 0:D], f.ones[:], k[:, t, :], start=(t == 0), stop=(t == NT - 1))
            mm.then_inc(s["mean_mm"], 1)
            pe.wait_ge(s["krot_ready"], 1)
            pe.wait_ge(s["v_sb"], 1)
            for c in range(KC):
                for t in range(NT):
                    mm = nc.tensor.matmul(tiles(5)[:, c], kr[:, t, c * P:(c + 1) * P], v[:, t, :],
                                          start=(t == 0), stop=(t == NT - 1))
            mm.then_inc(s["kv_mm"], 1)
            pe.wait_ge(s["qrot_ready"], 1)
            transpose_tokens(nc, tiles(6), qr, f.ident[:]).then_inc(s["qT_mm"], 1)
            pe.wait_ge(s["qT_sb"], 1)
            pe.wait_ge(s["kv_masked"], 1)
            for t in range(NT):
                for c in range(KC):
                    mm = nc.tensor.matmul(tiles(7)[:, t], qrT[:, c, t * P:(t + 1) * P], kv[:, c, :],
                                          start=(c == 0), stop=(c == KC - 1))
            mm.then_inc(s["out_mm"], 1)

        @block.scalar
        def _(act):
            take_root(f, act, s["var_ready"], s["root_ready"])
            act.wait_ge(s["zT_mm"], 1)
            nc.scalar.copy(zT[:], tiles(0)).then_inc(s["zT_sb"], 1)
            act.wait_ge(s["q_mm"], 1)
            nc.scalar.activation(q[:], tiles(1), ACT.Gelu).then_inc(s["q_gelu"], 1)
            act.wait_ge(s["k_mm"], 1)
            nc.scalar.activation(k[:], tiles(2), ACT.Gelu).then_inc(s["k_gelu"], 1)
            act.wait_ge(s["v_mm"], 1)
            nc.scalar.copy(v[:], tiles(3)).then_inc(s["v_sb"], 1)
            act.wait_ge(s["qT_mm"], 1)
            nc.scalar.copy(qrT[:], tiles(6)).then_inc(s["qT_sb"], 1)
            take_root(f, act, s["var_ready"], s["root_ready"], 1)

        def rotate(eng, step, out, a, tmp):
            o, p = (y[:].rearrange("p t (n two) -> p t n two", two=2) for y in (out, a))
            cos, sin = rope[:, 0], rope[:, 1]
            step(eng.tensor_tensor(o[:, :, :, 0], p[:, :, :, 0], cos, ALU.mult))
            step(eng.tensor_tensor(tmp[:], p[:, :, :, 1], sin, ALU.mult))
            step(eng.tensor_tensor(o[:, :, :, 0], o[:, :, :, 0], tmp[:], ALU.subtract))
            step(eng.tensor_tensor(o[:, :, :, 1], p[:, :, :, 1], cos, ALU.mult))
            step(eng.tensor_tensor(tmp[:], p[:, :, :, 0], sin, ALU.mult))
            step(eng.tensor_tensor(o[:, :, :, 1], o[:, :, :, 1], tmp[:], ALU.add))

        @block.gpsimd
        def _(pool):
            step = Chain(pool, s["pool_steps"])
            pool.wait_ge(s["loaded"], 160)
            pool.wait_ge(s["k_gelu"], 1)
            step(nc.gpsimd.tensor_scalar(k[:], k[:], 0.21, None, ALU.add))
            pool.sem_inc(s["k_ready"], 1)
            rotate(nc.gpsimd, step, kr, k, tk)
            pool.sem_inc(s["krot_ready"], 1)

        @block.vector
        def _(dve):
            step = Chain(dve, s["dve_steps"])
            layer_norm(f, dve, step, z, f.x, 1e-5, s["var_ready"], s["root_ready"])
            dve.sem_inc(s["z_ready"], 1)
            dve.wait_ge(s["loaded"], 160)
            dve.wait_ge(s["q_gelu"], 1)
            step(nc.vector.tensor_scalar(q[:], q[:], 0.21, None, ALU.add))
            rotate(nc.vector, step, qr, q, tq)
            dve.sem_inc(s["qrot_ready"], 1)
            dve.wait_ge(s["mean_mm"], 1)
            for t in range(NT):
                step(nc.vector.tensor_tensor(prod[:, t], q[:, t], ps[:, 4, 0:D], ALU.mult))
            heads = prod[:].rearrange("p t (h d) -> p t h d", h=H)
            step(nc.vector.tensor_reduce(den[:], heads, AX, ALU.add))
            step(nc.vector.tensor_scalar(den[:], den[:], 1.0 / S, 1e-6, ALU.mult, ALU.add))
            step(nc.vector.reciprocal(den[:], den[:]))
            dve.wait_ge(s["kv_mm"], 1)
            step(nc.vector.scalar_tensor_tensor(out=kv[:], in0=tiles(5), scalar=1.0 / S, in1=same_head[:],
                                                op0=ALU.mult, op1=ALU.mult))
            dve.sem_inc(s["kv_masked"], 1)
            dve.wait_ge(s["out_mm"], 1)
            for t in range(NT):
                step(nc.vector.tensor_tensor(res[:, t].rearrange("p (h d) -> p h d", h=H),
                                             tiles(7)[:, t].rearrange("p (h d) -> p h d", h=H),
                                             den[:, t].unsqueeze(2).to_broadcast([P, H, DK]), ALU.mult))
            step(nc.vector.tensor_tensor(res[:], res[:], z[:], ALU.add))
            layer_norm(f, dve, step, prod, res, 1e-12, s["var_ready"], s["root_ready"], 1)
            for t in range(NT):
                step(nc.vector.tensor_tensor(prod[:, t], prod[:, t], gain[:, 0], ALU.mult))
                step(nc.vector.tensor_tensor(prod[:, t], prod[:, t], gain[:, 1], ALU.add))
            step(nc.vector.tensor_tensor(f.x[:], f.x[:], prod[:], ALU.add))


TAU = 2 * np.pi
TAU_PARTS = (6.28125, float(np.float32(TAU - 6.28125) // 2 ** -21 * 2 ** -21), 0.0)
TAU_PARTS = TAU_PARTS[:2] + (float(TAU - TAU_PARTS[0] - TAU_PARTS[1]),)
ROUND = 1.5 * 2 ** 23
PI_BELOW = float(np.nextafter(np.float32(np.pi), np.float32(0)))
HD = 64
NF = BANK // D
E0, TOP0 = 31, 3
EXPERTS0 = E0 + 1
I0 = 256
EW0 = KC * I0 + I0 // P * D + I0 // P
RING = 4


def rms_norm(f, dve, step, y, x, gain, square, eps, var_ready, root_ready, n):
    nc = f.nc
    for t in range(NT):
        step(nc.vector.tensor_tensor_reduce(out=square[:, t], in0=x[:, t], in1=x[:, t], scale=1.0 / D, scalar=0.0,
                                            op0=ALU.mult, op1=ALU.add, accum_out=f.rstd[:, t:t + 1]))
    nc.vector.tensor_scalar(f.rstd[:], f.rstd[:], eps, None, ALU.add).then_inc(var_ready, 1)
    dve.wait_ge(root_ready, n + 1)
    step(nc.vector.reciprocal(f.rstd[:], f.rstd[:]))
    for t in range(NT):
        step(nc.vector.scalar_tensor_tensor(out=y[:, t], in0=x[:, t], scalar=f.rstd[:, t:t + 1], in1=gain,
                                            op0=ALU.mult, op1=ALU.mult))


class ShortAttention:

    DEEP = 4

    def __init__(self, f, ctx, heads, scale, causal):
        self.f, self.heads, self.scale, self.causal = f, heads, scale, causal
        self.s = {n: f.sem(n) for n in ("scored", "masked", "max_raw", "max_ready", "exp_done", "rz_ready",
                                        "normed", "probsT_mm", "probsT_sb", "attn_mm", "attn_sb")}
        self.scores = f.ps(ctx, "scores", [P, 2, NT, S])
        self.probsT_ps = f.ps(ctx, "probsT_ps", [P, 2, NT, S])
        self.attn_ps = f.ps(ctx, "attn_ps", [P, 2, BANK])
        self.masked = f.sb(ctx, "masked", [P, self.DEEP, NT, S])
        self.top = f.sb(ctx, "top", [P, self.DEEP, NT])
        self.ntop = f.sb(ctx, "ntop", [P, self.DEEP, NT])
        self.z = f.sb(ctx, "z", [P, self.DEEP, NT])
        self.rz = f.sb(ctx, "rz", [P, self.DEEP, NT])
        self.probs = f.sb(ctx, "probs", [P, self.DEEP, NT, S])
        self.normed = f.sb(ctx, "normed", [P, self.DEEP, NT, S])
        self.probsT = f.sb(ctx, "probsT", [P, 2, NT, S])
        self.attnT = f.sb(ctx, "attnT", [P, heads // 2, S])

    def tensor(self, pe, products, v):
        nc, s = self.f.nc, self.s
        for n in range(self.heads + 3):
            if n < self.heads:
                if n >= 2:
                    pe.wait_ge(s["masked"] if self.causal else s["exp_done"], n - 1)
                for t in range(NT):
                    pairs = products(n, t)
                    for k, (a, b) in enumerate(pairs):
                        mm = nc.tensor.matmul(self.scores[:, n % 2, t], a, b, start=(k == 0), stop=(k == len(pairs) - 1))
                mm.then_inc(s["scored"], 1)
            h = n - 2
            if 0 <= h < self.heads:
                pe.wait_ge(s["normed"], h + 1)
                if h >= 2:
                    pe.wait_ge(s["probsT_sb"], h - 1)
                for k in range(NT):
                    for t in range(NT):
                        mm = nc.tensor.transpose(self.probsT_ps[:, h % 2, k, t * P:(t + 1) * P],
                                                 self.normed[:, h % self.DEEP, t, k * P:(k + 1) * P], self.f.ident[:])
                mm.then_inc(s["probsT_mm"], 1)
            h = n - 3
            if h >= 0:
                pair, side = h // 2, h % 2
                pe.wait_ge(s["probsT_sb"], h + 1)
                if pair >= 2 and side == 0:
                    pe.wait_ge(s["attn_sb"], pair - 1)
                for k in range(NT):
                    mm = nc.tensor.matmul(self.attn_ps[side * HD:(side + 1) * HD, pair % 2, 0:S], v(h, k),
                                          self.probsT[:, h % 2, k], start=(k == 0), stop=(k == NT - 1))
                if side:
                    mm.then_inc(s["attn_mm"], 1)

    def scalar(self, act):
        nc, s = self.f.nc, self.s
        for n in range(self.heads + 2):
            h = n
            if h < self.heads:
                b = h % self.DEEP
                act.wait_ge(s["max_ready"], h + 1)
                if h >= self.DEEP:
                    act.wait_ge(s["normed"], h - self.DEEP + 1)
                for t in range(NT):
                    src = self.masked[:, b, t] if self.causal else self.scores[:, h % 2, t]
                    ins = nc.scalar.activation(self.probs[:, b, t], src, ACT.Exp, bias=self.ntop[:, b, t:t + 1],
                                               accum_out=self.z[:, b, t:t + 1])
                ins.then_inc(s["exp_done"], 1)
            h = n - 2
            if 0 <= h < self.heads:
                act.wait_ge(s["probsT_mm"], h + 1)
                nc.scalar.copy(self.probsT[:, h % 2], self.probsT_ps[:, h % 2]).then_inc(s["probsT_sb"], 1)

    def vector(self, dve, mask=None):
        nc, s = self.f.nc, self.s
        for n in range(self.heads + 4):
            h = n
            if h < self.heads:
                b = h % self.DEEP
                dve.wait_ge(s["scored"], h + 1)
                if h >= self.DEEP:
                    dve.wait_ge(s["exp_done"], h - self.DEEP + 1)
                src = self.scores[:, h % 2]
                if self.causal:
                    nc.vector.scalar_tensor_tensor(out=self.masked[:, b], in0=src, scalar=self.scale, in1=mask,
                                                   op0=ALU.mult, op1=ALU.add).then_inc(s["masked"], 1)
                    dve.wait_ge(s["masked"], h + 1)
                    src = self.masked[:, b]
                nc.vector.tensor_reduce(self.top[:, b], src, AX, ALU.max).then_inc(s["max_raw"], 1)
                dve.wait_ge(s["max_raw"], h + 1)
                nc.vector.tensor_scalar(self.ntop[:, b], self.top[:, b], -1.0, None, ALU.mult).then_inc(s["max_ready"], 1)
            h = n - 1
            if 0 <= h < self.heads:
                b = h % self.DEEP
                dve.wait_ge(s["exp_done"], h + 1)
                nc.vector.reciprocal(self.rz[:, b], self.z[:, b]).then_inc(s["rz_ready"], 1)
                dve.wait_ge(s["rz_ready"], h + 1)
                if h >= self.DEEP:
                    dve.wait_ge(s["probsT_mm"], h - self.DEEP + 1)
                for t in range(NT):
                    ins = nc.vector.tensor_scalar(self.normed[:, b, t], self.probs[:, b, t], self.rz[:, b, t:t + 1],
                                                  None, ALU.mult)
                ins.then_inc(s["normed"], 1)
            h = n - 4
            if h >= 0 and h % 2:
                dve.wait_ge(s["attn_mm"], h // 2 + 1)
                nc.vector.tensor_copy(self.attnT[:, h // 2], self.attn_ps[:, h // 2 % 2, 0:S]).then_inc(s["attn_sb"], 1)


def route(nc, step, gates, score, before, over, same, rank, top):
    n = score.shape[1]
    mine = score.unsqueeze(2).to_broadcast([P, n, n])
    other = score.unsqueeze(1).to_broadcast([P, n, n])
    step(nc.vector.tensor_tensor(over, other, mine, ALU.is_gt))
    step(nc.vector.tensor_tensor(same, other, mine, ALU.is_equal))
    step(nc.vector.tensor_tensor(same, same, before, ALU.mult))
    step(nc.vector.tensor_tensor(over, over, same, ALU.add))
    step(nc.vector.tensor_reduce(rank, over, AX, ALU.add))
    step(nc.vector.scalar_tensor_tensor(out=gates, in0=rank, scalar=float(top), in1=score, op0=ALU.is_lt, op1=ALU.mult))


def block0(f):
    nc, i = f.nc, f.ins
    f.layer = "b0"
    with ExitStack() as outer:
        xn = f.sb(outer, "xn", [P, NT, D])
        z = f.sb(outer, "zin", [P, NT, D])
        square = f.sb(outer, "square", [P, NT, D])
        gain1 = f.sb(outer, "gain1", [P, D])
        gain2 = f.sb(outer, "gain2", [P, D])
        G = D * 4 // (2 * P)
        NQ = H * HD
        with ExitStack() as ctx:
            s = {n: f.sem(n) for n in ("loaded", "w_loaded", "var_ready", "root_ready", "dve_steps", "pool_steps",
                                       "angles", "waves", "xn_ready", "xnT_mm", "xnT_sb", "v_mm", "v_sb", "qk_mm",
                                       "qk_sb", "q_rot", "k_rot", "out_mm")}
            wq, wk, wv = (f.sb(ctx, n, [P, KC, NQ]) for n in ("wq", "wk", "wv"))
            wo = f.sb(ctx, "wo", [P, NQ // P, D])
            bqk = f.sb(ctx, "bqk", [P, 2, NQ // P])
            bv = f.sb(ctx, "bv", [1, NQ])
            bo = f.sb(ctx, "bo", [1, D])
            mask = f.sb(ctx, "mask", [P, NT, S])
            theta = f.sb(ctx, "theta", [P, 1])
            pos = f.sb(ctx, "pos", [P, S])
            angle, turn, red = (f.sb(ctx, n, [P, 2, S]) for n in ("angle", "turn", "red"))
            waves = f.sb(ctx, "waves", [P, 2, S])
            xnT = f.sb(ctx, "xnT", [P, KC, S])
            v = f.sb(ctx, "v", [P, NT, NQ])
            raw = f.sb(ctx, "raw", [P, 2, 2, S])
            q = f.sb(ctx, "q", [P, G, 2, S])
            k = f.sb(ctx, "k", [P, G, 2, S])
            tc = f.sb(ctx, "tc", [P, 2, 2, S])
            ts = f.sb(ctx, "ts", [P, 2, 2, S])
            ps = f.ps(ctx, "ps", [P, 2, BANK])
            att = ShortAttention(f, ctx, H, HD ** -0.5, True)
            tiles = lambda n: ps[:, n].rearrange("p (t n) -> p t n", t=NT)
            block = ctx.enter_context(nc.Block())

            @block.sync
            def _(sp):
                for g in range(4):
                    sp.dma_start(theta[32 * g:32 * g + 32], i["L0_ffn_theta"]).then_inc(s["loaded"], 16)
                for dst, src in ((pos, "c_pos"), (mask, "c_causal"), (bqk, "L0_ffn_qk_b"), (bv, "L0_ffn_v_b"),
                                 (bo, "L0_ffn_o_b")):
                    sp.dma_start(dst[:], i[src]).then_inc(s["loaded"], 16)
                for dst, src in ((gain1, "L0_ffn_gamma1"), (gain2, "L0_ffn_gamma2")):
                    sp.dma_start(dst[:], i[src].partition_broadcast(P)).then_inc(s["loaded"], 16)
                for dst, src in ((wv, "L0_ffn_v_w"), (wq, "L0_ffn_q_w"), (wk, "L0_ffn_k_w"), (wo, "L0_ffn_o_w")):
                    sp.dma_start(dst[:], rows_of(i[src])).then_inc(s["w_loaded"], 16)

            @block.tensor
            def _(pe):
                pe.wait_ge(s["xn_ready"], 1)
                transpose_tokens(nc, tiles(0), xn, f.ident[:]).then_inc(s["xnT_mm"], 1)
                pe.wait_ge(s["w_loaded"], 64)
                pe.wait_ge(s["xnT_sb"], 1)
                n = 1
                for g in range(G):
                    for m, w in enumerate((wq, wk)):
                        if n >= 3:
                            pe.wait_ge(s["qk_sb"], n - 2)
                        for part in range(2):
                            for c in range(KC):
                                at = (2 * g + part) * P
                                mm = nc.tensor.matmul(tiles(n % 2)[:, part], w[:, c, at:at + P], xnT[:, c, :],
                                                      start=(c == 0), stop=(c == KC - 1))
                        mm.then_inc(s["qk_mm"], 1)
                        n += 1
                for t in range(NT):
                    for half in range(NQ // BANK):
                        pe.wait_ge(s["qk_sb"], n - 2) if n - 2 <= 2 * G else pe.wait_ge(s["v_sb"], n - 2 - 2 * G)
                        for c in range(KC):
                            nc.tensor.matmul(ps[:, n % 2], xnT[:, c, t * P:(t + 1) * P],
                                             wv[:, c, half * BANK:(half + 1) * BANK], start=(c == 0), stop=False)
                        nc.tensor.matmul(ps[:, n % 2], f.ones[0:1, :], bv[:, half * BANK:(half + 1) * BANK],
                                         start=False, stop=True).then_inc(s["v_mm"], 1)
                        n += 1
                pe.wait_ge(s["q_rot"], G)
                pe.wait_ge(s["k_rot"], G)
                pe.wait_ge(s["v_sb"], 4)

                def products(h, t):
                    g, at = h // 4, 32 * (h % 4)
                    return [(q[at:at + 32, g, part, t * P:(t + 1) * P], k[at:at + 32, g, part, :]) for part in range(2)]

                att.tensor(pe, products, lambda h, kt: v[:, kt, h * HD:(h + 1) * HD])
                pe.wait_ge(att.s["attn_sb"], H // 2)
                for t in range(NT):
                    out = tiles(0)[:, t]
                    for c in range(NQ // P):
                        nc.tensor.matmul(out, att.attnT[:, c, t * P:(t + 1) * P], wo[:, c, :], start=(c == 0), stop=False)
                    mm = nc.tensor.matmul(out, f.ones[0:1, :], bo[:], start=False, stop=True)
                mm.then_inc(s["out_mm"], 1)

            @block.scalar
            def _(act):
                act.wait_ge(s["angles"], 1)
                nc.scalar.activation(waves[:], red[:], ACT.Sin).then_inc(s["waves"], 1)
                take_root(f, act, s["var_ready"], s["root_ready"])
                take_root(f, act, s["var_ready"], s["root_ready"], 1)
                act.wait_ge(s["xnT_mm"], 1)
                nc.scalar.copy(xnT[:], tiles(0)).then_inc(s["xnT_sb"], 1)
                n = 1
                for g in range(G):
                    for m in range(2):
                        act.wait_ge(s["qk_mm"], n)
                        if g:
                            act.wait_ge(s["q_rot"] if m == 0 else s["k_rot"], g)
                        for part in range(2):
                            ins = nc.scalar.activation(raw[:, m, part], tiles(n % 2)[:, part], ACT.Identity,
                                                       bias=bqk[:, m, 2 * g + part:2 * g + part + 1])
                        ins.then_inc(s["qk_sb"], 1)
                        n += 1
                for t in range(NT):
                    for half in range(NQ // BANK):
                        act.wait_ge(s["v_mm"], t * NQ // BANK + half + 1)
                        nc.scalar.copy(v[:, t, half * BANK:(half + 1) * BANK], ps[:, n % 2]).then_inc(s["v_sb"], 1)
                        n += 1
                att.scalar(act)

            def rotate(eng, wait, step, m, dst, done):
                cos, sin = (waves[:, a].unsqueeze(1).to_broadcast([P, 2, S]) for a in range(2))
                for g in range(G):
                    wait(s["qk_sb"], 2 * g + m + 1)
                    step(eng.tensor_tensor(tc[:, m], raw[:, m], cos, ALU.mult))
                    step(eng.tensor_tensor(ts[:, m], raw[:, m], sin, ALU.mult))
                    eng.tensor_tensor(dst[:, g, 0], tc[:, m, 0], ts[:, m, 1], ALU.subtract)
                    step(eng.tensor_tensor(dst[:, g, 1], tc[:, m, 1], ts[:, m, 0], ALU.add))
                    step(eng.tensor_copy(mark[:, m:m + 1], dst[:, g, 1, 0:1]))
                    done(g)

            mark = f.sb(ctx, "mark", [P, 2])

            @block.gpsimd
            def _(pool):
                step = Chain(pool, s["pool_steps"])
                pool.wait_ge(s["waves"], 1)
                rotate(nc.gpsimd, pool.wait_ge, step, 1, k, lambda g: pool.sem_inc(s["k_rot"], 1))

            @block.vector
            def _(dve):
                step = Chain(dve, s["dve_steps"])
                dve.wait_ge(s["loaded"], 16 * 11)
                for a in range(2):
                    step(nc.vector.tensor_scalar(angle[:, a], pos[:], theta[:, 0:1], None, ALU.mult))
                    step(nc.vector.tensor_scalar(turn[:, a], angle[:, a], 1 / TAU, 0.25 * (1 - a), ALU.mult, ALU.add))
                step(nc.vector.tensor_scalar(turn[:], turn[:], ROUND, None, ALU.add))
                step(nc.vector.tensor_scalar(turn[:], turn[:], ROUND, None, ALU.subtract))
                step(nc.vector.scalar_tensor_tensor(out=red[:], in0=turn[:], scalar=-TAU_PARTS[0], in1=angle[:],
                                                    op0=ALU.mult, op1=ALU.add))
                for part in TAU_PARTS[1:]:
                    step(nc.vector.scalar_tensor_tensor(out=red[:], in0=turn[:], scalar=-part, in1=red[:],
                                                        op0=ALU.mult, op1=ALU.add))
                step(nc.vector.tensor_scalar(red[:, 0], red[:, 0], TAU / 4, None, ALU.add))
                step(nc.vector.tensor_scalar(red[:], red[:], PI_BELOW, -PI_BELOW, ALU.min, ALU.max))
                dve.sem_inc(s["angles"], 1)
                layer_norm(f, dve, step, z, f.x, 1e-5, s["var_ready"], s["root_ready"])
                rms_norm(f, dve, step, xn, z, gain1[:], square, 1e-5, s["var_ready"], s["root_ready"], 1)
                dve.sem_inc(s["xn_ready"], 1)
                dve.wait_ge(s["waves"], 1)
                rotate(nc.vector, dve.wait_ge, step, 0, q, lambda g: dve.sem_inc(s["q_rot"], 1))
                att.vector(dve, mask[:])
                dve.wait_ge(s["out_mm"], 1)
                step(nc.vector.tensor_tensor(xn[:], xn[:], tiles(0), ALU.add))

        with ExitStack() as ctx:
            s = {n: f.sem("e_" + n) for n in ("loaded", "w_free", "var_ready", "root_ready", "dve_steps", "an_ready",
                                              "anT_mm", "anT_sb", "logits_mm", "top_ready", "exp_done", "gates_ready",
                                              "gatesT_mm", "gatesT_sb", "b2_mm", "x_ready", "in_mm", "in_sb", "out_mm",
                                              "summed", "inner_used")}
            w_loaded = [f.sem(f"e_w_loaded{n}") for n in range(RING)]
            w = f.sb(ctx, "e_w", [P, RING, EW0])
            router = f.sb(ctx, "router", [P, KC, E0])
            rb = f.sb(ctx, "rb", [1, E0])
            b2 = f.sb(ctx, "e_b2", [EXPERTS0, D])
            before = f.sb(ctx, "before", [P, E0, E0])
            over, same = (f.sb(ctx, n, [P, E0, E0]) for n in ("over", "same"))
            an = f.sb(ctx, "an", [P, NT, D])
            anT = f.sb(ctx, "anT", [P, KC, S])
            top, ntop, zsum = (f.sb(ctx, n, [P, NT]) for n in ("e_top", "e_ntop", "zsum"))
            aff = f.sb(ctx, "aff", [P, NT, E0])
            rank = f.sb(ctx, "rank", [P, NT, E0])
            gates = f.sb(ctx, "gates", [P, NT, EXPERTS0])
            gatesT = f.sb(ctx, "gatesT", [EXPERTS0, S])
            inner = f.sb(ctx, "inner", [P, 2, I0 // P, S])
            ps = f.ps(ctx, "e_ps", [P, 4, BANK])
            in_ps = f.ps(ctx, "in_ps", [P, 2, I0 // P, S])
            out_ps = f.ps(ctx, "out_ps", [P, 2, NT, D])
            tiles = lambda n: ps[:, n].rearrange("p (t n) -> p t n", t=NT)
            block = ctx.enter_context(nc.Block())

            @block.sync
            def _(sp):
                for dst, src in ((router[:], rows_of(i["L0_ffn_router_w"])), (rb[:], i["L0_ffn_router_b"]),
                                 (b2[:], i["L0_ffn_e_b2"]), (before[:], i["c_before31"].partition_broadcast(P))):
                    sp.dma_start(dst, src).then_inc(s["loaded"], 16)
                for n in range(RING):
                    sp.dma_start(w[:, n], i["L0_ffn_e_w"][n]).then_inc(w_loaded[n], 16)
                with sp.Fori(1, EXPERTS0 // RING) as r:
                    for n in range(RING):
                        sp.wait_ge(s["w_free"], (r - 1) * RING + n + 1)
                        src = i["L0_ffn_e_w"][bass.ds(r * RING + n, 1)]
                        sp.dma_start(w[:, n:n + 1], src.rearrange("e p n -> p e n")).then_inc(w_loaded[n], 16)

            @block.tensor
            def _(pe):
                pe.wait_ge(s["an_ready"], 1)
                transpose_tokens(nc, tiles(0), an, f.ident[:]).then_inc(s["anT_mm"], 1)
                pe.wait_ge(s["loaded"], 64)
                pe.wait_ge(s["anT_sb"], 1)
                for t in range(NT):
                    out = ps[:, 1, t * E0:(t + 1) * E0]
                    for c in range(KC):
                        nc.tensor.matmul(out, anT[:, c, t * P:(t + 1) * P], router[:, c, :], start=(c == 0), stop=False)
                    mm = nc.tensor.matmul(out, f.ones[0:1, :], rb[:], start=False, stop=True)
                mm.then_inc(s["logits_mm"], 1)

                def expert_in(r, n):
                    pe.wait_ge(w_loaded[n], 16 * (r + 1))
                    pe.wait_ge(s["in_sb"], RING * r + n + 1)
                    for a in range(I0 // P):
                        for c in range(KC):
                            mm = nc.tensor.matmul(in_ps[:, n % 2, a], w[:, n, c * I0 + a * P:c * I0 + (a + 1) * P],
                                                  anT[:, c, :], start=(c == 0), stop=(c == KC - 1))
                    mm.then_inc(s["in_mm"], 1)

                def expert_out(r, n):
                    pe.wait_ge(s["in_sb"], RING * r + n + 3)
                    pe.wait_ge(s["summed"], 2 * (RING * r + n) + 2)
                    for t in range(NT):
                        for a in range(I0 // P):
                            at = KC * I0 + a * D
                            mm = nc.tensor.matmul(out_ps[:, n % 2, t], inner[:, n % 2, a, t * P:(t + 1) * P],
                                                  w[:, n, at:at + D], start=(a == 0), stop=(a == I0 // P - 1))
                    mm.then_inc(s["out_mm"], 1)
                    pe.wait_ge(s["out_mm"], RING * r + n + 1)
                    pe.sem_inc(s["w_free"], 1)
                    pe.sem_inc(s["inner_used"], 1)

                pe.sem_inc(s["inner_used"], 2)
                expert_in(0, 0)
                pe.wait_ge(s["gates_ready"], 1)
                for t in range(NT):
                    mm = nc.tensor.transpose(ps[0:EXPERTS0, 2, t * P:(t + 1) * P], gates[:, t, :], f.ident[:])
                mm.then_inc(s["gatesT_mm"], 1)
                pe.wait_ge(s["gatesT_sb"], 1)
                for t in range(NT):
                    mm = nc.tensor.matmul(tiles(3)[:, t], gatesT[:, t * P:(t + 1) * P], b2[:], start=True, stop=True)
                mm.then_inc(s["b2_mm"], 1)
                with pe.Fori(0, EXPERTS0 // RING - 1) as r:
                    for n in range(RING):
                        expert_in(r if n < RING - 1 else r + 1, (n + 1) % RING)
                        expert_out(r, n)
                r = EXPERTS0 // RING - 1
                for n in range(RING):
                    if n < RING - 1:
                        expert_in(r, n + 1)
                    expert_out(r, n)

            @block.scalar
            def _(act):
                act.sem_inc(s["in_sb"], 2)
                take_root(f, act, s["var_ready"], s["root_ready"])
                act.wait_ge(s["anT_mm"], 1)
                nc.scalar.copy(anT[:], tiles(0)).then_inc(s["anT_sb"], 1)
                act.wait_ge(s["top_ready"], 1)
                for t in range(NT):
                    ins = nc.scalar.activation(aff[:, t], ps[:, 1, t * E0:(t + 1) * E0], ACT.Exp, bias=ntop[:, t:t + 1],
                                               accum_out=zsum[:, t:t + 1])
                ins.then_inc(s["exp_done"], 1)
                act.wait_ge(s["gatesT_mm"], 1)
                nc.scalar.copy(gatesT[:], ps[0:EXPERTS0, 2, 0:S]).then_inc(s["gatesT_sb"], 1)
                with act.Fori(0, EXPERTS0 // RING) as r:
                    for n in range(RING):
                        act.wait_ge(s["in_mm"], RING * r + n + 1)
                        act.wait_ge(s["inner_used"], RING * r + n + 1)
                        for a in range(I0 // P):
                            at = EW0 - I0 // P + a
                            ins = nc.scalar.activation(inner[:, n % 2, a], in_ps[:, n % 2, a], ACT.Gelu,
                                                       bias=w[:, n, at:at + 1])
                        ins.then_inc(s["in_sb"], 1)

            @block.vector
            def _(dve):
                step = Chain(dve, s["dve_steps"])
                dve.sem_inc(s["summed"], 4)
                rms_norm(f, dve, step, an, xn, gain2[:], square, 1e-5, s["var_ready"], s["root_ready"], 0)
                dve.sem_inc(s["an_ready"], 1)
                step(nc.vector.tensor_tensor(f.x[:], f.x[:], xn[:], ALU.add))
                step(nc.vector.tensor_tensor(f.x[:], f.x[:], an[:], ALU.add))
                dve.wait_ge(s["logits_mm"], 1)
                step(nc.vector.tensor_reduce(top[:], ps[:, 1, 0:NT * E0].rearrange("p (t e) -> p t e", t=NT), AX, ALU.max))
                step(nc.vector.tensor_scalar(ntop[:], top[:], -1.0, None, ALU.mult))
                dve.sem_inc(s["top_ready"], 1)
                dve.wait_ge(s["exp_done"], 1)
                step(nc.vector.reciprocal(zsum[:], zsum[:]))
                step(nc.vector.memset(gates[:], 1.0))
                for t in range(NT):
                    step(nc.vector.tensor_scalar(aff[:, t], aff[:, t], zsum[:, t:t + 1], None, ALU.mult))
                    route(nc, step, gates[:, t, 0:E0], aff[:, t], before[:], over[:], same[:], rank[:, t], TOP0)
                dve.sem_inc(s["gates_ready"], 1)
                dve.wait_ge(s["b2_mm"], 1)
                step(nc.vector.tensor_tensor(f.x[:], f.x[:], tiles(3), ALU.add))
                with dve.Fori(0, EXPERTS0 // RING) as r:
                    for n in range(RING):
                        e = RING * r + n
                        dve.wait_ge(s["out_mm"], e + 1)
                        for t in range(NT):
                            dve.wait_ge(s["summed"], 2 * e + t + 3)
                            nc.vector.scalar_tensor_tensor(out=f.x[:, t], in0=out_ps[:, n % 2, t],
                                                           scalar=gates[:, t, bass.ds(e, 1)], in1=f.x[:, t],
                                                           op0=ALU.mult, op1=ALU.add).then_inc(s["summed"], 1)
                dve.wait_ge(s["summed"], 2 * EXPERTS0 + 4)


U = NT * NHALF
SUB = HALF // 2
CPS = SUB // P
UNITS = H * U
PITCH = S2 + 1


def cross1(f):
    nc, i = f.nc, f.ins
    f.layer = "xb"
    rel_dram = f.rel_dram
    with ExitStack() as ctx:
        bcols = f.sb(ctx, "bcols", [P, 3, KC])
        qc96 = f.sb(ctx, "qc96", [P, H, S], BF16)
        qr96 = f.sb(ctx, "qr96", [P, H, S], BF16)
        mask = f.sb(ctx, "mask", [P, NT, S2])
        minus = f.sb(ctx, "minus", [P, NT, S2])
        top_all = f.sb(ctx, "top_all", [P, H, U])
        o_all = f.sb(ctx, "o_all", [P, H, U, DV])
        mask_loaded = [f.sem(f"mask_loaded{t}") for t in range(NT)]

        with ExitStack() as inner:
            s = {n: f.sem("a_" + n) for n in ("loaded", "var_ready", "root_ready", "dve_steps", "xn_ready",
                                              "xnT_mm", "xnT_sb", "q_mm", "split", "stored", "q_loaded")}
            wq = f.sb(inner, "wq", [P, KC, D])
            xn = f.sb(inner, "xn", [P, NT, D])
            xnT = f.sb(inner, "xnT", [P, KC, S])
            q = f.sb(inner, "q", [P, KC, S])
            qb = f.sb(inner, "qb", [P, 2, KC, S])
            rest = f.sb(inner, "rest", [P, 2, KC, S])
            parts = f.sb(inner, "parts", [P, 2, 3, KC, S], BF16)
            ps = f.ps(inner, "a_ps", [P, 2, BANK])
            tiles = lambda n: ps[:, n].rearrange("p (t n) -> p t n", t=NT)
            block = inner.enter_context(nc.Block())

            @block.sync
            def _(sp):
                for dst, src in ((wq[:], rows_of(i["L1_xattn_Wq"])), (bcols[:], i["L1_xattn_bcols"])):
                    sp.dma_start(dst, src).then_inc(s["loaded"], 16)
                for t in range(NT):
                    sp.dma_start(mask[:, t], i["mask"][t * P:(t + 1) * P, :]).then_inc(mask_loaded[t], 16)
                sp.wait_ge(s["split"], 1)
                for m in range(2):
                    for part in range(3):
                        sp.dma_start(f.query_parts[1 + m, part].rearrange("(c p) n -> p c n", p=P),
                                     parts[:, m, part]).then_inc(s["stored"], 16)
                sp.wait_ge(s["stored"], 96)
                for m, dst in enumerate((qc96, qr96)):
                    for r, part in enumerate(Q_PARTS):
                        src = f.query_parts[1 + m, part].rearrange("(h d) n -> d h n", d=DK)
                        sp.dma_start(dst[r * DK:(r + 1) * DK], src).then_inc(s["q_loaded"], 16)
                sp.wait_ge(s["q_loaded"], 192)

            @block.tensor
            def _(pe):
                pe.wait_ge(s["xn_ready"], 1)
                transpose_tokens(nc, tiles(0), xn, f.ident[:]).then_inc(s["xnT_mm"], 1)
                pe.wait_ge(s["loaded"], 32)
                pe.wait_ge(s["xnT_sb"], 1)
                for m in range(KC):
                    for c in range(KC):
                        mm = nc.tensor.matmul(tiles(1)[:, m], wq[:, c, m * P:(m + 1) * P], xnT[:, c, :],
                                              start=(c == 0), stop=(c == KC - 1))
                mm.then_inc(s["q_mm"], 1)

            @block.scalar
            def _(act):
                take_root(f, act, s["var_ready"], s["root_ready"])
                act.wait_ge(s["xnT_mm"], 1)
                nc.scalar.copy(xnT[:], tiles(0)).then_inc(s["xnT_sb"], 1)

            @block.vector
            def _(dve):
                step = Chain(dve, s["dve_steps"])
                layer_norm(f, dve, step, xn, f.x, 1e-5, s["var_ready"], s["root_ready"])
                dve.sem_inc(s["xn_ready"], 1)
                dve.wait_ge(s["q_mm"], 1)
                dve.wait_ge(s["loaded"], 32)
                for c in range(KC):
                    step(nc.vector.tensor_scalar(q[:, c], tiles(1)[:, c], bcols[:, 0, c:c + 1], None, ALU.add))
                    for m in range(2):
                        step(nc.vector.tensor_scalar(qb[:, m, c], q[:, c], bcols[:, 1 + m, c:c + 1], DK ** -0.5,
                                                     ALU.add, ALU.mult))
                step(nc.vector.tensor_copy(parts[:, :, 0], qb[:]))
                step(nc.vector.tensor_tensor(rest[:], qb[:], parts[:, :, 0], ALU.subtract))
                step(nc.vector.tensor_copy(parts[:, :, 1], rest[:]))
                step(nc.vector.tensor_tensor(parts[:, :, 2], rest[:], parts[:, :, 1], ALU.subtract))
                dve.sem_inc(s["split"], 1)

        with ExitStack() as inner:
            names = ("rel_mm", "rel_out", "cont_mm", "cont_out", "masked", "halves_max", "top_raw", "top_ready",
                     "exp_done", "turned", "weighed", "sums_sb", "gathered", "sums_read", "zero_set", "g_loaded", "top_begun", "top_kept", "minus_ready", "row_free")
            s = {n: f.sem("b_" + n) for n in names}
            turned_sb = [f.sem(f"b_turned_sb{n}") for n in range(2)]
            rel_stored = [f.sem(f"b_rel_stored{n}") for n in range(U)]
            rel_back = [f.sem(f"b_rel_back{n}") for n in range(U)]
            kc_loaded = [f.sem(f"b_kc_loaded{n}") for n in range(2)]
            v_loaded = [f.sem(f"b_v_loaded{n}") for n in range(2)]
            kr_loaded = [f.sem(f"b_kr_loaded{n}") for n in range(2)]
            kc96 = f.sb(inner, "kc96", [ROWS, 2, S2], BF16)
            kr96 = f.sb(inner, "kr96", [ROWS, 2, S2], BF16)
            out0 = f.sb(inner, "out0", [P, HALF + 1])
            out1 = f.sb(inner, "out1", [P, HALF])
            row = f.sb(inner, "row", [P, U, HALF])
            top2 = f.sb(inner, "top2", [P, U, 2])
            top = f.sb(inner, "top", [P, U])
            ntop = f.sb(inner, "ntop", [P, U])
            turned = f.sb(inner, "turned", [P, 2, CPS, P])
            vhead = f.sb(inner, "vhead", [P, 2, NCH, DV])
            gather = f.sb(inner, "gather", [P, DV])
            sumsT = f.sb(inner, "sumsT", [P, 2, P])
            rel_ps = f.ps(inner, "rel_ps", [P, SUB])
            cont_ps = f.ps(inner, "cont_ps", [P, SUB])
            turn_ps = f.ps(inner, "turn_ps", [P, SUB])
            sum_ps = f.ps(inner, "sum_ps", [P, BANK])
            both = f.ps(inner, "both", [P, 2, QUAD])
            block = inner.enter_context(nc.Block())
            LOOPS = H // 2 - 2

            def where(p, c):
                return 2 * U * p + c, 2 * p + c // U, c % U, c // U % 2, c % U // NHALF, c % NHALF

            def slots(eng, slot, before=None):
                for n in range(-U, 3):
                    slot(0, n, n)
                with eng.Fori(0, LOOPS) as p:
                    for c in range(3, 3 + 2 * U):
                        slot(p, c, None)
                for n in range(2 * U * LOOPS + 3, UNITS + 3):
                    slot(LOOPS, n - 2 * U * LOOPS, n)

            def runs(n, ahead):
                return n is None or 0 <= n + ahead < UNITS

            @block.sync
            def _(sp):
                def load_keys(p, c, which, dst, loaded):
                    b = c // U % 2
                    load_key_parts(f, sp, dst[:, b], which, 2 * p + c // U, loaded[b])

                def read_back(p, c, first=False):
                    n, head, u, b, t, half = where(p, c)
                    if not first:
                        sp.wait_ge(s["turned"], 2 * n - 2 * U + 2)
                        sp.sem_inc(s["row_free"], 1)
                    for k in ((0, 1), (0, 1, 2), (2, 3), (2, 3))[u]:
                        sp.wait_ge(rel_stored[k], 16 * (head + 1))
                    src = rel_back_view[half][bass.ds(head, 1), t * P:(t + 1) * P, :]
                    sp.dma_start(row[:, u:u + 1, :], src.rearrange("h p n -> p h n")).then_inc(rel_back[u], 16)

                def store(p, c):
                    n, head, u, b, t, half = where(p, c)
                    sp.wait_ge(s["rel_out"], 2 * n + 3)
                    rows = rel_rows[bass.ds(head, 1), t * P:(t + 1) * P, :]
                    if half == 0:
                        dst, src = rows[:, :, 0:HALF + 1], out0
                    else:
                        dst, src = rows[:, :, HALF + 1:PITCH], out1
                    sp.dma_start(dst.rearrange("h p n -> p (h n)"), src[:]).then_inc(rel_stored[u], 16)

                rel_rows = rel_dram[:, 0:S * PITCH].rearrange("h (r n) -> h r n", n=PITCH)
                shifted = rel_dram[:, S:S + S * S2].rearrange("h (r n) -> h r n", n=S2)
                rel_back_view = [shifted[:, :, h * HALF:(h + 1) * HALF] for h in range(NHALF)]

                def slot(p, c, n):
                    if c % U == 0 and (n is None or 0 <= n < UNITS - 2 * U):
                        sp.wait_ge(s["rel_mm"], 2 * U * (2 * p + c // U + 1))
                        load_keys(p, c + 2 * U, 2, kr96, kr_loaded)
                    if c % U == 1 and (n is None or 0 < n < UNITS - U):
                        if n is None or n > U:
                            sp.wait_ge(s["cont_mm"], 2 * U * (2 * p + c // U))
                        load_keys(p, c + U, 1, kc96, kc_loaded)
                    if c % U == 2 and (n is None or 0 < n < UNITS - U):
                        if n is None or n > U:
                            sp.wait_ge(s["weighed"], 2 * U * (2 * p + c // U) + 2)
                        load_values(p, c + U)
                    if runs(n, 2):
                        read_back(p, c + 2, first=n is not None and n + 2 < U)
                    if runs(n, U):
                        store(p, c + U)

                def load_values(p, c):
                    b = c // U % 2
                    sp.dma_start(vhead[:, b:b + 1], f.value_rows[1, bass.ds(2 * p + c // U, 1)].rearrange(
                        "h p k d -> p h k d")).then_inc(v_loaded[b], 16)

                sp.dma_start(gather[:], i["c_gather"]).then_inc(s["g_loaded"], 16)
                load_keys(0, 0, 2, kr96, kr_loaded)
                load_keys(0, 0, 1, kc96, kc_loaded)
                load_keys(0, U, 2, kr96, kr_loaded)
                load_values(0, 0)
                slots(sp, slot)

            @block.tensor
            def _(pe):
                def scores(p, c, part, q96, k96, out, loaded, free, done):
                    n, head, u, b, t, half = where(p, c)
                    if u == 0 and part == 0:
                        pe.wait_ge(loaded[b], KEYS_IN * (p + c // U // 2 + 1))
                    pe.wait_ge(free, 2 * n + part + 1)
                    for k in range(SUB // BANK):
                        at = half * HALF + part * SUB + k * BANK
                        mm = nc.tensor.matmul(out[:, k * BANK:(k + 1) * BANK],
                                              q96[0:ROWS, bass.ds(head, 1), t * P:(t + 1) * P],
                                              k96[:, b, at:at + BANK], start=True, stop=True)
                    mm.then_inc(done, 1)

                def content(p, c, part):
                    scores(p, c, part, qc96, kc96, cont_ps, kc_loaded, s["cont_out"], s["cont_mm"])

                def relative(p, c, part):
                    scores(p, c, part, qr96, kr96, rel_ps, kr_loaded, s["rel_out"], s["rel_mm"])

                def turn(p, c, part):
                    n, head, u, b, t, half = where(p, c)
                    pe.wait_ge(s["exp_done"], n + 1)
                    pe.wait_ge(turned_sb[1 - part], n + 1)
                    for k in range(CPS):
                        at = part * SUB + k * P
                        mm = nc.tensor.transpose(turn_ps[:, k * P:(k + 1) * P], row[:, u, at:at + P], f.ident[:])
                    mm.then_inc(s["turned"], 1)

                def weigh(p, c, part):
                    n, head, u, b, t, half = where(p, c)
                    pe.wait_ge(turned_sb[part], n + 1 + part)
                    if u == 0 and part == 0:
                        pe.wait_ge(v_loaded[b], 16 * (p + c // U // 2 + 1))
                    if part == 0:
                        pe.wait_ge(s["sums_sb"], n + 1)
                    for k in range(CPS):
                        at = k % NQ4 * QUAD
                        mm = nc.tensor.matmul(sum_ps[at:at + DV, 0:P], vhead[:, b, half * NCH // 2 + part * CPS + k, :],
                                              turned[:, part, k, :], start=(part == 0 and k < NQ4),
                                              stop=(part == 1 and k >= CPS - NQ4))
                    mm.then_inc(s["weighed"], 1)

                def bring_together(p, c):
                    n, head, u, b, t, half = where(p, c)
                    pe.wait_ge(s["sums_sb"], n + 2)
                    pe.wait_ge(s["sums_read"], n + 1)
                    nc.tensor.matmul(both[:, u % 2, 0:DV], sumsT[:, u % 2, :], gather[:], start=True, stop=True
                                     ).then_inc(s["gathered"], 1)

                def slot(p, c, n):
                    if runs(n, 0):
                        content(p, c, 0)
                    if runs(n, -3):
                        bring_together(p, c - 3)
                    if runs(n, -2):
                        turn(p, c - 2, 0)
                    if runs(n, U):
                        relative(p, c + U, 0)
                    if runs(n, 0):
                        content(p, c, 1)
                    if runs(n, -2):
                        turn(p, c - 2, 1)
                        weigh(p, c - 2, 0)
                    if runs(n, U):
                        relative(p, c + U, 1)
                    if runs(n, -2):
                        weigh(p, c - 2, 1)

                pe.wait_ge(s["g_loaded"], 16)
                pe.wait_ge(s["zero_set"], 2)
                slots(pe, slot)

            @block.scalar
            def _(act):
                act.sem_inc(s["rel_out"], 1)

                def evacuate(p, c, part):
                    n, head, u, b, t, half = where(p, c)
                    act.wait_ge(s["rel_mm"], 2 * n + part + 1)
                    if part == 0 and u >= NHALF:
                        act.wait_ge(rel_stored[u - NHALF], 16 * (head + 1))
                    elif part == 0 and not (isinstance(n, int) and n < U):
                        act.wait_ge(rel_stored[u + NHALF], 16 * head)
                    elif part == 0 and u == 0:
                        act.wait_ge(s["zero_set"], 1)
                    out = out1 if half else out0[:, 1:HALF + 1]
                    nc.scalar.copy(out[:, part * SUB:(part + 1) * SUB], rel_ps[:]).then_inc(s["rel_out"], 1)

                def exponentials(p, c):
                    n, head, u, b, t, half = where(p, c)
                    act.wait_ge(s["top_ready"], n + 1)
                    nc.scalar.activation(row[:, u], row[:, u], ACT.Exp, bias=ntop[:, u:u + 1]).then_inc(s["exp_done"], 1)

                def copy_turned(p, c):
                    n, head, u, b, t, half = where(p, c)
                    act.wait_ge(s["turned"], 2 * n + 1)
                    act.wait_ge(s["weighed"], 2 * n + 1)
                    nc.scalar.copy(turned[:, 0].rearrange("p k n -> p (k n)"), turn_ps[:]).then_inc(turned_sb[0], 1)

                def slot(p, c, n):
                    if runs(n, -2):
                        copy_turned(p, c - 2)
                    if runs(n, U):
                        evacuate(p, c + U, 0)
                    if runs(n, -1):
                        exponentials(p, c - 1)
                    if runs(n, U):
                        evacuate(p, c + U, 1)

                slots(act, slot)
                act.wait_ge(s["exp_done"], UNITS)

            @block.gpsimd
            def _(pool):
                def slot(p, c, n):
                    if not runs(n, 0):
                        return
                    n, head, u, b, t, half = where(p, c)
                    for part in range(2):
                        at = part * SUB
                        pool.wait_ge(s["cont_out"], 2 * n + part + 2)
                        nc.gpsimd.tensor_tensor(row[:, u, at:at + SUB], row[:, u, at:at + SUB],
                                                mask[:, t, half * HALF + at:half * HALF + at + SUB],
                                                ALU.mult).then_inc(s["masked"], 1)

                for t in range(NT):
                    pool.wait_ge(mask_loaded[t], 16)
                slots(pool, slot)

            @block.vector
            def _(dve):
                nc.vector.memset(out0[:, 0:1], 0.0).then_inc(s["zero_set"], 1)
                nc.vector.memset(sum_ps[:], 0.0).then_inc(s["zero_set"], 1)
                dve.sem_inc(s["sums_sb"], 1)
                dve.sem_inc(s["cont_out"], 1)
                dve.sem_inc(turned_sb[1], 1)
                dve.sem_inc(s["weighed"], 2)
                dve.sem_inc(s["sums_read"], 2)
                for t in range(NT):
                    dve.wait_ge(mask_loaded[t], 16)
                    nc.vector.tensor_scalar(minus[:, t], mask[:, t], 1.0, 1e10, ALU.subtract, ALU.mult
                                            ).then_inc(s["minus_ready"], 1)
                dve.wait_ge(s["minus_ready"], NT)

                def add(p, c, part):
                    n, head, u, b, t, half = where(p, c)
                    if part == 0:
                        dve.wait_ge(rel_back[u], 16 * (head + 1))
                    dve.wait_ge(s["cont_mm"], 2 * n + part + 1)
                    at = part * SUB
                    nc.vector.tensor_tensor(row[:, u, at:at + SUB], cont_ps[:], row[:, u, at:at + SUB],
                                            ALU.add).then_inc(s["cont_out"], 1)

                def top_of(p, c, part):
                    n, head, u, b, t, half = where(p, c)
                    dve.wait_ge(s["masked"], 2 * n + part + 1)
                    dve.sem_inc(s["top_begun"], 1)
                    at = part * SUB
                    nc.vector.tensor_tensor_reduce(out=row[:, u, at:at + SUB], in0=row[:, u, at:at + SUB],
                                                   in1=minus[:, t, half * HALF + at:half * HALF + at + SUB], scale=1.0,
                                                   scalar=-3e38, op0=ALU.add, op1=ALU.max,
                                                   accum_out=top2[:, u, part:part + 1]).then_inc(s["halves_max"], 1)
                    if part == 1:
                        dve.wait_ge(s["halves_max"], 2 * n + 2)
                        nc.vector.tensor_tensor(top[:, u:u + 1], top2[:, u, 0:1], top2[:, u, 1:2], ALU.max
                                                ).then_inc(s["top_raw"], 1)
                        dve.wait_ge(s["top_raw"], n + 1)
                        nc.vector.tensor_scalar(ntop[:, u:u + 1], top[:, u:u + 1], -1.0, None, ALU.mult
                                                ).then_inc(s["top_ready"], 1)
                        nc.vector.tensor_copy(top_all[:, bass.ds(head, 1), u:u + 1], top[:, u:u + 1]
                                              ).then_inc(s["top_kept"], 1)

                def copy_turned(p, c):
                    n, head, u, b, t, half = where(p, c)
                    dve.wait_ge(s["turned"], 2 * n + 2)
                    dve.wait_ge(s["weighed"], 2 * n + 2)
                    nc.vector.tensor_copy(turned[:, 1].rearrange("p k n -> p (k n)"), turn_ps[:]
                                          ).then_inc(turned_sb[1], 1)

                def sums_out(p, c):
                    n, head, u, b, t, half = where(p, c)
                    dve.wait_ge(s["weighed"], 2 * n + 4)
                    nc.vector.tensor_copy(sumsT[:, u % 2], sum_ps[:, 0:P]).then_inc(s["sums_sb"], 1)

                def keep_sums(p, c):
                    n, head, u, b, t, half = where(p, c)
                    dve.wait_ge(s["gathered"], n + 1)
                    nc.vector.tensor_scalar(o_all[:, bass.ds(head, 1), u, :], both[:, u % 2, 0:DV], 1.0, None,
                                            ALU.mult).then_inc(s["sums_read"], 1)

                def slot(p, c, n):
                    if runs(n, -1):
                        top_of(p, c - 1, 0)
                    if runs(n, -3):
                        sums_out(p, c - 3)
                    if runs(n, 0):
                        add(p, c, 0)
                    if runs(n, -1):
                        top_of(p, c - 1, 1)
                    if runs(n, 0):
                        add(p, c, 1)
                    if runs(n, -2):
                        copy_turned(p, c - 2)
                    if runs(n, -3):
                        keep_sums(p, c - 3)

                slots(dve, slot)
                dve.wait_ge(s["sums_read"], UNITS + 2)
                dve.wait_ge(s["top_kept"], UNITS)

        with ExitStack() as inner:
            s = {n: f.sem("c_" + n) for n in ("loaded", "dve_steps", "w_in", "w_out", "o_ready", "oT_mm", "oT_sb", "out_mm")}
            wo = f.sb(inner, "wo", [P, KC, D])
            bo = f.sb(inner, "bo", [1, D])
            bv = f.sb(inner, "bv", [P, D])
            m = f.sb(inner, "m", [P, H, NT])
            wgt = f.sb(inner, "wgt", [P, H, U])
            total = f.sb(inner, "total", [P, NT, H, DV])
            z = f.sb(inner, "z", [P, NT, H])
            attn = f.sb(inner, "attn", [P, NT, H, DK])
            attnT = f.sb(inner, "attnT", [P, KC, S])
            ps = f.ps(inner, "c_ps", [P, 2, BANK])
            tiles = lambda n: ps[:, n].rearrange("p (t n) -> p t n", t=NT)
            block = inner.enter_context(nc.Block())

            @block.sync
            def _(sp):
                sp.dma_start(wo[:], rows_of(i["L1_xattn_Wo"])).then_inc(s["loaded"], 16)
                sp.dma_start(bo[:], i["L1_xattn_bo"]).then_inc(s["loaded"], 16)
                sp.dma_start(bv[:], i["L1_xattn_bv"].partition_broadcast(P)).then_inc(s["loaded"], 16)

            @block.vector
            def _(dve):
                step = Chain(dve, s["dve_steps"])
                halves = lambda y: y[:].rearrange("p h (t a) -> p h t a", a=NHALF)
                step(nc.vector.tensor_reduce(m[:], halves(top_all), AX, ALU.max))
                for a in range(NHALF):
                    step(nc.vector.tensor_tensor(halves(wgt)[:, :, :, a], halves(top_all)[:, :, :, a], m[:], ALU.subtract))
                dve.sem_inc(s["w_in"], 1)
                dve.wait_ge(s["w_out"], 1)
                step(nc.vector.tensor_tensor(o_all[:], o_all[:], wgt[:].unsqueeze(3).to_broadcast([P, H, U, DV]), ALU.mult))
                for t in range(NT):
                    step(nc.vector.tensor_tensor(total[:, t], o_all[:, :, NHALF * t, :], o_all[:, :, NHALF * t + 1, :],
                                                 ALU.add))
                step(nc.vector.reciprocal(z[:], total[:, :, :, DK]))
                for t in range(NT):
                    step(nc.vector.tensor_tensor(attn[:, t], total[:, t, :, 0:DK],
                                                 z[:, t].unsqueeze(2).to_broadcast([P, H, DK]), ALU.mult))
                dve.wait_ge(s["loaded"], 48)
                step(nc.vector.tensor_tensor(attn[:], attn[:], bv[:].rearrange("p (h d) -> p h d", h=H).unsqueeze(1)
                                             .to_broadcast([P, NT, H, DK]), ALU.add))
                dve.sem_inc(s["o_ready"], 1)
                dve.wait_ge(s["out_mm"], 1)
                step(nc.vector.tensor_tensor(f.x[:], f.x[:], tiles(1), ALU.add))

            @block.scalar
            def _(act):
                act.wait_ge(s["w_in"], 1)
                nc.scalar.activation(wgt[:], wgt[:], ACT.Exp).then_inc(s["w_out"], 1)
                act.wait_ge(s["oT_mm"], 1)
                nc.scalar.copy(attnT[:], tiles(0)).then_inc(s["oT_sb"], 1)

            @block.tensor
            def _(pe):
                pe.wait_ge(s["o_ready"], 1)
                transpose_tokens(nc, tiles(0), attn[:].rearrange("p t h d -> p t (h d)"), f.ident[:]
                                 ).then_inc(s["oT_mm"], 1)
                pe.wait_ge(s["loaded"], 48)
                pe.wait_ge(s["oT_sb"], 1)
                for t in range(NT):
                    for c in range(KC):
                        nc.tensor.matmul(tiles(1)[:, t], attnT[:, c, t * P:(t + 1) * P], wo[:, c, :],
                                         start=(c == 0), stop=False)
                    mm = nc.tensor.matmul(tiles(1)[:, t], f.ones[0:1, :], bo[:], start=False, stop=True)
                mm.then_inc(s["out_mm"], 1)


HM = 8
E1, TOP1 = 8, 2
I1 = 512
RING1 = 2


def multi_query(f):
    nc, i = f.nc, f.ins
    f.layer = "mq"
    s = {n: f.sem(n) for n in ("loaded", "var_ready", "root_ready", "dve_steps", "xn_ready", "xnT_mm", "xnT_sb",
                               "q_mm", "kv_mm", "sums_ready", "norms_ready", "scaled", "qT_mm", "qT_sb", "out_mm")}
    NQ = HM * HD
    with ExitStack() as ctx:
        wq = f.sb(ctx, "wq", [P, KC, NQ])
        wkv = f.sb(ctx, "wkv", [P, KC, 2 * HD])
        wo = f.sb(ctx, "wo", [P, NQ // P, D])
        gain = f.sb(ctx, "gain", [P, 2, D])
        z = f.sb(ctx, "zn", [P, NT, D])
        xn = f.sb(ctx, "xn", [P, NT, D])
        xnT = f.sb(ctx, "xnT", [P, KC, S])
        q = f.sb(ctx, "q", [P, NT, NQ])
        kv = f.sb(ctx, "kv", [P, NT, 2 * HD])
        square = f.sb(ctx, "square", [P, NT, NQ + HD])
        norms = f.sb(ctx, "norms", [P, NT, HM + 1])
        kk = f.sb(ctx, "kk", [P, NT, 2 * HD])
        qT = f.sb(ctx, "qT", [P, NQ // P, S])
        kT = f.sb(ctx, "kT", [P, S])
        ps = f.ps(ctx, "ps", [P, 2, BANK])
        att = ShortAttention(f, ctx, HM, 1.0, False)
        tiles = lambda n: ps[:, n].rearrange("p (t n) -> p t n", t=NT)
        block = ctx.enter_context(nc.Block())

        @block.sync
        def _(sp):
            loads = [(wq[:], rows_of(i["L1_attn_Wq"])), (wkv[:], rows_of(i["L1_attn_Wkv"])),
                     (wo[:], rows_of(i["L1_attn_Wout"]))]
            loads += [(gain[:, n], i[f"L1_attn_{m}"].partition_broadcast(P)) for n, m in enumerate(("norm_g", "out_norm_g"))]
            for dst, src in loads:
                sp.dma_start(dst, src).then_inc(s["loaded"], 16)

        @block.tensor
        def _(pe):
            pe.wait_ge(s["xn_ready"], 1)
            transpose_tokens(nc, tiles(0), xn, f.ident[:]).then_inc(s["xnT_mm"], 1)
            pe.wait_ge(s["loaded"], 80)
            pe.wait_ge(s["xnT_sb"], 1)
            for t in range(NT):
                if t == 1:
                    pe.wait_ge(s["xnT_sb"], 1)
                for c in range(KC):
                    mm = nc.tensor.matmul(ps[:, t], xnT[:, c, t * P:(t + 1) * P], wq[:, c, :],
                                          start=(c == 0), stop=(c == KC - 1))
                mm.then_inc(s["q_mm"], 1)
            for t in range(NT):
                for c in range(KC):
                    mm = nc.tensor.matmul(att.attn_ps[:, 0, t * 2 * HD:(t + 1) * 2 * HD], xnT[:, c, t * P:(t + 1) * P],
                                          wkv[:, c, :], start=(c == 0), stop=(c == KC - 1))
            mm.then_inc(s["kv_mm"], 1)
            pe.wait_ge(s["scaled"], 1)
            for n in range(NQ // P):
                for t in range(NT):
                    mm = nc.tensor.transpose(tiles(n // 2)[:, n % 2, t * P:(t + 1) * P], q[:, t, n * P:(n + 1) * P],
                                             f.ident[:])
            mm.then_inc(s["qT_mm"], 1)
            for t in range(NT):
                mm = nc.tensor.transpose(att.attn_ps[:, 1, t * P:(t + 1) * P], kk[:, t, :], f.ident[:])
            mm.then_inc(s["qT_mm"], 1)
            pe.wait_ge(s["qT_sb"], 3)

            def products(h, t):
                at = HD * (h % 2)
                return [(qT[at:at + HD, h // 2, t * P:(t + 1) * P], kT[at:at + HD, :])]

            att.tensor(pe, products, lambda h, kt: kv[:, kt, HD:2 * HD])
            pe.wait_ge(att.s["attn_sb"], HM // 2)
            for t in range(NT):
                for c in range(NQ // P):
                    mm = nc.tensor.matmul(tiles(0)[:, t], att.attnT[:, c, t * P:(t + 1) * P], wo[:, c, :],
                                          start=(c == 0), stop=(c == NQ // P - 1))
            mm.then_inc(s["out_mm"], 1)

        @block.scalar
        def _(act):
            take_root(f, act, s["var_ready"], s["root_ready"])
            take_root(f, act, s["var_ready"], s["root_ready"], 1)
            act.wait_ge(s["xnT_mm"], 1)
            nc.scalar.copy(xnT[:], tiles(0)).then_inc(s["xnT_sb"], 1)
            act.wait_ge(s["sums_ready"], 1)
            nc.scalar.sqrt(norms[:], norms[:]).then_inc(s["norms_ready"], 1)
            act.wait_ge(s["qT_mm"], 2)
            for n in range(2):
                nc.scalar.copy(qT[:, 2 * n:2 * n + 2], tiles(n)).then_inc(s["qT_sb"], 1)
            nc.scalar.copy(kT[:], att.attn_ps[:, 1, 0:S]).then_inc(s["qT_sb"], 1)
            att.scalar(act)
            take_root(f, act, s["var_ready"], s["root_ready"], 2)

        @block.vector
        def _(dve):
            step = Chain(dve, s["dve_steps"])
            layer_norm(f, dve, step, z, f.x, 1e-5, s["var_ready"], s["root_ready"])
            layer_norm(f, dve, step, xn, z, 1e-5, s["var_ready"], s["root_ready"], 1)
            dve.wait_ge(s["loaded"], 80)
            for t in range(NT):
                step(nc.vector.tensor_tensor(xn[:, t], xn[:, t], gain[:, 0], ALU.mult))
            dve.sem_inc(s["xn_ready"], 1)
            dve.wait_ge(s["q_mm"], 2)
            dve.wait_ge(s["kv_mm"], 1)
            step(nc.vector.tensor_copy(q[:], ps[:]))
            step(nc.vector.tensor_copy(kv[:], att.attn_ps[:, 0, 0:NT * 2 * HD].rearrange("p (t n) -> p t n", t=NT)))
            step(nc.vector.scalar_tensor_tensor(out=square[:, :, 0:NQ], in0=q[:], scalar=16.0 ** 2, in1=q[:],
                                                op0=ALU.mult, op1=ALU.mult))
            step(nc.vector.tensor_tensor(square[:, :, NQ:], kv[:, :, 0:HD], kv[:, :, 0:HD], ALU.mult))
            step(nc.vector.tensor_reduce(norms[:], square[:].rearrange("p t (h d) -> p t h d", d=HD), AX, ALU.add))
            dve.sem_inc(s["sums_ready"], 1)
            dve.wait_ge(s["norms_ready"], 1)
            step(nc.vector.tensor_scalar(norms[:], norms[:], 1e-12, None, ALU.max))
            step(nc.vector.reciprocal(norms[:], norms[:]))
            step(nc.vector.tensor_scalar(norms[:, :, 0:HM], norms[:, :, 0:HM], 16.0 * 4.0, None, ALU.mult))
            for t in range(NT):
                step(nc.vector.tensor_tensor(q[:, t].rearrange("p (h d) -> p h d", h=HM),
                                             q[:, t].rearrange("p (h d) -> p h d", h=HM),
                                             norms[:, t, 0:HM].unsqueeze(2).to_broadcast([P, HM, HD]), ALU.mult))
                for n in range(2):
                    step(nc.vector.tensor_scalar(kk[:, t, n * HD:(n + 1) * HD], kv[:, t, 0:HD], norms[:, t, HM:HM + 1],
                                                 4.0, ALU.mult, ALU.mult))
            dve.sem_inc(s["scaled"], 1)
            att.vector(dve)
            dve.wait_ge(s["out_mm"], 1)
            step(nc.vector.tensor_copy(z[:], tiles(0)))
            layer_norm(f, dve, step, xn, z, 1e-5, s["var_ready"], s["root_ready"], 2)
            for t in range(NT):
                step(nc.vector.tensor_tensor(xn[:, t], xn[:, t], gain[:, 1], ALU.mult))
            step(nc.vector.tensor_tensor(f.x[:], f.x[:], xn[:], ALU.add))


def mixture1(f):
    nc, i = f.nc, f.ins
    f.layer = "m1"
    s = {n: f.sem(n) for n in ("loaded", "w_free", "var_ready", "root_ready", "dve_steps", "xn_ready", "xnT_mm",
                               "xnT_sb", "logits_mm", "top_ready", "exp_done", "gated_mm", "silu_done", "silu_used",
                               "inner_done", "inner_used", "out_mm", "summed")}
    w_loaded = [f.sem(f"w_loaded{n}") for n in range(RING1)]
    NI = I1 // P
    with ExitStack() as ctx:
        w13 = f.sb(ctx, "w13", [P, RING1, 2, KC, I1])
        w2 = f.sb(ctx, "w2", [P, RING1, NI, D])
        wg = f.sb(ctx, "wg", [P, KC, E1])
        before = f.sb(ctx, "before", [P, E1, E1])
        over, same = (f.sb(ctx, n, [P, E1, E1]) for n in ("over", "same"))
        xn = f.sb(ctx, "xn", [P, NT, D])
        xnT = f.sb(ctx, "xnT", [P, KC, S])
        logits, exps, rank, gates = (f.sb(ctx, n, [P, NT, E1]) for n in ("logits", "exps", "rank", "gates"))
        ntop, zsum = (f.sb(ctx, n, [P, NT]) for n in ("ntop", "zsum"))
        act_in = f.sb(ctx, "act_in", [P, 2, 2, S])
        inner = f.sb(ctx, "inner", [P, 2, NI, S])
        in_ps = f.ps(ctx, "in_ps", [P, 2, 2, 2, S])
        out_ps = f.ps(ctx, "out_ps", [P, 2, NT, D])
        ps = f.ps(ctx, "ps", [P, 2, BANK])
        tiles = lambda n: ps[:, n].rearrange("p (t n) -> p t n", t=NT)
        block = ctx.enter_context(nc.Block())

        @block.sync
        def _(sp):
            sp.dma_start(wg[:], rows_of(i["L1_ffn_w_gate"])).then_inc(s["loaded"], 16)
            sp.dma_start(before[:], i["c_before8"].partition_broadcast(P)).then_inc(s["loaded"], 16)

            def load(e, n):
                for m, src in enumerate((i["L1_ffn_w1"], i["L1_ffn_w3"])):
                    sp.dma_start(w13[:, n, m], src[bass.ds(e, 1)].rearrange("e (c p) n -> p (e c) n", p=P)
                                 ).then_inc(w_loaded[n], 16)
                sp.dma_start(w2[:, n], i["L1_ffn_w2"][bass.ds(e, 1)].rearrange("e (c p) n -> p (e c) n", p=P)
                             ).then_inc(w_loaded[n], 16)

            for n in range(RING1):
                load(n, n)
            with sp.Fori(1, E1 // RING1) as r:
                for n in range(RING1):
                    sp.wait_ge(s["w_free"], (r - 1) * RING1 + n + 1)
                    load(r * RING1 + n, n)

        @block.tensor
        def _(pe):
            pe.sem_inc(s["inner_used"], 2)
            pe.wait_ge(s["xn_ready"], 1)
            transpose_tokens(nc, tiles(0), xn, f.ident[:]).then_inc(s["xnT_mm"], 1)
            pe.wait_ge(s["loaded"], 32)
            pe.wait_ge(s["xnT_sb"], 1)
            for t in range(NT):
                for c in range(KC):
                    mm = nc.tensor.matmul(ps[:, 1, t * E1:(t + 1) * E1], xnT[:, c, t * P:(t + 1) * P], wg[:, c, :],
                                          start=(c == 0), stop=(c == KC - 1))
            mm.then_inc(s["logits_mm"], 1)

            def expert_in(r, n, half):
                if half == 0:
                    pe.wait_ge(w_loaded[n], 48 * (r + 1))
                pe.wait_ge(s["silu_used"], 2 * (RING1 * r + n) + half + 1)
                for m in range(2):
                    for a in range(2):
                        at = (2 * half + a) * P
                        for c in range(KC):
                            mm = nc.tensor.matmul(in_ps[:, half, m, a], w13[:, n, m, c, at:at + P], xnT[:, c, :],
                                                  start=(c == 0), stop=(c == KC - 1))
                mm.then_inc(s["gated_mm"], 1)

            def expert_out(r, n):
                e = RING1 * r + n
                pe.wait_ge(s["inner_done"], 2 * e + 2)
                pe.wait_ge(s["summed"], 2 * e + 2)
                for t in range(NT):
                    for a in range(NI):
                        mm = nc.tensor.matmul(out_ps[:, n, t], inner[:, n, a, t * P:(t + 1) * P], w2[:, n, a, :],
                                              start=(a == 0), stop=(a == NI - 1))
                mm.then_inc(s["out_mm"], 1)
                pe.wait_ge(s["out_mm"], e + 1)
                pe.sem_inc(s["w_free"], 1)
                pe.sem_inc(s["inner_used"], 1)

            expert_in(0, 0, 0)
            with pe.Fori(0, E1 // RING1 - 1) as r:
                for n in range(RING1):
                    expert_in(r, n, 1)
                    expert_in(r + (n + 1) // RING1, (n + 1) % RING1, 0)
                    expert_out(r, n)
            r = E1 // RING1 - 1
            for n in range(RING1):
                expert_in(r, n, 1)
                if n < RING1 - 1:
                    expert_in(r, n + 1, 0)
                expert_out(r, n)

        @block.scalar
        def _(act):
            take_root(f, act, s["var_ready"], s["root_ready"])
            act.wait_ge(s["xnT_mm"], 1)
            nc.scalar.copy(xnT[:], tiles(0)).then_inc(s["xnT_sb"], 1)
            act.wait_ge(s["top_ready"], 1)
            for t in range(NT):
                ins = nc.scalar.activation(exps[:, t], logits[:, t], ACT.Exp, bias=ntop[:, t:t + 1])
            ins.then_inc(s["exp_done"], 1)
            with act.Fori(0, E1 // RING1) as r:
                for n in range(RING1):
                    for half in range(2):
                        u = 2 * (RING1 * r + n) + half
                        act.wait_ge(s["gated_mm"], u + 1)
                        act.wait_ge(s["silu_used"], u + 1)
                        nc.scalar.activation(act_in[:, half], in_ps[:, half, 0], ACT.Silu).then_inc(s["silu_done"], 1)

        @block.vector
        def _(dve):
            step = Chain(dve, s["dve_steps"])
            dve.sem_inc(s["silu_used"], 2)
            dve.sem_inc(s["summed"], 4)
            layer_norm(f, dve, step, xn, f.x, 1e-5, s["var_ready"], s["root_ready"])
            dve.sem_inc(s["xn_ready"], 1)
            dve.wait_ge(s["logits_mm"], 1)
            step(nc.vector.tensor_copy(logits[:], ps[:, 1, 0:NT * E1].rearrange("p (t e) -> p t e", t=NT)))
            step(nc.vector.tensor_reduce(ntop[:], logits[:], AX, ALU.max))
            step(nc.vector.tensor_scalar(ntop[:], ntop[:], -1.0, None, ALU.mult))
            dve.sem_inc(s["top_ready"], 1)
            dve.wait_ge(s["loaded"], 32)
            for t in range(NT):
                route(nc, step, gates[:, t], logits[:, t], before[:], over[:], same[:], rank[:, t], TOP1)
            dve.wait_ge(s["exp_done"], 1)
            for t in range(NT):
                step(nc.vector.scalar_tensor_tensor(out=gates[:, t], in0=rank[:, t], scalar=float(TOP1), in1=exps[:, t],
                                                    op0=ALU.is_lt, op1=ALU.mult))
            step(nc.vector.tensor_reduce(zsum[:], gates[:], AX, ALU.add))
            step(nc.vector.reciprocal(zsum[:], zsum[:]))
            for t in range(NT):
                step(nc.vector.tensor_scalar(gates[:, t], gates[:, t], zsum[:, t:t + 1], None, ALU.mult))

            def multiply(r, n):
                for half in range(2):
                    u = 2 * (RING1 * r + n) + half
                    dve.wait_ge(s["silu_done"], u + 1)
                    if half == 0:
                        dve.wait_ge(s["inner_used"], RING1 * r + n + 1)
                    ins = nc.vector.tensor_tensor(inner[:, n, 2 * half:2 * half + 2], act_in[:, half], in_ps[:, half, 1],
                                                  ALU.mult).then_inc(s["inner_done"], 1)
                    dve.wait_ge(s["inner_done"], u + 1)
                    dve.sem_inc(s["silu_used"], 1)

            def add(r, n):
                e = RING1 * r + n
                dve.wait_ge(s["out_mm"], e + 1)
                for t in range(NT):
                    dve.wait_ge(s["summed"], 2 * e + t + 3)
                    nc.vector.scalar_tensor_tensor(out=f.x[:, t], in0=out_ps[:, n, t], scalar=gates[:, t, bass.ds(e, 1)],
                                                   in1=f.x[:, t], op0=ALU.mult, op1=ALU.add).then_inc(s["summed"], 1)

            with dve.Fori(0, E1 // RING1) as r:
                for n in range(RING1):
                    multiply(r, n)
                    add(r, n)
            dve.wait_ge(s["summed"], 2 * E1 + 4)


def constants():
    c = {}
    c["c_ident"] = np.eye(P, dtype=np.float32)
    inv = np.exp(np.arange(D // 2, dtype=np.float32) * np.float32(-np.log(10000.0) / (D // 2 - 1)))
    st = np.arange(S2 - 1, -1, -1, dtype=np.float32)[None, :] * inv[:, None]
    c["c_sinusoids"] = np.concatenate([np.sin(st), np.cos(st)], 0).astype(np.float32)
    head = (np.arange(D) // DK)
    c["c_head_of"] = (head[:, None] == np.arange(H)[None, :]).astype(np.float32).reshape(KC, P, H).transpose(1, 0, 2)
    r = np.arange(P)
    c["c_gather"] = (r[:, None] % QUAD == np.arange(DV)[None, :]).astype(np.float32)
    inv = 1.0 / 10000.0 ** (np.arange(0, D, 2, dtype=np.float32) / D)
    ang = np.arange(S, dtype=np.float32)[:, None] * inv.astype(np.float32)
    c["c_rope"] = np.stack([np.cos(ang), np.sin(ang)]).astype(np.float32).reshape(2, NT, P, D // 2).transpose(2, 0, 1, 3)
    c["c_same_head"] = (head[:, None] == head[None, :]).astype(np.float32).reshape(KC, P, D).transpose(1, 0, 2)
    c["c_pos"] = np.broadcast_to(np.arange(S, dtype=np.float32), (P, S))
    q = np.arange(NT)[None, :, None] * P + np.arange(P)[:, None, None]
    c["c_causal"] = np.where(np.arange(S)[None, None, :] <= q, 0.0, -1e30).astype(np.float32)
    e = np.arange(E0)
    c["c_before31"] = (e[None, :] < e[:, None]).astype(np.float32).reshape(1, E0, E0)
    e = np.arange(E1)
    c["c_before8"] = (e[None, :] < e[:, None]).astype(np.float32).reshape(1, E1, E1)
    return {k: np.ascontiguousarray(v) for k, v in c.items()}


def columns(a):
    return np.ascontiguousarray(np.reshape(a, (-1, P)).T)


def lay_out(v):
    t = lambda a: np.ascontiguousarray(np.asarray(a).T)
    row = lambda a: np.ascontiguousarray(np.asarray(a).reshape(1, -1))
    col = lambda a: np.ascontiguousarray(np.asarray(a).reshape(-1, 1))
    a = {"x": np.asarray(v["x"]), "ctx_1024": t(np.asarray(v["ctx_1024"])[0])}
    for n in ("Wq", "Wk", "Wv", "Wo", "w1", "w2", "w3"):
        a[f"L0_xattn_{n}"] = t(v[f"L0_xattn_{n}"])
    for n in ("bq", "bk"):
        a[f"L0_xattn_{n}"] = columns(v[f"L0_xattn_{n}"])
    for n in ("bv", "bo", "b3"):
        a[f"L0_xattn_{n}"] = row(v[f"L0_xattn_{n}"])
    for n in ("b1", "b2"):
        a[f"L0_xattn_{n}"] = col(v[f"L0_xattn_{n}"])
    for n in ("Wq", "Wk", "Wv", "Wp", "Wo"):
        a[f"L1_xattn_{n}"] = np.asarray(v[f"L1_xattn_{n}"])
    for n in ("bk", "bp", "bq"):
        a[f"L1_xattn_{n}"] = columns(v[f"L1_xattn_{n}"])
    for n in ("bv", "bo"):
        a[f"L1_xattn_{n}"] = row(v[f"L1_xattn_{n}"])
    for n in "qkv":
        a[f"L0_attn_W{n}"] = t(v[f"L0_attn_W{n}"])
        a[f"L0_attn_b{n}"] = row(v[f"L0_attn_b{n}"])
    for n in ("gamma", "beta"):
        a[f"L0_attn_{n}"] = row(v[f"L0_attn_{n}"])
    n = "L0_ffn_"
    turned = lambda w: np.ascontiguousarray(np.asarray(w).reshape(-1, H // 4, 4, HD // 2, 2).transpose(0, 1, 4, 2, 3)
                                            ).reshape(-1, H * HD)
    a[n + "q_w"], a[n + "k_w"] = turned(v[n + "q_w"]), turned(v[n + "k_w"])
    a[n + "qk_b"] = np.ascontiguousarray(np.stack([columns(turned(v[n + b])) for b in ("q_b", "k_b")], 1))
    for m in ("v_w", "o_w", "router_w"):
        a[n + m] = np.asarray(v[n + m])
    for m in ("v_b", "o_b", "router_b", "gamma1", "gamma2"):
        a[n + m] = row(v[n + m])
    a[n + "theta"] = col(v[n + "theta"])
    both = lambda x, y: np.concatenate([np.asarray(x), np.asarray(y)[None]])
    w1 = both(v[n + "re_w1"], v[n + "sh_w1"]).reshape(EXPERTS0, KC, P, I0)
    w2 = both(v[n + "re_w2"], v[n + "sh_w2"]).reshape(EXPERTS0, I0 // P, P, D)
    b1 = both(v[n + "re_b1"], v[n + "sh_b1"]).reshape(EXPERTS0, I0 // P, P, 1)
    a[n + "e_w"] = np.ascontiguousarray(np.concatenate(
        [y.transpose(0, 2, 1, 3).reshape(EXPERTS0, P, -1) for y in (w1, w2, b1)], 2))
    a[n + "e_b2"] = both(v[n + "re_b2"], v[n + "sh_b2"])
    a["L1_xattn_bcols"] = np.ascontiguousarray(np.stack(
        [columns(v[f"L1_xattn_{m}"]) for m in ("bq", "r_w_bias", "r_r_bias")], 1))
    a["mask"] = np.asarray(v["mask_Bx1xSxS2_ff1"]).reshape(S, S2)
    for m in ("attn_Wq", "attn_Wkv", "attn_Wout", "ffn_w_gate", "ffn_w1", "ffn_w3", "ffn_w2"):
        a[f"L1_{m}"] = np.asarray(v[f"L1_{m}"])
    for m in ("norm_g", "out_norm_g"):
        a[f"L1_attn_{m}"] = row(v[f"L1_attn_{m}"])
    return a


LAYERS = [cross0, linear_attn, block0, cross1, multi_query, mixture1]


def run(f, layer):
    f.sems = []
    layer(f)
    f.nc.clear_and_free_semaphores(f.sems)
    f.nc.all_engine_barrier()


def build(nc, ins, out):
    with ExitStack() as ctx:
        f = Frame(nc, ctx, ins, out)
        f.key_parts = nc.dram_tensor("key_parts", (3, 3, D, S2), BF16, kind="Internal").ap()
        f.key_heads = f.key_parts.rearrange("m s (h d) n -> m s h d n", d=DK)
        f.query_parts = nc.dram_tensor("query_parts", (3, 3, D, S), BF16, kind="Internal").ap()
        f.value_rows = nc.dram_tensor("value_rows", (2, H, P, NCH, DV), F32, kind="Internal").ap()
        f.max_parts = nc.dram_tensor("max_parts", (3, H * S), BF16, kind="Internal").ap()
        f.rel_dram = nc.dram_tensor("rel_scores", (H, S * PITCH), F32, kind="Internal").ap()
        f.x = f.sb(ctx, "x", [P, NT, D])
        f.ident = f.sb(ctx, "ident", [P, P])
        f.ones = f.sb(ctx, "ones", [P, P])
        f.stats = f.sb(ctx, "stats", [P, NT, 6])
        f.mv = f.sb(ctx, "mv", [P, NT, 2])
        f.rstd = f.sb(ctx, "rstd", [P, NT])
        f.key_sums = f.sb(ctx, "key_sums", [P, KC, NQU])
        for layer in LAYERS:
            run(f, layer)
        f.layer, f.sems = "end", []
        stored = f.sem("stored")
        block = ctx.enter_context(nc.Block())

        @block.sync
        def _(sp):
            sp.dma_start(out.rearrange("b (t p) d -> p (b t) d", p=P), f.x[:]).then_inc(stored, 16)
            sp.wait_ge(stored, 16)


def kernel(**inputs):
    import concourse.bacc as bacc
    from concourse.bass_utils import run_bass_kernel_spmd

    nc = bacc.Bacc("TRN2", target_bir_lowering=False, num_devices=1)
    arrays = {**lay_out(inputs), **constants()}
    ins = {n: nc.dram_tensor(f"in_{n}", a.shape, mybir.dt.from_np(a.dtype), kind="ExternalInput").ap()
           for n, a in arrays.items()}
    out = nc.dram_tensor("out_x", (1, S, D), F32, kind="ExternalOutput").ap()
    build(nc, ins, out)
    r = run_bass_kernel_spmd(nc, [{f"in_{n}": a for n, a in arrays.items()}], core_ids=[0])
    return r.results[0]["out_x"]
```

```python
from contextlib import ExitStack

import numpy as np

import concourse.bass as bass
from concourse import mybir

F32 = mybir.dt.float32
BF16 = mybir.dt.bfloat16
ALU = mybir.AluOpType
ACT = mybir.ActivationFunctionType
AX = mybir.AxisListType.X

P = 128
S = 256
D = 256
NT = S // P
KC = D // P
S2 = 4096
NCH = S2 // P
NHALF = 2
HALF = S2 // NHALF
H = 16
DK = D // H
DV = DK + 1
QUAD = 32
NQ4 = P // QUAD
QUARTER = S2 // 4
NQU = S2 // QUARTER
ROWS = 6 * DK
MAXROWS = ROWS + 3
BANK = 512
LOG_T_MIN, LOG_T_MAX = float(np.log(0.1)), float(np.log(10.0))
Q_PARTS = (0, 1, 2, 0, 1, 0)
K_TIMES = ((0, 3), (1, 2), (2, 1))
KEYS_IN = 16 * len(K_TIMES)


class Chain:

    def __init__(self, eng, sem, base=0):
        self.eng, self.sem, self.n, self.base = eng, sem, 0, base

    def __call__(self, ins):
        self.n += 1
        ins.then_inc(self.sem, 1)
        self.eng.wait_ge(self.sem, self.base + self.n)


class Frame:

    def __init__(self, nc, ctx, ins, out):
        self.nc, self.ctx, self.ins, self.out = nc, ctx, ins, out
        self.layer, self.sems = "", []

    def sb(self, ctx, name, shape, dt=F32):
        return ctx.enter_context(self.nc.sbuf_tensor(f"{self.layer}_{name}", shape, dt))

    def ps(self, ctx, name, shape, dt=F32):
        return ctx.enter_context(self.nc.psum_tensor(f"{self.layer}_{name}", shape, dt))

    def sem(self, name):
        self.sems.append(self.nc.alloc_semaphore(name=f"{self.layer}_{name}"))
        return self.sems[-1]


def rows_of(dram):
    return dram.rearrange("(c p) n -> p c n", p=P)


def load_query_parts(f, sp, dst, which, loaded):
    for r, part in enumerate(Q_PARTS):
        src = f.query_parts[which, part].rearrange("(h d) n -> d h n", d=DK)
        sp.dma_start(dst[r * DK:(r + 1) * DK], src).then_inc(loaded, 16)


def load_key_parts(f, sp, dst, which, head, loaded, pieces=range(len(K_TIMES))):
    for n in pieces:
        part, times = K_TIMES[n]
        at = DK * sum(times for _, times in K_TIMES[:n])
        src = f.key_heads[which, part, bass.ds(head, 1)].to_broadcast([times, DK, S2])
        sp.dma_start(dst[at:at + times * DK], src).then_inc(loaded, 16)


def layer_norm(f, dve, step, y, x, eps, var_ready, root_ready, n=0):
    nc = f.nc
    for t in range(NT):
        step(nc.vector.bn_stats(f.stats[:, t, :], x[:, t, :]))
        step(nc.vector.bn_aggr(f.mv[:, t, :], f.stats[:, t, :]))
    nc.vector.tensor_scalar(f.rstd[:], f.mv[:, :, 1], eps, None, ALU.add).then_inc(var_ready, 1)
    dve.wait_ge(root_ready, n + 1)
    step(nc.vector.reciprocal(f.rstd[:], f.rstd[:]))
    for t in range(NT):
        step(nc.vector.tensor_scalar(y[:, t, :], x[:, t, :], f.mv[:, t, 0:1], f.rstd[:, t:t + 1],
                                     ALU.subtract, ALU.mult))


def take_root(f, act, var_ready, root_ready, n=0):
    act.wait_ge(var_ready, n + 1)
    f.nc.scalar.sqrt(f.rstd[:], f.rstd[:]).then_inc(root_ready, 1)


def transpose_tokens(nc, out_ps, y, ident):
    for c in range(y.shape[2] // P):
        for t in range(NT):
            last = nc.tensor.transpose(out_ps[:, c, t * P:(t + 1) * P], y[:, t, c * P:(c + 1) * P], ident)
    return last


def cross0(f):
    nc, i = f.nc, f.ins
    f.layer = "xa"
    parts_stored, q_loaded, k_free, kb_free = (f.sem(n) for n in ("parts_stored", "q_loaded", "k_free", "kb_free"))
    k_loaded = [f.sem(f"k_loaded{b}") for b in range(2)]
    kb_loaded = [f.sem(f"kb_loaded{b}") for b in range(2)]
    scoredT, probs_ready, probs_used, pv_done, pv_read = (
        f.sem(n) for n in ("scoredT", "probs_ready", "probs_used", "pv_done", "pv_read"))
    recip_done, sums_free = f.sem("recip_done"), f.sem("sums_free")
    small_loaded, later_loaded, sin_loaded = (f.sem(n) for n in ("small_loaded", "later_loaded", "sin_loaded"))
    with ExitStack() as ctx:
        wq = f.sb(ctx, "wq", [P, KC, D])
        wo = f.sb(ctx, "wo", [P, KC, D])
        bq = f.sb(ctx, "bq", [P, KC])
        bo = f.sb(ctx, "bo", [1, D])
        w1b = f.sb(ctx, "w1b", [P, 3, 64])
        w2 = f.sb(ctx, "w2", [64, 64])
        w3 = f.sb(ctx, "w3", [64, 1])
        w3b = f.sb(ctx, "w3b", [64, P])
        b1 = f.sb(ctx, "b1", [64, 1])
        b2 = f.sb(ctx, "b2", [64, 1])
        b3 = f.sb(ctx, "b3", [P, 1])
        head_of = f.sb(ctx, "head_of", [P, KC, H])
        xn = f.sb(ctx, "xn", [P, NT, D])
        xnT = f.sb(ctx, "xnT", [P, KC, S])
        q = f.sb(ctx, "q", [P, KC, S])
        qrest = f.sb(ctx, "qrest", [P, KC, S])
        qparts = f.sb(ctx, "qparts", [P, 3, KC, S], BF16)
        q_sums = f.sb(ctx, "q_sums", [P, KC])
        k_sums = f.sb(ctx, "k_sums", [P, KC])
        qk_sum = f.sb(ctx, "qk_sum", [P, KC, H])
        q96 = f.sb(ctx, "q96", [P, H, S], BF16)
        k96 = f.sb(ctx, "k96", [P, 2, S2], BF16)
        NU = NT * NQU
        stats_all = f.sb(ctx, "stats_all", [P, H, 3, NU])
        minima, zs, es = (stats_all[:, :, k] for k in range(3))
        m_all = f.sb(ctx, "m_all", [P, H, NT])
        wgt = f.sb(ctx, "wgt", [P, H, NU])
        z_all = f.sb(ctx, "z_all", [P, H, NT])
        e_all = f.sb(ctx, "e_all", [P, H, NT])
        mneg = f.sb(ctx, "mneg", [P, H * NT])
        mrow = f.sb(ctx, "mrow", [H * NT, P])
        mrest = f.sb(ctx, "mrest", [H * NT, P])
        mparts = f.sb(ctx, "mparts", [H * NT, 3, P], BF16)
        hid1 = f.sb(ctx, "hid1", [64, H])
        hid2 = f.sb(ctx, "hid2", [64, H])
        logt = f.sb(ctx, "logt", [P, H])
        tscale = f.sb(ctx, "tscale", [P, H + 2])
        t_now = f.sb(ctx, "t_now", [P, 2])
        bv = f.sb(ctx, "bv", [P, D])
        GC = 4
        NG = NCH // GC
        UNITS = H * NG
        attn = f.sb(ctx, "attn", [P, NT, H, DK])
        attnT = f.sb(ctx, "attnT", [P, KC, S])
        both_passes = ctx.enter_context(ExitStack())
        ctxT = f.sb(both_passes, "ctxT", [P, KC, S2])
        sinT = f.sb(both_passes, "sinT", [P, KC, S2])
        wk = f.sb(both_passes, "wk", [P, 3, KC, D])
        wv = f.sb(both_passes, "wv", [P, 2 * KC, KC, P])
        bcol = f.sb(both_passes, "bcol", [P, 3, KC])
        whole = f.sb(both_passes, "whole", [P, 2, QUARTER])
        rest = f.sb(both_passes, "rest", [P, QUARTER])
        parts = f.sb(both_passes, "parts", [P, 4, 3, QUARTER], BF16)
        key_groups = [(g, t) for t in range(KC) for g in range(NQU)]
        stored = [f.sem(f"key_stored{b}") for b in range(4)]

        with ExitStack() as inner:
            s = {n: f.sem("a_" + n) for n in ("x_loaded", "q_w_loaded", "k_w_loaded", "var_ready", "root_ready", "dve_steps",
                                              "xn_ready", "xnT_mm", "xnT_sb", "q_mm", "q_read", "q_split", "projected",
                                              "evacuated", "rest_done", "second_done", "split_done", "ones_set")}
            ctx_loaded = [f.sem(f"a_ctx_loaded{g}") for g in range(NQU)]
            block = inner.enter_context(nc.Block())
            ps = f.ps(inner, "a_ps", [P, 4, QUARTER])

            @block.sync
            def _(sp):
                sp.dma_start(f.x[:], i["x"].rearrange("b (t p) d -> p (b t) d", p=P)).then_inc(s["x_loaded"], 16)
                sp.dma_start(f.ident[:], i["c_ident"]).then_inc(s["x_loaded"], 16)
                sp.dma_start(wq[:], rows_of(i["L0_xattn_Wq"])).then_inc(s["q_w_loaded"], 16)
                sp.dma_start(bq[:], i["L0_xattn_bq"]).then_inc(s["q_w_loaded"], 16)
                sp.dma_start(wk[:, 0], rows_of(i["L0_xattn_Wk"])).then_inc(s["k_w_loaded"], 16)
                sp.dma_start(bcol[:, 0], i["L0_xattn_bk"]).then_inc(s["k_w_loaded"], 16)
                for g in range(NQU):
                    sp.dma_start(ctxT[:, :, g * QUARTER:(g + 1) * QUARTER],
                                 rows_of(i["ctx_1024"])[:, :, g * QUARTER:(g + 1) * QUARTER]).then_inc(ctx_loaded[g], 16)
                sp.wait_ge(s["q_split"], 1)
                for part in range(3):
                    sp.dma_start(f.query_parts[0, part].rearrange("(c p) n -> p c n", p=P),
                                 qparts[:, part]).then_inc(parts_stored, 16)
                sp.wait_ge(parts_stored, 48)
                load_query_parts(f, sp, q96, 0, q_loaded)
                for n, name in enumerate(("L1_xattn_Wk", "L1_xattn_Wp")):
                    sp.dma_start(wk[:, 1 + n], rows_of(i[name])).then_inc(later_loaded, 16)
                for n, name in enumerate(("L1_xattn_bk", "L1_xattn_bp")):
                    sp.dma_start(bcol[:, 1 + n], i[name]).then_inc(later_loaded, 16)
                for m in range(2):
                    for t in range(KC):
                        sp.dma_start(wv[:, m * KC + t], rows_of(i[f"L{m}_xattn_Wv"])[:, :, t * P:(t + 1) * P]
                                     ).then_inc(later_loaded, 16)
                for n, (g, t) in enumerate(key_groups):
                    sp.wait_ge(s["split_done"], n + 1)
                    dst = f.key_parts[0, :, t * P:(t + 1) * P, g * QUARTER:(g + 1) * QUARTER]
                    sp.dma_start(dst.rearrange("s p n -> p s n"), parts[:, n % 4]).then_inc(stored[n % 4], 16)
                    if n == NQU - 1:
                        for b in range(4):
                            sp.wait_ge(stored[b], 16)
                        for h in range(2):
                            load_key_parts(f, sp, k96[0:ROWS, h], 0, h, k_loaded[h])
                sp.wait_ge(q_loaded, 96)

            @block.tensor
            def _(pe):
                pe.wait_ge(s["x_loaded"], 32)
                pe.wait_ge(s["xn_ready"], 1)
                flat = ps[:, 0, 0:KC * S].rearrange("p (c n) -> p c n", c=KC)
                transpose_tokens(nc, flat, xn, f.ident[:]).then_inc(s["xnT_mm"], 1)
                pe.wait_ge(s["q_w_loaded"], 32)
                pe.wait_ge(s["xnT_sb"], 1)
                for m in range(KC):
                    for c in range(KC):
                        mm = nc.tensor.matmul(ps[:, 1, m * S:(m + 1) * S], wq[:, c, m * P:(m + 1) * P], xnT[:, c, :],
                                              start=(c == 0), stop=(c == KC - 1))
                mm.then_inc(s["q_mm"], 1)
                pe.wait_ge(s["k_w_loaded"], 32)
                for n, (g, t) in enumerate(key_groups):
                    pe.wait_ge(ctx_loaded[g], 16)
                    if n == 2:
                        pe.wait_ge(s["q_read"], 1)
                    if n >= 4:
                        pe.wait_ge(s["evacuated"], n - 3)
                    for k in range(QUARTER // BANK):
                        for c in range(KC):
                            at = g * QUARTER + k * BANK
                            mm = nc.tensor.matmul(ps[:, (n + 2) % 4, k * BANK:(k + 1) * BANK],
                                                  wk[:, 0, c, t * P:(t + 1) * P], ctxT[:, c, at:at + BANK],
                                                  start=(c == 0), stop=(c == KC - 1))
                    mm.then_inc(s["projected"], 1)

            @block.gpsimd
            def _(pool):
                nc.gpsimd.memset(k96[ROWS:MAXROWS], 1.0).then_inc(s["ones_set"], 1)
                pool.wait_ge(s["ones_set"], 1)

            @block.scalar
            def _(act):
                take_root(f, act, s["var_ready"], s["root_ready"])
                act.wait_ge(s["xnT_mm"], 1)
                nc.scalar.copy(xnT[:], ps[:, 0, 0:KC * S].rearrange("p (c n) -> p c n", c=KC)).then_inc(s["xnT_sb"], 1)
                act.wait_ge(s["k_w_loaded"], 32)
                for n, (g, t) in enumerate(key_groups):
                    act.wait_ge(s["projected"], n + 1)
                    if n >= 2:
                        act.wait_ge(s["split_done"], n - 1)
                    if n >= 4:
                        act.wait_ge(stored[n % 4], 16 * (n // 4))
                    nc.scalar.activation(whole[:, n % 2], ps[:, (n + 2) % 4], ACT.Identity, bias=bcol[:, 0, t:t + 1],
                                         accum_out=f.key_sums[:, t, g:g + 1])
                    nc.scalar.activation(parts[:, n % 4, 0], ps[:, (n + 2) % 4], ACT.Identity,
                                         bias=bcol[:, 0, t:t + 1]).then_inc(s["evacuated"], 1)

            @block.vector
            def _(dve):
                step = Chain(dve, s["dve_steps"])
                step(nc.vector.memset(f.ones[:], 1.0))
                dve.wait_ge(s["x_loaded"], 32)
                layer_norm(f, dve, step, xn, f.x, 1e-5, s["var_ready"], s["root_ready"])
                dve.sem_inc(s["xn_ready"], 1)
                dve.wait_ge(s["q_w_loaded"], 32)
                dve.wait_ge(s["q_mm"], 1)
                for m in range(KC):
                    step(nc.vector.tensor_scalar(q[:, m], ps[:, 1, m * S:(m + 1) * S], bq[:, m:m + 1], -DK ** -0.5,
                                                 ALU.add, ALU.mult))
                dve.sem_inc(s["q_read"], 1)
                step(nc.vector.tensor_copy(qparts[:, 0], q[:]))
                step(nc.vector.tensor_tensor(qrest[:], q[:], qparts[:, 0], ALU.subtract))
                step(nc.vector.tensor_copy(qparts[:, 1], qrest[:]))
                step(nc.vector.tensor_tensor(qparts[:, 2], qrest[:], qparts[:, 1], ALU.subtract))
                dve.sem_inc(s["q_split"], 1)
                step(nc.vector.tensor_reduce(q_sums[:], q[:], AX, ALU.add))
                for n in range(len(key_groups)):
                    dve.wait_ge(s["evacuated"], n + 1)
                    if n >= 1:
                        dve.wait_ge(s["split_done"], n)
                    nc.vector.tensor_tensor(rest[:], whole[:, n % 2], parts[:, n % 4, 0], ALU.subtract
                                            ).then_inc(s["rest_done"], 1)
                    dve.wait_ge(s["rest_done"], n + 1)
                    nc.vector.tensor_copy(parts[:, n % 4, 1], rest[:]).then_inc(s["second_done"], 1)
                    dve.wait_ge(s["second_done"], n + 1)
                    nc.vector.tensor_tensor(parts[:, n % 4, 2], rest[:], parts[:, n % 4, 1], ALU.subtract
                                            ).then_inc(s["split_done"], 1)

        with ExitStack() as inner:
            HPB = 2 * KC
            NB = H // HPB
            CPH = NCH // HPB
            SLOTS = NU + NU // 2
            exps = f.sb(inner, "exps", [P, 4, QUARTER])
            squares = f.sb(inner, "squares", [P, 2, QUARTER])
            stats = f.sb(inner, "stats", [P, 2, 3, NU])
            values = f.sb(inner, "values", [P, 2, H // 2, CPH, DV])
            s = {n: f.sem("b_" + n) for n in ("scored", "projected", "product_out", "min_ready", "exp_done", "even_squared",
                                              "odd_squared", "kept", "split_steps", "split_done",
                                              "ones_set", "squares_begun", "split_begun")}
            parts_out = [f.sem(f"b_parts_out{b}") for b in range(2)]
            values_stored = [f.sem(f"b_values_stored{b}") for b in range(2)]
            block = inner.enter_context(nc.Block())
            ps = f.ps(inner, "b_ps", [P, 4, QUARTER])

            def bodies(eng, body):
                body(0, True)
                with eng.Fori(1, NB) as it:
                    body(it, False)

            @block.sync
            def _(sp):
                key_stores = f.key_parts[:, :, :, :].rearrange("m s (t p) (g n) -> m t g p s n", p=P, g=NB)
                value_stores = f.value_rows.rearrange("m (t h) p k d -> (m t) p h k d", t=KC)
                sp.sem_inc(k_free, 2)
                for b in range(4):
                    sp.wait_ge(stored[b], 16 * len(key_groups) // 4)
                for b in range(2):
                    sp.sem_inc(parts_out[b], 16)

                def load_small():
                    small = [(wo[:], rows_of(i["L0_xattn_Wo"])), (bo[:], i["L0_xattn_bo"]),
                             (bv[:], i["L0_xattn_bv"].partition_broadcast(P)),
                             (w2[:], i["L0_xattn_w2"]), (w3[:], i["L0_xattn_w3"]),
                             (b1[:], i["L0_xattn_b1"]), (b2[:], i["L0_xattn_b2"]),
                             (b3[:], i["L0_xattn_b3"].partition_broadcast(P)), (head_of[:], i["c_head_of"]),
                             (w1b[:], i["L0_xattn_w1"].partition_broadcast(P))]
                    for dst, src in small:
                        sp.dma_start(dst, src).then_inc(small_loaded, 16)

                def store(it, c):
                    b = c % 2
                    sp.wait_ge(s["split_done"], HPB * it + c + 3)
                    sp.dma_start(key_stores[1 + c // KC, c % KC][bass.ds(it, 1)].rearrange("g p s n -> p (g s) n"),
                                 parts[:, b]).then_inc(parts_out[b], 16)
                    sp.wait_ge(s["product_out"], NU // 2 * (HPB * it + c + 2))
                    dst = value_stores[bass.ds(it, 1), :, :, c * CPH:(c + 1) * CPH, :]
                    sp.dma_start(dst.rearrange("m p h k d -> p (m h) k d"), values[:, b]).then_inc(values_stored[b], 16)

                def body(it, first):
                    for c in range(HPB):
                        if not first or c >= 2:
                            sp.wait_ge(k_free, HPB * it + c + 1)
                            load_key_parts(f, sp, k96[0:ROWS, c % 2], 0, HPB * it + c, k_loaded[c % 2])
                        if first and c == 1:
                            for g in range(NQU):
                                sp.dma_start(sinT[:, :, g * QUARTER:(g + 1) * QUARTER],
                                             rows_of(i["c_sinusoids"])[:, :, g * QUARTER:(g + 1) * QUARTER]
                                             ).then_inc(sin_loaded, 16)
                            load_small()
                        if c >= 2:
                            store(it, c - 2)
                        elif not first:
                            store(it - 1, c - 2 + HPB)

                bodies(sp, body)
                for c in (HPB - 2, HPB - 1):
                    store(NB - 1, c)

            @block.tensor
            def _(pe):
                pe.wait_ge(later_loaded, 16 * (4 + 2 * KC))

                def buffer_free(h, slot):
                    h, slot = (h, slot - 4) if slot >= 4 else (h - 1, slot - 4 + SLOTS)
                    j, u = slot // 3, 2 * (slot // 3) + slot % 3
                    if slot % 3 == 2:
                        pe.wait_ge(s["product_out"], NU // 2 * (h + 1) + j + 1)
                    else:
                        pe.wait_ge(s["exp_done"], NU * (h + 1) + u + 1)

                def scores(it, c, u):
                    h, slot = HPB * it + c, u + u // 2
                    buffer_free(h, slot)
                    t, g = u // NQU, u % NQU
                    for k in range(QUARTER // BANK):
                        at = g * QUARTER + k * BANK
                        mm = nc.tensor.matmul(ps[:, slot % 4, k * BANK:(k + 1) * BANK],
                                              q96[0:ROWS, bass.ds(h, 1), t * P:(t + 1) * P],
                                              k96[0:ROWS, c % 2, at:at + BANK], start=True, stop=True)
                    mm.then_inc(s["scored"], 1)

                def product(it, c, j):
                    h, slot = HPB * it + c, 3 * j + 2
                    buffer_free(h, slot)
                    out = ps[:, slot % 4, 0:BANK]
                    if j < 2:
                        src = (ctxT, sinT)[c // KC]
                        if src is sinT and j == 0:
                            pe.wait_ge(sin_loaded, 16 * NQU)
                        for k in range(KC):
                            mm = nc.tensor.matmul(out, wk[:, 1 + c // KC, k, c % KC * P:(c % KC + 1) * P],
                                                  src[:, k, bass.ds(it * QUARTER + j * BANK, BANK)],
                                                  start=(k == 0), stop=(k == KC - 1))
                    else:
                        for n in range(CPH // 2):
                            at = (c * CPH + (j - 2) * CPH // 2 + n) * P
                            for k in range(KC):
                                mm = nc.tensor.matmul(out[:, n * P:(n + 1) * P], ctxT[:, k, at:at + P],
                                                      wv[:, bass.ds(it, 1), k, :], start=(k == 0), stop=(k == KC - 1))
                    mm.then_inc(s["projected"], 1)

                with pe.Fori(0, NB) as it:
                    for c in range(HPB):
                        pe.wait_ge(k_loaded[c % 2], KEYS_IN * (it * HPB // 2 + c // 2 + 1))
                        for j in range(NU // 2):
                            scores(it, c, 2 * j)
                            scores(it, c, 2 * j + 1)
                            product(it, c, j)
                        pe.wait_ge(s["scored"], (HPB * it + c + 1) * NU)
                        pe.sem_inc(k_free, 1)

            @block.scalar
            def _(act):
                act.sem_inc(s["exp_done"], NU)
                act.sem_inc(s["product_out"], NU // 2)
                act.sem_inc(s["even_squared"], 2)
                act.wait_ge(s["ones_set"], 1)

                def exponential(it, c, u):
                    h, slot = HPB * it + c, u + u // 2
                    act.wait_ge(s["min_ready"], NU * h + u + 1)
                    act.wait_ge(s["odd_squared" if u % 2 else "even_squared"], NU // 2 * h + u // 2 + 1)
                    act.nop()
                    nc.scalar.activation(exps[:, u % 4], ps[:, slot % 4], ACT.Exp, scale=-1.0,
                                         bias=stats[:, c % 2, 0, u:u + 1], accum_out=stats[:, c % 2, 1, u:u + 1]
                                         ).then_inc(s["exp_done"], 1)

                def square(it, c, u):
                    h = HPB * it + c
                    act.wait_ge(s["exp_done"], NU * (h + 1) + u + 1)
                    act.wait_ge(s["even_squared"], NU // 2 * h + u // 2 + 2)
                    act.nop()
                    nc.scalar.activation(squares[:, 0], exps[:, u % 4], ACT.Square,
                                         accum_out=stats[:, c % 2, 2, u:u + 1]).then_inc(s["even_squared"], 1)

                def product_out(it, c, j):
                    h, slot = HPB * it + c, 3 * j + 2
                    act.wait_ge(s["projected"], NU // 2 * h + j + 1)
                    src = ps[:, slot % 4, 0:BANK]
                    if j < 2:
                        if j == 0:
                            act.wait_ge(s["split_done"], h + 1)
                        act.nop()
                        nc.scalar.activation(whole[:, c % 2, j * BANK:(j + 1) * BANK], src, ACT.Identity,
                                             bias=bcol[:, 1 + c // KC, c % KC:c % KC + 1]).then_inc(s["product_out"], 1)
                    else:
                        if j == 2:
                            act.wait_ge(values_stored[c % 2], 16 * (it * HPB // 2 + c // 2 + 1))
                        half = CPH // 2
                        dst = values[:, c % 2, :, (j - 2) * half:(j - 1) * half, 0:DK]
                        act.nop()
                        nc.scalar.copy(dst, src.rearrange("p (k h d) -> p h k d", k=half, h=H // 2)
                                       ).then_inc(s["product_out"], 1)

                with act.Fori(0, NB) as it:
                    for c in range(HPB):
                        act.wait_ge(s["kept"], HPB * it + c + 1)
                        for j in range(NU // 2):
                            exponential(it, c, 2 * j)
                            exponential(it, c, 2 * j + 1)
                            square(it, c, 2 * j)
                            product_out(it, c, j)

            @block.vector
            def _(dve):
                nc.vector.memset(values[:, :, :, :, DK:DV], 1.0).then_inc(s["ones_set"], 1)
                dve.sem_inc(s["odd_squared"], 2)
                dve.sem_inc(s["kept"], 2)

                def minimum(it, c, u):
                    h, slot = HPB * it + c, u + u // 2
                    dve.wait_ge(s["scored"], NU * h + u + 1)
                    nc.vector.tensor_reduce(stats[:, c % 2, 0, u:u + 1], ps[:, slot % 4], AX, ALU.min
                                            ).then_inc(s["min_ready"], 1)

                def square(it, c, u):
                    h = HPB * it + c
                    dve.wait_ge(s["exp_done"], NU * (h + 1) + u + 1)
                    dve.wait_ge(s["odd_squared"], NU // 2 * h + u // 2 + 2)
                    dve.sem_inc(s["squares_begun"], 1)
                    nc.vector.tensor_tensor_reduce(out=squares[:, 1], in0=exps[:, u % 4], in1=exps[:, u % 4], scale=1.0,
                                                   scalar=0.0, op0=ALU.mult, op1=ALU.add,
                                                   accum_out=stats[:, c % 2, 2, u:u + 1]).then_inc(s["odd_squared"], 1)

                def keep(it, c):
                    h = HPB * it + c
                    """Keeps the statistics of a head when all are there."""
                    dve.wait_ge(s["odd_squared"], NU // 2 * (h + 1) + 2)
                    dve.wait_ge(s["even_squared"], NU // 2 * (h + 1) + 2)
                    dve.wait_ge(s["exp_done"], NU * (h + 2))
                    nc.vector.tensor_scalar(stats_all[:, bass.ds(h, 1)].rearrange("p h k u -> p (h k) u"), stats[:, c % 2],
                                            1.0, None, ALU.mult).then_inc(s["kept"], 1)

                def body(it, first):
                    for c in range(HPB):
                        dve.wait_ge(s["kept"], HPB * it + c + 1)
                        for j in range(NU // 2):
                            minimum(it, c, 2 * j)
                            if j > 0:
                                square(it, c, 2 * j - 1)
                            elif c > 0:
                                square(it, c - 1, NU - 1)
                            elif not first:
                                square(it - 1, HPB - 1, NU - 1)
                            minimum(it, c, 2 * j + 1)
                            if j == 1 and c > 0:
                                keep(it, c - 1)
                            elif j == 1 and not first:
                                keep(it - 1, HPB - 1)

                bodies(dve, body)
                square(NB - 1, HPB - 1, NU - 1)
                keep(NB - 1, HPB - 1)
                dve.wait_ge(s["kept"], H + 2)

            @block.gpsimd
            def _(pool):
                pool.sem_inc(s["split_done"], 2)
                for b in range(2):
                    pool.sem_inc(values_stored[b], 16)

                def split(it, c):
                    h, b = HPB * it + c, c % 2
                    pool.wait_ge(s["product_out"], NU // 2 * (h + 1) + 2)
                    pool.wait_ge(parts_out[b], 16 * (it * HPB // 2 + c // 2 + 1))
                    steps = [lambda: nc.gpsimd.tensor_scalar(parts[:, b, 0], whole[:, b], 1.0, None, ALU.mult),
                             lambda: nc.gpsimd.tensor_tensor(rest[:], whole[:, b], parts[:, b, 0], ALU.subtract),
                             lambda: nc.gpsimd.tensor_scalar(parts[:, b, 1], rest[:], 1.0, None, ALU.mult),
                             lambda: nc.gpsimd.tensor_tensor(parts[:, b, 2], rest[:], parts[:, b, 1], ALU.subtract)]
                    for n, piece in enumerate(steps):
                        pool.sem_inc(s["split_begun"], 1)
                        piece().then_inc(s["split_steps"], 1)
                        pool.wait_ge(s["split_steps"], len(steps) * h + n + 1)
                    pool.sem_inc(s["split_done"], 1)

                with pool.Fori(0, NB) as it:
                    for c in range(HPB):
                        split(it, c)

        both_passes.close()
        vhead = f.sb(ctx, "vhead", [P, 2, NCH, DV])
        gather = f.sb(ctx, "gather", [P, DV])
        g_loaded = f.sem("g_loaded")

        def load_head(sp, head, b):
            load_key_parts(f, sp, k96[0:ROWS, b], 0, head, kb_loaded[b])
            sp.dma_start(vhead[:, b:b + 1], f.value_rows[0, bass.ds(head, 1)].rearrange("h p k d -> p h k d")
                         ).then_inc(kb_loaded[b], 16)

        with ExitStack() as inner:
            block = inner.enter_context(nc.Block())
            small = f.ps(inner, "small", [P, 4, BANK])
            featured, hid_mm, hid_act, t_mm, t_ready = (
                f.sem(n) for n in ("featured", "hid_mm", "hid_act", "t_mm", "t_ready"))
            m_T, m_split, m_stored, m_loaded, w_in, w_out, w3_set = (
                f.sem(n) for n in ("m_T", "m_split", "m_stored", "m_loaded", "w_in", "w_out", "w3_set"))
            dve_steps2 = f.sem("dve_steps2")

            @block.sync
            def _(sp):
                for b in range(2):
                    sp.wait_ge(values_stored[b], 16 * H // 2 + 16)
                    sp.wait_ge(parts_out[b], 16 * H // 2 + 16)
                load_head(sp, 0, 0)
                sp.dma_start(gather[:], i["c_gather"]).then_inc(g_loaded, 16)
                sp.wait_ge(m_split, 1)
                sp.dma_start(f.max_parts.rearrange("s (r p) -> r s p", p=P), mparts[:]).then_inc(m_stored, 16)
                sp.wait_ge(m_stored, 16)
                sp.dma_start(q96[ROWS:MAXROWS], f.max_parts.rearrange("s (h n) -> s h n", h=H)).then_inc(m_loaded, 16)
                load_head(sp, 1, 1)
                sp.wait_ge(m_loaded, 16)

            @block.vector
            def _(dve):
                step = Chain(dve, dve_steps2)
                dve.wait_ge(small_loaded, 160)
                step(nc.vector.tensor_scalar(w3b[:], f.ident[0:64, :], 0.0, w3[:, 0:1], ALU.mult, ALU.add))
                dve.sem_inc(w3_set, 1)
                quarters = lambda y: y.rearrange("p h (t a) -> p h t a", a=NQU)
                step(nc.vector.tensor_reduce(m_all[:], quarters(minima), AX, ALU.min))
                step(nc.vector.tensor_scalar(mneg[:], m_all[:].rearrange("p h t -> p (h t)"), -1.0, None, ALU.mult))
                dve.sem_inc(m_T, 1)
                for a in range(NQU):
                    step(nc.vector.tensor_tensor(quarters(wgt[:])[:, :, :, a], m_all[:], quarters(minima)[:, :, :, a],
                                                 ALU.subtract))
                dve.sem_inc(w_in, 1)
                dve.wait_ge(w_out, 1)
                step(nc.vector.tensor_tensor(zs, zs, wgt[:], ALU.mult))
                step(nc.vector.tensor_tensor(es, es, wgt[:], ALU.mult))
                step(nc.vector.tensor_tensor(es, es, wgt[:], ALU.mult))
                step(nc.vector.tensor_reduce(z_all[:], quarters(zs), AX, ALU.add))
                step(nc.vector.tensor_reduce(e_all[:], quarters(es), AX, ALU.add))
                step(nc.vector.reciprocal(z_all[:], z_all[:]))
                step(nc.vector.tensor_tensor(e_all[:], e_all[:], z_all[:], ALU.mult))
                step(nc.vector.tensor_tensor(e_all[:], e_all[:], z_all[:], ALU.mult))
                step(nc.vector.tensor_scalar(e_all[:], e_all[:], 1.0 / S2, 1.0 / ((S2 - 1) * S), ALU.subtract, ALU.mult))
                step(nc.vector.tensor_scalar(m_all[:], m_all[:], -1.0 / S, None, ALU.mult))
                step(nc.vector.tensor_reduce(k_sums[:], f.key_sums[:], AX, ALU.add))
                step(nc.vector.tensor_tensor(k_sums[:], k_sums[:], q_sums[:], ALU.mult))
                step(nc.vector.tensor_scalar(k_sums[:], k_sums[:], -1.0 / S / S2, None, ALU.mult))
                for c in range(KC):
                    step(nc.vector.tensor_scalar(qk_sum[:, c], head_of[:, c], k_sums[:, c:c + 1], None, ALU.mult))
                dve.sem_inc(featured, 1)
                dve.wait_ge(m_T, 2)
                step(nc.vector.tensor_copy(mrow[:], small[0:H * NT, 3, 0:P]))
                step(nc.vector.tensor_copy(mparts[:, 0], mrow[:]))
                step(nc.vector.tensor_tensor(mrest[:], mrow[:], mparts[:, 0], ALU.subtract))
                step(nc.vector.tensor_copy(mparts[:, 1], mrest[:]))
                step(nc.vector.tensor_tensor(mparts[:, 2], mrest[:], mparts[:, 1], ALU.subtract))
                dve.sem_inc(m_split, 1)
                dve.wait_ge(t_mm, 1)
                step(nc.vector.tensor_scalar(logt[:], small[:, 2, 0:H], b3[:, 0:1], LOG_T_MIN, ALU.add, ALU.max))
                step(nc.vector.tensor_scalar(logt[:], logt[:], LOG_T_MAX, None, ALU.min))
                dve.sem_inc(t_ready, 1)
                dve.wait_ge(t_ready, 2)
                step(nc.vector.tensor_scalar(tscale[:, 0:H], tscale[:, 0:H], -2.0, None, ALU.mult))
                step(nc.vector.memset(tscale[:, H:H + 2], 1.0))

            @block.scalar
            def _(act):
                act.wait_ge(small_loaded, 160)
                act.wait_ge(w_in, 1)
                nc.scalar.activation(wgt[:], wgt[:], ACT.Exp).then_inc(w_out, 1)
                act.wait_ge(hid_mm, 1)
                nc.scalar.activation(hid1[:], small[0:64, 0, 0:H], ACT.Gelu, bias=b1[:, 0:1]).then_inc(hid_act, 1)
                act.wait_ge(hid_mm, 2)
                nc.scalar.activation(hid2[:], small[0:64, 1, 0:H], ACT.Gelu, bias=b2[:, 0:1]).then_inc(hid_act, 1)
                act.wait_ge(t_ready, 1)
                nc.scalar.activation(tscale[:, 0:H], logt[:], ACT.Exp, scale=-1.0).then_inc(t_ready, 1)

            @block.tensor
            def _(pe):
                pe.wait_ge(small_loaded, 160)
                pe.wait_ge(m_T, 1)
                nc.tensor.transpose(small[0:H * NT, 3, 0:P], mneg[:], f.ident[:]).then_inc(m_T, 1)
                pe.wait_ge(featured, 1)
                pairs = [(w1b[:, 0], qk_sum[:, c]) for c in range(KC)]
                pairs += [(w1b[:, 1], m_all[:, :, t]) for t in range(NT)]
                pairs += [(w1b[:, 2], e_all[:, :, t]) for t in range(NT)]
                for n, (a, b) in enumerate(pairs):
                    mm = nc.tensor.matmul(small[0:64, 0, 0:H], a, b, start=(n == 0), stop=(n == len(pairs) - 1))
                mm.then_inc(hid_mm, 1)
                pe.wait_ge(hid_act, 1)
                nc.tensor.matmul(small[0:64, 1, 0:H], w2[:], hid1[:], start=True, stop=True).then_inc(hid_mm, 1)
                pe.wait_ge(hid_act, 2)
                pe.wait_ge(w3_set, 1)
                nc.tensor.matmul(small[:, 2, 0:H], w3b[:], hid2[:], start=True, stop=True).then_inc(t_mm, 1)

        with ExitStack() as inner:
            block = inner.enter_context(nc.Block())
            probs = f.sb(inner, "probs", [P, 4, GC, S])
            rz = f.sb(inner, "rz", [P, 2, NT])
            sumsT = f.sb(inner, "sumsT", [P, 2, S])
            ps = f.ps(inner, "psT", [P, 2, GC * S])
            sums = f.ps(inner, "sums", [P, 2, BANK])
            both = f.ps(inner, "both", [P, 2 * NT, QUAD])
            out_T, out_sb, out_mm, out_ready = f.sem("out_T"), f.sem("out_sb"), f.sem("out_mm"), f.sem("out_ready")
            t_now_ready, sums_sb, gathered, zeroed = (f.sem(n) for n in ("t_now_ready", "sums_sb", "gathered", "zeroed"))

            @block.sync
            def _(sp):
                with sp.Fori(1, H // 2) as pair:
                    for b in range(2):
                        sp.wait_ge(kb_free, 2 * pair + b + 1)
                        load_head(sp, 2 * pair + b, b)

            @block.tensor
            def _(pe):
                pe.sem_inc(kb_free, 2)
                pe.wait_ge(g_loaded, 16)
                pe.wait_ge(zeroed, 1)

                def weigh(head, b, g, n):
                    for c in range(GC):
                        mm = nc.tensor.matmul(sums[c * QUAD:c * QUAD + DV, b, 0:S], vhead[:, b, g * GC + c, :],
                                              probs[:, g % 4, c, :], start=(g == 0), stop=(g == NG - 1))
                    mm.then_inc(probs_used, 1)
                    if g == NG - 1:
                        pe.wait_ge(probs_used, n + 5)
                        pe.sem_inc(pv_done, 1)
                        pe.sem_inc(kb_free, 1)

                def bring_together(head, b):
                    pe.wait_ge(sums_sb, head + 1)
                    pe.wait_ge(pv_read, head + 1)
                    for t in range(NT):
                        mm = nc.tensor.matmul(both[:, NT * b + t, 0:DV], sumsT[:, b, t * P:(t + 1) * P], gather[:],
                                              start=True, stop=True)
                    mm.then_inc(gathered, 1)

                def heads(pair, first):
                    for b in range(2):
                        head = 2 * pair + b
                        pe.wait_ge(kb_loaded[b], (KEYS_IN + 16) * (pair + 1))
                        for g in range(NG):
                            n = head * NG + g
                            pe.wait_ge(probs_ready, n + 1)
                            for c in range(GC):
                                at = (g * GC + c) * P
                                mm = nc.tensor.matmul(ps[:, g % 2, c * S:(c + 1) * S], k96[0:MAXROWS, b, at:at + P],
                                                      q96[0:MAXROWS, bass.ds(head, 1), :], start=True, stop=True)
                            mm.then_inc(scoredT, 1)
                            if g >= 2:
                                if g == 2:
                                    pe.wait_ge(sums_free, head + 1)
                                weigh(head, b, g - 2, n - 2)
                            elif not (first and b == 0):
                                weigh(head - 1, 1 - b, NG + g - 2, n - 2)
                            if g == 3 and not (first and b == 0):
                                bring_together(head - 1, 1 - b)

                heads(0, True)
                with pe.Fori(1, H // 2) as pair:
                    heads(pair, False)
                for g in (NG - 2, NG - 1):
                    pe.wait_ge(probs_ready, UNITS - NG + g + 3)
                    weigh(H - 1, 1, g, UNITS - NG + g)
                bring_together(H - 1, 1)
                pe.wait_ge(out_T, 1)
                flat = ps[:, 0, 0:KC * S].rearrange("p (c n) -> p c n", c=KC)
                attn_rows = attn[:].rearrange("p t h d -> p t (h d)")
                transpose_tokens(nc, flat, attn_rows, f.ident[:]).then_inc(out_T, 1)
                pe.wait_ge(out_sb, 1)
                for t in range(NT):
                    out = ps[:, 1, t * D:(t + 1) * D]
                    for c in range(KC):
                        nc.tensor.matmul(out, attnT[:, c, t * P:(t + 1) * P], wo[:, c, :], start=(c == 0), stop=False)
                    mm = nc.tensor.matmul(out, f.ones[0:1, :], bo[:], start=False, stop=True)
                mm.then_inc(out_mm, 1)

            @block.scalar
            def _(act):
                act.sem_inc(probs_ready, 2)
                with act.Fori(0, H // 2) as pair:
                    for b in range(2):
                        act.wait_ge(t_now_ready, 2 * pair + b + 1)
                        for g in range(NG):
                            n = (2 * pair + b) * NG + g
                            act.wait_ge(scoredT, n + 1)
                            act.wait_ge(probs_used, n + 1)
                            nc.scalar.activation(probs[:, g % 4].rearrange("p c n -> p (c n)"), ps[:, g % 2], ACT.Exp,
                                                 scale=t_now[:, b:b + 1]).then_inc(probs_ready, 1)
                act.wait_ge(out_T, 2)
                nc.scalar.copy(attnT[:], ps[:, 0, 0:KC * S].rearrange("p (c n) -> p c n", c=KC)).then_inc(out_sb, 1)

            @block.vector
            def _(dve):
                nc.vector.memset(sums[:], 0.0).then_inc(zeroed, 1)
                dve.sem_inc(probs_used, 4)
                dve.sem_inc(pv_read, 2)
                dve.sem_inc(sums_free, 2)
                nc.vector.tensor_copy(t_now[:], tscale[:, 0:2]).then_inc(t_now_ready, 2)
                with dve.Fori(0, H // 2) as pair:
                    for b in range(2):
                        head = 2 * pair + b
                        dve.wait_ge(pv_done, head + 1)
                        nc.vector.tensor_scalar(t_now[:, b:b + 1], tscale[:, bass.ds(head + 2, 1)], 1.0, None, ALU.mult
                                                ).then_inc(t_now_ready, 1)
                        nc.vector.tensor_copy(sumsT[:, b], sums[:, b, 0:S]).then_inc(sums_sb, 1)
                        dve.wait_ge(sums_sb, head + 1)
                        dve.sem_inc(sums_free, 1)
                        dve.wait_ge(gathered, head + 1)
                        nc.vector.reciprocal(rz[:, b], both[:, NT * b:NT * (b + 1), DK]).then_inc(recip_done, 1)
                        dve.wait_ge(recip_done, head + 1)
                        for t in range(NT):
                            ins = nc.vector.tensor_scalar(attn[:, t, bass.ds(head, 1), :], both[:, NT * b + t, 0:DK],
                                                          rz[:, b, t:t + 1], None, ALU.mult)
                        ins.then_inc(pv_read, 1)
                dve.wait_ge(pv_read, H + 2)
                nc.vector.tensor_tensor(attn[:], attn[:], bv[:].rearrange("p (h d) -> p h d", h=H).unsqueeze(1)
                                        .to_broadcast([P, NT, H, DK]), ALU.add).then_inc(pv_read, 1)
                dve.wait_ge(pv_read, H + 3)
                dve.sem_inc(out_T, 1)
                dve.wait_ge(out_mm, 1)
                nc.vector.tensor_tensor(f.x[:], f.x[:], ps[:, 1, 0:NT * D].rearrange("p (t n) -> p t n", t=NT),
                                        ALU.add).then_inc(out_ready, 1)
                dve.wait_ge(out_ready, 1)


def linear_attn(f, w0):
    nc, i = f.nc, f.ins
    f.layer = "la"
    s = {n: f.sem(n) for n in ("w_loaded", "loaded", "next_loaded", "var_ready", "root_ready", "dve_steps",
                               "pool_steps", "z_ready", "zT_mm",
                               "zT_sb", "q_mm", "k_mm", "v_mm", "q_gelu", "k_gelu", "v_sb", "k_ready", "mean_mm",
                               "krot_ready", "kv_mm", "kv_masked", "qrot_ready", "qT_mm", "qT_sb", "out_mm")}
    with ExitStack() as ctx:
        w = f.sb(ctx, "w", [P, 3, KC, D])
        b = f.sb(ctx, "b", [1, 3, D])
        gain = f.sb(ctx, "gain", [P, 2, D])
        rope = f.sb(ctx, "rope", [P, 2, NT, D // 2])
        same_head = f.sb(ctx, "same_head", [P, KC, D])
        z = f.sb(ctx, "z", [P, NT, D])
        zT = f.sb(ctx, "zT", [P, KC, S])
        q, k, v = (f.sb(ctx, n, [P, NT, D]) for n in "qkv")
        qr, kr = (f.sb(ctx, n, [P, NT, D]) for n in ("qr", "kr"))
        tq, tk = (f.sb(ctx, n, [P, NT, D // 2]) for n in ("tq", "tk"))
        qrT = f.sb(ctx, "qrT", [P, KC, S])
        kv = f.sb(ctx, "kv", [P, KC, D])
        prod = f.sb(ctx, "prod", [P, NT, D])
        den = f.sb(ctx, "den", [P, NT, H])
        res = f.sb(ctx, "res", [P, NT, D])
        ps = f.ps(ctx, "ps", [P, 8, BANK])
        tiles = lambda n: ps[:, n].rearrange("p (t n) -> p t n", t=NT)
        block = ctx.enter_context(nc.Block())

        @block.sync
        def _(sp):
            loads = [(w[:, n], rows_of(i[f"L0_attn_W{c}"])) for n, c in enumerate("qkv")]
            loads += [(b[:, n], i[f"L0_attn_b{c}"]) for n, c in enumerate("qkv")]
            loads += [(gain[:, n], i[f"L0_attn_{c}"].partition_broadcast(P)) for n, c in enumerate(("gamma", "beta"))]
            loads += [(rope[:], i["c_rope"]), (same_head[:], i["c_same_head"])]
            for n, (dst, src) in enumerate(loads):
                sp.dma_start(dst, src).then_inc(s["w_loaded" if n < 6 else "loaded"], 16)
            for dst, src in w0.loads:
                sp.dma_start(dst, src).then_inc(s["next_loaded"], 16)
            sp.wait_ge(s["next_loaded"], 16 * len(w0.loads))

        @block.tensor
        def _(pe):
            pe.wait_ge(s["z_ready"], 1)
            transpose_tokens(nc, tiles(0), z, f.ident[:]).then_inc(s["zT_mm"], 1)
            pe.wait_ge(s["w_loaded"], 96)
            pe.wait_ge(s["zT_sb"], 1)
            for m, done in ((1, "k_mm"), (2, "v_mm"), (0, "q_mm")):
                for t in range(NT):
                    out = tiles(1 + m)[:, t]
                    for c in range(KC):
                        nc.tensor.matmul(out, zT[:, c, t * P:(t + 1) * P], w[:, m, c, :], start=(c == 0), stop=False)
                    mm = nc.tensor.matmul(out, f.ones[0:1, :], b[:, m, :], start=False, stop=True)
                mm.then_inc(s[done], 1)
            pe.wait_ge(s["k_ready"], 1)
            for t in range(NT):
                mm = nc.tensor.matmul(ps[:, 4, 0:D], f.ones[:], k[:, t, :], start=(t == 0), stop=(t == NT - 1))
            mm.then_inc(s["mean_mm"], 1)
            pe.wait_ge(s["krot_ready"], 1)
            pe.wait_ge(s["v_sb"], 1)
            for c in range(KC):
                for t in range(NT):
                    mm = nc.tensor.matmul(tiles(5)[:, c], kr[:, t, c * P:(c + 1) * P], v[:, t, :],
                                          start=(t == 0), stop=(t == NT - 1))
            mm.then_inc(s["kv_mm"], 1)
            pe.wait_ge(s["qrot_ready"], 1)
            transpose_tokens(nc, tiles(6), qr, f.ident[:]).then_inc(s["qT_mm"], 1)
            pe.wait_ge(s["qT_sb"], 1)
            pe.wait_ge(s["kv_masked"], 1)
            for t in range(NT):
                for c in range(KC):
                    mm = nc.tensor.matmul(tiles(7)[:, t], qrT[:, c, t * P:(t + 1) * P], kv[:, c, :],
                                          start=(c == 0), stop=(c == KC - 1))
            mm.then_inc(s["out_mm"], 1)

        @block.scalar
        def _(act):
            take_root(f, act, s["var_ready"], s["root_ready"])
            act.wait_ge(s["zT_mm"], 1)
            nc.scalar.copy(zT[:], tiles(0)).then_inc(s["zT_sb"], 1)
            act.wait_ge(s["k_mm"], 1)
            nc.scalar.activation(k[:], tiles(2), ACT.Gelu).then_inc(s["k_gelu"], 1)
            act.wait_ge(s["v_mm"], 1)
            nc.scalar.copy(v[:], tiles(3)).then_inc(s["v_sb"], 1)
            act.wait_ge(s["q_mm"], 1)
            nc.scalar.activation(q[:], tiles(1), ACT.Gelu).then_inc(s["q_gelu"], 1)
            act.wait_ge(s["qT_mm"], 1)
            nc.scalar.copy(qrT[:], tiles(6)).then_inc(s["qT_sb"], 1)
            take_root(f, act, s["var_ready"], s["root_ready"], 1)

        def rotate(eng, step, out, a, tmp):
            o, p = (y[:].rearrange("p t (n two) -> p t n two", two=2) for y in (out, a))
            cos, sin = rope[:, 0], rope[:, 1]
            step(eng.tensor_tensor(o[:, :, :, 0], p[:, :, :, 0], cos, ALU.mult))
            step(eng.tensor_tensor(tmp[:], p[:, :, :, 1], sin, ALU.mult))
            step(eng.tensor_tensor(o[:, :, :, 0], o[:, :, :, 0], tmp[:], ALU.subtract))
            step(eng.tensor_tensor(o[:, :, :, 1], p[:, :, :, 1], cos, ALU.mult))
            step(eng.tensor_tensor(tmp[:], p[:, :, :, 0], sin, ALU.mult))
            step(eng.tensor_tensor(o[:, :, :, 1], o[:, :, :, 1], tmp[:], ALU.add))

        @block.gpsimd
        def _(pool):
            step = Chain(pool, s["pool_steps"])
            pool.wait_ge(s["loaded"], 64)
            pool.wait_ge(s["k_gelu"], 1)
            step(nc.gpsimd.tensor_scalar(k[:], k[:], 0.21, None, ALU.add))
            pool.sem_inc(s["k_ready"], 1)
            rotate(nc.gpsimd, step, kr, k, tk)
            pool.sem_inc(s["krot_ready"], 1)

        @block.vector
        def _(dve):
            step = Chain(dve, s["dve_steps"])
            layer_norm(f, dve, step, z, f.x, 1e-5, s["var_ready"], s["root_ready"])
            dve.sem_inc(s["z_ready"], 1)
            dve.wait_ge(s["loaded"], 64)
            dve.wait_ge(s["q_gelu"], 1)
            step(nc.vector.tensor_scalar(q[:], q[:], 0.21, None, ALU.add))
            rotate(nc.vector, step, qr, q, tq)
            dve.sem_inc(s["qrot_ready"], 1)
            dve.wait_ge(s["mean_mm"], 1)
            for t in range(NT):
                step(nc.vector.tensor_tensor(prod[:, t], q[:, t], ps[:, 4, 0:D], ALU.mult))
            heads = prod[:].rearrange("p t (h d) -> p t h d", h=H)
            step(nc.vector.tensor_reduce(den[:], heads, AX, ALU.add))
            step(nc.vector.tensor_scalar(den[:], den[:], 1.0 / S, 1e-6, ALU.mult, ALU.add))
            step(nc.vector.reciprocal(den[:], den[:]))
            dve.wait_ge(s["kv_mm"], 1)
            step(nc.vector.scalar_tensor_tensor(out=kv[:], in0=tiles(5), scalar=1.0 / S, in1=same_head[:],
                                                op0=ALU.mult, op1=ALU.mult))
            dve.sem_inc(s["kv_masked"], 1)
            dve.wait_ge(s["out_mm"], 1)
            for t in range(NT):
                step(nc.vector.tensor_tensor(res[:, t].rearrange("p (h d) -> p h d", h=H),
                                             tiles(7)[:, t].rearrange("p (h d) -> p h d", h=H),
                                             den[:, t].unsqueeze(2).to_broadcast([P, H, DK]), ALU.mult))
            step(nc.vector.tensor_tensor(res[:], res[:], z[:], ALU.add))
            layer_norm(f, dve, step, prod, res, 1e-12, s["var_ready"], s["root_ready"], 1)
            for t in range(NT):
                step(nc.vector.tensor_tensor(prod[:, t], prod[:, t], gain[:, 0], ALU.mult))
                step(nc.vector.tensor_tensor(prod[:, t], prod[:, t], gain[:, 1], ALU.add))
            step(nc.vector.tensor_tensor(f.x[:], f.x[:], prod[:], ALU.add))


TAU = 2 * np.pi
TAU_PARTS = (6.28125, float(np.float32(TAU - 6.28125) // 2 ** -21 * 2 ** -21), 0.0)
TAU_PARTS = TAU_PARTS[:2] + (float(TAU - TAU_PARTS[0] - TAU_PARTS[1]),)
ROUND = 1.5 * 2 ** 23
PI_BELOW = float(np.nextafter(np.float32(np.pi), np.float32(0)))
HD = 64
E0, TOP0 = 31, 3
EXPERTS0 = E0 + 1
I0 = 256
EW0 = KC * I0 + I0 // P * D + I0 // P
RING = 4


def rms_norm(f, dve, step, y, x, gain, square, eps, var_ready, root_ready, n):
    nc = f.nc
    for t in range(NT):
        step(nc.vector.tensor_tensor_reduce(out=square[:, t], in0=x[:, t], in1=x[:, t], scale=1.0 / D, scalar=0.0,
                                            op0=ALU.mult, op1=ALU.add, accum_out=f.rstd[:, t:t + 1]))
    nc.vector.tensor_scalar(f.rstd[:], f.rstd[:], eps, None, ALU.add).then_inc(var_ready, 1)
    dve.wait_ge(root_ready, n + 1)
    step(nc.vector.reciprocal(f.rstd[:], f.rstd[:]))
    for t in range(NT):
        step(nc.vector.scalar_tensor_tensor(out=y[:, t], in0=x[:, t], scalar=f.rstd[:, t:t + 1], in1=gain,
                                            op0=ALU.mult, op1=ALU.mult))


class ShortAttention:

    DEEP = 4

    def __init__(self, f, ctx, heads, scale, causal):
        self.f, self.heads, self.scale, self.causal = f, heads, scale, causal
        self.s = {n: f.sem(n) for n in ("scored", "masked", "max_raw", "max_ready", "exp_done", "rz_ready",
                                        "normed", "probsT_mm", "probsT_sb", "attn_mm", "attn_sb")}
        self.scores = f.ps(ctx, "scores", [P, 2, NT, S])
        self.probsT_ps = f.ps(ctx, "probsT_ps", [P, 2, NT, S])
        self.attn_ps = f.ps(ctx, "attn_ps", [P, 2, BANK])
        self.masked = f.sb(ctx, "masked", [P, self.DEEP, NT, S])
        self.top = f.sb(ctx, "top", [P, self.DEEP, NT])
        self.ntop = f.sb(ctx, "ntop", [P, self.DEEP, NT])
        self.z = f.sb(ctx, "z", [P, self.DEEP, NT])
        self.rz = f.sb(ctx, "rz", [P, self.DEEP, NT])
        self.probs = f.sb(ctx, "probs", [P, self.DEEP, NT, S])
        self.normed = f.sb(ctx, "normed", [P, self.DEEP, NT, S])
        self.probsT = f.sb(ctx, "probsT", [P, 2, NT, S])
        self.attnT = f.sb(ctx, "attnT", [P, heads // 2, S])

    def tensor(self, pe, products, v):
        nc, s = self.f.nc, self.s
        for n in range(self.heads + 3):
            if n < self.heads:
                if n >= 2:
                    pe.wait_ge(s["masked"] if self.causal else s["exp_done"], n - 1)
                for t in range(NT):
                    pairs = products(n, t)
                    for k, (a, b) in enumerate(pairs):
                        mm = nc.tensor.matmul(self.scores[:, n % 2, t], a, b, start=(k == 0), stop=(k == len(pairs) - 1))
                mm.then_inc(s["scored"], 1)
            h = n - 2
            if 0 <= h < self.heads:
                pe.wait_ge(s["normed"], h + 1)
                if h >= 2:
                    pe.wait_ge(s["probsT_sb"], h - 1)
                for k in range(NT):
                    for t in range(NT):
                        mm = nc.tensor.transpose(self.probsT_ps[:, h % 2, k, t * P:(t + 1) * P],
                                                 self.normed[:, h % self.DEEP, t, k * P:(k + 1) * P], self.f.ident[:])
                mm.then_inc(s["probsT_mm"], 1)
            h = n - 3
            if h >= 0:
                pair, side = h // 2, h % 2
                pe.wait_ge(s["probsT_sb"], h + 1)
                if pair >= 2 and side == 0:
                    pe.wait_ge(s["attn_sb"], pair - 1)
                for k in range(NT):
                    mm = nc.tensor.matmul(self.attn_ps[side * HD:(side + 1) * HD, pair % 2, 0:S], v(h, k),
                                          self.probsT[:, h % 2, k], start=(k == 0), stop=(k == NT - 1))
                if side:
                    mm.then_inc(s["attn_mm"], 1)

    def scalar(self, act):
        nc, s = self.f.nc, self.s
        for n in range(self.heads + 2):
            h = n
            if h < self.heads:
                b = h % self.DEEP
                act.wait_ge(s["max_ready"], h + 1)
                if h >= self.DEEP:
                    act.wait_ge(s["normed"], h - self.DEEP + 1)
                for t in range(NT):
                    src = self.masked[:, b, t] if self.causal else self.scores[:, h % 2, t]
                    ins = nc.scalar.activation(self.probs[:, b, t], src, ACT.Exp, bias=self.ntop[:, b, t:t + 1],
                                               accum_out=self.z[:, b, t:t + 1])
                ins.then_inc(s["exp_done"], 1)
            h = n - 2
            if 0 <= h < self.heads:
                act.wait_ge(s["probsT_mm"], h + 1)
                nc.scalar.copy(self.probsT[:, h % 2], self.probsT_ps[:, h % 2]).then_inc(s["probsT_sb"], 1)

    def vector(self, dve, mask=None):
        nc, s = self.f.nc, self.s
        for n in range(self.heads + 4):
            h = n
            if h < self.heads:
                b = h % self.DEEP
                dve.wait_ge(s["scored"], h + 1)
                if h >= self.DEEP:
                    dve.wait_ge(s["exp_done"], h - self.DEEP + 1)
                src = self.scores[:, h % 2]
                if self.causal:
                    nc.vector.scalar_tensor_tensor(out=self.masked[:, b], in0=src, scalar=self.scale, in1=mask,
                                                   op0=ALU.mult, op1=ALU.add).then_inc(s["masked"], 1)
                    dve.wait_ge(s["masked"], h + 1)
                    src = self.masked[:, b]
                nc.vector.tensor_reduce(self.top[:, b], src, AX, ALU.max).then_inc(s["max_raw"], 1)
                dve.wait_ge(s["max_raw"], h + 1)
                nc.vector.tensor_scalar(self.ntop[:, b], self.top[:, b], -1.0, None, ALU.mult).then_inc(s["max_ready"], 1)
            h = n - 1
            if 0 <= h < self.heads:
                b = h % self.DEEP
                dve.wait_ge(s["exp_done"], h + 1)
                nc.vector.reciprocal(self.rz[:, b], self.z[:, b]).then_inc(s["rz_ready"], 1)
                dve.wait_ge(s["rz_ready"], h + 1)
                if h >= self.DEEP:
                    dve.wait_ge(s["probsT_mm"], h - self.DEEP + 1)
                for t in range(NT):
                    ins = nc.vector.tensor_scalar(self.normed[:, b, t], self.probs[:, b, t], self.rz[:, b, t:t + 1],
                                                  None, ALU.mult)
                ins.then_inc(s["normed"], 1)
            h = n - 4
            if h >= 0 and h % 2:
                dve.wait_ge(s["attn_mm"], h // 2 + 1)
                nc.vector.tensor_copy(self.attnT[:, h // 2], self.attn_ps[:, h // 2 % 2, 0:S]).then_inc(s["attn_sb"], 1)


def route(nc, step, gates, score, before, over, same, rank, top):
    n = score.shape[1]
    mine = score.unsqueeze(2).to_broadcast([P, n, n])
    other = score.unsqueeze(1).to_broadcast([P, n, n])
    step(nc.vector.tensor_tensor(over, other, mine, ALU.is_gt))
    step(nc.vector.tensor_tensor(same, other, mine, ALU.is_equal))
    step(nc.vector.tensor_tensor(same, same, before, ALU.mult))
    step(nc.vector.tensor_tensor(over, over, same, ALU.add))
    step(nc.vector.tensor_reduce(rank, over, AX, ALU.add))
    step(nc.vector.scalar_tensor_tensor(out=gates, in0=rank, scalar=float(top), in1=score, op0=ALU.is_lt, op1=ALU.mult))


class Block0Weights:

    def __init__(self, f, ctx):
        i = f.ins
        self.wq, self.wk, self.wv = (f.sb(ctx, n, [P, KC, H * HD]) for n in ("wq", "wk", "wv"))
        self.wo = f.sb(ctx, "wo", [P, H * HD // P, D])
        self.bqk = f.sb(ctx, "bqk", [P, 2, H * HD // P])
        self.bv = f.sb(ctx, "bv", [1, H * HD])
        self.bo = f.sb(ctx, "bo", [1, D])
        self.mask = f.sb(ctx, "mask", [P, NT, S])
        self.theta = f.sb(ctx, "theta", [P, 1])
        self.pos = f.sb(ctx, "pos", [P, S])
        self.gain1 = f.sb(ctx, "gain1", [P, D])
        self.gain2 = f.sb(ctx, "gain2", [P, D])
        self.loads = [(self.theta[g * 32:g * 32 + 32], i["L0_ffn_theta"]) for g in range(4)]
        self.loads += [(dst[:], i[src]) for dst, src in (
            (self.pos, "c_pos"), (self.mask, "c_causal"), (self.bqk, "L0_ffn_qk_b"), (self.bv, "L0_ffn_v_b"),
            (self.bo, "L0_ffn_o_b"))]
        self.loads += [(dst[:], i[src].partition_broadcast(P)) for dst, src in (
            (self.gain1, "L0_ffn_gamma1"), (self.gain2, "L0_ffn_gamma2"))]
        self.loads += [(dst[:], rows_of(i[src])) for dst, src in (
            (self.wq, "L0_ffn_q_w"), (self.wk, "L0_ffn_k_w"), (self.wv, "L0_ffn_v_w"), (self.wo, "L0_ffn_o_w"))]


def block0(f, w0, mask1):
    nc, i = f.nc, f.ins
    f.layer = "b0"
    wq, wk, wv, wo, bqk, bv, bo, mask, theta, pos, gain1, gain2 = (
        w0.wq, w0.wk, w0.wv, w0.wo, w0.bqk, w0.bv, w0.bo, w0.mask, w0.theta, w0.pos, w0.gain1, w0.gain2)
    with ExitStack() as outer:
        xn = f.sb(outer, "xn", [P, NT, D])
        z = f.sb(outer, "zin", [P, NT, D])
        square = f.sb(outer, "square", [P, NT, D])
        w = f.sb(outer, "e_w", [P, RING, EW0])
        router = f.sb(outer, "router", [P, KC, E0])
        rb = f.sb(outer, "rb", [1, E0])
        b2 = f.sb(outer, "e_b2", [EXPERTS0, D])
        before = f.sb(outer, "before", [P, E0, E0])
        G = D * 4 // (2 * P)
        NQ = H * HD
        with ExitStack() as ctx:
            s = {n: f.sem(n) for n in ("next_loaded", "var_ready", "root_ready", "dve_steps", "pool_steps",
                                       "angles", "waves", "xn_ready", "xnT_mm", "xnT_sb", "v_mm", "v_sb", "qk_mm",
                                       "qk_sb", "q_rot", "k_rot", "out_mm")}
            angle, turn, red = (f.sb(ctx, n, [P, 2, S]) for n in ("angle", "turn", "red"))
            waves = f.sb(ctx, "waves", [P, 2, S])
            xnT = f.sb(ctx, "xnT", [P, KC, S])
            v = f.sb(ctx, "v", [P, NT, NQ])
            raw = f.sb(ctx, "raw", [P, G, 2, 2, S])
            q = f.sb(ctx, "q", [P, G, 2, S])
            k = f.sb(ctx, "k", [P, G, 2, S])
            tc = f.sb(ctx, "tc", [P, 2, 2, S])
            ts = f.sb(ctx, "ts", [P, 2, 2, S])
            ps = f.ps(ctx, "ps", [P, 2, BANK])
            att = ShortAttention(f, ctx, H, HD ** -0.5, True)
            tiles = lambda n: ps[:, n].rearrange("p (t n) -> p t n", t=NT)
            uses = [(g, m) for g in range(G) for m in range(3)]
            block = ctx.enter_context(nc.Block())

            @block.sync
            def _(sp):
                for dst, src in ((router[:], rows_of(i["L0_ffn_router_w"])), (rb[:], i["L0_ffn_router_b"]),
                                 (b2[:], i["L0_ffn_e_b2"]), (before[:], i["c_before31"].partition_broadcast(P))):
                    sp.dma_start(dst, src).then_inc(s["next_loaded"], 16)
                for n in range(RING):
                    sp.dma_start(w[:, n], i["L0_ffn_e_w"][n]).then_inc(s["next_loaded"], 16)
                sp.wait_ge(s["next_loaded"], 16 * (4 + RING))

            @block.tensor
            def _(pe):
                pe.wait_ge(s["xn_ready"], 1)
                transpose_tokens(nc, tiles(0), xn, f.ident[:]).then_inc(s["xnT_mm"], 1)
                pe.wait_ge(s["xnT_sb"], 1)
                for n, (g, m) in enumerate(uses):
                    if n >= 2:
                        back, what = uses[n - 2]
                        if what < 2:
                            pe.wait_ge(s["qk_sb"], 2 * back + what + 1)
                        else:
                            pe.wait_ge(s["v_sb"], back + 1)
                    if n == 1:
                        pe.wait_ge(s["xnT_sb"], 1)
                    if m < 2:
                        w = (wq, wk)[m]
                        for part in range(2):
                            for c in range(KC):
                                at = (2 * g + part) * P
                                mm = nc.tensor.matmul(tiles(n % 2)[:, part], w[:, c, at:at + P], xnT[:, c, :],
                                                      start=(c == 0), stop=(c == KC - 1))
                        mm.then_inc(s["qk_mm"], 1)
                    else:
                        t, half = g // (NQ // BANK), g % (NQ // BANK)
                        for c in range(KC):
                            nc.tensor.matmul(ps[:, n % 2], xnT[:, c, t * P:(t + 1) * P],
                                             wv[:, c, half * BANK:(half + 1) * BANK], start=(c == 0), stop=False)
                        nc.tensor.matmul(ps[:, n % 2], f.ones[0:1, :], bv[:, half * BANK:(half + 1) * BANK],
                                         start=False, stop=True).then_inc(s["v_mm"], 1)

                def products(h, t):
                    g, at = h // 4, 32 * (h % 4)
                    if h % 4 == 0 and t == 0:
                        pe.wait_ge(s["q_rot"], g + 1)
                        pe.wait_ge(s["k_rot"], g + 1)
                        pe.wait_ge(s["v_sb"], 4)
                    return [(q[at:at + 32, g, part, t * P:(t + 1) * P], k[at:at + 32, g, part, :]) for part in range(2)]

                att.tensor(pe, products, lambda h, kt: v[:, kt, h * HD:(h + 1) * HD])
                pe.wait_ge(att.s["attn_sb"], H // 2)
                for t in range(NT):
                    out = tiles(0)[:, t]
                    for c in range(NQ // P):
                        nc.tensor.matmul(out, att.attnT[:, c, t * P:(t + 1) * P], wo[:, c, :], start=(c == 0), stop=False)
                    mm = nc.tensor.matmul(out, f.ones[0:1, :], bo[:], start=False, stop=True)
                mm.then_inc(s["out_mm"], 1)

            @block.scalar
            def _(act):
                take_root(f, act, s["var_ready"], s["root_ready"])
                take_root(f, act, s["var_ready"], s["root_ready"], 1)
                act.wait_ge(s["xnT_mm"], 1)
                nc.scalar.copy(xnT[:], tiles(0)).then_inc(s["xnT_sb"], 1)
                act.wait_ge(s["angles"], 1)
                nc.scalar.activation(waves[:], red[:], ACT.Sin).then_inc(s["waves"], 1)
                for n, (g, m) in enumerate(uses):
                    if m < 2:
                        act.wait_ge(s["qk_mm"], 2 * g + m + 1)
                        for part in range(2):
                            ins = nc.scalar.activation(raw[:, g, m, part], tiles(n % 2)[:, part], ACT.Identity,
                                                       bias=bqk[:, m, 2 * g + part:2 * g + part + 1])
                        ins.then_inc(s["qk_sb"], 1)
                    else:
                        t, half = g // (NQ // BANK), g % (NQ // BANK)
                        act.wait_ge(s["v_mm"], g + 1)
                        nc.scalar.copy(v[:, t, half * BANK:(half + 1) * BANK], ps[:, n % 2]).then_inc(s["v_sb"], 1)
                att.scalar(act)

            def rotate(eng, wait, step, m, dst, done):
                cos, sin = (waves[:, a].unsqueeze(1).to_broadcast([P, 2, S]) for a in range(2))
                for g in range(G):
                    wait(s["qk_sb"], 2 * g + m + 1)
                    step(eng.tensor_tensor(tc[:, m], raw[:, g, m], cos, ALU.mult))
                    step(eng.tensor_tensor(ts[:, m], raw[:, g, m], sin, ALU.mult))
                    step(eng.tensor_tensor(dst[:, g, 0], tc[:, m, 0], ts[:, m, 1], ALU.subtract))
                    step(eng.tensor_tensor(dst[:, g, 1], tc[:, m, 1], ts[:, m, 0], ALU.add))
                    done(g)

            @block.gpsimd
            def _(pool):
                step = Chain(pool, s["pool_steps"])
                pool.wait_ge(s["waves"], 1)
                rotate(nc.gpsimd, pool.wait_ge, step, 1, k, lambda g: pool.sem_inc(s["k_rot"], 1))

            @block.vector
            def _(dve):
                step = Chain(dve, s["dve_steps"])
                layer_norm(f, dve, step, z, f.x, 1e-5, s["var_ready"], s["root_ready"])
                rms_norm(f, dve, step, xn, z, gain1[:], square, 1e-5, s["var_ready"], s["root_ready"], 1)
                dve.sem_inc(s["xn_ready"], 1)
                for a in range(2):
                    step(nc.vector.tensor_scalar(angle[:, a], pos[:], theta[:, 0:1], None, ALU.mult))
                    step(nc.vector.tensor_scalar(turn[:, a], angle[:, a], 1 / TAU, 0.25 * (1 - a), ALU.mult, ALU.add))
                step(nc.vector.tensor_scalar(turn[:], turn[:], ROUND, None, ALU.add))
                step(nc.vector.tensor_scalar(turn[:], turn[:], ROUND, None, ALU.subtract))
                step(nc.vector.scalar_tensor_tensor(out=red[:], in0=turn[:], scalar=-TAU_PARTS[0], in1=angle[:],
                                                    op0=ALU.mult, op1=ALU.add))
                for part in TAU_PARTS[1:]:
                    step(nc.vector.scalar_tensor_tensor(out=red[:], in0=turn[:], scalar=-part, in1=red[:],
                                                        op0=ALU.mult, op1=ALU.add))
                step(nc.vector.tensor_scalar(red[:, 0], red[:, 0], TAU / 4, None, ALU.add))
                step(nc.vector.tensor_scalar(red[:], red[:], PI_BELOW, -PI_BELOW, ALU.min, ALU.max))
                dve.sem_inc(s["angles"], 1)
                dve.wait_ge(s["waves"], 1)
                rotate(nc.vector, dve.wait_ge, step, 0, q, lambda g: dve.sem_inc(s["q_rot"], 1))
                att.vector(dve, mask[:])
                dve.wait_ge(s["out_mm"], 1)
                step(nc.vector.tensor_tensor(xn[:], xn[:], tiles(0), ALU.add))

        with ExitStack() as ctx:
            s = {n: f.sem("e_" + n) for n in ("mask_loaded", "var_ready", "root_ready", "dve_steps", "an_ready",
                                              "anT_mm", "anT_sb", "logits_mm", "top_ready", "exp_done", "gates_ready",
                                              "gatesT_mm", "gatesT_sb", "b2_mm", "in_mm", "in_sb", "out_mm",
                                              "summed")}
            w_loaded = [f.sem(f"e_w_loaded{n}") for n in range(RING)]
            over, same = (f.sb(ctx, n, [P, E0, E0]) for n in ("over", "same"))
            an = f.sb(ctx, "an", [P, NT, D])
            anT = f.sb(ctx, "anT", [P, KC, S])
            top, ntop, zsum = (f.sb(ctx, n, [P, NT]) for n in ("e_top", "e_ntop", "zsum"))
            aff = f.sb(ctx, "aff", [P, NT, E0])
            rank = f.sb(ctx, "rank", [P, NT, E0])
            gates = f.sb(ctx, "gates", [P, NT, EXPERTS0])
            gatesT = f.sb(ctx, "gatesT", [EXPERTS0, S])
            inner = f.sb(ctx, "inner", [P, 2, I0 // P, S])
            ps = f.ps(ctx, "e_ps", [P, 4, BANK])
            in_ps = f.ps(ctx, "in_ps", [P, 2, I0 // P, S])
            out_ps = f.ps(ctx, "out_ps", [P, 2, NT, D])
            tiles = lambda n: ps[:, n].rearrange("p (t n) -> p t n", t=NT)
            block = ctx.enter_context(nc.Block())

            @block.sync
            def _(sp):
                with sp.Fori(1, EXPERTS0 // RING) as r:
                    for n in range(RING):
                        sp.wait_ge(s["out_mm"], (r - 1) * RING + n + 3)
                        src = i["L0_ffn_e_w"][bass.ds(r * RING + n, 1)]
                        sp.dma_start(w[:, n:n + 1], src.rearrange("e p n -> p e n")).then_inc(w_loaded[n], 16)
                for t in range(NT):
                    sp.dma_start(mask1[:, t], i["mask"][t * P:(t + 1) * P, :]).then_inc(s["mask_loaded"], 16)
                sp.wait_ge(s["mask_loaded"], 16 * NT)

            @block.tensor
            def _(pe):
                pe.wait_ge(s["an_ready"], 1)
                transpose_tokens(nc, tiles(0), an, f.ident[:]).then_inc(s["anT_mm"], 1)
                pe.wait_ge(s["anT_sb"], 1)
                for t in range(NT):
                    out = ps[:, 1, t * E0:(t + 1) * E0]
                    for c in range(KC):
                        nc.tensor.matmul(out, anT[:, c, t * P:(t + 1) * P], router[:, c, :], start=(c == 0), stop=False)
                    mm = nc.tensor.matmul(out, f.ones[0:1, :], rb[:], start=False, stop=True)
                mm.then_inc(s["logits_mm"], 1)

                def expert_in(r, n):
                    if not (isinstance(r, int) and r == 0):
                        pe.wait_ge(w_loaded[n], 16 * r)
                    pe.wait_ge(s["in_sb"], RING * r + n + 1)
                    for a in range(I0 // P):
                        for c in range(KC):
                            mm = nc.tensor.matmul(in_ps[:, n % 2, a], w[:, n, c * I0 + a * P:c * I0 + (a + 1) * P],
                                                  anT[:, c, :], start=(c == 0), stop=(c == KC - 1))
                    mm.then_inc(s["in_mm"], 1)

                def expert_out(r, n):
                    pe.wait_ge(s["in_sb"], RING * r + n + 3)
                    pe.wait_ge(s["summed"], 2 * (RING * r + n) + 2)
                    for t in range(NT):
                        for a in range(I0 // P):
                            at = KC * I0 + a * D
                            mm = nc.tensor.matmul(out_ps[:, n % 2, t], inner[:, n % 2, a, t * P:(t + 1) * P],
                                                  w[:, n, at:at + D], start=(a == 0), stop=(a == I0 // P - 1))
                    mm.then_inc(s["out_mm"], 1)

                pe.sem_inc(s["out_mm"], 2)
                expert_in(0, 0)
                for n in range(RING):
                    expert_in(0 if n < RING - 1 else 1, (n + 1) % RING)
                    expert_out(0, n)
                with pe.Fori(1, EXPERTS0 // RING - 1) as r:
                    for n in range(RING):
                        expert_in(r if n < RING - 1 else r + 1, (n + 1) % RING)
                        expert_out(r, n)
                r = EXPERTS0 // RING - 1
                for n in range(RING):
                    if n < RING - 1:
                        expert_in(r, n + 1)
                    if n == RING - 2:
                        pe.wait_ge(s["gates_ready"], 1)
                        for t in range(NT):
                            mm = nc.tensor.transpose(ps[0:EXPERTS0, 2, t * P:(t + 1) * P], gates[:, t, :], f.ident[:])
                        mm.then_inc(s["gatesT_mm"], 1)
                        pe.wait_ge(s["gatesT_sb"], 1)
                        for t in range(NT):
                            mm = nc.tensor.matmul(tiles(3)[:, t], gatesT[:, t * P:(t + 1) * P], b2[:], start=True, stop=True)
                        mm.then_inc(s["b2_mm"], 1)
                    expert_out(r, n)

            @block.scalar
            def _(act):
                act.sem_inc(s["in_sb"], 2)
                take_root(f, act, s["var_ready"], s["root_ready"])
                act.wait_ge(s["anT_mm"], 1)
                nc.scalar.copy(anT[:], tiles(0)).then_inc(s["anT_sb"], 1)
                act.wait_ge(s["top_ready"], 1)
                for t in range(NT):
                    ins = nc.scalar.activation(aff[:, t], ps[:, 1, t * E0:(t + 1) * E0], ACT.Exp, bias=ntop[:, t:t + 1],
                                               accum_out=zsum[:, t:t + 1])
                ins.then_inc(s["exp_done"], 1)

                def gelu(r, n):
                    act.wait_ge(s["in_mm"], RING * r + n + 1)
                    act.wait_ge(s["out_mm"], RING * r + n + 1)
                    for a in range(I0 // P):
                        at = EW0 - I0 // P + a
                        ins = nc.scalar.activation(inner[:, n % 2, a], in_ps[:, n % 2, a], ACT.Gelu,
                                                   bias=w[:, n, at:at + 1])
                    ins.then_inc(s["in_sb"], 1)

                with act.Fori(0, EXPERTS0 // RING - 1) as r:
                    for n in range(RING):
                        gelu(r, n)
                for n in range(RING):
                    gelu(EXPERTS0 // RING - 1, n)
                    if n == RING - 2:
                        act.wait_ge(s["gatesT_mm"], 1)
                        nc.scalar.copy(gatesT[:], ps[0:EXPERTS0, 2, 0:S]).then_inc(s["gatesT_sb"], 1)

            @block.vector
            def _(dve):
                step = Chain(dve, s["dve_steps"])
                dve.sem_inc(s["summed"], 4)
                rms_norm(f, dve, step, an, xn, gain2[:], square, 1e-5, s["var_ready"], s["root_ready"], 0)
                dve.sem_inc(s["an_ready"], 1)
                step(nc.vector.tensor_tensor(f.x[:], f.x[:], xn[:], ALU.add))
                step(nc.vector.tensor_tensor(f.x[:], f.x[:], an[:], ALU.add))
                dve.wait_ge(s["logits_mm"], 1)
                step(nc.vector.tensor_reduce(top[:], ps[:, 1, 0:NT * E0].rearrange("p (t e) -> p t e", t=NT), AX, ALU.max))
                step(nc.vector.tensor_scalar(ntop[:], top[:], -1.0, None, ALU.mult))
                dve.sem_inc(s["top_ready"], 1)
                dve.wait_ge(s["exp_done"], 1)
                step(nc.vector.reciprocal(zsum[:], zsum[:]))
                step(nc.vector.memset(gates[:], 1.0))
                for t in range(NT):
                    step(nc.vector.tensor_scalar(aff[:, t], aff[:, t], zsum[:, t:t + 1], None, ALU.mult))
                    route(nc, step, gates[:, t, 0:E0], aff[:, t], before[:], over[:], same[:], rank[:, t], TOP0)
                dve.sem_inc(s["gates_ready"], 1)
                with dve.Fori(0, EXPERTS0 // RING) as r:
                    for n in range(RING):
                        e = RING * r + n
                        dve.wait_ge(s["out_mm"], e + 3)
                        for t in range(NT):
                            dve.wait_ge(s["summed"], 2 * e + t + 3)
                            nc.vector.scalar_tensor_tensor(out=f.x[:, t], in0=out_ps[:, n % 2, t],
                                                           scalar=gates[:, t, bass.ds(e, 1)], in1=f.x[:, t],
                                                           op0=ALU.mult, op1=ALU.add).then_inc(s["summed"], 1)
                dve.wait_ge(s["summed"], 2 * EXPERTS0 + 4)
                dve.wait_ge(s["b2_mm"], 1)
                step(nc.vector.tensor_tensor(f.x[:], f.x[:], tiles(3), ALU.add))


U = NT * NHALF
SUB = HALF // 2
CPS = SUB // P
UNITS = H * U
PITCH = S2 + 1


def cross1(f, mask):
    nc, i = f.nc, f.ins
    f.layer = "xb"
    rel_dram = f.rel_dram
    with ExitStack() as ctx:
        bcols = f.sb(ctx, "bcols", [P, 3, KC])
        qc96 = f.sb(ctx, "qc96", [P, H, S], BF16)
        qr96 = f.sb(ctx, "qr96", [P, H, S], BF16)
        minus = f.sb(ctx, "minus", [P, NT, S2])
        ntop_all = f.sb(ctx, "ntop_all", [P, H, U])
        o_all = f.sb(ctx, "o_all", [P, H, U, DV])
        kc96 = f.sb(ctx, "kc96", [ROWS, 2, S2], BF16)
        kr96 = f.sb(ctx, "kr96", [ROWS, 2, S2], BF16)
        vhead = f.sb(ctx, "vhead", [P, 2, NCH, DV])
        gather = f.sb(ctx, "gather", [P, DV])
        kc_loaded, kr_loaded, v_loaded = ([f.sem(f"{n}_loaded{b}") for b in range(2)] for n in ("kc", "kr", "v"))
        g_loaded = f.sem("g_loaded")
        stored = [f.sem(f"q_stored{m}") for m in range(2)]
        q_loaded = [f.sem(f"q_loaded{m}") for m in range(2)]

        with ExitStack() as inner:
            s = {n: f.sem("a_" + n) for n in ("loaded", "var_ready", "root_ready", "dve_steps", "xn_ready",
                                              "xnT_mm", "xnT_sb", "q_mm", "split")}

            wq = f.sb(inner, "wq", [P, KC, D])
            xn = f.sb(inner, "xn", [P, NT, D])
            xnT = f.sb(inner, "xnT", [P, KC, S])
            q = f.sb(inner, "q", [P, KC, S])
            qb = f.sb(inner, "qb", [P, 2, KC, S])
            rest = f.sb(inner, "rest", [P, 2, KC, S])
            parts = f.sb(inner, "parts", [P, 2, 3, KC, S], BF16)
            ps = f.ps(inner, "a_ps", [P, 2, BANK])
            tiles = lambda n: ps[:, n].rearrange("p (t n) -> p t n", t=NT)
            block = inner.enter_context(nc.Block())

            @block.sync
            def _(sp):
                for dst, src in ((wq[:], rows_of(i["L1_xattn_Wq"])), (bcols[:], i["L1_xattn_bcols"])):
                    sp.dma_start(dst, src).then_inc(s["loaded"], 16)
                load_key_parts(f, sp, kr96[:, 0], 2, 0, kr_loaded[0])
                load_key_parts(f, sp, kc96[:, 0], 1, 0, kc_loaded[0])
                load_key_parts(f, sp, kr96[:, 1], 2, 1, kr_loaded[1])
                for m in (1, 0):
                    sp.wait_ge(s["split"], 2 - m)
                    for part in range(3):
                        sp.dma_start(f.query_parts[1 + m, part].rearrange("(c p) n -> p c n", p=P),
                                     parts[:, m, part]).then_inc(stored[m], 16)
                sp.wait_ge(stored[1], 48)
                load_query_parts(f, sp, qr96, 2, q_loaded[1])

            @block.tensor
            def _(pe):
                pe.wait_ge(s["xn_ready"], 1)
                transpose_tokens(nc, tiles(0), xn, f.ident[:]).then_inc(s["xnT_mm"], 1)
                pe.wait_ge(s["loaded"], 32)
                pe.wait_ge(s["xnT_sb"], 1)
                for m in range(KC):
                    for c in range(KC):
                        mm = nc.tensor.matmul(tiles(1)[:, m], wq[:, c, m * P:(m + 1) * P], xnT[:, c, :],
                                              start=(c == 0), stop=(c == KC - 1))
                mm.then_inc(s["q_mm"], 1)

            @block.scalar
            def _(act):
                take_root(f, act, s["var_ready"], s["root_ready"])
                act.wait_ge(s["xnT_mm"], 1)
                nc.scalar.copy(xnT[:], tiles(0)).then_inc(s["xnT_sb"], 1)

            @block.vector
            def _(dve):
                step = Chain(dve, s["dve_steps"])
                layer_norm(f, dve, step, xn, f.x, 1e-5, s["var_ready"], s["root_ready"])
                dve.sem_inc(s["xn_ready"], 1)
                dve.wait_ge(s["q_mm"], 1)
                dve.wait_ge(s["loaded"], 32)
                for c in range(KC):
                    step(nc.vector.tensor_scalar(q[:, c], tiles(1)[:, c], bcols[:, 0, c:c + 1], None, ALU.add))
                for m in (1, 0):
                    for c in range(KC):
                        step(nc.vector.tensor_scalar(qb[:, m, c], q[:, c], bcols[:, 1 + m, c:c + 1], DK ** -0.5,
                                                     ALU.add, ALU.mult))
                    step(nc.vector.tensor_copy(parts[:, m, 0], qb[:, m]))
                    step(nc.vector.tensor_tensor(rest[:, m], qb[:, m], parts[:, m, 0], ALU.subtract))
                    step(nc.vector.tensor_copy(parts[:, m, 1], rest[:, m]))
                    step(nc.vector.tensor_tensor(parts[:, m, 2], rest[:, m], parts[:, m, 1], ALU.subtract))
                    dve.sem_inc(s["split"], 1)
                for t in range(NT):
                    step(nc.vector.tensor_scalar(minus[:, t], mask[:, t], 1.0, 1e10, ALU.subtract, ALU.mult))

        with ExitStack() as inner:
            names = ("rel_mm", "rel_out", "cont_mm", "cont_out", "masked", "halves_max", "top_ready",
                     "exp_done", "turned", "weighed", "sums_sb", "gathered", "sums_read", "zero_set",
                     "top_begun", "top_kept", "row_free")
            s = {n: f.sem("b_" + n) for n in names}
            turned_sb = [f.sem(f"b_turned_sb{n}") for n in range(2)]
            rel_stored = [f.sem(f"b_rel_stored{n}") for n in range(U)]
            rel_back = [[f.sem(f"b_rel_back{n}_{part}") for part in range(2)] for n in range(U)]
            out0 = f.sb(inner, "out0", [P, HALF + 1])
            out1 = f.sb(inner, "out1", [P, HALF])
            row = f.sb(inner, "row", [P, U, HALF])
            top2 = f.sb(inner, "top2", [P, U, 2])
            ntop = f.sb(inner, "ntop", [P, U])
            turned = f.sb(inner, "turned", [P, 2, CPS, P])
            sumsT = f.sb(inner, "sumsT", [P, 2, P])
            rel_ps = f.ps(inner, "rel_ps", [P, SUB])
            cont_ps = f.ps(inner, "cont_ps", [P, SUB])
            turn_ps = f.ps(inner, "turn_ps", [P, SUB])
            sum_ps = f.ps(inner, "sum_ps", [P, BANK])
            both = f.ps(inner, "both", [P, 2, QUAD])
            block = inner.enter_context(nc.Block())
            LOOPS = H // 2 - 2
            SHARES = (((0,), (2,)), ((1, 2), ()), ((), (0, 1)), ((), ()))

            def where(p, c):
                return 2 * U * p + c, 2 * p + c // U, c % U, c // U % 2, c % U // NHALF, c % NHALF

            def slots(eng, slot, before=None):
                for n in range(-U, 3):
                    slot(0, n, n)
                with eng.Fori(0, LOOPS) as p:
                    for c in range(3, 3 + 2 * U):
                        slot(p, c, None)
                for n in range(2 * U * LOOPS + 3, UNITS + 3):
                    slot(LOOPS, n - 2 * U * LOOPS, n)

            def runs(n, ahead):
                return n is None or 0 <= n + ahead < UNITS

            @block.sync
            def _(sp):
                def load_keys(p, c, which, dst, loaded, pieces):
                    b = c // U % 2
                    load_key_parts(f, sp, dst[:, b], which, 2 * p + c // U, loaded[b], pieces)

                def read_back(p, c, part, first=False):
                    n, head, u, b, t, half = where(p, c)
                    if not first:
                        sp.wait_ge(s["turned"], 2 * n - 2 * U + part + 1)
                        sp.sem_inc(s["row_free"], 1)
                    for k in ((0, 1), (0, 1, 2), (2, 3), (2, 3))[u] if part == 0 else ():
                        sp.wait_ge(rel_stored[k], 16 * (head + 1))
                    columns = slice(part * SUB, (part + 1) * SUB)
                    src = rel_back_view[half][bass.ds(head, 1), t * P:(t + 1) * P, columns]
                    sp.dma_start(row[:, u:u + 1, columns], src.rearrange("h p n -> p h n")
                                 ).then_inc(rel_back[u][part], 16)

                def store(p, c):
                    n, head, u, b, t, half = where(p, c)
                    sp.wait_ge(s["rel_out"], 2 * n + 3)
                    rows = rel_rows[bass.ds(head, 1), t * P:(t + 1) * P, :]
                    if half == 0:
                        dst, src = rows[:, :, 0:HALF + 1], out0
                    else:
                        dst, src = rows[:, :, HALF + 1:PITCH], out1
                    sp.dma_start(dst.rearrange("h p n -> p (h n)"), src[:]).then_inc(rel_stored[u], 16)

                rel_rows = rel_dram[:, 0:S * PITCH].rearrange("h (r n) -> h r n", n=PITCH)
                shifted = rel_dram[:, S:S + S * S2].rearrange("h (r n) -> h r n", n=S2)
                rel_back_view = [shifted[:, :, h * HALF:(h + 1) * HALF] for h in range(NHALF)]

                def slot(p, c, n):
                    pieces_kr, pieces_kc = SHARES[c % U]
                    if pieces_kr and (n is None or 0 <= n < UNITS - 2 * U):
                        sp.wait_ge(s["rel_mm"], 2 * U * (2 * p + c // U + 1))
                        load_keys(p, c + 2 * U, 2, kr96, kr_loaded, pieces_kr)
                    if pieces_kc and (n is None or 0 <= n < UNITS - U):
                        if n is None or n >= U:
                            sp.wait_ge(s["cont_mm"], 2 * U * (2 * p + c // U))
                        load_keys(p, c + U, 1, kc96, kc_loaded, pieces_kc)
                    if c % U == 3 and (n is None or 0 < n < UNITS - U):
                        if n is None or n > U:
                            sp.wait_ge(s["weighed"], 2 * U * (2 * p + c // U) + 2)
                        load_values(p, c + U)
                    if runs(n, 2):
                        read_back(p, c + 2, 0, first=n is not None and n + 2 < U)
                    if runs(n, U):
                        store(p, c + U)
                    if runs(n, 2):
                        read_back(p, c + 2, 1, first=n is not None and n + 2 < U)

                def load_values(p, c):
                    b = c // U % 2
                    sp.dma_start(vhead[:, b:b + 1], f.value_rows[1, bass.ds(2 * p + c // U, 1)].rearrange(
                        "h p k d -> p h k d")).then_inc(v_loaded[b], 16)

                sp.wait_ge(stored[0], 48)
                load_query_parts(f, sp, qc96, 1, q_loaded[0])
                sp.dma_start(gather[:], i["c_gather"]).then_inc(g_loaded, 16)
                sp.dma_start(vhead[:, 0:1], f.value_rows[1, 0:1].rearrange("h p k d -> p h k d")).then_inc(v_loaded[0], 16)
                slots(sp, slot)

            @block.tensor
            def _(pe):
                def scores(p, c, part, q96, k96, out, loaded, free, done):
                    n, head, u, b, t, half = where(p, c)
                    if u == 0 and part == 0:
                        pe.wait_ge(loaded[b], KEYS_IN * (p + c // U // 2 + 1))
                    pe.wait_ge(free, 2 * n + part + 1)
                    for k in range(SUB // BANK):
                        at = half * HALF + part * SUB + k * BANK
                        mm = nc.tensor.matmul(out[:, k * BANK:(k + 1) * BANK],
                                              q96[0:ROWS, bass.ds(head, 1), t * P:(t + 1) * P],
                                              k96[:, b, at:at + BANK], start=True, stop=True)
                    mm.then_inc(done, 1)

                def content(p, c, part):
                    scores(p, c, part, qc96, kc96, cont_ps, kc_loaded, s["cont_out"], s["cont_mm"])

                def relative(p, c, part):
                    scores(p, c, part, qr96, kr96, rel_ps, kr_loaded, s["rel_out"], s["rel_mm"])

                def turn(p, c, part):
                    n, head, u, b, t, half = where(p, c)
                    pe.wait_ge(s["exp_done"], n + 1)
                    pe.wait_ge(turned_sb[1 - part], n + 1)
                    for k in range(CPS):
                        at = part * SUB + k * P
                        mm = nc.tensor.transpose(turn_ps[:, k * P:(k + 1) * P], row[:, u, at:at + P], f.ident[:])
                    mm.then_inc(s["turned"], 1)

                def weigh(p, c, part):
                    n, head, u, b, t, half = where(p, c)
                    pe.wait_ge(turned_sb[part], n + 1 + part)
                    if u == 0 and part == 0:
                        pe.wait_ge(v_loaded[b], 16 * (p + c // U // 2 + 1))
                    if part == 0:
                        pe.wait_ge(s["sums_sb"], n + 1)
                    for k in range(CPS):
                        at = k % NQ4 * QUAD
                        mm = nc.tensor.matmul(sum_ps[at:at + DV, 0:P], vhead[:, b, half * NCH // 2 + part * CPS + k, :],
                                              turned[:, part, k, :], start=(part == 0 and k < NQ4),
                                              stop=(part == 1 and k >= CPS - NQ4))
                    mm.then_inc(s["weighed"], 1)

                def bring_together(p, c):
                    n, head, u, b, t, half = where(p, c)
                    pe.wait_ge(s["sums_sb"], n + 2)
                    pe.wait_ge(s["sums_read"], n + 1)
                    nc.tensor.matmul(both[:, u % 2, 0:DV], sumsT[:, u % 2, :], gather[:], start=True, stop=True
                                     ).then_inc(s["gathered"], 1)

                def slot(p, c, n):
                    if isinstance(n, int) and n == 0:
                        pe.wait_ge(q_loaded[0], 96)
                        pe.wait_ge(g_loaded, 16)
                    if runs(n, 0):
                        content(p, c, 0)
                    if runs(n, -3):
                        bring_together(p, c - 3)
                    if runs(n, -2):
                        turn(p, c - 2, 0)
                    if runs(n, U):
                        relative(p, c + U, 0)
                    if runs(n, 0):
                        content(p, c, 1)
                    if runs(n, -2):
                        turn(p, c - 2, 1)
                        weigh(p, c - 2, 0)
                    if runs(n, U):
                        relative(p, c + U, 1)
                    if runs(n, -2):
                        weigh(p, c - 2, 1)

                pe.wait_ge(q_loaded[1], 96)
                pe.wait_ge(s["zero_set"], 2)
                slots(pe, slot)

            @block.scalar
            def _(act):
                act.sem_inc(s["rel_out"], 1)

                def evacuate(p, c, part):
                    n, head, u, b, t, half = where(p, c)
                    act.wait_ge(s["rel_mm"], 2 * n + part + 1)
                    if part == 0 and u >= NHALF:
                        act.wait_ge(rel_stored[u - NHALF], 16 * (head + 1))
                    elif part == 0 and not (isinstance(n, int) and n < U):
                        act.wait_ge(rel_stored[u + NHALF], 16 * head)
                    elif part == 0 and u == 0:
                        act.wait_ge(s["zero_set"], 1)
                    out = out1 if half else out0[:, 1:HALF + 1]
                    nc.scalar.copy(out[:, part * SUB:(part + 1) * SUB], rel_ps[:]).then_inc(s["rel_out"], 1)

                def exponentials(p, c):
                    n, head, u, b, t, half = where(p, c)
                    act.wait_ge(s["top_ready"], n + 1)
                    nc.scalar.activation(row[:, u], row[:, u], ACT.Exp, bias=ntop[:, u:u + 1]).then_inc(s["exp_done"], 1)

                def copy_turned(p, c):
                    n, head, u, b, t, half = where(p, c)
                    act.wait_ge(s["turned"], 2 * n + 1)
                    act.wait_ge(s["weighed"], 2 * n + 1)
                    nc.scalar.copy(turned[:, 0].rearrange("p k n -> p (k n)"), turn_ps[:]).then_inc(turned_sb[0], 1)

                def slot(p, c, n):
                    if runs(n, -2):
                        copy_turned(p, c - 2)
                    if runs(n, U):
                        evacuate(p, c + U, 0)
                    if runs(n, -1):
                        exponentials(p, c - 1)
                    if runs(n, U):
                        evacuate(p, c + U, 1)

                slots(act, slot)
                act.wait_ge(s["exp_done"], UNITS)

            @block.gpsimd
            def _(pool):
                def slot(p, c, n):
                    if not runs(n, 0):
                        return
                    n, head, u, b, t, half = where(p, c)
                    for part in range(2):
                        at = part * SUB
                        pool.wait_ge(s["cont_out"], 2 * n + part + 2)
                        nc.gpsimd.tensor_tensor(row[:, u, at:at + SUB], row[:, u, at:at + SUB],
                                                mask[:, t, half * HALF + at:half * HALF + at + SUB],
                                                ALU.mult).then_inc(s["masked"], 1)

                slots(pool, slot)

            @block.vector
            def _(dve):
                nc.vector.memset(out0[:, 0:1], 0.0).then_inc(s["zero_set"], 1)
                nc.vector.memset(sum_ps[:], 0.0).then_inc(s["zero_set"], 1)
                dve.sem_inc(s["sums_sb"], 1)
                dve.sem_inc(s["cont_out"], 1)
                dve.sem_inc(turned_sb[1], 1)
                dve.sem_inc(s["weighed"], 2)
                dve.sem_inc(s["sums_read"], 2)
                def add(p, c, part):
                    n, head, u, b, t, half = where(p, c)
                    dve.wait_ge(rel_back[u][part], 16 * (head + 1))
                    dve.wait_ge(s["cont_mm"], 2 * n + part + 1)
                    at = part * SUB
                    nc.vector.tensor_tensor(row[:, u, at:at + SUB], cont_ps[:], row[:, u, at:at + SUB],
                                            ALU.add).then_inc(s["cont_out"], 1)

                def top_of(p, c, part):
                    n, head, u, b, t, half = where(p, c)
                    dve.wait_ge(s["masked"], 2 * n + part + 1)
                    dve.sem_inc(s["top_begun"], 1)
                    at = part * SUB
                    nc.vector.tensor_tensor_reduce(out=row[:, u, at:at + SUB], in0=row[:, u, at:at + SUB],
                                                   in1=minus[:, t, half * HALF + at:half * HALF + at + SUB], scale=1.0,
                                                   scalar=-3e38, op0=ALU.add, op1=ALU.max,
                                                   accum_out=top2[:, u, part:part + 1]).then_inc(s["halves_max"], 1)
                    if part == 1:
                        dve.wait_ge(s["halves_max"], 2 * n + 2)
                        nc.vector.tensor_scalar(ntop[:, u:u + 1], top2[:, u, 0:1], top2[:, u, 1:2], -1.0, ALU.max,
                                                ALU.mult).then_inc(s["top_ready"], 1)
                        dve.wait_ge(s["top_ready"], n + 1)
                        nc.vector.tensor_copy(ntop_all[:, bass.ds(head, 1), u:u + 1], ntop[:, u:u + 1]
                                              ).then_inc(s["top_kept"], 1)

                def copy_turned(p, c):
                    n, head, u, b, t, half = where(p, c)
                    dve.wait_ge(s["turned"], 2 * n + 2)
                    dve.wait_ge(s["weighed"], 2 * n + 2)
                    nc.vector.tensor_copy(turned[:, 1].rearrange("p k n -> p (k n)"), turn_ps[:]
                                          ).then_inc(turned_sb[1], 1)

                def sums_out(p, c):
                    n, head, u, b, t, half = where(p, c)
                    dve.wait_ge(s["weighed"], 2 * n + 4)
                    nc.vector.tensor_copy(sumsT[:, u % 2], sum_ps[:, 0:P]).then_inc(s["sums_sb"], 1)

                def keep_sums(p, c):
                    n, head, u, b, t, half = where(p, c)
                    dve.wait_ge(s["gathered"], n + 1)
                    nc.vector.tensor_scalar(o_all[:, bass.ds(head, 1), u, :], both[:, u % 2, 0:DV], 1.0, None,
                                            ALU.mult).then_inc(s["sums_read"], 1)

                def slot(p, c, n):
                    if runs(n, -1):
                        top_of(p, c - 1, 0)
                    if runs(n, -3):
                        sums_out(p, c - 3)
                    if runs(n, 0):
                        add(p, c, 0)
                    if runs(n, -1):
                        top_of(p, c - 1, 1)
                    if runs(n, 0):
                        add(p, c, 1)
                    if runs(n, -2):
                        copy_turned(p, c - 2)
                    if runs(n, -3):
                        keep_sums(p, c - 3)

                slots(dve, slot)
                dve.wait_ge(s["sums_read"], UNITS + 2)
                dve.wait_ge(s["top_kept"], UNITS)

        with ExitStack() as inner:
            s = {n: f.sem("c_" + n) for n in ("loaded", "dve_steps", "w_in", "w_out", "o_ready", "oT_mm", "oT_sb", "out_mm")}
            wo = f.sb(inner, "wo", [P, KC, D])
            bo = f.sb(inner, "bo", [1, D])
            bv = f.sb(inner, "bv", [P, D])
            m = f.sb(inner, "m", [P, H, NT])
            wgt = f.sb(inner, "wgt", [P, H, U])
            total = f.sb(inner, "total", [P, NT, H, DV])
            z = f.sb(inner, "z", [P, NT, H])
            attn = f.sb(inner, "attn", [P, NT, H, DK])
            attnT = f.sb(inner, "attnT", [P, KC, S])
            ps = f.ps(inner, "c_ps", [P, 2, BANK])
            tiles = lambda n: ps[:, n].rearrange("p (t n) -> p t n", t=NT)
            block = inner.enter_context(nc.Block())

            @block.sync
            def _(sp):
                sp.dma_start(wo[:], rows_of(i["L1_xattn_Wo"])).then_inc(s["loaded"], 16)
                sp.dma_start(bo[:], i["L1_xattn_bo"]).then_inc(s["loaded"], 16)
                sp.dma_start(bv[:], i["L1_xattn_bv"].partition_broadcast(P)).then_inc(s["loaded"], 16)

            @block.vector
            def _(dve):
                step = Chain(dve, s["dve_steps"])
                halves = lambda y: y[:].rearrange("p h (t a) -> p h t a", a=NHALF)
                step(nc.vector.tensor_reduce(m[:], halves(ntop_all), AX, ALU.min))
                for a in range(NHALF):
                    step(nc.vector.tensor_tensor(halves(wgt)[:, :, :, a], m[:], halves(ntop_all)[:, :, :, a], ALU.subtract))
                dve.sem_inc(s["w_in"], 1)
                dve.wait_ge(s["w_out"], 1)
                step(nc.vector.tensor_tensor(o_all[:], o_all[:], wgt[:].unsqueeze(3).to_broadcast([P, H, U, DV]), ALU.mult))
                for t in range(NT):
                    step(nc.vector.tensor_tensor(total[:, t], o_all[:, :, NHALF * t, :], o_all[:, :, NHALF * t + 1, :],
                                                 ALU.add))
                step(nc.vector.reciprocal(z[:], total[:, :, :, DK]))
                for t in range(NT):
                    step(nc.vector.tensor_tensor(attn[:, t], total[:, t, :, 0:DK],
                                                 z[:, t].unsqueeze(2).to_broadcast([P, H, DK]), ALU.mult))
                dve.wait_ge(s["loaded"], 48)
                step(nc.vector.tensor_tensor(attn[:], attn[:], bv[:].rearrange("p (h d) -> p h d", h=H).unsqueeze(1)
                                             .to_broadcast([P, NT, H, DK]), ALU.add))
                dve.sem_inc(s["o_ready"], 1)
                dve.wait_ge(s["out_mm"], 1)
                step(nc.vector.tensor_tensor(f.x[:], f.x[:], tiles(1), ALU.add))

            @block.scalar
            def _(act):
                act.wait_ge(s["w_in"], 1)
                nc.scalar.activation(wgt[:], wgt[:], ACT.Exp).then_inc(s["w_out"], 1)
                act.wait_ge(s["oT_mm"], 1)
                nc.scalar.copy(attnT[:], tiles(0)).then_inc(s["oT_sb"], 1)

            @block.tensor
            def _(pe):
                pe.wait_ge(s["o_ready"], 1)
                transpose_tokens(nc, tiles(0), attn[:].rearrange("p t h d -> p t (h d)"), f.ident[:]
                                 ).then_inc(s["oT_mm"], 1)
                pe.wait_ge(s["loaded"], 48)
                pe.wait_ge(s["oT_sb"], 1)
                for t in range(NT):
                    for c in range(KC):
                        nc.tensor.matmul(tiles(1)[:, t], attnT[:, c, t * P:(t + 1) * P], wo[:, c, :],
                                         start=(c == 0), stop=False)
                    mm = nc.tensor.matmul(tiles(1)[:, t], f.ones[0:1, :], bo[:], start=False, stop=True)
                mm.then_inc(s["out_mm"], 1)


HM = 8
E1, TOP1 = 8, 2
I1 = 512
RING1 = 4


class Mixture1Weights:

    def __init__(self, f, ctx):
        self.f = f
        self.w13 = f.sb(ctx, "w13", [P, RING1, 2, KC, I1])
        self.w2 = f.sb(ctx, "w2", [P, RING1, I1 // P, D])
        self.wg = f.sb(ctx, "wg", [P, KC, E1])
        self.before = f.sb(ctx, "before", [P, E1, E1])
        self.loads = [(self.wg[:], rows_of(f.ins["L1_ffn_w_gate"])),
                      (self.before[:], f.ins["c_before8"].partition_broadcast(P))]
        for n in range(RING1):
            self.loads += self.expert(n, n)

    def expert(self, e, n):
        src = lambda m: self.f.ins[f"L1_ffn_w{m}"][bass.ds(e, 1)].rearrange("e (c p) n -> p (e c) n", p=P)
        return [(self.w13[:, n, 0], src(1)), (self.w13[:, n, 1], src(3)), (self.w2[:, n], src(2))]


def multi_query(f, w1):
    nc, i = f.nc, f.ins
    f.layer = "mq"
    s = {n: f.sem(n) for n in ("loaded", "next_loaded", "var_ready", "root_ready", "dve_steps", "xn_ready",
                               "xnT_mm", "xnT_sb",
                               "q_mm", "kv_mm", "sums_ready", "norms_ready", "scaled", "qT_mm", "qT_sb", "out_mm")}
    NQ = HM * HD
    with ExitStack() as ctx:
        wq = f.sb(ctx, "wq", [P, KC, NQ])
        wkv = f.sb(ctx, "wkv", [P, KC, 2 * HD])
        wo = f.sb(ctx, "wo", [P, NQ // P, D])
        gain = f.sb(ctx, "gain", [P, 2, D])
        z = f.sb(ctx, "zn", [P, NT, D])
        xn = f.sb(ctx, "xn", [P, NT, D])
        xnT = f.sb(ctx, "xnT", [P, KC, S])
        q = f.sb(ctx, "q", [P, NT, NQ])
        kv = f.sb(ctx, "kv", [P, NT, 2 * HD])
        square = f.sb(ctx, "square", [P, NT, NQ + HD])
        norms = f.sb(ctx, "norms", [P, NT, HM + 1])
        kk = f.sb(ctx, "kk", [P, NT, 2 * HD])
        qT = f.sb(ctx, "qT", [P, NQ // P, S])
        kT = f.sb(ctx, "kT", [P, S])
        ps = f.ps(ctx, "ps", [P, 2, BANK])
        att = ShortAttention(f, ctx, HM, 1.0, False)
        tiles = lambda n: ps[:, n].rearrange("p (t n) -> p t n", t=NT)
        block = ctx.enter_context(nc.Block())

        @block.sync
        def _(sp):
            loads = [(wq[:], rows_of(i["L1_attn_Wq"])), (wkv[:], rows_of(i["L1_attn_Wkv"])),
                     (wo[:], rows_of(i["L1_attn_Wout"]))]
            loads += [(gain[:, n], i[f"L1_attn_{m}"].partition_broadcast(P)) for n, m in enumerate(("norm_g", "out_norm_g"))]
            for dst, src in loads:
                sp.dma_start(dst, src).then_inc(s["loaded"], 16)
            for dst, src in w1.loads:
                sp.dma_start(dst, src).then_inc(s["next_loaded"], 16)
            sp.wait_ge(s["next_loaded"], 16 * len(w1.loads))

        @block.tensor
        def _(pe):
            pe.wait_ge(s["xn_ready"], 1)
            transpose_tokens(nc, tiles(0), xn, f.ident[:]).then_inc(s["xnT_mm"], 1)
            pe.wait_ge(s["loaded"], 80)
            pe.wait_ge(s["xnT_sb"], 1)
            for t in range(NT):
                if t == 1:
                    pe.wait_ge(s["xnT_sb"], 1)
                for c in range(KC):
                    mm = nc.tensor.matmul(ps[:, t], xnT[:, c, t * P:(t + 1) * P], wq[:, c, :],
                                          start=(c == 0), stop=(c == KC - 1))
                mm.then_inc(s["q_mm"], 1)
            for t in range(NT):
                for c in range(KC):
                    mm = nc.tensor.matmul(att.attn_ps[:, 0, t * 2 * HD:(t + 1) * 2 * HD], xnT[:, c, t * P:(t + 1) * P],
                                          wkv[:, c, :], start=(c == 0), stop=(c == KC - 1))
            mm.then_inc(s["kv_mm"], 1)
            pe.wait_ge(s["scaled"], 1)
            for n in range(NQ // P):
                for t in range(NT):
                    mm = nc.tensor.transpose(tiles(n // 2)[:, n % 2, t * P:(t + 1) * P], q[:, t, n * P:(n + 1) * P],
                                             f.ident[:])
            mm.then_inc(s["qT_mm"], 1)
            for t in range(NT):
                mm = nc.tensor.transpose(att.attn_ps[:, 1, t * P:(t + 1) * P], kk[:, t, :], f.ident[:])
            mm.then_inc(s["qT_mm"], 1)
            pe.wait_ge(s["qT_sb"], 3)

            def products(h, t):
                at = HD * (h % 2)
                return [(qT[at:at + HD, h // 2, t * P:(t + 1) * P], kT[at:at + HD, :])]

            att.tensor(pe, products, lambda h, kt: kv[:, kt, HD:2 * HD])
            pe.wait_ge(att.s["attn_sb"], HM // 2)
            for t in range(NT):
                for c in range(NQ // P):
                    mm = nc.tensor.matmul(tiles(0)[:, t], att.attnT[:, c, t * P:(t + 1) * P], wo[:, c, :],
                                          start=(c == 0), stop=(c == NQ // P - 1))
            mm.then_inc(s["out_mm"], 1)

        @block.scalar
        def _(act):
            take_root(f, act, s["var_ready"], s["root_ready"])
            take_root(f, act, s["var_ready"], s["root_ready"], 1)
            act.wait_ge(s["xnT_mm"], 1)
            nc.scalar.copy(xnT[:], tiles(0)).then_inc(s["xnT_sb"], 1)
            act.wait_ge(s["sums_ready"], 1)
            nc.scalar.sqrt(norms[:], norms[:]).then_inc(s["norms_ready"], 1)
            act.wait_ge(s["qT_mm"], 2)
            for n in range(2):
                nc.scalar.copy(qT[:, 2 * n:2 * n + 2], tiles(n)).then_inc(s["qT_sb"], 1)
            nc.scalar.copy(kT[:], att.attn_ps[:, 1, 0:S]).then_inc(s["qT_sb"], 1)
            att.scalar(act)
            take_root(f, act, s["var_ready"], s["root_ready"], 2)

        @block.vector
        def _(dve):
            step = Chain(dve, s["dve_steps"])
            layer_norm(f, dve, step, z, f.x, 1e-5, s["var_ready"], s["root_ready"])
            layer_norm(f, dve, step, xn, z, 1e-5, s["var_ready"], s["root_ready"], 1)
            dve.wait_ge(s["loaded"], 80)
            for t in range(NT):
                step(nc.vector.tensor_tensor(xn[:, t], xn[:, t], gain[:, 0], ALU.mult))
            dve.sem_inc(s["xn_ready"], 1)
            dve.wait_ge(s["q_mm"], 2)
            dve.wait_ge(s["kv_mm"], 1)
            step(nc.vector.tensor_copy(q[:], ps[:]))
            step(nc.vector.tensor_copy(kv[:], att.attn_ps[:, 0, 0:NT * 2 * HD].rearrange("p (t n) -> p t n", t=NT)))
            step(nc.vector.scalar_tensor_tensor(out=square[:, :, 0:NQ], in0=q[:], scalar=16.0 ** 2, in1=q[:],
                                                op0=ALU.mult, op1=ALU.mult))
            step(nc.vector.tensor_tensor(square[:, :, NQ:], kv[:, :, 0:HD], kv[:, :, 0:HD], ALU.mult))
            step(nc.vector.tensor_reduce(norms[:], square[:].rearrange("p t (h d) -> p t h d", d=HD), AX, ALU.add))
            dve.sem_inc(s["sums_ready"], 1)
            dve.wait_ge(s["norms_ready"], 1)
            step(nc.vector.tensor_scalar(norms[:], norms[:], 1e-12, None, ALU.max))
            step(nc.vector.reciprocal(norms[:], norms[:]))
            step(nc.vector.tensor_scalar(norms[:, :, 0:HM], norms[:, :, 0:HM], 16.0 * 4.0, None, ALU.mult))
            for t in range(NT):
                step(nc.vector.tensor_tensor(q[:, t].rearrange("p (h d) -> p h d", h=HM),
                                             q[:, t].rearrange("p (h d) -> p h d", h=HM),
                                             norms[:, t, 0:HM].unsqueeze(2).to_broadcast([P, HM, HD]), ALU.mult))
                for n in range(2):
                    step(nc.vector.tensor_scalar(kk[:, t, n * HD:(n + 1) * HD], kv[:, t, 0:HD], norms[:, t, HM:HM + 1],
                                                 4.0, ALU.mult, ALU.mult))
            dve.sem_inc(s["scaled"], 1)
            att.vector(dve)
            dve.wait_ge(s["out_mm"], 1)
            step(nc.vector.tensor_copy(z[:], tiles(0)))
            layer_norm(f, dve, step, xn, z, 1e-5, s["var_ready"], s["root_ready"], 2)
            for t in range(NT):
                step(nc.vector.tensor_tensor(xn[:, t], xn[:, t], gain[:, 1], ALU.mult))
            step(nc.vector.tensor_tensor(f.x[:], f.x[:], xn[:], ALU.add))


def mixture1(f, w1):
    nc, w13, w2, wg, before = f.nc, w1.w13, w1.w2, w1.wg, w1.before
    f.layer = "m1"
    s = {n: f.sem(n) for n in ("var_ready", "root_ready", "dve_steps", "xn_ready", "xnT_mm",
                               "xnT_sb", "logits_mm", "top_ready", "exp_done", "gated_mm", "silu_done", "silu_used",
                               "inner_done", "out_mm", "summed")}
    w_loaded = [f.sem(f"w_loaded{n}") for n in range(RING1)]
    NI = I1 // P
    with ExitStack() as ctx:
        over, same = (f.sb(ctx, n, [P, E1, E1]) for n in ("over", "same"))
        xn = f.sb(ctx, "xn", [P, NT, D])
        xnT = f.sb(ctx, "xnT", [P, KC, S])
        logits, exps, rank, gates = (f.sb(ctx, n, [P, NT, E1]) for n in ("logits", "exps", "rank", "gates"))
        ntop, zsum = (f.sb(ctx, n, [P, NT]) for n in ("ntop", "zsum"))
        act_in = f.sb(ctx, "act_in", [P, 2, 2, S])
        inner = f.sb(ctx, "inner", [P, 2, NI, S])
        in_ps = f.ps(ctx, "in_ps", [P, 2, 2, 2, S])
        out_ps = f.ps(ctx, "out_ps", [P, 2, NT, D])
        ps = f.ps(ctx, "ps", [P, 2, BANK])
        tiles = lambda n: ps[:, n].rearrange("p (t n) -> p t n", t=NT)
        block = ctx.enter_context(nc.Block())

        @block.sync
        def _(sp):
            with sp.Fori(1, E1 // RING1) as r:
                for n in range(RING1):
                    sp.wait_ge(s["out_mm"], (r - 1) * RING1 + n + 3)
                    for dst, src in w1.expert(r * RING1 + n, n):
                        sp.dma_start(dst, src).then_inc(w_loaded[n], 16)

        @block.tensor
        def _(pe):
            pe.sem_inc(s["out_mm"], 2)
            pe.wait_ge(s["xn_ready"], 1)
            transpose_tokens(nc, tiles(0), xn, f.ident[:]).then_inc(s["xnT_mm"], 1)
            pe.wait_ge(s["xnT_sb"], 1)
            for t in range(NT):
                for c in range(KC):
                    mm = nc.tensor.matmul(ps[:, 1, t * E1:(t + 1) * E1], xnT[:, c, t * P:(t + 1) * P], wg[:, c, :],
                                          start=(c == 0), stop=(c == KC - 1))
            mm.then_inc(s["logits_mm"], 1)

            def expert_in(r, n, half):
                if half == 0 and not (isinstance(r, int) and r == 0):
                    pe.wait_ge(w_loaded[n], 48 * r)
                pe.wait_ge(s["silu_used"], 2 * (RING1 * r + n) + half + 1)
                for m in range(2):
                    for a in range(2):
                        at = (2 * half + a) * P
                        for c in range(KC):
                            mm = nc.tensor.matmul(in_ps[:, half, m, a], w13[:, n, m, c, at:at + P], xnT[:, c, :],
                                                  start=(c == 0), stop=(c == KC - 1))
                mm.then_inc(s["gated_mm"], 1)

            def expert_out(r, n):
                e = RING1 * r + n
                pe.wait_ge(s["inner_done"], 2 * e + 2)
                pe.wait_ge(s["summed"], 2 * e + 2)
                for t in range(NT):
                    for a in range(NI):
                        mm = nc.tensor.matmul(out_ps[:, n % 2, t], inner[:, n % 2, a, t * P:(t + 1) * P], w2[:, n, a, :],
                                              start=(a == 0), stop=(a == NI - 1))
                mm.then_inc(s["out_mm"], 1)

            expert_in(0, 0, 0)
            for r in range(E1 // RING1):
                for n in range(RING1):
                    expert_in(r, n, 1)
                    if RING1 * r + n < E1 - 1:
                        expert_in(r + (n + 1) // RING1, (n + 1) % RING1, 0)
                    expert_out(r, n)

        @block.scalar
        def _(act):
            take_root(f, act, s["var_ready"], s["root_ready"])
            act.wait_ge(s["xnT_mm"], 1)
            nc.scalar.copy(xnT[:], tiles(0)).then_inc(s["xnT_sb"], 1)
            act.wait_ge(s["top_ready"], 1)
            for t in range(NT):
                ins = nc.scalar.activation(exps[:, t], logits[:, t], ACT.Exp, bias=ntop[:, t:t + 1])
            ins.then_inc(s["exp_done"], 1)
            with act.Fori(0, E1 // RING1) as r:
                for n in range(RING1):
                    for half in range(2):
                        u = 2 * (RING1 * r + n) + half
                        act.wait_ge(s["gated_mm"], u + 1)
                        act.wait_ge(s["silu_used"], u + 1)
                        nc.scalar.activation(act_in[:, half], in_ps[:, half, 0], ACT.Silu).then_inc(s["silu_done"], 1)

        @block.vector
        def _(dve):
            step = Chain(dve, s["dve_steps"])
            dve.sem_inc(s["silu_used"], 2)
            dve.sem_inc(s["summed"], 4)
            layer_norm(f, dve, step, xn, f.x, 1e-5, s["var_ready"], s["root_ready"])
            dve.sem_inc(s["xn_ready"], 1)
            dve.wait_ge(s["logits_mm"], 1)
            step(nc.vector.tensor_copy(logits[:], ps[:, 1, 0:NT * E1].rearrange("p (t e) -> p t e", t=NT)))
            step(nc.vector.tensor_reduce(ntop[:], logits[:], AX, ALU.max))
            step(nc.vector.tensor_scalar(ntop[:], ntop[:], -1.0, None, ALU.mult))
            dve.sem_inc(s["top_ready"], 1)
            for t in range(NT):
                route(nc, step, gates[:, t], logits[:, t], before[:], over[:], same[:], rank[:, t], TOP1)
            dve.wait_ge(s["exp_done"], 1)
            for t in range(NT):
                step(nc.vector.scalar_tensor_tensor(out=gates[:, t], in0=rank[:, t], scalar=float(TOP1), in1=exps[:, t],
                                                    op0=ALU.is_lt, op1=ALU.mult))
            step(nc.vector.tensor_reduce(zsum[:], gates[:], AX, ALU.add))
            step(nc.vector.reciprocal(zsum[:], zsum[:]))
            for t in range(NT):
                step(nc.vector.tensor_scalar(gates[:, t], gates[:, t], zsum[:, t:t + 1], None, ALU.mult))

            def multiply(r, n):
                for half in range(2):
                    u = 2 * (RING1 * r + n) + half
                    dve.wait_ge(s["silu_done"], u + 1)
                    if half == 0:
                        dve.wait_ge(s["out_mm"], RING1 * r + n + 1)
                    ins = nc.vector.tensor_tensor(inner[:, n % 2, 2 * half:2 * half + 2], act_in[:, half], in_ps[:, half, 1],
                                                  ALU.mult).then_inc(s["inner_done"], 1)
                    dve.wait_ge(s["inner_done"], u + 1)
                    dve.sem_inc(s["silu_used"], 1)

            def add(r, n):
                e = RING1 * r + n
                dve.wait_ge(s["out_mm"], e + 3)
                for t in range(NT):
                    dve.wait_ge(s["summed"], 2 * e + t + 3)
                    nc.vector.scalar_tensor_tensor(out=f.x[:, t], in0=out_ps[:, n % 2, t], scalar=gates[:, t, bass.ds(e, 1)],
                                                   in1=f.x[:, t], op0=ALU.mult, op1=ALU.add).then_inc(s["summed"], 1)

            with dve.Fori(0, E1 // RING1) as r:
                for n in range(RING1):
                    multiply(r, n)
                    add(r, n)
            dve.wait_ge(s["summed"], 2 * E1 + 4)


def constants():
    c = {}
    c["c_ident"] = np.eye(P, dtype=np.float32)
    inv = np.exp(np.arange(D // 2, dtype=np.float32) * np.float32(-np.log(10000.0) / (D // 2 - 1)))
    st = np.arange(S2 - 1, -1, -1, dtype=np.float32)[None, :] * inv[:, None]
    c["c_sinusoids"] = np.concatenate([np.sin(st), np.cos(st)], 0).astype(np.float32)
    head = (np.arange(D) // DK)
    c["c_head_of"] = (head[:, None] == np.arange(H)[None, :]).astype(np.float32).reshape(KC, P, H).transpose(1, 0, 2)
    r = np.arange(P)
    c["c_gather"] = (r[:, None] % QUAD == np.arange(DV)[None, :]).astype(np.float32)
    inv = 1.0 / 10000.0 ** (np.arange(0, D, 2, dtype=np.float32) / D)
    ang = np.arange(S, dtype=np.float32)[:, None] * inv.astype(np.float32)
    c["c_rope"] = np.stack([np.cos(ang), np.sin(ang)]).astype(np.float32).reshape(2, NT, P, D // 2).transpose(2, 0, 1, 3)
    c["c_same_head"] = (head[:, None] == head[None, :]).astype(np.float32).reshape(KC, P, D).transpose(1, 0, 2)
    c["c_pos"] = np.broadcast_to(np.arange(S, dtype=np.float32), (P, S))
    q = np.arange(NT)[None, :, None] * P + np.arange(P)[:, None, None]
    c["c_causal"] = np.where(np.arange(S)[None, None, :] <= q, 0.0, -1e30).astype(np.float32)
    e = np.arange(E0)
    c["c_before31"] = (e[None, :] < e[:, None]).astype(np.float32).reshape(1, E0, E0)
    e = np.arange(E1)
    c["c_before8"] = (e[None, :] < e[:, None]).astype(np.float32).reshape(1, E1, E1)
    return {k: np.ascontiguousarray(v) for k, v in c.items()}


def columns(a):
    return np.ascontiguousarray(np.reshape(a, (-1, P)).T)


def lay_out(v):
    t = lambda a: np.ascontiguousarray(np.asarray(a).T)
    row = lambda a: np.ascontiguousarray(np.asarray(a).reshape(1, -1))
    col = lambda a: np.ascontiguousarray(np.asarray(a).reshape(-1, 1))
    a = {"x": np.asarray(v["x"]), "ctx_1024": t(np.asarray(v["ctx_1024"])[0])}
    for n in ("Wq", "Wk", "Wv", "Wo", "w1", "w2", "w3"):
        a[f"L0_xattn_{n}"] = t(v[f"L0_xattn_{n}"])
    for n in ("bq", "bk"):
        a[f"L0_xattn_{n}"] = columns(v[f"L0_xattn_{n}"])
    for n in ("bv", "bo", "b3"):
        a[f"L0_xattn_{n}"] = row(v[f"L0_xattn_{n}"])
    for n in ("b1", "b2"):
        a[f"L0_xattn_{n}"] = col(v[f"L0_xattn_{n}"])
    for n in ("Wq", "Wk", "Wv", "Wp", "Wo"):
        a[f"L1_xattn_{n}"] = np.asarray(v[f"L1_xattn_{n}"])
    for n in ("bk", "bp", "bq"):
        a[f"L1_xattn_{n}"] = columns(v[f"L1_xattn_{n}"])
    for n in ("bv", "bo"):
        a[f"L1_xattn_{n}"] = row(v[f"L1_xattn_{n}"])
    for n in "qkv":
        a[f"L0_attn_W{n}"] = t(v[f"L0_attn_W{n}"])
        a[f"L0_attn_b{n}"] = row(v[f"L0_attn_b{n}"])
    for n in ("gamma", "beta"):
        a[f"L0_attn_{n}"] = row(v[f"L0_attn_{n}"])
    n = "L0_ffn_"
    turned = lambda w: np.ascontiguousarray(np.asarray(w).reshape(-1, H // 4, 4, HD // 2, 2).transpose(0, 1, 4, 2, 3)
                                            ).reshape(-1, H * HD)
    a[n + "q_w"], a[n + "k_w"] = turned(v[n + "q_w"]), turned(v[n + "k_w"])
    a[n + "qk_b"] = np.ascontiguousarray(np.stack([columns(turned(v[n + b])) for b in ("q_b", "k_b")], 1))
    for m in ("v_w", "o_w", "router_w"):
        a[n + m] = np.asarray(v[n + m])
    for m in ("v_b", "o_b", "router_b", "gamma1", "gamma2"):
        a[n + m] = row(v[n + m])
    a[n + "theta"] = col(v[n + "theta"])
    both = lambda x, y: np.concatenate([np.asarray(x), np.asarray(y)[None]])
    w1 = both(v[n + "re_w1"], v[n + "sh_w1"]).reshape(EXPERTS0, KC, P, I0)
    w2 = both(v[n + "re_w2"], v[n + "sh_w2"]).reshape(EXPERTS0, I0 // P, P, D)
    b1 = both(v[n + "re_b1"], v[n + "sh_b1"]).reshape(EXPERTS0, I0 // P, P, 1)
    a[n + "e_w"] = np.ascontiguousarray(np.concatenate(
        [y.transpose(0, 2, 1, 3).reshape(EXPERTS0, P, -1) for y in (w1, w2, b1)], 2))
    a[n + "e_b2"] = both(v[n + "re_b2"], v[n + "sh_b2"])
    a["L1_xattn_bcols"] = np.ascontiguousarray(np.stack(
        [columns(v[f"L1_xattn_{m}"]) for m in ("bq", "r_w_bias", "r_r_bias")], 1))
    a["mask"] = np.asarray(v["mask_Bx1xSxS2_ff1"]).reshape(S, S2)
    for m in ("attn_Wq", "attn_Wkv", "attn_Wout", "ffn_w_gate", "ffn_w1", "ffn_w3", "ffn_w2"):
        a[f"L1_{m}"] = np.asarray(v[f"L1_{m}"])
    for m in ("norm_g", "out_norm_g"):
        a[f"L1_attn_{m}"] = row(v[f"L1_attn_{m}"])
    return a


def run(f, layer):
    f.sems = []
    layer(f)
    f.nc.clear_and_free_semaphores(f.sems)
    f.nc.all_engine_barrier()


def middle(f):
    with ExitStack() as outer:
        f.layer = "w0"
        mask = f.sb(outer, "mask1", [P, NT, S2])
        with ExitStack() as ctx:
            w0 = Block0Weights(f, ctx)
            run(f, lambda f: linear_attn(f, w0))
            run(f, lambda f: block0(f, w0, mask))
        run(f, lambda f: cross1(f, mask))


def latent1(f):
    with ExitStack() as ctx:
        f.layer = "w1"
        w1 = Mixture1Weights(f, ctx)
        run(f, lambda f: multi_query(f, w1))
        run(f, lambda f: mixture1(f, w1))


LAYERS = [lambda f: run(f, cross0), middle, latent1]


def build(nc, ins, out):
    with ExitStack() as ctx:
        f = Frame(nc, ctx, ins, out)
        f.key_parts = nc.dram_tensor("key_parts", (3, 3, D, S2), BF16, kind="Internal").ap()
        f.key_heads = f.key_parts.rearrange("m s (h d) n -> m s h d n", d=DK)
        f.query_parts = nc.dram_tensor("query_parts", (3, 3, D, S), BF16, kind="Internal").ap()
        f.value_rows = nc.dram_tensor("value_rows", (2, H, P, NCH, DV), F32, kind="Internal").ap()
        f.max_parts = nc.dram_tensor("max_parts", (3, H * S), BF16, kind="Internal").ap()
        f.rel_dram = nc.dram_tensor("rel_scores", (H, S * PITCH), F32, kind="Internal").ap()
        f.x = f.sb(ctx, "x", [P, NT, D])
        f.ident = f.sb(ctx, "ident", [P, P])
        f.ones = f.sb(ctx, "ones", [P, P])
        f.stats = f.sb(ctx, "stats", [P, NT, 6])
        f.mv = f.sb(ctx, "mv", [P, NT, 2])
        f.rstd = f.sb(ctx, "rstd", [P, NT])
        f.key_sums = f.sb(ctx, "key_sums", [P, KC, NQU])
        for layer in LAYERS:
            layer(f)
        f.layer, f.sems = "end", []
        stored = f.sem("stored")
        block = ctx.enter_context(nc.Block())

        @block.sync
        def _(sp):
            sp.dma_start(out.rearrange("b (t p) d -> p (b t) d", p=P), f.x[:]).then_inc(stored, 16)
            sp.wait_ge(stored, 16)


def kernel(**inputs):
    import concourse.bacc as bacc
    from concourse.bass_utils import run_bass_kernel_spmd

    nc = bacc.Bacc("TRN2", target_bir_lowering=False, num_devices=1)
    arrays = {**lay_out(inputs), **constants()}
    ins = {n: nc.dram_tensor(f"in_{n}", a.shape, mybir.dt.from_np(a.dtype), kind="ExternalInput").ap()
           for n, a in arrays.items()}
    out = nc.dram_tensor("out_x", (1, S, D), F32, kind="ExternalOutput").ap()
    build(nc, ins, out)
    r = run_bass_kernel_spmd(nc, [{f"in_{n}": a for n, a in arrays.items()}], core_ids=[0])
    return r.results[0]["out_x"]
```
